# Optimizing a Trainium2 kernel written in Bass

```python
import numpy as np
import jax
import jax.numpy as jnp

def _softmax(x, axis=-1):
    return jax.nn.softmax(x, axis=axis)

def _gelu(x):
    return jax.nn.gelu(x, approximate=True)

def _silu(x):
    return jax.nn.silu(x)

def _sigmoid(x):
    return jax.nn.sigmoid(x)

def _layernorm(x, axis=-1, eps=1e-05):
    m = jnp.mean(x, axis=axis, keepdims=True)
    v = jnp.var(x, axis=axis, keepdims=True)
    return (x - m) / jnp.sqrt(v + eps)

def _scatter_add(tgt, idx, src, axis=0):
    return tgt.at[idx].add(src)

def _segment_sum(src, seg, n):
    return jax.ops.segment_sum(src, seg, n)
kernel_name = 'mk_perceiver_d4_seqx_r8_1b890d'

def setup_inputs(seed: int=0):
    np.random.seed(seed)
    _w = jnp.asarray

    def _rec_inputs():
        import jax
        import jax.numpy as jnp
        _rk = jax.random.key(seed)
        x = -0.0002928 + 1 * jax.random.normal(jax.random.fold_in(_rk, 1), (1, 64, 128), jnp.float32)
        _lenS = 64 - jax.random.randint(jax.random.fold_in(_rk, 7), (1,), 0, max(1, 64 // 4) + 1, jnp.int32)
        _lenS2 = 6272 - jax.random.randint(jax.random.fold_in(_rk, 8), (1,), 0, max(1, 6272 // 4) + 1, jnp.int32)
        _ctx_768P = jax.random.normal(jax.random.fold_in(_rk, 11), (1, 16, 96), jnp.float32)
        _ctx_768c = jax.random.dirichlet(jax.random.fold_in(_rk, 511), 0.3 * jnp.ones((16,), jnp.float32), (1, 6272))
        _ctx_768t = jnp.einsum('bsk,bkd->bsd', _ctx_768c, _ctx_768P)
        _ctx_768t = _ctx_768t * jax.lax.rsqrt(jnp.mean(jnp.square(_ctx_768t)) + 1e-12) * 0.953939
        ctx_768 = 2.09791e-05 + 1.00001 * (_ctx_768t + 0.3 * jax.random.normal(jax.random.fold_in(_rk, 611), (1, 6272, 96), jnp.float32))
        _validS = jnp.arange(64)[None, :] < _lenS[:, None]
        _validS2 = jnp.arange(6272)[None, :] < _lenS2[:, None]
        _causal = jnp.tril(jnp.ones((64, 64), dtype=bool))
        mask_BxS_bf1 = jnp.ones((1, 64), dtype=bool)
        mask_BxS2_bf1 = jnp.ones((1, 6272), dtype=bool)
        return (x, ctx_768, mask_BxS_bf1, mask_BxS2_bf1)
    x, ctx_768, mask_BxS_bf1, mask_BxS2_bf1 = _rec_inputs()

    def _L0_xattn_setup():
        import jax, jax.numpy as jnp
        import numpy as np
        QUERY_DIM, KV_DIM, EMBED_DIM, NUM_HEADS = (128, 96, 128, 16)
        HEAD_DIM = EMBED_DIM // NUM_HEADS
        SCALE = HEAD_DIM ** (-0.5)
        LN_EPS = 1e-05

        def _l2norm(x, eps=1e-12):
            n = jnp.sqrt(jnp.sum(x * x, axis=-1, keepdims=True))
            return x / jnp.maximum(n, eps)
        key = jax.random.key(seed)
        ks = jax.random.split(key, 12)
        B, Nq, Nk = (2, 256, 256)
        s = lambda d: 1.0 / np.sqrt(d)
        return {'query': jax.random.normal(ks[0], (B, Nq, QUERY_DIM), jnp.float32), 'key': jax.random.normal(ks[1], (B, Nk, KV_DIM), jnp.float32), 'value': jax.random.normal(ks[2], (B, Nk, KV_DIM), jnp.float32), 'Wq': jax.random.normal(ks[3], (QUERY_DIM, EMBED_DIM), jnp.float32) * s(QUERY_DIM), 'bq': jnp.zeros((EMBED_DIM,), jnp.float32), 'Wk': jax.random.normal(ks[4], (KV_DIM, EMBED_DIM), jnp.float32) * s(KV_DIM), 'bk': jnp.zeros((EMBED_DIM,), jnp.float32), 'Wv': jax.random.normal(ks[5], (KV_DIM, EMBED_DIM), jnp.float32) * s(KV_DIM), 'bv': jnp.zeros((EMBED_DIM,), jnp.float32), 'Wo': jax.random.normal(ks[6], (EMBED_DIM, EMBED_DIM), jnp.float32) * s(EMBED_DIM), 'bo': jnp.zeros((EMBED_DIM,), jnp.float32), 'ln_gamma': jnp.ones((EMBED_DIM,), jnp.float32), 'ln_beta': jnp.zeros((EMBED_DIM,), jnp.float32)}
    _L0_xattn_all = _L0_xattn_setup()
    _L0_xattn_in = {k: v for k, v in _L0_xattn_all.items() if k in ('Wq', 'bq', 'Wk', 'bk', 'Wv', 'bv', 'Wo', 'bo', 'ln_gamma', 'ln_beta')}
    del _L0_xattn_all

    def _L0_attn_setup():
        import jax, jax.numpy as jnp
        import numpy as np
        B, T, C, F = (8, 256, 128, 512)

        def _ln(x, g, b):
            m = jnp.mean(x, axis=-1, keepdims=True)
            v = jnp.mean((x - m) ** 2, axis=-1, keepdims=True)
            return (x - m) * jax.lax.rsqrt(v + 1e-05) * g + b

        def _shift(x):
            return jnp.pad(x, ((0, 0), (1, 0), (0, 0)))[:, :-1]

        def _wkv(w, u, k, v):
            kT = jnp.swapaxes(k, 0, 1)
            vT = jnp.swapaxes(v, 0, 1)
            b, c = (k.shape[0], k.shape[2])
            aa = jnp.zeros((b, c), k.dtype)
            bb = jnp.zeros((b, c), k.dtype)
            pp = jnp.full((b, c), -1e+38, k.dtype)

            def step(carry, kv_t):
                aa, bb, pp = carry
                kt, vt = kv_t
                ww = u + kt
                p = jnp.maximum(pp, ww)
                e1 = jnp.exp(pp - p)
                e2 = jnp.exp(ww - p)
                out = (e1 * aa + e2 * vt) / (e1 * bb + e2)
                ww2 = pp + w
                p2 = jnp.maximum(ww2, kt)
                e1 = jnp.exp(ww2 - p2)
                e2 = jnp.exp(kt - p2)
                return ((e1 * aa + e2 * vt, e1 * bb + e2, p2), out)
            _, outs = jax.lax.scan(step, (aa, bb, pp), (kT, vT))
            return jnp.swapaxes(outs, 0, 1)
        key = jax.random.key(seed)
        ks = jax.random.split(key, 16)
        s = 1.0 / np.sqrt(C)
        inp = {'x': jax.random.normal(ks[0], (B, T, C), jnp.float32), 'ln0_g': jnp.ones((C,), jnp.float32), 'ln0_b': jnp.zeros((C,), jnp.float32), 'ln1_g': jnp.ones((C,), jnp.float32), 'ln1_b': jnp.zeros((C,), jnp.float32), 'time_decay': jax.random.normal(ks[1], (C,), jnp.float32) * 0.5, 'time_first': jax.random.normal(ks[2], (C,), jnp.float32) * 0.5, 'tm_k': jax.random.uniform(ks[3], (C,), jnp.float32), 'tm_v': jax.random.uniform(ks[4], (C,), jnp.float32), 'tm_r': jax.random.uniform(ks[5], (C,), jnp.float32), 'Wk': jax.random.normal(ks[6], (C, C), jnp.float32) * s, 'Wv': jax.random.normal(ks[7], (C, C), jnp.float32) * s, 'Wr': jax.random.normal(ks[8], (C, C), jnp.float32) * s, 'Wo': jax.random.normal(ks[9], (C, C), jnp.float32) * s, 'cm_k': jax.random.uniform(ks[10], (C,), jnp.float32), 'cm_r': jax.random.uniform(ks[11], (C,), jnp.float32), 'Wck': jax.random.normal(ks[12], (C, F), jnp.float32) * s, 'Wcv': jax.random.normal(ks[13], (F, C), jnp.float32) * (1.0 / np.sqrt(F)), 'Wcr': jax.random.normal(ks[14], (C, C), jnp.float32) * s}
        return inp
    _L0_attn_all = _L0_attn_setup()
    _L0_attn_in = {k: v for k, v in _L0_attn_all.items() if k in ('ln0_g', 'ln0_b', 'ln1_g', 'ln1_b', 'time_decay', 'time_first', 'tm_k', 'tm_v', 'tm_r', 'Wk', 'Wv', 'Wr', 'Wo', 'cm_k', 'cm_r', 'Wck', 'Wcv', 'Wcr')}
    del _L0_attn_all

    def _L0_ffn_setup():
        import jax, jax.numpy as jnp
        import numpy as np
        EMBED_DIM = 128
        HIDDEN_DIM = 512
        NUM_EXPERTS = 8
        TOP_K = 2
        key = jax.random.key(seed)
        ks = jax.random.split(key, 4)
        std1 = float(np.sqrt(2.0 / EMBED_DIM))
        std2 = float(np.sqrt(2.0 / HIDDEN_DIM))
        x = jax.random.normal(ks[0], (1, 256, EMBED_DIM), dtype=jnp.float32)
        w_router = jax.random.normal(ks[1], (EMBED_DIM, NUM_EXPERTS), dtype=jnp.float32) * 0.02
        w1 = jax.random.normal(ks[2], (NUM_EXPERTS, EMBED_DIM, HIDDEN_DIM), dtype=jnp.float32) * std1
        b1 = jnp.zeros((NUM_EXPERTS, HIDDEN_DIM), dtype=jnp.float32)
        w2 = jax.random.normal(ks[3], (NUM_EXPERTS, HIDDEN_DIM, EMBED_DIM), dtype=jnp.float32) * std2
        b2 = jnp.zeros((NUM_EXPERTS, EMBED_DIM), dtype=jnp.float32)
        return {'x': x, 'w_router': w_router, 'w1': w1, 'b1': b1, 'w2': w2, 'b2': b2}
    _L0_ffn_all = _L0_ffn_setup()
    _L0_ffn_in = {k: v for k, v in _L0_ffn_all.items() if k in ('w_router', 'w1', 'b1', 'w2', 'b2')}
    del _L0_ffn_all

    def _L1_xattn_setup():
        import jax, jax.numpy as jnp
        import numpy as np
        IN_DIM = 128
        CTX_DIM = 96
        NUM_HEADS = 16
        HEAD_DIM = IN_DIM // NUM_HEADS
        SCALE = 1.0 / float(np.sqrt(HEAD_DIM))
        key = jax.random.key(seed)
        ks = jax.random.split(key, 10)
        B, NQ, NKV = (8, 128, 64)
        s_in = 1.0 / float(np.sqrt(IN_DIM))
        s_ctx = 1.0 / float(np.sqrt(CTX_DIM))
        return {'x': jax.random.normal(ks[0], (B, NQ, IN_DIM), dtype=jnp.float32), 'context': jax.random.normal(ks[1], (B, NKV, CTX_DIM), dtype=jnp.float32), 'Wq': jax.random.normal(ks[2], (IN_DIM, IN_DIM), dtype=jnp.float32) * s_in, 'bq': jax.random.normal(ks[3], (IN_DIM,), dtype=jnp.float32) * 0.01, 'Wk': jax.random.normal(ks[4], (IN_DIM, CTX_DIM), dtype=jnp.float32) * s_ctx, 'bk': jax.random.normal(ks[5], (IN_DIM,), dtype=jnp.float32) * 0.01, 'Wv': jax.random.normal(ks[6], (IN_DIM, CTX_DIM), dtype=jnp.float32) * s_ctx, 'bv': jax.random.normal(ks[7], (IN_DIM,), dtype=jnp.float32) * 0.01, 'Wo': jax.random.normal(ks[8], (IN_DIM, IN_DIM), dtype=jnp.float32) * s_in, 'bo': jax.random.normal(ks[9], (IN_DIM,), dtype=jnp.float32) * 0.01}
    _L1_xattn_all = _L1_xattn_setup()
    _L1_xattn_in = {k: v for k, v in _L1_xattn_all.items() if k in ('Wq', 'bq', 'Wk', 'bk', 'Wv', 'bv', 'Wo', 'bo')}
    del _L1_xattn_all

    def _L1_attn_setup():
        import jax, jax.numpy as jnp
        import numpy as np
        D = 128
        H = 16
        G = 4
        HD = D // H
        HPG = H // G
        THETA = 10000.0
        EPS = 1e-10

        def _l2_qk_norm(t):
            return t / (jnp.sqrt(jnp.sum(t * t, axis=-1, keepdims=True)) + EPS)

        def _rope(t):
            T = t.shape[1]
            half = HD // 2
            inv_freq = 1.0 / THETA ** (jnp.arange(half, dtype=jnp.float32) / half)
            ang = jnp.arange(T, dtype=jnp.float32)[:, None] * inv_freq[None, :]
            cos = jnp.cos(ang)[None, :, None, :]
            sin = jnp.sin(ang)[None, :, None, :]
            x1, x2 = (t[..., :half], t[..., half:])
            return jnp.concatenate([x1 * cos - x2 * sin, x2 * cos + x1 * sin], axis=-1)
        key = jax.random.key(seed)
        k1, k2, k3 = jax.random.split(key, 3)
        x = jax.random.normal(k1, (1, 512, D), jnp.float32)
        w_qkv = jax.random.normal(k2, (D, H * HD + 2 * G * HD), jnp.float32) * 0.02
        w_o = jax.random.normal(k3, (D, D), jnp.float32) * 0.02
        return {'x': x, 'w_qkv': w_qkv, 'w_o': w_o}
    _L1_attn_all = _L1_attn_setup()
    _L1_attn_in = {k: v for k, v in _L1_attn_all.items() if k in ('w_qkv', 'w_o')}
    del _L1_attn_all

    def _L1_ffn_setup():
        import jax, jax.numpy as jnp
        import numpy as np
        QMAX = 127.0

        def _ste_round(v):
            return v + jax.lax.stop_gradient(jnp.round(v) - v)

        def _act_fake_quant(x, clip_factor):
            scale = jax.nn.sigmoid(clip_factor) * jnp.max(jnp.abs(x)) / QMAX
            return jnp.clip(_ste_round(x / scale), -QMAX - 1.0, QMAX) * scale

        def _weight_fake_quant(w):
            scale = jnp.max(jnp.abs(w), axis=1, keepdims=True) / QMAX
            return jnp.clip(_ste_round(w / scale), -QMAX - 1.0, QMAX) * scale
        key = jax.random.key(seed)
        k1, k2, k3, k4 = jax.random.split(key, 4)
        B, S, H, I = (8, 1024, 128, 352)
        return {'x': jax.random.normal(k1, (B, S, H), dtype=jnp.float32), 'clip_x': jnp.full((1,), 4.0, dtype=jnp.float32), 'clip_down': jnp.full((1,), 4.0, dtype=jnp.float32), 'w_gate': jax.random.normal(k2, (I, H), dtype=jnp.float32) * 0.02, 'w_up': jax.random.normal(k3, (I, H), dtype=jnp.float32) * 0.02, 'w_down': jax.random.normal(k4, (H, I), dtype=jnp.float32) * 0.02}
    _L1_ffn_all = _L1_ffn_setup()
    _L1_ffn_in = {k: v for k, v in _L1_ffn_all.items() if k in ('clip_x', 'clip_down', 'w_gate', 'w_up', 'w_down')}
    del _L1_ffn_all

    def _L2_xattn_setup():
        import jax, jax.numpy as jnp
        import numpy as np
        B, T, DT, G, DV = (16, 64, 128, 72, 96)
        H, DH = (4, 32)
        INNER = H * DH
        HID = 4 * DT
        N_STATE = 64
        K_TOP = 32

        def layernorm(x, g, b, eps=1e-05):
            m = x.mean(-1, keepdims=True)
            v = x.var(-1, keepdims=True)
            return (x - m) * jax.lax.rsqrt(v + eps) * g + b

        def s4d(x, log_dt, A_re, A_im, C_re, C_im, D_skip):
            Bb, L, D = x.shape
            dt = jnp.exp(log_dt)
            A = A_re + 1j * A_im
            C = C_re + 1j * C_im
            dtA = dt[:, None] * A
            dC = C * (jnp.exp(dtA) - 1.0) / A
            powers = jnp.exp(dtA[:, :, None] * jnp.arange(L))
            K = 2.0 * jnp.einsum('dn,dnl->dl', dC, powers).real
            n = 2 * L
            Kf = jnp.fft.rfft(K, n=n, axis=-1)
            xf = jnp.fft.rfft(x, n=n, axis=1)
            y = jnp.fft.irfft(xf * Kf.T[None], n=n, axis=1)[:, :L]
            return y + x * D_skip
        key = jax.random.key(seed)
        ks = jax.random.split(key, 16)
        s = 0.02
        inp = {'x_text': jax.random.normal(ks[0], (B, T, DT), jnp.float32), 'x_vision': jax.random.normal(ks[1], (B, G, DV), jnp.float32), 'text_mask': jnp.ones((B, T), bool), 'vision_mask': jnp.ones((B, G), bool), 'Wq': jax.random.normal(ks[2], (DT, INNER), jnp.float32) * s, 'Wk': jax.random.normal(ks[3], (DV, INNER), jnp.float32) * s, 'Wv': jax.random.normal(ks[4], (DV, DT), jnp.float32) * s, 'W_film_in': jax.random.normal(ks[5], (DT, 2 * DT), jnp.float32) * s, 'b_film_in': jnp.zeros((2 * DT,), jnp.float32), 'W_film_out': jax.random.normal(ks[6], (DT, 2 * DT), jnp.float32) * s, 'b_film_out': jnp.zeros((2 * DT,), jnp.float32), 'g_norm_in': jnp.ones((DT,), jnp.float32), 'b_norm_in': jnp.zeros((DT,), jnp.float32), 'g_norm_out': jnp.ones((DT,), jnp.float32), 'b_norm_out': jnp.zeros((DT,), jnp.float32), 'g_ffn': jnp.ones((DT,), jnp.float32), 'b_ffn': jnp.zeros((DT,), jnp.float32), 'W1': jax.random.normal(ks[7], (DT, HID), jnp.float32) * s, 'b1': jnp.zeros((HID,), jnp.float32), 'W2': jax.random.normal(ks[8], (HID, DT), jnp.float32) * s, 'b2': jnp.zeros((DT,), jnp.float32), 'log_dt': jnp.log(0.001) + jax.random.uniform(ks[9], (DT,), jnp.float32) * (jnp.log(0.1) - jnp.log(0.001)), 'A_re': -0.5 * jnp.ones((DT, N_STATE), jnp.float32), 'A_im': jnp.tile(jnp.pi * jnp.arange(N_STATE, dtype=jnp.float32), (DT, 1)), 'C_re': jax.random.normal(ks[10], (DT, N_STATE), jnp.float32) * 0.5 ** 0.5, 'C_im': jax.random.normal(ks[11], (DT, N_STATE), jnp.float32) * 0.5 ** 0.5, 'D_skip': jax.random.normal(ks[12], (DT,), jnp.float32), 'mod_gate': jnp.array(0.5, jnp.float32)}
        return inp
    _L2_xattn_all = _L2_xattn_setup()
    _L2_xattn_in = {k: v for k, v in _L2_xattn_all.items() if k in ('Wq', 'Wk', 'Wv', 'W_film_in', 'b_film_in', 'W_film_out', 'b_film_out', 'g_norm_in', 'b_norm_in', 'g_norm_out', 'b_norm_out', 'g_ffn', 'b_ffn', 'W1', 'b1', 'W2', 'b2', 'log_dt', 'A_re', 'A_im', 'C_re', 'C_im', 'D_skip', 'mod_gate')}
    del _L2_xattn_all

    def _L2_attn_setup():
        import jax, jax.numpy as jnp
        import numpy as np
        B, S, H = (2, 1024, 128)
        NUM_HEADS = 16
        HEAD_DIM = H // NUM_HEADS
        KERNEL = 7
        DILATION = 1
        SCALE = 1.0 / np.sqrt(HEAD_DIM)
        key = jax.random.key(seed)
        ks = jax.random.split(key, 9)
        init = 0.02
        return {'hidden_states': jax.random.normal(ks[0], (B, S, H), dtype=jnp.float32), 'w_q': jax.random.normal(ks[1], (H, H), dtype=jnp.float32) * init, 'b_q': jnp.zeros((H,), dtype=jnp.float32), 'w_k': jax.random.normal(ks[2], (H, H), dtype=jnp.float32) * init, 'b_k': jnp.zeros((H,), dtype=jnp.float32), 'w_v': jax.random.normal(ks[3], (H, H), dtype=jnp.float32) * init, 'b_v': jnp.zeros((H,), dtype=jnp.float32), 'w_o': jax.random.normal(ks[4], (H, H), dtype=jnp.float32) * init, 'b_o': jnp.zeros((H,), dtype=jnp.float32)}
    _L2_attn_all = _L2_attn_setup()
    _L2_attn_in = {k: v for k, v in _L2_attn_all.items() if k in ('w_q', 'b_q', 'w_k', 'b_k', 'w_v', 'b_v', 'w_o', 'b_o')}
    del _L2_attn_all

    def _L2_ffn_setup():
        import jax, jax.numpy as jnp
        import numpy as np
        NHEAD = 16
        NUM_GROUPS = 4
        EXPERTS_PER_GROUP = 2
        LN_EPS = 1e-05

        def _layernorm(x, g, b):
            mu = jnp.mean(x, axis=-1, keepdims=True)
            var = jnp.mean(jnp.square(x - mu), axis=-1, keepdims=True)
            return (x - mu) * jax.lax.rsqrt(var + LN_EPS) * g + b

        def _mha(x, wi, bi, wo, bo):
            B, S, D = x.shape
            hd = D // NHEAD
            qkv = x @ wi.T + bi
            q, k, v = jnp.split(qkv, 3, axis=-1)

            def heads(t):
                return t.reshape(B, S, NHEAD, hd).transpose(0, 2, 1, 3)
            q, k, v = (heads(q), heads(k), heads(v))
            scores = jnp.einsum('bhqd,bhkd->bhqk', q, k) / jnp.sqrt(jnp.asarray(hd, x.dtype))
            attn = jax.nn.softmax(scores, axis=-1)
            o = jnp.einsum('bhqk,bhkd->bhqd', attn, v)
            o = o.transpose(0, 2, 1, 3).reshape(B, S, D)
            return o @ wo.T + bo

        def _hier_moe(x, w_group, b_group, w_expert, b_expert, w1, b1, w2, b2):
            B, S, D = x.shape
            xt = x.reshape(B * S, D)
            T = xt.shape[0]
            E = NUM_GROUPS * EXPERTS_PER_GROUP
            gp = jax.nn.softmax(xt @ w_group + b_group, axis=-1)
            g_idx = jnp.argmax(gp, axis=-1)
            g_prob = jnp.max(gp, axis=-1)
            elog = jnp.einsum('td,gde->tge', xt, w_expert) + b_expert
            ep = jax.nn.softmax(elog, axis=-1)
            ep_sel = jnp.take_along_axis(ep, g_idx[:, None, None], axis=1)[:, 0, :]
            e_idx_local = jnp.argmax(ep_sel, axis=-1)
            e_prob = jnp.max(ep_sel, axis=-1)
            flat_e = g_idx * EXPERTS_PER_GROUP + e_idx_local
            combine = jax.nn.one_hot(flat_e, E, dtype=xt.dtype) * (g_prob * e_prob)[:, None]
            h = jax.nn.relu(jnp.einsum('td,edf->etf', xt, w1) + b1[:, None, :])
            y = jnp.einsum('etf,efd->etd', h, w2) + b2[:, None, :]
            out = jnp.einsum('te,etd->td', combine, y)
            return out.reshape(B, S, D)
        key = jax.random.key(seed)
        ks = jax.random.split(key, 8)
        B, S, D, F = (2, 128, 128, 256)
        G, Epg = (NUM_GROUPS, EXPERTS_PER_GROUP)
        E = G * Epg
        sc = lambda fan: 1.0 / np.sqrt(fan)
        return {'x': jax.random.normal(ks[0], (B, S, D), jnp.float32), 'in_proj_w': jax.random.normal(ks[1], (3 * D, D), jnp.float32) * sc(D), 'in_proj_b': jnp.zeros((3 * D,), jnp.float32), 'out_proj_w': jax.random.normal(ks[2], (D, D), jnp.float32) * sc(D), 'out_proj_b': jnp.zeros((D,), jnp.float32), 'ln1_g': jnp.ones((D,), jnp.float32), 'ln1_b': jnp.zeros((D,), jnp.float32), 'ln2_g': jnp.ones((D,), jnp.float32), 'ln2_b': jnp.zeros((D,), jnp.float32), 'w_group': jax.random.normal(ks[3], (D, G), jnp.float32) * sc(D), 'b_group': jnp.zeros((G,), jnp.float32), 'w_expert': jax.random.normal(ks[4], (G, D, Epg), jnp.float32) * sc(D), 'b_expert': jnp.zeros((G, Epg), jnp.float32), 'w1': jax.random.normal(ks[5], (E, D, F), jnp.float32) * sc(D), 'b1': jnp.zeros((E, F), jnp.float32), 'w2': jax.random.normal(ks[6], (E, F, D), jnp.float32) * sc(F), 'b2': jnp.zeros((E, D), jnp.float32)}
    _L2_ffn_all = _L2_ffn_setup()
    _L2_ffn_in = {k: v for k, v in _L2_ffn_all.items() if k in ('in_proj_w', 'in_proj_b', 'out_proj_w', 'out_proj_b', 'ln1_g', 'ln1_b', 'ln2_g', 'ln2_b', 'w_group', 'b_group', 'w_expert', 'b_expert', 'w1', 'b1', 'w2', 'b2')}
    del _L2_ffn_all

    def _L3_xattn_setup():
        import jax, jax.numpy as jnp
        import numpy as np
        N_HEADS = 16
        key = jax.random.key(seed)
        ks = jax.random.split(key, 8)
        b, l, m = (8, 128, 128)
        d_embed, d_cross = (128, 96)
        s_q = 1.0 / np.sqrt(d_embed)
        s_kv = 1.0 / np.sqrt(d_cross)
        return {'x': jax.random.normal(ks[0], (b, l, d_embed), jnp.float32), 'y': jax.random.normal(ks[1], (b, m, d_cross), jnp.float32), 'Wq': jax.random.normal(ks[2], (d_embed, d_embed), jnp.float32) * s_q, 'bq': jax.random.normal(ks[3], (d_embed,), jnp.float32) * 0.01, 'Wkv': jax.random.normal(ks[4], (2 * d_embed, d_cross), jnp.float32) * s_kv, 'bkv': jax.random.normal(ks[5], (2 * d_embed,), jnp.float32) * 0.01, 'Wo': jax.random.normal(ks[6], (d_embed, d_embed), jnp.float32) * s_q, 'bo': jax.random.normal(ks[7], (d_embed,), jnp.float32) * 0.01}
    _L3_xattn_all = _L3_xattn_setup()
    _L3_xattn_in = {k: v for k, v in _L3_xattn_all.items() if k in ('Wq', 'bq', 'Wkv', 'bkv', 'Wo', 'bo')}
    del _L3_xattn_all

    def _L3_attn_setup():
        import jax, jax.numpy as jnp
        import numpy as np
        B, S, D = (8, 256, 128)
        key = jax.random.key(seed)
        k1, k2, k3, k4 = jax.random.split(key, 4)
        return {'hidden_states': jax.random.normal(k1, (B, S, D), dtype=jnp.float32), 'w_dec_attn': jax.random.normal(k2, (D, D), dtype=jnp.float32), 'w_out': jax.random.normal(k3, (D, 2 * D), dtype=jnp.float32) * 0.02, 'b_out': jnp.zeros((D,), dtype=jnp.float32)}
    _L3_attn_all = _L3_attn_setup()
    _L3_attn_in = {k: v for k, v in _L3_attn_all.items() if k in ('w_dec_attn', 'w_out', 'b_out')}
    del _L3_attn_all

    def _L3_ffn_setup():
        import jax, jax.numpy as jnp
        import numpy as np
        import math
        N_EMBD = 128
        HIDDEN = 4 * N_EMBD
        N_EXPERTS = 8
        TOP_K = 2
        B, T = (4, 256)

        def new_gelu(x):
            c = math.sqrt(2.0 / math.pi)
            return 0.5 * x * (1.0 + jnp.tanh(c * (x + 0.044715 * x * x * x)))

        def _moe_forward(x, Wfc_s, bfc_s, Wproj_s, bproj_s, Wr, Wfc, bfc, Wproj, bproj):
            Bb, Tt, C = x.shape
            xf = x.reshape(Bb * Tt, C)
            N = Bb * Tt
            shared = new_gelu(xf @ Wfc_s + bfc_s) @ Wproj_s + bproj_s
            logits = xf @ Wr
            probs = jax.nn.softmax(logits, axis=-1)
            topk_p, topk_i = jax.lax.top_k(probs, TOP_K)
            topk_p = topk_p / jnp.sum(topk_p, axis=-1, keepdims=True)
            gate = jnp.zeros((N, N_EXPERTS), dtype=xf.dtype)
            gate = gate.at[jnp.arange(N)[:, None], topk_i].add(topk_p)
            routed = jnp.zeros_like(xf)
            for e in range(N_EXPERTS):
                h = new_gelu(xf @ Wfc[e] + bfc[e]) @ Wproj[e] + bproj[e]
                routed = routed + h * gate[:, e:e + 1]
            return (shared + routed).reshape(Bb, Tt, C)
        key = jax.random.key(seed)
        ks = jax.random.split(key, 10)
        s = 0.02
        return {'x': jax.random.normal(ks[0], (B, T, N_EMBD), dtype=jnp.float32), 'Wfc_s': jax.random.normal(ks[1], (N_EMBD, HIDDEN), dtype=jnp.float32) * s, 'bfc_s': jnp.zeros((HIDDEN,), dtype=jnp.float32), 'Wproj_s': jax.random.normal(ks[2], (HIDDEN, N_EMBD), dtype=jnp.float32) * s, 'bproj_s': jnp.zeros((N_EMBD,), dtype=jnp.float32), 'Wr': jax.random.normal(ks[3], (N_EMBD, N_EXPERTS), dtype=jnp.float32) * s, 'Wfc': jax.random.normal(ks[4], (N_EXPERTS, N_EMBD, HIDDEN), dtype=jnp.float32) * s, 'bfc': jnp.zeros((N_EXPERTS, HIDDEN), dtype=jnp.float32), 'Wproj': jax.random.normal(ks[5], (N_EXPERTS, HIDDEN, N_EMBD), dtype=jnp.float32) * s, 'bproj': jnp.zeros((N_EXPERTS, N_EMBD), dtype=jnp.float32)}
    _L3_ffn_all = _L3_ffn_setup()
    _L3_ffn_in = {k: v for k, v in _L3_ffn_all.items() if k in ('Wfc_s', 'bfc_s', 'Wproj_s', 'bproj_s', 'Wr', 'Wfc', 'bfc', 'Wproj', 'bproj')}
    del _L3_ffn_all
    return {'x': x, 'ctx_768': ctx_768, 'mask_BxS_bf1': mask_BxS_bf1, 'mask_BxS2_bf1': mask_BxS2_bf1, 'L0_xattn_Wq': _L0_xattn_in['Wq'], 'L0_xattn_bq': _L0_xattn_in['bq'], 'L0_xattn_Wk': _L0_xattn_in['Wk'], 'L0_xattn_bk': _L0_xattn_in['bk'], 'L0_xattn_Wv': _L0_xattn_in['Wv'], 'L0_xattn_bv': _L0_xattn_in['bv'], 'L0_xattn_Wo': _L0_xattn_in['Wo'], 'L0_xattn_bo': _L0_xattn_in['bo'], 'L0_xattn_ln_gamma': _L0_xattn_in['ln_gamma'], 'L0_xattn_ln_beta': _L0_xattn_in['ln_beta'], 'L0_attn_ln0_g': _L0_attn_in['ln0_g'], 'L0_attn_ln0_b': _L0_attn_in['ln0_b'], 'L0_attn_ln1_g': _L0_attn_in['ln1_g'], 'L0_attn_ln1_b': _L0_attn_in['ln1_b'], 'L0_attn_time_decay': _L0_attn_in['time_decay'], 'L0_attn_time_first': _L0_attn_in['time_first'], 'L0_attn_tm_k': _L0_attn_in['tm_k'], 'L0_attn_tm_v': _L0_attn_in['tm_v'], 'L0_attn_tm_r': _L0_attn_in['tm_r'], 'L0_attn_Wk': _L0_attn_in['Wk'], 'L0_attn_Wv': _L0_attn_in['Wv'], 'L0_attn_Wr': _L0_attn_in['Wr'], 'L0_attn_Wo': _L0_attn_in['Wo'], 'L0_attn_cm_k': _L0_attn_in['cm_k'], 'L0_attn_cm_r': _L0_attn_in['cm_r'], 'L0_attn_Wck': _L0_attn_in['Wck'], 'L0_attn_Wcv': _L0_attn_in['Wcv'], 'L0_attn_Wcr': _L0_attn_in['Wcr'], 'L0_ffn_w_router': _L0_ffn_in['w_router'], 'L0_ffn_w1': _L0_ffn_in['w1'], 'L0_ffn_b1': _L0_ffn_in['b1'], 'L0_ffn_w2': _L0_ffn_in['w2'], 'L0_ffn_b2': _L0_ffn_in['b2'], 'L1_xattn_Wq': _L1_xattn_in['Wq'], 'L1_xattn_bq': _L1_xattn_in['bq'], 'L1_xattn_Wk': _L1_xattn_in['Wk'], 'L1_xattn_bk': _L1_xattn_in['bk'], 'L1_xattn_Wv': _L1_xattn_in['Wv'], 'L1_xattn_bv': _L1_xattn_in['bv'], 'L1_xattn_Wo': _L1_xattn_in['Wo'], 'L1_xattn_bo': _L1_xattn_in['bo'], 'L1_attn_w_qkv': _L1_attn_in['w_qkv'], 'L1_attn_w_o': _L1_attn_in['w_o'], 'L1_ffn_clip_x': _L1_ffn_in['clip_x'], 'L1_ffn_clip_down': _L1_ffn_in['clip_down'], 'L1_ffn_w_gate': _L1_ffn_in['w_gate'], 'L1_ffn_w_up': _L1_ffn_in['w_up'], 'L1_ffn_w_down': _L1_ffn_in['w_down'], 'L2_xattn_Wq': _L2_xattn_in['Wq'], 'L2_xattn_Wk': _L2_xattn_in['Wk'], 'L2_xattn_Wv': _L2_xattn_in['Wv'], 'L2_xattn_W_film_in': _L2_xattn_in['W_film_in'], 'L2_xattn_b_film_in': _L2_xattn_in['b_film_in'], 'L2_xattn_W_film_out': _L2_xattn_in['W_film_out'], 'L2_xattn_b_film_out': _L2_xattn_in['b_film_out'], 'L2_xattn_g_norm_in': _L2_xattn_in['g_norm_in'], 'L2_xattn_b_norm_in': _L2_xattn_in['b_norm_in'], 'L2_xattn_g_norm_out': _L2_xattn_in['g_norm_out'], 'L2_xattn_b_norm_out': _L2_xattn_in['b_norm_out'], 'L2_xattn_g_ffn': _L2_xattn_in['g_ffn'], 'L2_xattn_b_ffn': _L2_xattn_in['b_ffn'], 'L2_xattn_W1': _L2_xattn_in['W1'], 'L2_xattn_b1': _L2_xattn_in['b1'], 'L2_xattn_W2': _L2_xattn_in['W2'], 'L2_xattn_b2': _L2_xattn_in['b2'], 'L2_xattn_log_dt': _L2_xattn_in['log_dt'], 'L2_xattn_A_re': _L2_xattn_in['A_re'], 'L2_xattn_A_im': _L2_xattn_in['A_im'], 'L2_xattn_C_re': _L2_xattn_in['C_re'], 'L2_xattn_C_im': _L2_xattn_in['C_im'], 'L2_xattn_D_skip': _L2_xattn_in['D_skip'], 'L2_xattn_mod_gate': _L2_xattn_in['mod_gate'], 'L2_attn_w_q': _L2_attn_in['w_q'], 'L2_attn_b_q': _L2_attn_in['b_q'], 'L2_attn_w_k': _L2_attn_in['w_k'], 'L2_attn_b_k': _L2_attn_in['b_k'], 'L2_attn_w_v': _L2_attn_in['w_v'], 'L2_attn_b_v': _L2_attn_in['b_v'], 'L2_attn_w_o': _L2_attn_in['w_o'], 'L2_attn_b_o': _L2_attn_in['b_o'], 'L2_ffn_in_proj_w': _L2_ffn_in['in_proj_w'], 'L2_ffn_in_proj_b': _L2_ffn_in['in_proj_b'], 'L2_ffn_out_proj_w': _L2_ffn_in['out_proj_w'], 'L2_ffn_out_proj_b': _L2_ffn_in['out_proj_b'], 'L2_ffn_ln1_g': _L2_ffn_in['ln1_g'], 'L2_ffn_ln1_b': _L2_ffn_in['ln1_b'], 'L2_ffn_ln2_g': _L2_ffn_in['ln2_g'], 'L2_ffn_ln2_b': _L2_ffn_in['ln2_b'], 'L2_ffn_w_group': _L2_ffn_in['w_group'], 'L2_ffn_b_group': _L2_ffn_in['b_group'], 'L2_ffn_w_expert': _L2_ffn_in['w_expert'], 'L2_ffn_b_expert': _L2_ffn_in['b_expert'], 'L2_ffn_w1': _L2_ffn_in['w1'], 'L2_ffn_b1': _L2_ffn_in['b1'], 'L2_ffn_w2': _L2_ffn_in['w2'], 'L2_ffn_b2': _L2_ffn_in['b2'], 'L3_xattn_Wq': _L3_xattn_in['Wq'], 'L3_xattn_bq': _L3_xattn_in['bq'], 'L3_xattn_Wkv': _L3_xattn_in['Wkv'], 'L3_xattn_bkv': _L3_xattn_in['bkv'], 'L3_xattn_Wo': _L3_xattn_in['Wo'], 'L3_xattn_bo': _L3_xattn_in['bo'], 'L3_attn_w_dec_attn': _L3_attn_in['w_dec_attn'], 'L3_attn_w_out': _L3_attn_in['w_out'], 'L3_attn_b_out': _L3_attn_in['b_out'], 'L3_ffn_Wfc_s': _L3_ffn_in['Wfc_s'], 'L3_ffn_bfc_s': _L3_ffn_in['bfc_s'], 'L3_ffn_Wproj_s': _L3_ffn_in['Wproj_s'], 'L3_ffn_bproj_s': _L3_ffn_in['bproj_s'], 'L3_ffn_Wr': _L3_ffn_in['Wr'], 'L3_ffn_Wfc': _L3_ffn_in['Wfc'], 'L3_ffn_bfc': _L3_ffn_in['bfc'], 'L3_ffn_Wproj': _L3_ffn_in['Wproj'], 'L3_ffn_bproj': _L3_ffn_in['bproj']}

def reference(x, ctx_768, mask_BxS_bf1, mask_BxS2_bf1, L0_xattn_Wq, L0_xattn_bq, L0_xattn_Wk, L0_xattn_bk, L0_xattn_Wv, L0_xattn_bv, L0_xattn_Wo, L0_xattn_bo, L0_xattn_ln_gamma, L0_xattn_ln_beta, L0_attn_ln0_g, L0_attn_ln0_b, L0_attn_ln1_g, L0_attn_ln1_b, L0_attn_time_decay, L0_attn_time_first, L0_attn_tm_k, L0_attn_tm_v, L0_attn_tm_r, L0_attn_Wk, L0_attn_Wv, L0_attn_Wr, L0_attn_Wo, L0_attn_cm_k, L0_attn_cm_r, L0_attn_Wck, L0_attn_Wcv, L0_attn_Wcr, L0_ffn_w_router, L0_ffn_w1, L0_ffn_b1, L0_ffn_w2, L0_ffn_b2, L1_xattn_Wq, L1_xattn_bq, L1_xattn_Wk, L1_xattn_bk, L1_xattn_Wv, L1_xattn_bv, L1_xattn_Wo, L1_xattn_bo, L1_attn_w_qkv, L1_attn_w_o, L1_ffn_clip_x, L1_ffn_clip_down, L1_ffn_w_gate, L1_ffn_w_up, L1_ffn_w_down, L2_xattn_Wq, L2_xattn_Wk, L2_xattn_Wv, L2_xattn_W_film_in, L2_xattn_b_film_in, L2_xattn_W_film_out, L2_xattn_b_film_out, L2_xattn_g_norm_in, L2_xattn_b_norm_in, L2_xattn_g_norm_out, L2_xattn_b_norm_out, L2_xattn_g_ffn, L2_xattn_b_ffn, L2_xattn_W1, L2_xattn_b1, L2_xattn_W2, L2_xattn_b2, L2_xattn_log_dt, L2_xattn_A_re, L2_xattn_A_im, L2_xattn_C_re, L2_xattn_C_im, L2_xattn_D_skip, L2_xattn_mod_gate, L2_attn_w_q, L2_attn_b_q, L2_attn_w_k, L2_attn_b_k, L2_attn_w_v, L2_attn_b_v, L2_attn_w_o, L2_attn_b_o, L2_ffn_in_proj_w, L2_ffn_in_proj_b, L2_ffn_out_proj_w, L2_ffn_out_proj_b, L2_ffn_ln1_g, L2_ffn_ln1_b, L2_ffn_ln2_g, L2_ffn_ln2_b, L2_ffn_w_group, L2_ffn_b_group, L2_ffn_w_expert, L2_ffn_b_expert, L2_ffn_w1, L2_ffn_b1, L2_ffn_w2, L2_ffn_b2, L3_xattn_Wq, L3_xattn_bq, L3_xattn_Wkv, L3_xattn_bkv, L3_xattn_Wo, L3_xattn_bo, L3_attn_w_dec_attn, L3_attn_w_out, L3_attn_b_out, L3_ffn_Wfc_s, L3_ffn_bfc_s, L3_ffn_Wproj_s, L3_ffn_bproj_s, L3_ffn_Wr, L3_ffn_Wfc, L3_ffn_bfc, L3_ffn_Wproj, L3_ffn_bproj):
    import jax
    import jax.numpy as jnp

    def _L0_xattn_ref(query, key, value, Wq, bq, Wk, bk, Wv, bv, Wo, bo, ln_gamma, ln_beta):
        import jax, jax.numpy as jnp
        import numpy as np
        QUERY_DIM, KV_DIM, EMBED_DIM, NUM_HEADS = (128, 96, 128, 16)
        HEAD_DIM = EMBED_DIM // NUM_HEADS
        SCALE = HEAD_DIM ** (-0.5)
        LN_EPS = 1e-05

        def _l2norm(x, eps=1e-12):
            n = jnp.sqrt(jnp.sum(x * x, axis=-1, keepdims=True))
            return x / jnp.maximum(n, eps)
        B, Nq, _ = query.shape
        Nk = key.shape[1]
        Qp = query @ Wq + bq
        K = _l2norm(key @ Wk + bk)
        V = value @ Wv + bv
        Q = _l2norm(Qp)
        Q = Q.reshape(B, Nq, NUM_HEADS, HEAD_DIM).transpose(0, 2, 1, 3)
        K = K.reshape(B, Nk, NUM_HEADS, HEAD_DIM).transpose(0, 2, 1, 3)
        V = V.reshape(B, Nk, NUM_HEADS, HEAD_DIM).transpose(0, 2, 1, 3)
        scores = jnp.einsum('bhqd,bhkd->bhqk', Q, K) * SCALE
        attn = jax.nn.softmax(scores, axis=-1)
        out = jnp.einsum('bhqk,bhkd->bhqd', attn, V)
        out = out.transpose(0, 2, 1, 3).reshape(B, Nq, EMBED_DIM)
        out = out @ Wo + bo
        x = out + Qp
        mu = jnp.mean(x, axis=-1, keepdims=True)
        var = jnp.mean((x - mu) ** 2, axis=-1, keepdims=True)
        return (x - mu) / jnp.sqrt(var + LN_EPS) * ln_gamma + ln_beta

    def _L0_attn_ref(x, ln0_g, ln0_b, ln1_g, ln1_b, time_decay, time_first, tm_k, tm_v, tm_r, Wk, Wv, Wr, Wo, cm_k, cm_r, Wck, Wcv, Wcr):
        import jax, jax.numpy as jnp
        import numpy as np
        B, T, C, F = (8, 256, 128, 512)

        def _ln(x, g, b):
            m = jnp.mean(x, axis=-1, keepdims=True)
            v = jnp.mean((x - m) ** 2, axis=-1, keepdims=True)
            return (x - m) * jax.lax.rsqrt(v + 1e-05) * g + b

        def _shift(x):
            return jnp.pad(x, ((0, 0), (1, 0), (0, 0)))[:, :-1]

        def _wkv(w, u, k, v):
            kT = jnp.swapaxes(k, 0, 1)
            vT = jnp.swapaxes(v, 0, 1)
            b, c = (k.shape[0], k.shape[2])
            aa = jnp.zeros((b, c), k.dtype)
            bb = jnp.zeros((b, c), k.dtype)
            pp = jnp.full((b, c), -1e+38, k.dtype)

            def step(carry, kv_t):
                aa, bb, pp = carry
                kt, vt = kv_t
                ww = u + kt
                p = jnp.maximum(pp, ww)
                e1 = jnp.exp(pp - p)
                e2 = jnp.exp(ww - p)
                out = (e1 * aa + e2 * vt) / (e1 * bb + e2)
                ww2 = pp + w
                p2 = jnp.maximum(ww2, kt)
                e1 = jnp.exp(ww2 - p2)
                e2 = jnp.exp(kt - p2)
                return ((e1 * aa + e2 * vt, e1 * bb + e2, p2), out)
            _, outs = jax.lax.scan(step, (aa, bb, pp), (kT, vT))
            return jnp.swapaxes(outs, 0, 1)
        xa = _ln(x, ln0_g, ln0_b)
        xs = _shift(xa)
        k = (xa * tm_k + xs * (1.0 - tm_k)) @ Wk
        v = (xa * tm_v + xs * (1.0 - tm_v)) @ Wv
        r = jax.nn.sigmoid((xa * tm_r + xs * (1.0 - tm_r)) @ Wr)
        w = -jnp.exp(time_decay)
        wkv = _wkv(w, time_first, k, v)
        x = x + r * wkv @ Wo
        xc = _ln(x, ln1_g, ln1_b)
        xs = _shift(xc)
        kk = (xc * cm_k + xs * (1.0 - cm_k)) @ Wck
        kv = jnp.square(jax.nn.relu(kk)) @ Wcv
        rr = jax.nn.sigmoid((xc * cm_r + xs * (1.0 - cm_r)) @ Wcr)
        return x + rr * kv

    def _L0_ffn_ref(x, w_router, w1, b1, w2, b2):
        import jax, jax.numpy as jnp
        import numpy as np
        EMBED_DIM = 128
        HIDDEN_DIM = 512
        NUM_EXPERTS = 8
        TOP_K = 2
        orig_shape = x.shape
        xf = x.reshape(-1, EMBED_DIM)
        logits = xf @ w_router
        probs = jax.nn.softmax(logits, axis=-1)
        topk_w, topk_idx = jax.lax.top_k(probs, TOP_K)
        mask = jax.nn.one_hot(topk_idx, NUM_EXPERTS, dtype=xf.dtype)
        weights = jnp.sum(topk_w[..., None] * mask, axis=1)
        h = jnp.einsum('te,ieh->tih', xf, w1) + b1
        h = jax.nn.gelu(h)
        out = jnp.einsum('tih,ihe->tie', h, w2) + b2
        out = jnp.sum(out * weights[..., None], axis=1)
        return out.reshape(orig_shape)

    def _L1_xattn_ref(x, context, Wq, bq, Wk, bk, Wv, bv, Wo, bo):
        import jax, jax.numpy as jnp
        import numpy as np
        IN_DIM = 128
        CTX_DIM = 96
        NUM_HEADS = 16
        HEAD_DIM = IN_DIM // NUM_HEADS
        SCALE = 1.0 / float(np.sqrt(HEAD_DIM))
        q = x @ Wq.T + bq
        k = context @ Wk.T + bk
        v = context @ Wv.T + bv
        B, NQ, _ = q.shape
        NKV = k.shape[1]
        q = q.reshape(B, NQ, NUM_HEADS, HEAD_DIM)
        k = k.reshape(B, NKV, NUM_HEADS, HEAD_DIM)
        v = v.reshape(B, NKV, NUM_HEADS, HEAD_DIM)
        attn = jnp.einsum('bihd,bjhd->bhij', q, k) * SCALE
        attn = jax.nn.softmax(attn, axis=-1)
        out = jnp.einsum('bhij,bjhd->bihd', attn, v)
        out = out.reshape(B, NQ, IN_DIM)
        return out @ Wo.T + bo

    def _L1_attn_ref(x, w_qkv, w_o):
        import jax, jax.numpy as jnp
        import numpy as np
        D = 128
        H = 16
        G = 4
        HD = D // H
        HPG = H // G
        THETA = 10000.0
        EPS = 1e-10

        def _l2_qk_norm(t):
            return t / (jnp.sqrt(jnp.sum(t * t, axis=-1, keepdims=True)) + EPS)

        def _rope(t):
            T = t.shape[1]
            half = HD // 2
            inv_freq = 1.0 / THETA ** (jnp.arange(half, dtype=jnp.float32) / half)
            ang = jnp.arange(T, dtype=jnp.float32)[:, None] * inv_freq[None, :]
            cos = jnp.cos(ang)[None, :, None, :]
            sin = jnp.sin(ang)[None, :, None, :]
            x1, x2 = (t[..., :half], t[..., half:])
            return jnp.concatenate([x1 * cos - x2 * sin, x2 * cos + x1 * sin], axis=-1)
        B, T, _ = x.shape
        qkv = x @ w_qkv
        q, k, v = jnp.split(qkv, [H * HD, H * HD + G * HD], axis=-1)
        q = q.reshape(B, T, H, HD)
        k = k.reshape(B, T, G, HD)
        v = v.reshape(B, T, G, HD)
        q = _l2_qk_norm(q)
        k = _l2_qk_norm(k)
        q = _rope(q)
        k = _rope(k)
        k = jnp.repeat(k, HPG, axis=2)
        v = jnp.repeat(v, HPG, axis=2)
        q = jnp.transpose(q, (0, 2, 1, 3))
        k = jnp.transpose(k, (0, 2, 1, 3))
        v = jnp.transpose(v, (0, 2, 1, 3))
        scale = 1.0 / np.sqrt(HD).astype(np.float32)
        scores = jnp.einsum('bhqd,bhkd->bhqk', q, k) * scale
        causal = jnp.tril(jnp.ones((T, T), dtype=bool))
        scores = jnp.where(causal[None, None], scores, jnp.float32(-1e+30))
        attn = jax.nn.softmax(scores, axis=-1)
        out = jnp.einsum('bhqk,bhkd->bhqd', attn, v)
        out = jnp.transpose(out, (0, 2, 1, 3)).reshape(B, T, H * HD)
        return out @ w_o

    def _L1_ffn_ref(x, clip_x, clip_down, w_gate, w_up, w_down):
        import jax, jax.numpy as jnp
        import numpy as np
        QMAX = 127.0

        def _ste_round(v):
            return v + jax.lax.stop_gradient(jnp.round(v) - v)

        def _act_fake_quant(x, clip_factor):
            scale = jax.nn.sigmoid(clip_factor) * jnp.max(jnp.abs(x)) / QMAX
            return jnp.clip(_ste_round(x / scale), -QMAX - 1.0, QMAX) * scale

        def _weight_fake_quant(w):
            scale = jnp.max(jnp.abs(w), axis=1, keepdims=True) / QMAX
            return jnp.clip(_ste_round(w / scale), -QMAX - 1.0, QMAX) * scale
        xq = _act_fake_quant(x, clip_x[0])
        gate = jnp.einsum('bsh,ih->bsi', xq, _weight_fake_quant(w_gate))
        up = jnp.einsum('bsh,ih->bsi', xq, _weight_fake_quant(w_up))
        h = _act_fake_quant(jax.nn.silu(gate) * up, clip_down[0])
        return jnp.einsum('bsi,hi->bsh', h, _weight_fake_quant(w_down))

    def _L2_xattn_ref(x_text, x_vision, text_mask, vision_mask, Wq, Wk, Wv, W_film_in, b_film_in, W_film_out, b_film_out, g_norm_in, b_norm_in, g_norm_out, b_norm_out, g_ffn, b_ffn, W1, b1, W2, b2, log_dt, A_re, A_im, C_re, C_im, D_skip, mod_gate):
        import jax, jax.numpy as jnp
        import numpy as np
        B, T, DT, G, DV = (16, 64, 128, 72, 96)
        H, DH = (4, 32)
        INNER = H * DH
        HID = 4 * DT
        N_STATE = 64
        K_TOP = 32

        def layernorm(x, g, b, eps=1e-05):
            m = x.mean(-1, keepdims=True)
            v = x.var(-1, keepdims=True)
            return (x - m) * jax.lax.rsqrt(v + eps) * g + b

        def s4d(x, log_dt, A_re, A_im, C_re, C_im, D_skip):
            Bb, L, D = x.shape
            dt = jnp.exp(log_dt)
            A = A_re + 1j * A_im
            C = C_re + 1j * C_im
            dtA = dt[:, None] * A
            dC = C * (jnp.exp(dtA) - 1.0) / A
            powers = jnp.exp(dtA[:, :, None] * jnp.arange(L))
            K = 2.0 * jnp.einsum('dn,dnl->dl', dC, powers).real
            n = 2 * L
            Kf = jnp.fft.rfft(K, n=n, axis=-1)
            xf = jnp.fft.rfft(x, n=n, axis=1)
            y = jnp.fft.irfft(xf * Kf.T[None], n=n, axis=1)[:, :L]
            return y + x * D_skip
        Bb, Tt, D = x_text.shape
        Gg = x_vision.shape[1]
        Q = (x_text @ Wq).reshape(Bb, Tt, H, DH)
        K = (x_vision @ Wk).reshape(Bb, Gg, H, DH)
        scores = jnp.einsum('bthd,bghd->bhtg', Q, K) / np.sqrt(DH).astype(np.float32)
        scores = jnp.where(vision_mask[:, None, None, :], scores, -jnp.inf)
        topv, topi = jax.lax.top_k(scores, K_TOP)
        probs = jax.nn.softmax(topv, axis=-1)
        bi = jnp.arange(Bb)[:, None, None, None]
        hi = jnp.arange(H)[None, :, None, None]
        ti = jnp.arange(Tt)[None, None, :, None]
        attn = jnp.zeros_like(scores).at[bi, hi, ti, topi].set(probs)
        attn_mean = attn.mean(axis=1)
        V = x_vision @ Wv
        c_t = jnp.einsum('btg,bgd->btd', attn_mean, V)
        c_t = c_t * text_mask[..., None]
        x = layernorm(x_text, g_norm_in, b_norm_in)
        scale_in, shift_in = jnp.split(c_t @ W_film_in + b_film_in, 2, axis=-1)
        x = x * (1.0 + mod_gate * scale_in) + mod_gate * shift_in
        y = s4d(x, log_dt, A_re, A_im, C_re, C_im, D_skip)
        scale_out, shift_out = jnp.split(c_t @ W_film_out + b_film_out, 2, axis=-1)
        y = y * (1.0 + mod_gate * scale_out) + mod_gate * shift_out
        xt = x_text + y
        h = layernorm(xt, g_ffn, b_ffn)
        h = jax.nn.gelu(h @ W1 + b1, approximate=False) @ W2 + b2
        xt = xt + h
        return layernorm(xt, g_norm_out, b_norm_out)

    def _L2_attn_ref(hidden_states, w_q, b_q, w_k, b_k, w_v, b_v, w_o, b_o):
        import jax, jax.numpy as jnp
        import numpy as np
        B, S, H = (2, 1024, 128)
        NUM_HEADS = 16
        HEAD_DIM = H // NUM_HEADS
        KERNEL = 7
        DILATION = 1
        SCALE = 1.0 / np.sqrt(HEAD_DIM)
        b, s, h = hidden_states.shape
        q = hidden_states @ w_q + b_q
        k = hidden_states @ w_k + b_k
        v = hidden_states @ w_v + b_v
        q = q.reshape(b, s, NUM_HEADS, HEAD_DIM).transpose(0, 2, 1, 3)
        k = k.reshape(b, s, NUM_HEADS, HEAD_DIM).transpose(0, 2, 1, 3)
        v = v.reshape(b, s, NUM_HEADS, HEAD_DIM).transpose(0, 2, 1, 3)
        offsets = (jnp.arange(KERNEL) - KERNEL // 2) * DILATION
        idx = jnp.arange(s)[:, None] + offsets[None, :]
        valid = (idx >= 0) & (idx < s)
        idx_c = jnp.clip(idx, 0, s - 1)
        k_win = k[:, :, idx_c, :]
        v_win = v[:, :, idx_c, :]
        scores = jnp.einsum('bhsd,bhskd->bhsk', q, k_win) * SCALE
        scores = jnp.where(valid[None, None], scores, -jnp.inf)
        attn = jax.nn.softmax(scores, axis=-1)
        out = jnp.einsum('bhsk,bhskd->bhsd', attn, v_win)
        out = out.transpose(0, 2, 1, 3).reshape(b, s, h)
        return out @ w_o + b_o

    def _L2_ffn_ref(x, in_proj_w, in_proj_b, out_proj_w, out_proj_b, ln1_g, ln1_b, ln2_g, ln2_b, w_group, b_group, w_expert, b_expert, w1, b1, w2, b2):
        import jax, jax.numpy as jnp
        import numpy as np
        NHEAD = 16
        NUM_GROUPS = 4
        EXPERTS_PER_GROUP = 2
        LN_EPS = 1e-05

        def _layernorm(x, g, b):
            mu = jnp.mean(x, axis=-1, keepdims=True)
            var = jnp.mean(jnp.square(x - mu), axis=-1, keepdims=True)
            return (x - mu) * jax.lax.rsqrt(var + LN_EPS) * g + b

        def _mha(x, wi, bi, wo, bo):
            B, S, D = x.shape
            hd = D // NHEAD
            qkv = x @ wi.T + bi
            q, k, v = jnp.split(qkv, 3, axis=-1)

            def heads(t):
                return t.reshape(B, S, NHEAD, hd).transpose(0, 2, 1, 3)
            q, k, v = (heads(q), heads(k), heads(v))
            scores = jnp.einsum('bhqd,bhkd->bhqk', q, k) / jnp.sqrt(jnp.asarray(hd, x.dtype))
            attn = jax.nn.softmax(scores, axis=-1)
            o = jnp.einsum('bhqk,bhkd->bhqd', attn, v)
            o = o.transpose(0, 2, 1, 3).reshape(B, S, D)
            return o @ wo.T + bo

        def _hier_moe(x, w_group, b_group, w_expert, b_expert, w1, b1, w2, b2):
            B, S, D = x.shape
            xt = x.reshape(B * S, D)
            T = xt.shape[0]
            E = NUM_GROUPS * EXPERTS_PER_GROUP
            gp = jax.nn.softmax(xt @ w_group + b_group, axis=-1)
            g_idx = jnp.argmax(gp, axis=-1)
            g_prob = jnp.max(gp, axis=-1)
            elog = jnp.einsum('td,gde->tge', xt, w_expert) + b_expert
            ep = jax.nn.softmax(elog, axis=-1)
            ep_sel = jnp.take_along_axis(ep, g_idx[:, None, None], axis=1)[:, 0, :]
            e_idx_local = jnp.argmax(ep_sel, axis=-1)
            e_prob = jnp.max(ep_sel, axis=-1)
            flat_e = g_idx * EXPERTS_PER_GROUP + e_idx_local
            combine = jax.nn.one_hot(flat_e, E, dtype=xt.dtype) * (g_prob * e_prob)[:, None]
            h = jax.nn.relu(jnp.einsum('td,edf->etf', xt, w1) + b1[:, None, :])
            y = jnp.einsum('etf,efd->etd', h, w2) + b2[:, None, :]
            out = jnp.einsum('te,etd->td', combine, y)
            return out.reshape(B, S, D)
        attn_out = _mha(x, in_proj_w, in_proj_b, out_proj_w, out_proj_b)
        x = _layernorm(x + attn_out, ln1_g, ln1_b)
        moe_out = _hier_moe(x, w_group, b_group, w_expert, b_expert, w1, b1, w2, b2)
        x = _layernorm(x + moe_out, ln2_g, ln2_b)
        return x

    def _L3_xattn_ref(x, y, Wq, bq, Wkv, bkv, Wo, bo):
        import jax, jax.numpy as jnp
        import numpy as np
        N_HEADS = 16
        b, l, d = x.shape
        m = y.shape[1]
        h = N_HEADS
        dh = d // h
        q = (jnp.einsum('bld,ed->ble', x, Wq) + bq).reshape(b, l, h, dh)
        kv = (jnp.einsum('bmc,ec->bme', y, Wkv) + bkv).reshape(b, m, h, 2 * dh)
        k, v = (kv[..., :dh], kv[..., dh:])
        scale = 1.0 / jnp.sqrt(jnp.asarray(dh, x.dtype))
        att = jax.nn.softmax(jnp.einsum('blhd,bmhd->blmh', q, k) * scale, axis=2)
        out = jnp.einsum('blmh,bmhd->blhd', att, v).reshape(b, l, d)
        return jnp.einsum('bld,ed->ble', out, Wo) + bo

    def _L3_attn_ref(hidden_states, w_dec_attn, w_out, b_out):
        import jax, jax.numpy as jnp
        import numpy as np
        B, S, D = (8, 256, 128)
        b, s, d = hidden_states.shape
        q = hidden_states @ w_dec_attn
        scores = jnp.einsum('bid,bjd->bij', q, hidden_states)
        i_idx = jnp.arange(s)[:, None]
        j_idx = jnp.arange(s)[None, :]
        mask = j_idx < i_idx
        mask = mask.at[0, 0].set(True)
        attn = jax.nn.softmax(jnp.where(mask, scores, -jnp.inf), axis=-1)
        context = jnp.einsum('bij,bjd->bid', attn, hidden_states)
        combined = jnp.concatenate([hidden_states, context], axis=-1)
        out = jnp.tanh(combined @ w_out.T + b_out)
        return out

    def _L3_ffn_ref(x, Wfc_s, bfc_s, Wproj_s, bproj_s, Wr, Wfc, bfc, Wproj, bproj):
        import jax, jax.numpy as jnp
        import numpy as np
        import math
        N_EMBD = 128
        HIDDEN = 4 * N_EMBD
        N_EXPERTS = 8
        TOP_K = 2
        B, T = (4, 256)

        def new_gelu(x):
            c = math.sqrt(2.0 / math.pi)
            return 0.5 * x * (1.0 + jnp.tanh(c * (x + 0.044715 * x * x * x)))

        def _moe_forward(x, Wfc_s, bfc_s, Wproj_s, bproj_s, Wr, Wfc, bfc, Wproj, bproj):
            Bb, Tt, C = x.shape
            xf = x.reshape(Bb * Tt, C)
            N = Bb * Tt
            shared = new_gelu(xf @ Wfc_s + bfc_s) @ Wproj_s + bproj_s
            logits = xf @ Wr
            probs = jax.nn.softmax(logits, axis=-1)
            topk_p, topk_i = jax.lax.top_k(probs, TOP_K)
            topk_p = topk_p / jnp.sum(topk_p, axis=-1, keepdims=True)
            gate = jnp.zeros((N, N_EXPERTS), dtype=xf.dtype)
            gate = gate.at[jnp.arange(N)[:, None], topk_i].add(topk_p)
            routed = jnp.zeros_like(xf)
            for e in range(N_EXPERTS):
                h = new_gelu(xf @ Wfc[e] + bfc[e]) @ Wproj[e] + bproj[e]
                routed = routed + h * gate[:, e:e + 1]
            return (shared + routed).reshape(Bb, Tt, C)
        return _moe_forward(x, Wfc_s, bfc_s, Wproj_s, bproj_s, Wr, Wfc, bfc, Wproj, bproj)
    x = x + _L0_xattn_ref(_layernorm(x, axis=-1), ctx_768, ctx_768, L0_xattn_Wq, L0_xattn_bq, L0_xattn_Wk, L0_xattn_bk, L0_xattn_Wv, L0_xattn_bv, L0_xattn_Wo, L0_xattn_bo, L0_xattn_ln_gamma, L0_xattn_ln_beta)
    x = x + _L0_attn_ref(_layernorm(x, axis=-1), L0_attn_ln0_g, L0_attn_ln0_b, L0_attn_ln1_g, L0_attn_ln1_b, L0_attn_time_decay, L0_attn_time_first, L0_attn_tm_k, L0_attn_tm_v, L0_attn_tm_r, L0_attn_Wk, L0_attn_Wv, L0_attn_Wr, L0_attn_Wo, L0_attn_cm_k, L0_attn_cm_r, L0_attn_Wck, L0_attn_Wcv, L0_attn_Wcr)
    x = x + _L0_ffn_ref(_layernorm(x, axis=-1), L0_ffn_w_router, L0_ffn_w1, L0_ffn_b1, L0_ffn_w2, L0_ffn_b2)
    x = x + _L1_xattn_ref(_layernorm(x, axis=-1), ctx_768, L1_xattn_Wq, L1_xattn_bq, L1_xattn_Wk, L1_xattn_bk, L1_xattn_Wv, L1_xattn_bv, L1_xattn_Wo, L1_xattn_bo)
    x = x + _L1_attn_ref(_layernorm(x, axis=-1), L1_attn_w_qkv, L1_attn_w_o)
    x = x + _L1_ffn_ref(_layernorm(x, axis=-1), L1_ffn_clip_x, L1_ffn_clip_down, L1_ffn_w_gate, L1_ffn_w_up, L1_ffn_w_down)
    x = x + _L2_xattn_ref(_layernorm(x, axis=-1), ctx_768, mask_BxS_bf1, mask_BxS2_bf1, L2_xattn_Wq, L2_xattn_Wk, L2_xattn_Wv, L2_xattn_W_film_in, L2_xattn_b_film_in, L2_xattn_W_film_out, L2_xattn_b_film_out, L2_xattn_g_norm_in, L2_xattn_b_norm_in, L2_xattn_g_norm_out, L2_xattn_b_norm_out, L2_xattn_g_ffn, L2_xattn_b_ffn, L2_xattn_W1, L2_xattn_b1, L2_xattn_W2, L2_xattn_b2, L2_xattn_log_dt, L2_xattn_A_re, L2_xattn_A_im, L2_xattn_C_re, L2_xattn_C_im, L2_xattn_D_skip, L2_xattn_mod_gate)
    x = x + _L2_attn_ref(_layernorm(x, axis=-1), L2_attn_w_q, L2_attn_b_q, L2_attn_w_k, L2_attn_b_k, L2_attn_w_v, L2_attn_b_v, L2_attn_w_o, L2_attn_b_o)
    x = x + _L2_ffn_ref(_layernorm(x, axis=-1), L2_ffn_in_proj_w, L2_ffn_in_proj_b, L2_ffn_out_proj_w, L2_ffn_out_proj_b, L2_ffn_ln1_g, L2_ffn_ln1_b, L2_ffn_ln2_g, L2_ffn_ln2_b, L2_ffn_w_group, L2_ffn_b_group, L2_ffn_w_expert, L2_ffn_b_expert, L2_ffn_w1, L2_ffn_b1, L2_ffn_w2, L2_ffn_b2)
    x = x + _L3_xattn_ref(_layernorm(x, axis=-1), ctx_768, L3_xattn_Wq, L3_xattn_bq, L3_xattn_Wkv, L3_xattn_bkv, L3_xattn_Wo, L3_xattn_bo)
    x = x + _L3_attn_ref(_layernorm(x, axis=-1), L3_attn_w_dec_attn, L3_attn_w_out, L3_attn_b_out)
    x = x + _L3_ffn_ref(_layernorm(x, axis=-1), L3_ffn_Wfc_s, L3_ffn_bfc_s, L3_ffn_Wproj_s, L3_ffn_bproj_s, L3_ffn_Wr, L3_ffn_Wfc, L3_ffn_bfc, L3_ffn_Wproj, L3_ffn_bproj)
    return x

_drawn_inputs = setup_inputs


def setup_inputs(seed=0):
    import zlib

    import numpy as np

    out = dict(_drawn_inputs(seed))
    spreads = {'L0_xattn_bq': (0.0, 0.1),
     'L0_xattn_bk': (0.0, 2.0),
     'L0_xattn_bv': (0.0, 0.1),
     'L0_xattn_bo': (0.0, 0.1),
     'L0_xattn_ln_gamma': (1.0, 0.2),
     'L0_xattn_ln_beta': (0.0, 0.1),
     'L0_attn_ln0_g': (1.0, 0.2),
     'L0_attn_ln0_b': (0.0, 0.1),
     'L0_attn_ln1_g': (1.0, 0.2),
     'L0_attn_ln1_b': (0.0, 0.1),
     'L0_ffn_b1': (0.0, 0.725),
     'L0_ffn_b2': (0.0, 0.8),
     'L2_xattn_b_film_in': (0.0, 1.246),
     'L2_xattn_b_film_out': (0.0, 0.5),
     'L2_xattn_g_norm_in': (1.0, 0.592),
     'L2_xattn_b_norm_in': (0.0, 0.374),
     'L2_xattn_g_norm_out': (1.0, 0.2),
     'L2_xattn_b_norm_out': (0.0, 0.275),
     'L2_xattn_g_ffn': (1.0, 0.6),
     'L2_xattn_b_ffn': (0.0, 0.8),
     'L2_xattn_b1': (0.0, 0.8),
     'L2_xattn_b2': (0.0, 0.4),
     'L2_xattn_A_re': (-0.5, 0.6),
     'L2_attn_b_q': (0.0, 0.8),
     'L2_attn_b_k': (0.0, 2.0),
     'L2_attn_b_v': (0.0, 0.8),
     'L2_attn_b_o': (0.0, 0.289),
     'L2_ffn_in_proj_b': (0.0, 0.339),
     'L2_ffn_out_proj_b': (0.0, 0.307),
     'L2_ffn_ln1_g': (1.0, 0.2),
     'L2_ffn_ln1_b': (0.0, 0.8),
     'L2_ffn_ln2_g': (1.0, 0.2),
     'L2_ffn_ln2_b': (0.0, 0.338),
     'L2_ffn_b_group': (0.0, 1.792),
     'L2_ffn_b_expert': (0.0, 0.8),
     'L2_ffn_b1': (0.0, 2.0),
     'L2_ffn_b2': (0.0, 0.8),
     'L3_attn_b_out': (0.0, 0.391),
     'L3_ffn_bfc_s': (0.0, 0.8),
     'L3_ffn_bproj_s': (0.0, 0.352),
     'L3_ffn_bfc': (0.0, 0.8),
     'L3_ffn_bproj': (0.0, 0.498)}
    factors = {'L0_xattn_Wk': 8.0,
     'L1_xattn_bq': 8.0,
     'L1_xattn_bk': 200.0,
     'L1_xattn_bv': 8.0,
     'L1_xattn_bo': 8.0,
     'L1_attn_w_qkv': 5.396,
     'L1_attn_w_o': 4.9,
     'L1_ffn_w_gate': 8.0,
     'L1_ffn_w_up': 8.0,
     'L1_ffn_w_down': 8.0,
     'L2_xattn_Wq': 8.0,
     'L2_xattn_Wk': 8.0,
     'L2_xattn_Wv': 7.962,
     'L2_xattn_W_film_in': 8.0,
     'L2_xattn_W_film_out': 8.0,
     'L2_xattn_W1': 5.26,
     'L2_xattn_W2': 4.512,
     'L2_attn_w_q': 8.0,
     'L2_attn_w_k': 8.0,
     'L2_attn_w_v': 6.699,
     'L2_attn_w_o': 5.673,
     'L3_xattn_bq': 64.0,
     'L3_xattn_bkv': 47.45,
     'L3_xattn_bo': 21.345,
     'L3_ffn_Wfc_s': 4.693,
     'L3_ffn_Wproj_s': 4.134,
     'L3_ffn_Wr': 3.457,
     'L3_ffn_Wfc': 6.747,
     'L3_ffn_Wproj': 5.953,
     'L3_attn_w_dec_attn': 2.677}
    for name, (base, spread) in spreads.items():
        noise = np.random.default_rng([zlib.crc32(name.encode()), seed]).standard_normal(out[name].shape)
        drawn = base * np.exp(spread * noise) if base else spread * noise
        out[name] = jnp.asarray(drawn.astype(out[name].dtype))
    for name, factor in factors.items():
        out[name] = (out[name] * factor).astype(out[name].dtype)
    return out
```

```python
from contextlib import ExitStack

import concourse.bass as bass
from concourse import mybir
import numpy as np

F32 = mybir.dt.float32
BF16 = mybir.dt.bfloat16
I32 = mybir.dt.int32
U8 = mybir.dt.uint8
ACT = mybir.ActivationFunctionType
ALU = mybir.AluOpType
AX_X = mybir.AxisListType.X

T = 64
C = 128
H = 16
DH = C // H
G = 4
HG = H // G
KEYS = 6272
CTX = 96
KT_TILES = KEYS // 128
CHUNK = 512
CHUNKS = -(-KEYS // CHUNK)
TPC = CHUNK // 128
E = 8
HID = 512
HID2 = 256
FFQ = 352
FFQ_CHUNKS = [(0, 128), (128, 128), (256, 96)]
H2, D2, TOPK = 4, 32, 32
NSTATE = 64
LN_EPS = 1e-5
SCALE = DH ** -0.5
LOWEST = -3.0e38
ROUND = 12582912.0
LOG2E = 1.4426950408889634
LN2_HI, LN2_LO = 0.693145751953125, 1.4286068203094172e-06
TWO_PI_HI, TWO_PI_MID, TWO_PI_LO = 6.28125, 0.0019350051879882812, 3.0199157663e-07

PACKS = {
    "consts": [("ident", 128, 128), ("four_heads", 128, HG), ("two_heads", 128, 2),
               ("even_out", 128, 128), ("odd_out", 128, 128), ("causal", 128, T), ("band", 128, T),
               ("strict", T, T), ("cos", T, DH), ("sin", T, DH), ("mean_heads", 128, T)],
    "l0x": [("Wq", C, C), ("Wk", CTX + 1, C), ("Wv", CTX + 1, C), ("Wo", C, C)],
    "l0a": [("Wk", C, C), ("Wv", C, C), ("Wr", C, C), ("Wo", C, C), ("Wck", C, HID),
            ("Wcv", C, HID), ("Wcr", C, C), ("ln0_g", C, 1), ("ln0_b", C, 1), ("ln1_g", C, 1),
            ("ln1_b", C, 1), ("time_decay", C, 1), ("time_first", C, 1), ("tm_k", C, 1),
            ("tm_v", C, 1), ("tm_r", C, 1), ("cm_k", C, 1), ("cm_r", C, 1)],
    "l0f": [("w_router", C, E), ("b1", C, E * HID // C), ("b2", E, C)],
    "l1x": [("Wq", C, C), ("Wk", CTX + 1, C), ("Wv", CTX + 1, C), ("Wo", C, C), ("bq", C, 1)],
    "l1a": [("w_qkv", C, 192), ("w_o", C, C)],
    "l1f": [("w_gate", C, 3 * C), ("w_up", C, 3 * C), ("w_down", C, FFQ), ("clip_x", C, 1),
            ("clip_down", C, 1)],
    "l2x": [("Wq", C, C), ("Wk", CTX, C), ("Wv", CTX, C), ("W_film_in", C, 2 * C),
            ("W_film_out", C, 2 * C), ("W1", C, HID), ("W2", C, HID), ("b_film_in", C, 2),
            ("b_film_out", C, 2), ("g_norm_in", C, 1), ("b_norm_in", C, 1), ("g_ffn", C, 1),
            ("b_ffn", C, 1), ("b1", C, HID // C), ("D_skip", C, 1), ("log_dt", C, 1),
            ("mod_gate", C, 1), ("A_re", C, NSTATE), ("A_im", C, NSTATE), ("C_re", C, NSTATE),
            ("C_im", C, NSTATE)],
    "l2a": [("w_q", C, C), ("w_k", C, C), ("w_v", C, C), ("w_o", C, C), ("b_q", C, 1), ("b_k", C, 1)],
    "l2f": [("w_in", C, 3 * C), ("w_out", C, C), ("w_group", C, 4), ("w_expert", C, E),
            ("b1", C, E * HID2 // C), ("b2", E, C)],
    "l3x": [("Wq", C, C), ("Wk", CTX + 1, C), ("Wv", CTX + 1, C), ("Wo", C, C), ("bq", C, 1)],
    "l3a": [("w_dec", C, C), ("w_out", C, 2 * C)],
    "l3f": [("w_router", C, E), ("b1", C, (E + 1) * HID // C), ("b2", E + 1, C)],
    "experts0": [("w1", C, E * HID), ("w2", C, E * HID)],
    "experts2": [("w1", C, E * HID2), ("w2", C, E * HID2)],
    "experts3": [("w1", C, (E + 1) * HID), ("w2", C, (E + 1) * HID)],
    "rows": [(n, 1, w) for n, w in [
        ("l0x_bq", C), ("l0x_bo", C), ("l0x_gamma", C), ("l0x_beta", C), ("l1x_bo", C),
        ("l2x_g_out", C), ("l2x_b_out", C), ("l2x_b2", C), ("l2a_bv", C), ("l2a_bo", C),
        ("l2f_b_in", 3 * C), ("l2f_b_out", C), ("l2f_g1", C), ("l2f_b1", C), ("l2f_g2", C),
        ("l2f_b2", C), ("l2f_b_group", 4), ("l2f_b_expert", E), ("l3x_bo", C), ("l3a_bo", C)]],
}
SMALL = ["consts", "l0x", "l0a", "l0f", "l1x", "l1a", "l1f", "l2x", "l2a", "l2f", "l3x", "l3a", "l3f"]


def width(pack):
    return sum(cols for _, _, cols in PACKS[pack])


def column(pack, name):
    at = 0
    for n, rows, cols in PACKS[pack]:
        if n == name:
            return at, rows, cols
        at += cols
    raise KeyError(name)


class Events:

    def __init__(self, sem):
        self.sem, self.base, self.order, self.sent = sem, 0, [], 0

    def stage(self, *names):
        assert self.sent == len(self.order), self.order[self.sent:]
        self.base += len(self.order)
        self.order, self.sent = list(names), 0

    def mark(self, name):
        assert self.order[self.sent] == name, (self.order[self.sent], name)
        self.sent += 1
        return self.sem, 1

    def at(self, name):
        return self.sem, self.base + self.order.index(name) + 1


class Chain:

    def __init__(self, engine, sem):
        self.engine, self.sem, self.n = engine, sem, 0

    def __call__(self, ins):
        self.n += 1
        ins.then_inc(self.sem, 1)
        self.engine.wait_ge(self.sem, self.n)


def spread(ap, axis, shape):
    return ap.unsqueeze(axis).to_broadcast(shape)


class Memory:

    def __init__(self, nc, ctx, dram):
        self.nc, self.ctx, self.dram = nc, ctx, dram

        def sb(name, shape, dt=F32):
            return ctx.enter_context(nc.sbuf_tensor(name, shape, dt))

        self.sem = lambda name: ctx.enter_context(nc.semaphore(name))
        self.psum = ctx.enter_context(nc.psum_tensor("psum", [128, 8, 512], F32))
        self.x = sb("x", [T, C])
        self.ctx_t = sb("ctx_t", [CTX + 1, KEYS])
        self.keys_t = sb("keys_t", [128, KEYS])
        self.values = sb("values", [128, KT_TILES * C])
        self.rows = sb("rows", [T, width("rows")])
        self.packs = {p: sb("w_" + p, [128, width(p)]) for p in SMALL}
        self.minus_half = sb("minus_half", [128, KT_TILES])
        self.ones = sb("ones", [128, 128])
        self.kernel_reversed = sb("kernel_reversed", [C, T])
        self.xn = sb("xn", [T, C])
        self.stats = sb("stats", [T, 6])
        self.moments = sb("moments", [T, 2])
        self.rstd = sb("rstd", [T, 2])
        self.loaded = {p: self.sem("loaded_" + p) for p in
                       SMALL + ["x", "ctx", "rows", "experts0", "experts2", "experts3"]}
        self.pe_done = Events(self.sem("pe_done"))
        self.act_done = Events(self.sem("act_done"))
        self.dve_done = Events(self.sem("dve_done"))
        self.pool_done = Events(self.sem("pool_done"))
        self.dve_step = Chain(nc.vector, self.sem("dve_order"))
        self.act_step = Chain(nc.scalar, self.sem("act_order"))
        self.pool_step = Chain(nc.gpsimd, self.sem("pool_order"))

    def w(self, pack, name):
        at, rows, cols = column(pack, name)
        return self.packs[pack][0:rows, at:at + cols]

    def row(self, name):
        at, _, cols = column("rows", name)
        return self.rows[:, at:at + cols]



def pool_power(mem, out, base, exponent, when, event):
    nc = mem.nc
    nc.gpsimd.wait_ge(*when)
    nc.gpsimd.tensor_tensor(out, base, exponent, ALU.pow).then_inc(*mem.pool_done.mark(event))


def dve_moments(mem, source, event, slot=0):
    nc, step = mem.nc, mem.dve_step
    step(nc.vector.bn_stats(mem.stats[:, :], source))
    step(nc.vector.bn_aggr(mem.moments[:, :], mem.stats[:, :]))
    nc.vector.tensor_scalar(mem.rstd[:, 0:1], mem.moments[:, 1:2], LN_EPS, None, ALU.add)\
        .then_inc(*mem.dve_done.mark(event))


def pool_rstd(mem, when, event):
    pool_power(mem, mem.rstd[:, 1:2], mem.rstd[:, 0:1], mem.minus_half[0:T, 0:1],
               mem.dve_done.at(when), event)


def dve_normalised(mem, out, source, when):
    mem.nc.vector.wait_ge(*mem.pool_done.at(when))
    return mem.nc.vector.tensor_scalar(out, source, mem.moments[:, 0:1], mem.rstd[:, 1:2],
                                       ALU.subtract, ALU.mult)



def stage_load(mem):
    nc, dram = mem.nc, mem.dram
    constants_set = mem.sem("constants_set")

    def load_pack(engine, pack, target):
        engine.dma_start(target[:, :], dram[pack]).then_inc(mem.loaded[pack], 16)

    with nc.Block(no_gpsimd_drain=True) as block:

        @block.sync
        def _(sp):
            sp.dma_start(mem.x[:, :], dram["x"]).then_inc(mem.loaded["x"], 16)
            load_pack(sp, "l0x", mem.packs["l0x"])
            load_pack(sp, "consts", mem.packs["consts"])
            for lo in range(0, KEYS, KEYS // 4):
                sp.dma_start(mem.ctx_t[:, lo:lo + KEYS // 4], dram["ctx_t"][:, lo:lo + KEYS // 4])\
                    .then_inc(mem.loaded["ctx"], 16)
            sp.dma_start(mem.rows[:, :], dram["rows"].to_broadcast([T, width("rows")]))\
                .then_inc(mem.loaded["rows"], 16)
            for pack in ["l0a", "l0f"]:
                load_pack(sp, pack, mem.packs[pack])
            load_pack(sp, "experts0", mem.experts)
            for pack in ["l1x", "l1a", "l1f", "l2x", "l2a", "l2f"]:
                load_pack(sp, pack, mem.packs[pack])
            for pack in ["l3x", "l3a", "l3f"]:
                load_pack(sp, pack, mem.packs[pack])

        @block.vector
        def _(dve):
            nc.vector.memset(mem.ones[:, :], 1.0).then_inc(constants_set, 1)
            nc.vector.memset(mem.minus_half[:, :], -0.5).then_inc(constants_set, 1)
            dve.wait_ge(constants_set, 2)




def stage_load_late(mem):
    nc = mem.nc
    with nc.Block(no_gpsimd_drain=True) as block:

        @block.sync
        def _(sp):
            sp.dma_start(mem.packs["experts2"][:, :], mem.dram["experts2"]).then_inc(mem.loaded["experts2"], 16)
            sp.dma_start(mem.experts[:, :], mem.dram["experts3"]).then_inc(mem.loaded["experts3"], 16)


def stage_cross_attention(mem, level):
    nc = mem.nc
    pe_done, act_done, dve_done, pool_done = mem.pe_done, mem.act_done, mem.dve_done, mem.pool_done
    step = mem.dve_step
    pack = f"l{level}x"
    unit = level == 0
    ps = mem.psum
    ident = mem.w("consts", "ident")
    four_heads = mem.w("consts", "four_heads")
    RING = 7
    O_BANK, DEN_BANK, Y_BANK = 7, 0, 1
    PAIRS = -(-KT_TILES // 2)

    act_done.stage()
    if unit:
        pe_done.stage("xnT", "Qp", "QT", "den", "projected")
        dve_done.stage("var", "xn", "xnT", "q_sum", "Qn", "Qbd", "OT",
                       "out_var", "x")
        pool_done.stage("rstd", "q_rsqrt", "out_rstd")
    else:
        pe_done.stage("xnT", "QT", "max_cols", "den", "projected")
        dve_done.stage("var", "xn", "xnT", "Qbd", "max_parts", "max_cols", "OT", "x")
        pool_done.stage("rstd")

    def sem(name):
        return mem.sem(f"{pack}_{name}")

    keys_projected, keys_copied = sem("keys_projected"), sem("keys_copied")
    values_projected, values_copied = sem("values_projected"), sem("values_copied")
    scores_ready, probs_ready = sem("scores_ready"), sem("probs_ready")
    pv_done, sum_done = sem("pv_done"), sem("sum_done")
    if unit:
        raw_copied, key_sums_ready, keys_scaled = sem("raw_copied"), sem("key_sums_ready"), sem("keys_scaled")
        key_rsqrt_ready, keys_turned = sem("key_rsqrt_ready"), sem("keys_turned")
    else:
        max_scores, max_taken = sem("max_scores"), sem("max_taken")

    def chunk_keys(c):
        return c * CHUNK, min(KEYS, (c + 1) * CHUNK)

    def pair_tiles(u):
        return range(2 * u, min(KT_TILES, 2 * u + 2))

    def chunk_tiles(c):
        return range(c * TPC, min(KT_TILES, (c + 1) * TPC))

    with ExitStack() as local:
        def sb(name, shape, dt=F32):
            return local.enter_context(nc.sbuf_tensor(f"{pack}_{name}", shape, dt))

        xnT = sb("xnT", [C, T])
        QT = sb("QT", [C, T])
        Qbd = sb("Qbd", [C, HG, T])
        probs = sb("probs", [128, 2, G, 2, HG * T])
        prob_sum = sb("prob_sum", [128, G, 2, HG * T])
        rden = sb("rden", [C, HG, T])
        weighted = sb("weighted", [C, HG, T])
        OT = sb("OT", [C, T])
        residual = sb("residual", [T, C])
        if unit:
            Qp, Qn, sq = sb("Qp", [T, C]), sb("Qn", [T, C]), sb("sq", [T, C])
            q_sum, q_rsqrt = sb("q_sum", [T, 1]), sb("q_rsqrt", [T, 1])
            raw, squares = sb("raw", [128, 2, TPC, C]), sb("squares", [128, TPC, C])
            scaled = sb("scaled", [128, 2, TPC, C])
            key_sums, key_rsqrt = sb("key_sums", [128, KT_TILES]), sb("key_rsqrt", [128, KT_TILES])
            z, zn = sb("z", [T, C]), sb("zn", [T, C])
        else:
            maxima = sb("maxima", [128, 2, G, CHUNKS])
            row_max = sb("row_max", [128, G * 2])
            high16 = sb("high16", [128, G * 2], BF16)
            parts = sb("parts", [128, 2, G * 2])
            diag = sb("diag", [128, 2, G * 2, 128], BF16)
            picks = sb("picks", [128, 2, 128], BF16)
            ones16 = sb("ones16", [128, 128], BF16)
            max_cols = sb("max_cols", [128, H * T], BF16)

        with nc.Block(no_gpsimd_drain=True) as block:

            @block.tensor
            def _(pe):
                pe.wait_ge(*dve_done.at("xn"))
                pe.wait_ge(mem.loaded["consts"], 16)
                pe.wait_ge(mem.loaded[pack], 16)
                nc.tensor.transpose(ps[0:C, 0, 0:T], mem.xn[:, :], ident[0:T, 0:T])\
                    .then_inc(*pe_done.mark("xnT"))
                pe.wait_ge(*dve_done.at("xnT"))
                if unit:
                    nc.tensor.matmul(ps[0:T, 0, 128:256], xnT[:, :], mem.w(pack, "Wq"), start=True,
                                     stop=True).then_inc(*pe_done.mark("Qp"))
                    pe.wait_ge(*dve_done.at("Qn"))
                    nc.tensor.transpose(ps[0:C, 0, 256:320], Qn[:, :], ident[0:T, 0:T])\
                        .then_inc(*pe_done.mark("QT"))
                else:
                    nc.tensor.matmul(ps[0:C, 0, 256:320], mem.w(pack, "Wq"), xnT[:, :], start=True,
                                     stop=True).then_inc(*pe_done.mark("QT"))

                pe.wait_ge(mem.loaded["ctx"], 64)
                if not unit:
                    for c in range(CHUNKS):
                        lo, hi = chunk_keys(c)
                        if c >= 3:
                            pe.wait_ge(keys_copied, c - 2)
                        nc.tensor.matmul(ps[:, 1 + c % 3, 0:hi - lo], mem.w(pack, "Wk"),
                                         mem.ctx_t[:, lo:hi], start=True, stop=True)\
                            .then_inc(keys_projected, 1)
                else:
                    def turn(c):
                        pe.wait_ge(keys_scaled, c + 1)
                        if c >= 1:
                            pe.wait_ge(keys_copied, c)
                        for t in chunk_tiles(c):
                            last = nc.tensor.transpose(ps[:, 3, (t % TPC) * 128:(t % TPC + 1) * 128],
                                                       scaled[:, c % 2, t % TPC, :], ident)
                        last.then_inc(keys_turned, 1)

                    for c in range(CHUNKS):
                        if c >= 2:
                            pe.wait_ge(raw_copied, c - 1)
                        for t in chunk_tiles(c):
                            last = nc.tensor.matmul(
                                ps[:, 1 + c % 2, (t % TPC) * C:(t % TPC + 1) * C],
                                mem.ctx_t[:, t * 128:(t + 1) * 128], mem.w(pack, "Wk"), start=True, stop=True)
                        last.then_inc(keys_projected, 1)
                        if c >= 1:
                            turn(c - 1)
                    turn(CHUNKS - 1)
                for c in range(CHUNKS):
                    if c >= 3:
                        pe.wait_ge(values_copied, c - 2)
                    for t in chunk_tiles(c):
                        last = nc.tensor.matmul(
                            ps[:, 4 + c % 3, (t % TPC) * C:(t % TPC + 1) * C],
                            mem.ctx_t[:, t * 128:(t + 1) * 128], mem.w(pack, "Wv"), start=True, stop=True)
                    last.then_inc(values_projected, 1)
                pe.wait_ge(*dve_done.at("Qbd"))
                pe.wait_ge(keys_copied, CHUNKS)
                pe.wait_ge(values_copied, CHUNKS)
                if not unit:
                    for n in range(2 * CHUNKS):
                        lo, hi = chunk_keys(n // 2)
                        if n >= 2:
                            pe.wait_ge(max_taken, n - 1)
                        for g in range(G):
                            rows = slice(32 * g, 32 * g + 32)
                            last = nc.tensor.matmul(
                                ps[:, (n % 2) * G + g, 0:hi - lo], Qbd[rows, 2 * (n % 2):2 * (n % 2) + 2, :],
                                mem.keys_t[rows, lo:hi], start=True, stop=True)
                        last.then_inc(max_scores, 1)
                    pe.wait_ge(*dve_done.at("max_parts"))
                    for half in range(2):
                        for part in range(2):
                            last = nc.tensor.matmul(
                                ps[:, half, :], picks[:, part, :],
                                diag[:, part, 4 * half:4 * half + 4, :], start=part == 0, stop=part == 1)
                    last.then_inc(*pe_done.mark("max_cols"))
                    pe.wait_ge(*dve_done.at("max_cols"))

                def scores(u):
                    for g in range(G):
                        if 4 * u + g >= RING:
                            pe.wait_ge(probs_ready, 4 * u + g - RING + 1)
                    for t in pair_tiles(u):
                        half = slice((t % 2) * 256, (t % 2) * 256 + 256)
                        for g in range(G):
                            rows = slice(32 * g, 32 * g + 32)
                            last = nc.tensor.matmul(
                                ps[:, (4 * u + g) % RING, half], mem.keys_t[rows, t * 128:(t + 1) * 128],
                                Qbd[rows, :, :], start=True, stop=unit)
                            if unit and t == pair_tiles(u)[-1]:
                                last.then_inc(scores_ready, 1)
                        if unit:
                            continue
                        for g in range(G):
                            rows = slice(32 * g, 32 * g + 2)
                            last = nc.tensor.matmul(ps[:, (4 * u + g) % RING, half], ones16[rows, :],
                                                    max_cols[rows, 256 * g:256 * g + 256],
                                                    start=False, stop=True)
                            if t == pair_tiles(u)[-1]:
                                last.then_inc(scores_ready, 1)

                def weigh(u):
                    pe.wait_ge(probs_ready, 4 * u + 4)
                    for t in pair_tiles(u):
                        for g in range(G):
                            last = nc.tensor.matmul(
                                ps[32 * g:32 * g + 32, O_BANK, 0:256],
                                mem.values[:, t * C + 32 * g:t * C + 32 * g + 32],
                                probs[:, u % 2, g, t % 2, :], start=t == 0, stop=t == KT_TILES - 1)
                    last.then_inc(pv_done, 1)

                scores(0)
                for u in range(PAIRS):
                    if u + 1 < PAIRS:
                        scores(u + 1)
                    weigh(u)
                pe.wait_ge(sum_done, PAIRS)
                pe.wait_ge(probs_ready, G * PAIRS)
                for g in range(G):
                    for half in range(2):
                        last = nc.tensor.matmul(ps[32 * g:32 * g + 32, DEN_BANK, 0:256], mem.ones[:, 0:32],
                                                prob_sum[:, g, half, :], start=half == 0, stop=half == 1)
                last.then_inc(*pe_done.mark("den"))
                pe.wait_ge(*dve_done.at("OT"))
                nc.tensor.matmul(ps[0:T, Y_BANK, 0:C], OT[:, :], mem.w(pack, "Wo"), start=True,
                                 stop=True).then_inc(*pe_done.mark("projected"))

            @block.scalar
            def _(act):
                def copy_keys(act, c):
                    lo, hi = chunk_keys(c)
                    act.wait_ge(keys_turned, c + 1)
                    nc.scalar.activation(mem.keys_t[:, lo:hi], ps[:, 3, 0:hi - lo], ACT.Identity)\
                        .then_inc(keys_copied, 1)

                for c in range(CHUNKS):
                    lo, hi = chunk_keys(c)
                    if unit:
                        act.wait_ge(keys_projected, c + 1)
                        if c >= 2:
                            act.wait_ge(keys_scaled, c - 1)
                        n = len(chunk_tiles(c))
                        nc.scalar.activation(raw[:, c % 2, 0:n, :],
                                             ps[:, 1 + c % 2, 0:n * C].rearrange("p (t n) -> p t n", n=C),
                                             ACT.Identity).then_inc(raw_copied, 1)
                        if c >= 1:
                            copy_keys(act, c - 1)
                    else:
                        act.wait_ge(keys_projected, c + 1)
                        nc.scalar.activation(mem.keys_t[:, lo:hi], ps[:, 1 + c % 3, 0:hi - lo],
                                             ACT.Identity).then_inc(keys_copied, 1)
                if unit:
                    copy_keys(act, CHUNKS - 1)
                for u in range(PAIRS):
                    tiles = len(pair_tiles(u))
                    for g in range(G):
                        act.wait_ge(scores_ready, 4 * u + g + 1)
                        if u >= 2:
                            act.wait_ge(pv_done, u - 1)
                            act.wait_ge(sum_done, u - 1)
                        nc.scalar.activation(
                            probs[:, u % 2, g, 0:tiles, :],
                            ps[:, (4 * u + g) % RING, 0:256 * tiles].rearrange("p (t n) -> p t n", t=tiles),
                            ACT.Exp).then_inc(probs_ready, 1)

            @block.gpsimd
            def _(pool):
                pool_rstd(mem, "var", "rstd")
                if unit:
                    pool_power(mem, q_rsqrt[:, :], q_sum[:, :], mem.minus_half[0:T, 0:1],
                               dve_done.at("q_sum"), "q_rsqrt")
                    for c in range(CHUNKS):
                        t = slice(c * TPC, min(KT_TILES, (c + 1) * TPC))
                        pool.wait_ge(key_sums_ready, c + 1)
                        nc.gpsimd.tensor_tensor(key_rsqrt[:, t], key_sums[:, t], mem.minus_half[:, t], ALU.pow)\
                            .then_inc(key_rsqrt_ready, 1)
                    pool_rstd(mem, "out_var", "out_rstd")

            @block.vector
            def _(dve):
                if unit:
                    dve.wait_ge(mem.loaded["x"], 16)
                dve_moments(mem, mem.x[:, :], "var")
                dve_normalised(mem, mem.xn[:, :], mem.x[:, :], "rstd").then_inc(*dve_done.mark("xn"))
                dve.wait_ge(*pe_done.at("xnT"))
                nc.vector.tensor_copy(xnT[:, :], ps[0:C, 0, 0:T]).then_inc(*dve_done.mark("xnT"))
                dve.wait_ge(mem.loaded[pack], 16)
                dve.wait_ge(mem.loaded["consts"], 16)
                dve.wait_ge(mem.loaded["rows"], 16)
                if unit:
                    dve.wait_ge(*pe_done.at("Qp"))
                    step(nc.vector.tensor_tensor(Qp[:, :], ps[0:T, 0, 128:256], mem.row("l0x_bq"), ALU.add))
                    step(nc.vector.tensor_tensor(sq[:, :], Qp[:, :], Qp[:, :], ALU.mult))
                    step(nc.vector.tensor_reduce(q_sum[:, :], sq[:, :], AX_X, ALU.add))
                    nc.vector.tensor_scalar(q_sum[:, :], q_sum[:, :], 1e-24, None, ALU.max)\
                        .then_inc(*dve_done.mark("q_sum"))
                    dve.wait_ge(*pool_done.at("q_rsqrt"))
                    nc.vector.tensor_scalar(Qn[:, :], Qp[:, :], q_rsqrt[:, :], None, ALU.mult)\
                        .then_inc(*dve_done.mark("Qn"))
                    dve.wait_ge(*pe_done.at("QT"))
                    step(nc.vector.tensor_scalar(QT[:, :], ps[0:C, 0, 256:320], SCALE, None, ALU.mult))
                    step(nc.vector.tensor_tensor(residual[:, :], Qp[:, :], mem.row("l0x_bo"), ALU.add))
                else:
                    dve.wait_ge(*pe_done.at("QT"))
                    step(nc.vector.tensor_scalar(QT[:, :], ps[0:C, 0, 256:320], mem.w(pack, "bq"), SCALE,
                                                 ALU.add, ALU.mult))
                    step(nc.vector.tensor_tensor(residual[:, :], mem.x[:, :], mem.row(f"{pack}_bo"), ALU.add))
                nc.vector.tensor_tensor(Qbd[:, :, :], spread(QT[:, :], 1, [C, HG, T]),
                                        spread(four_heads, 2, [C, HG, T]), ALU.mult)\
                    .then_inc(*dve_done.mark("Qbd"))
                if unit:
                    def scale_keys(c):
                        n, ts = len(chunk_tiles(c)), slice(c * TPC, min(KT_TILES, (c + 1) * TPC))
                        dve.wait_ge(key_rsqrt_ready, c + 1)
                        if c >= 2:
                            dve.wait_ge(keys_turned, c - 1)
                        nc.vector.tensor_tensor(scaled[:, c % 2, 0:n, :], raw[:, c % 2, 0:n, :],
                                                spread(key_rsqrt[:, ts], 2, [128, n, C]), ALU.mult)\
                            .then_inc(keys_scaled, 1)

                    for c in range(CHUNKS):
                        n, ts = len(chunk_tiles(c)), slice(c * TPC, min(KT_TILES, (c + 1) * TPC))
                        dve.wait_ge(raw_copied, c + 1)
                        step(nc.vector.tensor_tensor(squares[:, 0:n, :], raw[:, c % 2, 0:n, :],
                                                     raw[:, c % 2, 0:n, :], ALU.mult))
                        step(nc.vector.tensor_reduce(key_sums[:, ts], squares[:, 0:n, :], AX_X, ALU.add))
                        nc.vector.tensor_scalar(key_sums[:, ts], key_sums[:, ts], 1e-24, None, ALU.max)\
                            .then_inc(key_sums_ready, 1)
                        if c >= 1:
                            scale_keys(c - 1)
                    scale_keys(CHUNKS - 1)
                for c in range(CHUNKS):
                    n = len(chunk_tiles(c)) * C
                    dve.wait_ge(values_projected, c + 1)
                    nc.vector.tensor_copy(mem.values[:, c * CHUNK:c * CHUNK + n], ps[:, 4 + c % 3, 0:n])\
                        .then_inc(values_copied, 1)
                if not unit:
                    nc.vector.memset(ones16[:, :], 1.0)
                    nc.vector.tensor_copy(picks[:, 0, :], mem.w("consts", "even_out"))
                    step(nc.vector.tensor_copy(picks[:, 1, :], mem.w("consts", "odd_out")))
                    for n in range(2 * CHUNKS):
                        lo, hi = chunk_keys(n // 2)
                        dve.wait_ge(max_scores, n + 1)
                        nc.vector.tensor_reduce(
                            maxima[:, n % 2, :, n // 2], ps[:, (n % 2) * G:(n % 2) * G + G, 0:hi - lo],
                            AX_X, ALU.max).then_inc(max_taken, 1)
                    dve.wait_ge(max_taken, 2 * CHUNKS)
                    step(nc.vector.tensor_reduce(row_max[:, :].rearrange("p (g s) -> p s g", g=G),
                                                 maxima[:, :, :, :], AX_X, ALU.max))
                    step(nc.vector.tensor_scalar(high16[:, :], row_max[:, :], -1.0, None, ALU.mult))
                    step(nc.vector.tensor_copy(parts[:, 0, :], high16[:, :]))
                    step(nc.vector.scalar_tensor_tensor(out=parts[:, 1, :], in0=row_max[:, :], scalar=-1.0,
                                                        in1=parts[:, 0, :], op0=ALU.mult,
                                                        op1=ALU.subtract))
                    nc.vector.tensor_tensor(diag[:, 0, :, :], spread(ident, 1, [128, G * 2, 128]),
                                            spread(parts[:, 0, :], 2, [128, G * 2, 128]), ALU.mult)
                    nc.vector.tensor_tensor(diag[:, 1, :, :], spread(ident, 1, [128, G * 2, 128]),
                                            spread(parts[:, 1, :], 2, [128, G * 2, 128]), ALU.mult)\
                        .then_inc(*dve_done.mark("max_parts"))
                    dve.wait_ge(*pe_done.at("max_cols"))
                    nc.vector.tensor_copy(max_cols[:, :].rearrange("p (b n) -> p b n", b=2), ps[:, 0:2, :])\
                        .then_inc(*dve_done.mark("max_cols"))
                for u in range(PAIRS):
                    n = len(pair_tiles(u))
                    dve.wait_ge(probs_ready, 4 * u + 4)
                    if u == 0:
                        ins = nc.vector.tensor_copy(prob_sum[:, :, :, :], probs[:, 0, :, :, :])
                    else:
                        dve.wait_ge(sum_done, u)
                        ins = nc.vector.tensor_tensor(prob_sum[:, :, 0:n, :], prob_sum[:, :, 0:n, :],
                                                      probs[:, u % 2, :, 0:n, :], ALU.add)
                    ins.then_inc(sum_done, 1)
                dve.wait_ge(*pe_done.at("den"))
                step(nc.vector.reciprocal(rden[:, :, :], ps[:, DEN_BANK, 0:256].rearrange("p (h q) -> p h q", h=HG)))
                step(nc.vector.tensor_tensor(weighted[:, :, :],
                                             ps[:, O_BANK, 0:256].rearrange("p (h q) -> p h q", h=HG),
                                             rden[:, :, :], ALU.mult))
                step(nc.vector.tensor_tensor(weighted[:, :, :], weighted[:, :, :],
                                             spread(four_heads, 2, [C, HG, T]), ALU.mult))
                nc.vector.tensor_reduce(OT[:, :], weighted[:, :, :].rearrange("p h q -> p q h"), AX_X,
                                        ALU.add).then_inc(*dve_done.mark("OT"))
                dve.wait_ge(*pe_done.at("projected"))
                if unit:
                    step(nc.vector.tensor_tensor(z[:, :], ps[0:T, Y_BANK, 0:C], residual[:, :], ALU.add))
                    dve_moments(mem, z[:, :], "out_var")
                    step(dve_normalised(mem, zn[:, :], z[:, :], "out_rstd"))
                    step(nc.vector.tensor_tensor(zn[:, :], zn[:, :], mem.row("l0x_gamma"), ALU.mult))
                    step(nc.vector.tensor_tensor(zn[:, :], zn[:, :], mem.row("l0x_beta"), ALU.add))
                    nc.vector.tensor_tensor(mem.x[:, :], mem.x[:, :], zn[:, :], ALU.add)\
                        .then_inc(*dve_done.mark("x"))
                else:
                    nc.vector.tensor_tensor(mem.x[:, :], ps[0:T, Y_BANK, 0:C], residual[:, :], ALU.add)\
                        .then_inc(*dve_done.mark("x"))



def stage_rwkv(mem):
    nc = mem.nc
    pe_done, act_done, dve_done, pool_done = mem.pe_done, mem.act_done, mem.dve_done, mem.pool_done
    step = mem.dve_step
    ps = mem.psum
    ident = mem.w("consts", "ident")
    pe_done.stage("aT", "kvr", "time_mixed", "cT", "kk", "kv")
    dve_done.stage("var", "z", "a_var", "a", "mixed", "scan_args", "rwkv", "c_var", "c", "c_mixed", "kk2", "x")
    act_done.stage("decay", "r_exp", "scan_exps", "rr_exp")
    pool_done.stage("rstd", "a_rstd", "c_rstd")

    def w(name):
        return mem.w("l0a", name)

    with ExitStack() as local:
        def sb(name, shape, dt=F32):
            return local.enter_context(nc.sbuf_tensor("l0a_" + name, shape, dt))

        a, c = sb("a", [T, C]), sb("c", [T, C])
        shifted_a, shifted_c = sb("shifted_a", [C, T + 1]), sb("shifted_c", [C, T + 1])
        delta = sb("delta", [C, T])
        mix = sb("mix", [C, 3, T])
        cmix = sb("cmix", [C, 2, T])
        kvr = sb("kvr", [C, 2, T])
        r_exp = sb("r_exp", [C, T])
        decay = sb("decay", [C, 1])
        decays = sb("decays", [C, T])
        top = sb("top", [C, T + 1])
        now = sb("now", [C, 2, T])
        args = sb("args", [C, 4, T])
        exps = sb("exps", [C, 4, T])
        sum_a, sum_b = sb("sum_a", [C, T + 1]), sb("sum_b", [C, T + 1])
        terms = sb("terms", [C, 4, T])
        rwkv = sb("rwkv", [C, T])
        x1 = sb("x1", [T, C])
        kk = sb("kk", [C, HID // C, T])
        kk2 = sb("kk2", [C, HID // C, T])
        rr = sb("rr", [T, C])
        gated = sb("gated", [T, C])

        with nc.Block(no_gpsimd_drain=True) as block:

            @block.tensor
            def _(pe):
                pe.wait_ge(*dve_done.at("a"))
                nc.tensor.transpose(ps[0:C, 0, 0:T], a[:, :], ident[0:T, 0:T]).then_inc(*pe_done.mark("aT"))
                pe.wait_ge(mem.loaded["l0a"], 16)
                pe.wait_ge(*dve_done.at("mixed"))
                for n, name in enumerate(["Wk", "Wv", "Wr"]):
                    out = ps[0:C, 1, n * T:(n + 1) * T] if n < 2 else ps[0:C, 7, 0:T]
                    last = nc.tensor.matmul(out, w(name), mix[:, n, :], start=True, stop=True)
                last.then_inc(*pe_done.mark("kvr"))
                pe.wait_ge(*dve_done.at("rwkv"))
                nc.tensor.matmul(ps[0:T, 2, 0:C], rwkv[:, :], w("Wo"), start=True, stop=True)\
                    .then_inc(*pe_done.mark("time_mixed"))
                pe.wait_ge(*dve_done.at("c"))
                nc.tensor.transpose(ps[0:C, 3, 0:T], c[:, :], ident[0:T, 0:T]).then_inc(*pe_done.mark("cT"))
                pe.wait_ge(*dve_done.at("c_mixed"))
                for n in range(HID // C):
                    nc.tensor.matmul(ps[0:C, 4, n * T:(n + 1) * T], w("Wck")[:, n * C:(n + 1) * C],
                                     cmix[:, 0, :], start=True, stop=True)
                nc.tensor.matmul(ps[0:T, 5, 0:C], cmix[:, 1, :], w("Wcr"), start=True, stop=True)\
                    .then_inc(*pe_done.mark("kk"))
                pe.wait_ge(*dve_done.at("kk2"))
                for n in range(HID // C):
                    last = nc.tensor.matmul(ps[0:T, 6, 0:C], kk2[:, n, :], w("Wcv")[:, n * C:(n + 1) * C],
                                            start=n == 0, stop=n == HID // C - 1)
                last.then_inc(*pe_done.mark("kv"))

            @block.scalar
            def _(act):
                act.wait_ge(mem.loaded["l0a"], 16)
                nc.scalar.activation(decay[:, :], w("time_decay"), ACT.Exp).then_inc(*act_done.mark("decay"))
                act.wait_ge(*pe_done.at("kvr"))
                nc.scalar.activation(r_exp[:, :], ps[0:C, 7, 0:T], ACT.Exp, scale=-1.0)\
                    .then_inc(*act_done.mark("r_exp"))
                act.wait_ge(*dve_done.at("scan_args"))
                nc.scalar.activation(exps[:, :, :], args[:, :, :], ACT.Exp).then_inc(*act_done.mark("scan_exps"))
                act.wait_ge(*pe_done.at("kk"))
                nc.scalar.activation(rr[:, :], ps[0:T, 5, 0:C], ACT.Exp, scale=-1.0)\
                    .then_inc(*act_done.mark("rr_exp"))

            @block.gpsimd
            def _(pool):
                pool_rstd(mem, "var", "rstd")
                pool_rstd(mem, "a_var", "a_rstd")
                pool_rstd(mem, "c_var", "c_rstd")

            @block.vector
            def _(dve):
                v = nc.vector
                dve_moments(mem, mem.x[:, :], "var")
                dve_normalised(mem, mem.xn[:, :], mem.x[:, :], "rstd").then_inc(*dve_done.mark("z"))
                dve.wait_ge(*dve_done.at("z"))
                dve_moments(mem, mem.xn[:, :], "a_var")
                dve_normalised(mem, a[:, :], mem.xn[:, :], "a_rstd").then_inc(*dve_done.mark("a"))

                dve.wait_ge(mem.loaded["l0a"], 16)
                v.memset(shifted_a[:, 0:1], 0.0)
                v.memset(shifted_c[:, 0:1], 0.0)
                v.memset(sum_a[:, 0:1], 0.0)
                v.memset(sum_b[:, 0:1], 0.0)
                step(v.memset(top[:, 0:1], -1e38))

                dve.wait_ge(*pe_done.at("aT"))
                step(v.tensor_scalar(shifted_a[:, 1:T + 1], ps[0:C, 0, 0:T], w("ln0_g"), w("ln0_b"),
                                     ALU.mult, ALU.add))
                step(v.tensor_tensor(delta[:, :], shifted_a[:, 1:T + 1], shifted_a[:, 0:T], ALU.subtract))
                for n, name in enumerate(["tm_k", "tm_v", "tm_r"]):
                    ins = v.scalar_tensor_tensor(out=mix[:, n, :], in0=delta[:, :], scalar=w(name),
                                                 in1=shifted_a[:, 0:T], op0=ALU.mult, op1=ALU.add)
                ins.then_inc(*dve_done.mark("mixed"))
                dve.wait_ge(*act_done.at("decay"))
                step(v.tensor_scalar(decays[:, :], mem.ones[:, 0:T], decay[:, :], -1.0, ALU.mult, ALU.mult))
                dve.wait_ge(*pe_done.at("kvr"))
                step(v.tensor_copy(kvr[:, :, :], ps[0:C, 1, 0:2 * T].rearrange("p (n t) -> p n t", n=2)))
                k, val = kvr[:, 0, :], kvr[:, 1, :]
                step(v.tensor_tensor_scan(top[:, 1:T + 1], decays[:, :], k, -1e38, ALU.add, ALU.max))
                step(v.tensor_scalar(now[:, 0, :], k, w("time_first"), None, ALU.add))
                step(v.tensor_tensor(now[:, 1, :], top[:, 0:T], now[:, 0, :], ALU.max))
                v.tensor_tensor(args[:, 0, :], top[:, 0:T], now[:, 1, :], ALU.subtract)
                v.tensor_tensor(args[:, 1, :], now[:, 0, :], now[:, 1, :], ALU.subtract)
                v.tensor_tensor(args[:, 3, :], k, top[:, 1:T + 1], ALU.subtract)
                step(v.tensor_tensor(args[:, 2, :], top[:, 0:T], decays[:, :], ALU.add))
                v.tensor_tensor(args[:, 2, :], args[:, 2, :], top[:, 1:T + 1], ALU.subtract)\
                    .then_inc(*dve_done.mark("scan_args"))
                dve.wait_ge(*act_done.at("scan_exps"))
                v.tensor_tensor(terms[:, 0, :], exps[:, 3, :], val, ALU.mult)
                v.tensor_tensor(terms[:, 1, :], exps[:, 1, :], val, ALU.mult)
                step(v.tensor_tensor_scan(sum_b[:, 1:T + 1], exps[:, 2, :], exps[:, 3, :], 0.0, ALU.mult, ALU.add))
                step(v.tensor_tensor_scan(sum_a[:, 1:T + 1], exps[:, 2, :], terms[:, 0, :], 0.0, ALU.mult, ALU.add))
                v.tensor_tensor(terms[:, 2, :], exps[:, 0, :], sum_a[:, 0:T], ALU.mult)
                step(v.tensor_tensor(terms[:, 3, :], exps[:, 0, :], sum_b[:, 0:T], ALU.mult))
                v.tensor_tensor(terms[:, 2, :], terms[:, 2, :], terms[:, 1, :], ALU.add)
                step(v.tensor_tensor(terms[:, 3, :], terms[:, 3, :], exps[:, 1, :], ALU.add))
                dve.wait_ge(*act_done.at("r_exp"))
                step(v.scalar_tensor_tensor(out=terms[:, 3, :], in0=r_exp[:, :], scalar=1.0,
                                            in1=terms[:, 3, :], op0=ALU.add, op1=ALU.mult))
                step(v.reciprocal(terms[:, 3, :], terms[:, 3, :]))
                v.tensor_tensor(rwkv[:, :], terms[:, 2, :], terms[:, 3, :], ALU.mult)\
                    .then_inc(*dve_done.mark("rwkv"))
                dve.wait_ge(*pe_done.at("time_mixed"))
                step(v.tensor_tensor(x1[:, :], ps[0:T, 2, 0:C], mem.xn[:, :], ALU.add))
                dve_moments(mem, x1[:, :], "c_var")
                dve_normalised(mem, c[:, :], x1[:, :], "c_rstd").then_inc(*dve_done.mark("c"))
                step(v.tensor_tensor(x1[:, :], x1[:, :], mem.x[:, :], ALU.add))
                dve.wait_ge(*pe_done.at("cT"))
                step(v.tensor_scalar(shifted_c[:, 1:T + 1], ps[0:C, 3, 0:T], w("ln1_g"), w("ln1_b"),
                                     ALU.mult, ALU.add))
                step(v.tensor_tensor(delta[:, :], shifted_c[:, 1:T + 1], shifted_c[:, 0:T], ALU.subtract))
                for n, name in enumerate(["cm_k", "cm_r"]):
                    ins = v.scalar_tensor_tensor(out=cmix[:, n, :], in0=delta[:, :], scalar=w(name),
                                                 in1=shifted_c[:, 0:T], op0=ALU.mult, op1=ALU.add)
                ins.then_inc(*dve_done.mark("c_mixed"))
                dve.wait_ge(*pe_done.at("kk"))
                step(v.tensor_scalar(kk[:, :, :], ps[0:C, 4, 0:4 * T].rearrange("p (n t) -> p n t", n=4),
                                     0.0, None, ALU.max))
                v.tensor_tensor(kk2[:, :, :], kk[:, :, :], kk[:, :, :], ALU.mult)\
                    .then_inc(*dve_done.mark("kk2"))
                dve.wait_ge(*act_done.at("rr_exp"))
                step(v.tensor_scalar(rr[:, :], rr[:, :], 1.0, None, ALU.add))
                step(v.reciprocal(rr[:, :], rr[:, :]))
                dve.wait_ge(*pe_done.at("kv"))
                step(v.tensor_tensor(gated[:, :], ps[0:T, 6, 0:C], rr[:, :], ALU.mult))
                v.tensor_tensor(mem.x[:, :], x1[:, :], gated[:, :], ALU.add).then_inc(*dve_done.mark("x"))



class Experts:

    def __init__(self, mem, sb, name, experts, hidden, function, tensors):
        self.mem, self.name, self.n, self.chunks, self.function = mem, name, experts, hidden // C, function
        self.w1, self.w2 = tensors
        self.b1, self.b2 = mem.w(name, "b1"), mem.w(name, "b2")
        self.per_bank = CHUNK // (self.chunks * T)
        self.banks = -(-experts // self.per_bank)
        self.hidden_ready, self.biased, self.activated, self.gated = (
            mem.sem(f"{name}_{x}") for x in ["hidden_ready", "biased", "activated", "gated"])
        self.pre = sb("pre", [C, experts * self.chunks * T])
        self.act = sb("act", [C, experts * self.chunks * T])
        self.spread_gates = sb("spread_gates", [T, experts, T])
        self.gates = sb("gates", [T, experts])
        self.gatesT = sb("gatesT", [experts, T])
        self.yT = sb("yT", [C, T])

    def of_bank(self, b):
        lo, hi = b * self.per_bank, min(self.n, (b + 1) * self.per_bank)
        return lo, hi, slice(lo * self.chunks * T, hi * self.chunks * T)

    def pe_hidden(self, pe, xT):
        nc, w = self.mem.nc, self.chunks * C
        for b in range(self.banks):
            lo, hi, _ = self.of_bank(b)
            for e in range(lo, hi):
                for c in range(self.chunks):
                    o = ((e - lo) * self.chunks + c) * T
                    last = nc.tensor.matmul(self.mem.psum[0:C, 1 + b, o:o + T],
                                            self.w1[:, e * w + c * C:e * w + (c + 1) * C], xT,
                                            start=True, stop=True)
            last.then_inc(self.hidden_ready, 1)

    def pe_gates(self, pe, first):
        mem, nc = self.mem, self.mem.nc
        pe.wait_ge(*mem.dve_done.at("gates"))
        nc.tensor.transpose(mem.psum[0:self.n, 0, 256:256 + T], self.gates[:, :],
                            mem.w("consts", "ident")[0:T, 0:T])
        nc.tensor.matmul(mem.psum[0:C, first, 0:8 * T], mem.ones[0:T, 0:C], self.spread_gates[:, 0:8, :],
                         start=True, stop=True).then_inc(*mem.pe_done.mark("gates"))

    def pe_out(self, pe):
        mem, nc, w = self.mem, self.mem.nc, self.chunks
        total = self.n * w
        for b in range(self.banks):
            lo, hi, _ = self.of_bank(b)
            if lo < E:
                pe.wait_ge(self.gated, b + 1)
            else:
                pe.wait_ge(self.activated, b + 1)
            for n in range(lo * w, hi * w):
                last = nc.tensor.matmul(mem.psum[0:C, 7, 0:T], self.w2[:, n * C:(n + 1) * C],
                                        self.act[:, n * T:(n + 1) * T], start=n == 0, stop=n == total - 1)
        last.then_inc(*mem.pe_done.mark("yT"))
        pe.wait_ge(*mem.dve_done.at("yT"))
        nc.tensor.matmul(mem.psum[0:T, 7, 128:128 + C], self.yT[:, :], mem.w("consts", "ident"),
                         start=True, stop=False)
        nc.tensor.matmul(mem.psum[0:T, 7, 128:128 + C], self.gatesT[:, :], self.b2,
                         start=False, stop=True).then_inc(*mem.pe_done.mark("y"))

    def act_hidden(self, act):
        for b in range(self.banks):
            _, _, cols = self.of_bank(b)
            act.wait_ge(self.biased, b + 1)
            self.mem.nc.scalar.activation(self.act[:, cols], self.pre[:, cols], self.function)\
                .then_inc(self.activated, 1)

    def dve_gates(self, dve):
        mem, v = self.mem, self.mem.nc.vector
        shape = [T, self.n, T]
        v.tensor_tensor(self.spread_gates[:, :, :], spread(mem.w("consts", "ident")[0:T, 0:T], 1, shape),
                        spread(self.gates[:, :], 2, shape), ALU.mult).then_inc(*mem.dve_done.mark("gates"))

    def dve_bias(self, dve):
        v, ch = self.mem.nc.vector, self.chunks
        for b in range(self.banks):
            lo, hi, cols = self.of_bank(b)
            n = (hi - lo) * ch
            dve.wait_ge(self.hidden_ready, b + 1)
            v.tensor_tensor(self.pre[:, cols].rearrange("p (n t) -> p n t", t=T),
                            self.mem.psum[0:C, 1 + b, 0:n * T].rearrange("p (n t) -> p n t", t=T),
                            spread(self.b1[:, lo * ch:hi * ch], 2, [C, n, T]), ALU.add)\
                .then_inc(self.biased, 1)

    def dve_gate(self, dve, gate_bank):
        mem, v, ch = self.mem, self.mem.nc.vector, self.chunks
        dve.wait_ge(*mem.pe_done.at("gates"))
        mem.dve_step(v.tensor_copy(self.gatesT[:, :], mem.psum[0:self.n, 0, 256:256 + T]))
        for b in range(self.banks):
            lo, hi, cols = self.of_bank(b)
            if lo >= E:
                continue
            dve.wait_ge(self.activated, b + 1)
            n = hi - lo
            act = self.act[:, cols].rearrange("p (e c t) -> p e c t", e=n, t=T)
            gate = mem.psum[0:C, gate_bank, lo * T:hi * T].rearrange("p (e t) -> p e t", t=T)
            v.tensor_tensor(act, act, spread(gate, 2, [C, n, ch, T]), ALU.mult).then_inc(self.gated, 1)

    def dve_yT(self, dve):
        mem = self.mem
        dve.wait_ge(*mem.pe_done.at("yT"))
        mem.nc.vector.tensor_copy(self.yT[:, :], mem.psum[0:C, 7, 0:T]).then_inc(*mem.dve_done.mark("yT"))


def dve_softmax(mem, sb_tiles, scores, out, event_scores, event_exp):
    v, step = mem.nc.vector, mem.dve_step
    top, total = sb_tiles
    step(v.tensor_reduce(top, scores, AX_X, ALU.max))
    v.tensor_scalar(scores, scores, top, None, ALU.subtract).then_inc(*mem.dve_done.mark(event_scores))
    mem.nc.vector.wait_ge(*mem.act_done.at(event_exp))
    step(v.tensor_reduce(total, out, AX_X, ALU.add))
    step(v.reciprocal(total, total))
    step(v.tensor_scalar(out, out, total, None, ALU.mult))


def dve_first_largest(mem, padded, best, work, mask, n, count):
    v, step = mem.nc.vector, mem.dve_step
    step(v.max(best, padded))
    step(v.memset(best[:, count:8], -1.0))
    step(v.match_replace(work, best, padded, -2.0))
    step(v.tensor_scalar(mask, work[:, 0:n], -2.0, None, ALU.is_equal))


def stage_topk_experts(mem, level):
    nc = mem.nc
    pe_done, act_done, dve_done, pool_done = mem.pe_done, mem.act_done, mem.dve_done, mem.pool_done
    step = mem.dve_step
    name = f"l{level}f"
    n_experts = E + (level == 3)
    ps = mem.psum
    pe_done.stage("xnT", "logits", "gates", "yT", "y")
    dve_done.stage("var", "xn", "xnT", "scores", "gates", "yT", "x")
    act_done.stage("exp")
    pool_done.stage("rstd")
    weights = mem.experts
    w1 = weights[:, 0:n_experts * HID]
    w2 = weights[:, n_experts * HID:2 * n_experts * HID]

    with ExitStack() as local:
        def sb(label, shape, dt=F32):
            return local.enter_context(nc.sbuf_tensor(f"{name}_{label}", shape, dt))

        experts = Experts(mem, sb, name, n_experts, HID, ACT.Gelu_apprx_tanh, (w1, w2))
        xnT = sb("xnT", [C, T])
        scores, top, total = sb("scores", [T, E]), sb("top", [T, 1]), sb("total", [T, 1])
        padded, work, best, mask = sb("padded", [T, 16]), sb("work", [T, 16]), sb("best", [T, 8]), sb("mask", [T, E])

        with nc.Block(no_gpsimd_drain=True) as block:

            @block.tensor
            def _(pe):
                pe.wait_ge(*dve_done.at("xn"))
                nc.tensor.transpose(ps[0:C, 0, 0:T], mem.xn[:, :], mem.w("consts", "ident")[0:T, 0:T])\
                    .then_inc(*pe_done.mark("xnT"))
                pe.wait_ge(mem.loaded[name], 16)
                pe.wait_ge(*dve_done.at("xnT"))
                nc.tensor.matmul(ps[0:T, 0, 128:128 + E], xnT[:, :], mem.w(name, "w_router"), start=True,
                                 stop=True).then_inc(*pe_done.mark("logits"))
                pe.wait_ge(mem.loaded[f"experts{level}"], 16)
                experts.pe_hidden(pe, xnT[:, :])
                experts.pe_gates(pe, 6)
                experts.pe_out(pe)

            @block.scalar
            def _(act):
                act.wait_ge(*dve_done.at("scores"))
                nc.scalar.activation(padded[:, 0:E], scores[:, :], ACT.Exp).then_inc(*act_done.mark("exp"))
                experts.act_hidden(act)

            @block.gpsimd
            def _(pool):
                pool_rstd(mem, "var", "rstd")

            @block.vector
            def _(dve):
                v = nc.vector
                dve_moments(mem, mem.x[:, :], "var")
                dve_normalised(mem, mem.xn[:, :], mem.x[:, :], "rstd").then_inc(*dve_done.mark("xn"))
                v.memset(padded[:, E:16], -1.0)
                dve.wait_ge(*pe_done.at("xnT"))
                v.tensor_copy(xnT[:, :], ps[0:C, 0, 0:T]).then_inc(*dve_done.mark("xnT"))
                dve.wait_ge(*pe_done.at("logits"))
                step(v.tensor_copy(scores[:, :], ps[0:T, 0, 128:128 + E]))
                dve_softmax(mem, (top[:, :], total[:, :]), scores[:, :], padded[:, 0:E], "scores", "exp")
                dve_first_largest(mem, padded[:, :], best[:, :], work[:, :], mask[:, :], E, 2)
                if level == 3:
                    step(v.memset(experts.gates[:, E:E + 1], 1.0))
                step(v.tensor_tensor(experts.gates[:, 0:E], padded[:, 0:E], mask[:, :], ALU.mult))
                if level == 3:
                    step(v.tensor_reduce(total[:, :], experts.gates[:, 0:E], AX_X, ALU.add))
                    step(v.reciprocal(total[:, :], total[:, :]))
                    step(v.tensor_scalar(experts.gates[:, 0:E], experts.gates[:, 0:E], total[:, :], None,
                                         ALU.mult))
                dve.wait_ge(mem.loaded[name], 16)
                experts.dve_gates(dve)
                experts.dve_bias(dve)
                experts.dve_gate(dve, 6)
                experts.dve_yT(dve)
                dve.wait_ge(*pe_done.at("y"))
                v.tensor_tensor(mem.x[:, :], mem.x[:, :], ps[0:T, 7, 128:128 + C], ALU.add)\
                    .then_inc(*dve_done.mark("x"))



class SmallHeads:
    PE = ["scores", "probsT", "heads"]
    DVE = ["Qbd", "less_max", "probs", "PT", "OT"]

    def __init__(self, mem, sb, mask):
        self.mem, self.mask = mem, mask
        self.QT, self.KT, self.V = sb("QT", [C, T]), sb("KT", [C, T]), sb("V", [T, C])
        self.Qbd = sb("Qbd", [C, HG, T])
        self.S = sb("S", [128, 2 * G, T])
        self.P = sb("P", [128, 2 * G, T])
        self.top, self.total = sb("top", [128, 2 * G]), sb("total", [128, 2 * G])
        self.PT = sb("PT", [T, H * T])
        self.weighted = sb("weighted", [C, HG, T])
        self.OT = sb("OT", [C, T])

    def pe(self, pe, v_event):
        nc, mem, ps = self.mem.nc, self.mem, self.mem.psum
        pe.wait_ge(*mem.dve_done.at("Qbd"))
        for s in range(2):
            for g in range(G):
                rows = slice(32 * g, 32 * g + 32)
                last = nc.tensor.matmul(ps[:, 1 + g, s * T:(s + 1) * T], self.Qbd[rows, 2 * s:2 * s + 2, :],
                                        self.KT[rows, :], start=True, stop=True)
        last.then_inc(*mem.pe_done.mark("scores"))
        pe.wait_ge(*mem.dve_done.at("probs"))
        for n in range(2 * G):
            last = nc.tensor.transpose(ps[0:T, 5 + n // G, (n % G) * 128:(n % G + 1) * 128],
                                       self.P[:, n, :], mem.w("consts", "ident"))
        last.then_inc(*mem.pe_done.mark("probsT"))
        pe.wait_ge(*mem.dve_done.at("PT"))
        pe.wait_ge(*mem.dve_done.at(v_event))
        for g in range(G):
            last = nc.tensor.matmul(ps[32 * g:32 * g + 32, 7, 0:HG * T], self.V[:, 32 * g:32 * g + 32],
                                    self.PT[:, 256 * g:256 * g + 256], start=True, stop=True)
        last.then_inc(*mem.pe_done.mark("heads"))

    def act(self, act):
        mem = self.mem
        act.wait_ge(*mem.dve_done.at("less_max"))
        mem.nc.scalar.activation(self.P[:, :, :], self.S[:, :, :], ACT.Exp).then_inc(*mem.act_done.mark("exps"))

    def dve_Qbd(self, dve):
        mem, shape = self.mem, [C, HG, T]
        mem.nc.vector.tensor_tensor(self.Qbd[:, :, :], spread(self.QT[:, :], 1, shape),
                                    spread(mem.w("consts", "four_heads"), 2, shape), ALU.mult)\
            .then_inc(*mem.dve_done.mark("Qbd"))

    def dve(self, dve):
        mem, v, step, ps = self.mem, self.mem.nc.vector, self.mem.dve_step, self.mem.psum
        shape = [128, 2 * G, T]
        dve.wait_ge(*mem.pe_done.at("scores"))
        scores = ps[:, 1:1 + G, 0:2 * T].rearrange("p g (s k) -> p g s k", s=2)
        if self.mask is None:
            step(v.tensor_copy(self.S[:, :, :].rearrange("p (g s) k -> p g s k", g=G), scores))
        else:
            mask = self.mask.unsqueeze(1).unsqueeze(1).to_broadcast([128, G, 2, T])
            step(v.tensor_tensor(self.S[:, :, :].rearrange("p (g s) k -> p g s k", g=G), scores, mask, ALU.add))
        step(v.tensor_reduce(self.top[:, :], self.S[:, :, :], AX_X, ALU.max))
        v.tensor_tensor(self.S[:, :, :], self.S[:, :, :], spread(self.top[:, :], 2, shape), ALU.subtract)\
            .then_inc(*mem.dve_done.mark("less_max"))
        dve.wait_ge(*mem.act_done.at("exps"))
        step(v.tensor_reduce(self.total[:, :], self.P[:, :, :], AX_X, ALU.add))
        step(v.reciprocal(self.total[:, :], self.total[:, :]))
        v.tensor_tensor(self.P[:, :, :], self.P[:, :, :], spread(self.total[:, :], 2, shape), ALU.mult)\
            .then_inc(*mem.dve_done.mark("probs"))
        dve.wait_ge(*mem.pe_done.at("probsT"))
        v.tensor_copy(self.PT[:, :].rearrange("p (b n) -> p b n", b=2), ps[0:T, 5:7, :])\
            .then_inc(*mem.dve_done.mark("PT"))
        dve.wait_ge(*mem.pe_done.at("heads"))
        step(v.tensor_tensor(self.weighted[:, :, :], ps[:, 7, 0:HG * T].rearrange("p (h q) -> p h q", h=HG),
                             spread(mem.w("consts", "four_heads"), 2, [C, HG, T]), ALU.mult))
        v.tensor_reduce(self.OT[:, :], self.weighted[:, :, :].rearrange("p h q -> p q h"), AX_X, ALU.add)\
            .then_inc(*mem.dve_done.mark("OT"))



def stage_rope_attention(mem):
    nc = mem.nc
    pe_done, act_done, dve_done, pool_done = mem.pe_done, mem.act_done, mem.dve_done, mem.pool_done
    step, ps = mem.dve_step, mem.psum
    ident = mem.w("consts", "ident")
    QK = H + G
    pe_done.stage("xnT", "qkv", "turned", *SmallHeads.PE, "projected")
    dve_done.stage("var", "xn", "xnT", "squares", "rotated", *SmallHeads.DVE, "x")
    act_done.stage("exps")
    pool_done.stage("rstd", "norms")

    with ExitStack() as local:
        def sb(name, shape, dt=F32):
            return local.enter_context(nc.sbuf_tensor("l1a_" + name, shape, dt))

        heads = SmallHeads(mem, sb, mem.w("consts", "causal"))
        xnT = sb("xnT", [C, T])
        qkv = sb("qkv", [T, (QK + G) * DH])
        squares, unit = sb("squares", [T, QK, DH]), sb("unit", [T, QK, DH])
        sums, norms, half = sb("sums", [T, QK]), sb("norms", [T, QK]), sb("half", [T, QK])
        straight, crossed = sb("straight", [T, QK, DH]), sb("crossed", [T, QK, DH])
        k_all = sb("k_all", [T, C])

        with nc.Block(no_gpsimd_drain=True) as block:

            @block.tensor
            def _(pe):
                pe.wait_ge(*dve_done.at("xn"))
                nc.tensor.transpose(ps[0:C, 0, 0:T], mem.xn[:, :], ident[0:T, 0:T]).then_inc(*pe_done.mark("xnT"))
                pe.wait_ge(mem.loaded["l1a"], 16)
                pe.wait_ge(*dve_done.at("xnT"))
                nc.tensor.matmul(ps[0:T, 1, 0:192], xnT[:, :], mem.w("l1a", "w_qkv"), start=True, stop=True)\
                    .then_inc(*pe_done.mark("qkv"))
                pe.wait_ge(*dve_done.at("rotated"))
                nc.tensor.transpose(ps[0:C, 0, 0:T], straight[:, 0:H, :], ident[0:T, 0:T])
                nc.tensor.transpose(ps[0:C, 0, T:2 * T], k_all[:, :], ident[0:T, 0:T])\
                    .then_inc(*pe_done.mark("turned"))
                heads.pe(pe, "rotated")
                pe.wait_ge(*dve_done.at("OT"))
                nc.tensor.matmul(ps[0:T, 0, 0:C], heads.OT[:, :], mem.w("l1a", "w_o"), start=True, stop=True)\
                    .then_inc(*pe_done.mark("projected"))

            @block.scalar
            def _(act):
                heads.act(act)

            @block.gpsimd
            def _(pool):
                pool_rstd(mem, "var", "rstd")
                pool_power(mem, norms[:, :], sums[:, :], half[:, :], dve_done.at("squares"), "norms")

            @block.vector
            def _(dve):
                v = nc.vector
                dve_moments(mem, mem.x[:, :], "var")
                dve_normalised(mem, mem.xn[:, :], mem.x[:, :], "rstd").then_inc(*dve_done.mark("xn"))
                v.memset(half[:, :], 0.5)
                dve.wait_ge(*pe_done.at("xnT"))
                v.tensor_copy(xnT[:, :], ps[0:C, 0, 0:T]).then_inc(*dve_done.mark("xnT"))
                dve.wait_ge(*pe_done.at("qkv"))
                step(v.tensor_copy(qkv[:, :], ps[0:T, 1, 0:192]))
                qk = qkv[:, 0:QK * DH].rearrange("t (h d) -> t h d", d=DH)
                step(v.tensor_tensor(squares[:, :, :], qk, qk, ALU.mult))
                v.tensor_reduce(sums[:, :], squares[:, :, :], AX_X, ALU.add).then_inc(*dve_done.mark("squares"))
                dve.wait_ge(*pool_done.at("norms"))
                step(v.tensor_scalar(norms[:, :], norms[:, :], 1e-10, None, ALU.add))
                step(v.reciprocal(norms[:, :], norms[:, :]))
                step(v.tensor_tensor(unit[:, :, :], qk, spread(norms[:, :], 2, [T, QK, DH]), ALU.mult))
                f, h = DH, DH // 2
                sin = mem.w("consts", "sin")
                v.tensor_tensor(straight[:, :, :], unit[:, :, :],
                                spread(mem.w("consts", "cos"), 1, [T, QK, f]), ALU.mult)
                v.tensor_tensor(crossed[:, :, 0:h], unit[:, :, h:f], spread(sin[:, 0:h], 1, [T, QK, h]), ALU.mult)
                step(v.tensor_tensor(crossed[:, :, h:f], unit[:, :, 0:h], spread(sin[:, h:f], 1, [T, QK, h]), ALU.mult))
                step(v.tensor_tensor(straight[:, :, :], straight[:, :, :], crossed[:, :, :], ALU.add))
                v.tensor_copy(k_all[:, :].rearrange("t (g r d) -> t g r d", g=G, r=HG),
                              spread(straight[:, H:QK, :], 2, [T, G, HG, DH]))
                v.tensor_copy(heads.V[:, :].rearrange("t (g r d) -> t g r d", g=G, r=HG),
                              spread(qkv[:, QK * DH:192].rearrange("t (g d) -> t g d", g=G), 2, [T, G, HG, DH]))\
                    .then_inc(*dve_done.mark("rotated"))
                dve.wait_ge(*pe_done.at("turned"))
                v.tensor_copy(heads.KT[:, :], ps[0:C, 0, T:2 * T])
                step(v.tensor_scalar(heads.QT[:, :], ps[0:C, 0, 0:T], SCALE, None, ALU.mult))
                heads.dve_Qbd(dve)
                heads.dve(dve)
                dve.wait_ge(*pe_done.at("projected"))
                v.tensor_tensor(mem.x[:, :], mem.x[:, :], ps[0:T, 0, 0:C], ALU.add).then_inc(*dve_done.mark("x"))



def stage_quantised_ffn(mem):
    nc = mem.nc
    pe_done, act_done, dve_done, pool_done = mem.pe_done, mem.act_done, mem.dve_done, mem.pool_done
    step, ps = mem.dve_step, mem.psum
    ident = mem.w("consts", "ident")
    pe_done.stage("weightsT", "x_topT", "x_top", "xqT", "gate_up", "h_topT", "h_top", "hT", "out")
    dve_done.stage("var", "xn", "w_quantised", "wT", "x_top1", "x_top", "xq", "xqT",
                   "h", "h_top1", "h_top", "hq", "hT", "x")
    act_done.stage("clips", "silu")
    pool_done.stage("rstd")

    with ExitStack() as local:
        def sb(name, shape, dt=F32):
            return local.enter_context(nc.sbuf_tensor("l1f_" + name, shape, dt))

        gate_up = sb("gate_up", [128, 6, C])
        down = sb("down", [C, FFQ])
        tops, steps_, inverse = sb("tops", [128, 7]), sb("steps", [128, 7]), sb("inverse", [128, 7])
        gate_upT = sb("gate_upT", [C, 2, FFQ])
        downT = sb("downT", [128, 3, C])
        clips = sb("clips", [C, 2])
        top, top1 = sb("top", [T, 2]), sb("top1", [1, 2])
        a_step, a_inv = sb("a_step", [T, 2]), sb("a_inv", [T, 2])
        xq, xqT = sb("xq", [T, C]), sb("xqT", [C, T])
        silu, h = sb("silu", [T, FFQ]), sb("h", [T, FFQ])
        hT = sb("hT", [128, 3, T])

        with nc.Block(no_gpsimd_drain=True) as block:

            @block.tensor
            def _(pe):
                def spread_top(n):
                    name = "xh"[n]
                    pe.wait_ge(*dve_done.at(f"{name}_top1"))
                    nc.tensor.matmul(ps[0:T, 4, 128 + n:129 + n], mem.ones[0:1, 0:T], top1[0:1, n:n + 1],
                                     start=True, stop=True).then_inc(*pe_done.mark(f"{name}_top"))

                pe.wait_ge(*dve_done.at("w_quantised"))
                for m in range(2):
                    for n, (lo, rows) in enumerate(FFQ_CHUNKS):
                        nc.tensor.transpose(ps[0:C, 1 + m, lo:lo + rows], gate_up[0:rows, 3 * m + n, :],
                                            ident[0:rows, 0:rows])
                for n, (lo, rows) in enumerate(FFQ_CHUNKS):
                    last = nc.tensor.transpose(ps[0:rows, 3, n * C:(n + 1) * C], down[:, lo:lo + rows], ident)
                last.then_inc(*pe_done.mark("weightsT"))
                pe.wait_ge(*dve_done.at("xn"))
                nc.tensor.transpose(ps[0:1, 4, 0:T], top[:, 0:1], ident[0:T, 0:T])\
                    .then_inc(*pe_done.mark("x_topT"))
                spread_top(0)
                pe.wait_ge(*dve_done.at("xq"))
                nc.tensor.transpose(ps[0:C, 0, 0:T], xq[:, :], ident[0:T, 0:T]).then_inc(*pe_done.mark("xqT"))
                pe.wait_ge(*dve_done.at("xqT"))
                for m in range(2):
                    last = nc.tensor.matmul(ps[0:T, 5 + m, 0:FFQ], xqT[:, :], gate_upT[:, m, :], start=True,
                                            stop=True)
                last.then_inc(*pe_done.mark("gate_up"))
                pe.wait_ge(*dve_done.at("h"))
                nc.tensor.transpose(ps[0:1, 4, 0:T], top[:, 1:2], ident[0:T, 0:T])\
                    .then_inc(*pe_done.mark("h_topT"))
                spread_top(1)
                pe.wait_ge(*dve_done.at("hq"))
                for n, (lo, rows) in enumerate(FFQ_CHUNKS):
                    last = nc.tensor.transpose(ps[0:rows, 7, n * T:(n + 1) * T], h[:, lo:lo + rows],
                                               ident[0:T, 0:T])
                last.then_inc(*pe_done.mark("hT"))
                pe.wait_ge(*dve_done.at("hT"))
                for n, (lo, rows) in enumerate(FFQ_CHUNKS):
                    last = nc.tensor.matmul(ps[0:T, 0, 0:C], hT[0:rows, n, :], downT[0:rows, n, :],
                                            start=n == 0, stop=n == 2)
                last.then_inc(*pe_done.mark("out"))

            @block.scalar
            def _(act):
                act.wait_ge(mem.loaded["l1f"], 16)
                at, _, _ = column("l1f", "clip_x")
                nc.scalar.activation(clips[:, :], mem.packs["l1f"][:, at:at + 2], ACT.Exp, scale=-1.0)\
                    .then_inc(*act_done.mark("clips"))
                act.wait_ge(*pe_done.at("gate_up"))
                nc.scalar.activation(silu[:, :], ps[0:T, 5, 0:FFQ], ACT.Silu).then_inc(*act_done.mark("silu"))

            @block.gpsimd
            def _(pool):
                pool_rstd(mem, "var", "rstd")

            @block.vector
            def _(dve):
                v = nc.vector

                def rounded(out, scaled):
                    step(v.tensor_scalar(out, scaled, ROUND, ROUND, ALU.add, ALU.subtract))
                    step(v.tensor_scalar(out, out, 127.0, -128.0, ALU.min, ALU.max))

                def activation_step(n):
                    name = "xh"[n]
                    dve.wait_ge(*pe_done.at(f"{name}_topT"))
                    v.tensor_reduce(top1[0:1, n:n + 1], ps[0:1, 4, 0:T], AX_X, ALU.max)\
                        .then_inc(*dve_done.mark(f"{name}_top1"))
                    dve.wait_ge(*pe_done.at(f"{name}_top"))
                    step(v.tensor_scalar(a_step[:, n:n + 1], ps[0:T, 4, 128 + n:129 + n], clips[0:T, n:n + 1],
                                         1.0 / 127.0, ALU.mult, ALU.mult))
                    v.reciprocal(a_inv[:, n:n + 1], a_step[:, n:n + 1]).then_inc(*dve_done.mark(f"{name}_top"))
                    dve.wait_ge(*dve_done.at(f"{name}_top"))

                dve_moments(mem, mem.x[:, :], "var")
                step(dve_normalised(mem, mem.xn[:, :], mem.x[:, :], "rstd"))
                v.tensor_reduce(top[:, 0:1], mem.xn[:, :], AX_X, ALU.max, apply_absolute_value=True)\
                    .then_inc(*dve_done.mark("xn"))
                dve.wait_ge(mem.loaded["l1f"], 16)
                raw = mem.packs["l1f"][:, 0:6 * C].rearrange("p (n m) -> p n m", n=6)
                v.tensor_reduce(tops[:, 0:6], raw, AX_X, ALU.max, apply_absolute_value=True)
                step(v.tensor_reduce(tops[:, 6:7], mem.w("l1f", "w_down"), AX_X, ALU.max,
                                     apply_absolute_value=True))
                step(v.tensor_scalar(steps_[:, :], tops[:, :], 1e-30, 1.0 / 127.0, ALU.max, ALU.mult))
                step(v.reciprocal(inverse[:, :], steps_[:, :]))
                step(v.tensor_tensor(gate_up[:, :, :], raw, spread(inverse[:, 0:6], 2, [128, 6, C]), ALU.mult))
                rounded(gate_up[:, :, :], gate_up[:, :, :])
                step(v.tensor_tensor(gate_up[:, :, :], gate_up[:, :, :],
                                     spread(steps_[:, 0:6], 2, [128, 6, C]), ALU.mult))
                step(v.tensor_scalar(down[:, :], mem.w("l1f", "w_down"), inverse[:, 6:7], None, ALU.mult))
                rounded(down[:, :], down[:, :])
                v.tensor_scalar(down[:, :], down[:, :], steps_[:, 6:7], None, ALU.mult)\
                    .then_inc(*dve_done.mark("w_quantised"))
                dve.wait_ge(*pe_done.at("weightsT"))
                v.tensor_copy(gate_upT[:, :, :], ps[0:C, 1:3, 0:FFQ])
                v.tensor_copy(downT[:, 0:2, :], ps[:, 3, 0:2 * C].rearrange("p (n m) -> p n m", n=2))
                v.tensor_copy(downT[0:96, 2, :], ps[0:96, 3, 2 * C:3 * C]).then_inc(*dve_done.mark("wT"))
                dve.wait_ge(*act_done.at("clips"))
                step(v.tensor_scalar(clips[:, :], clips[:, :], 1.0, None, ALU.add))
                step(v.reciprocal(clips[:, :], clips[:, :]))
                activation_step(0)
                step(v.tensor_scalar(xq[:, :], mem.xn[:, :], a_inv[:, 0:1], None, ALU.mult))
                rounded(xq[:, :], xq[:, :])
                v.tensor_scalar(xq[:, :], xq[:, :], a_step[:, 0:1], None, ALU.mult)\
                    .then_inc(*dve_done.mark("xq"))
                dve.wait_ge(*pe_done.at("xqT"))
                v.tensor_copy(xqT[:, :], ps[0:C, 0, 0:T]).then_inc(*dve_done.mark("xqT"))
                dve.wait_ge(*act_done.at("silu"))
                step(v.tensor_tensor(h[:, :], silu[:, :], ps[0:T, 6, 0:FFQ], ALU.mult))
                v.tensor_reduce(top[:, 1:2], h[:, :], AX_X, ALU.max, apply_absolute_value=True)\
                    .then_inc(*dve_done.mark("h"))
                activation_step(1)
                step(v.tensor_scalar(h[:, :], h[:, :], a_inv[:, 1:2], None, ALU.mult))
                rounded(h[:, :], h[:, :])
                v.tensor_scalar(h[:, :], h[:, :], a_step[:, 1:2], None, ALU.mult).then_inc(*dve_done.mark("hq"))
                dve.wait_ge(*pe_done.at("hT"))
                v.tensor_copy(hT[:, 0:2, :], ps[:, 7, 0:2 * T].rearrange("p (n t) -> p n t", n=2))
                v.tensor_copy(hT[0:96, 2, :], ps[0:96, 7, 2 * T:3 * T]).then_inc(*dve_done.mark("hT"))
                dve.wait_ge(*pe_done.at("out"))
                v.tensor_tensor(mem.x[:, :], mem.x[:, :], ps[0:T, 0, 0:C], ALU.add).then_inc(*dve_done.mark("x"))



def stage_local_attention(mem):
    nc = mem.nc
    pe_done, act_done, dve_done, pool_done = mem.pe_done, mem.act_done, mem.dve_done, mem.pool_done
    step, ps = mem.dve_step, mem.psum
    ident = mem.w("consts", "ident")
    pe_done.stage("xnT", "qkv", *SmallHeads.PE, "projected")
    dve_done.stage("var", "xn", "xnT", *SmallHeads.DVE[:1], "V", *SmallHeads.DVE[1:], "x")
    act_done.stage("exps")
    pool_done.stage("rstd")

    def w(name):
        return mem.w("l2a", name)

    with ExitStack() as local:
        def sb(name, shape, dt=F32):
            return local.enter_context(nc.sbuf_tensor("l2a_" + name, shape, dt))

        heads = SmallHeads(mem, sb, mem.w("consts", "band"))
        xnT = sb("xnT", [C, T])
        residual = sb("residual", [T, C])

        with nc.Block(no_gpsimd_drain=True) as block:

            @block.tensor
            def _(pe):
                pe.wait_ge(*dve_done.at("xn"))
                nc.tensor.transpose(ps[0:C, 0, 0:T], mem.xn[:, :], ident[0:T, 0:T]).then_inc(*pe_done.mark("xnT"))
                pe.wait_ge(mem.loaded["l2a"], 16)
                pe.wait_ge(*dve_done.at("xnT"))
                nc.tensor.matmul(ps[0:C, 0, 0:T], w("w_q"), xnT[:, :], start=True, stop=True)
                nc.tensor.matmul(ps[0:C, 0, T:2 * T], w("w_k"), xnT[:, :], start=True, stop=True)
                nc.tensor.matmul(ps[0:T, 0, 128:256], xnT[:, :], w("w_v"), start=True, stop=True)\
                    .then_inc(*pe_done.mark("qkv"))
                heads.pe(pe, "V")
                pe.wait_ge(*dve_done.at("OT"))
                nc.tensor.matmul(ps[0:T, 0, 0:C], heads.OT[:, :], w("w_o"), start=True, stop=True)\
                    .then_inc(*pe_done.mark("projected"))

            @block.scalar
            def _(act):
                heads.act(act)

            @block.gpsimd
            def _(pool):
                pool_rstd(mem, "var", "rstd")

            @block.vector
            def _(dve):
                v = nc.vector
                dve_moments(mem, mem.x[:, :], "var")
                dve_normalised(mem, mem.xn[:, :], mem.x[:, :], "rstd").then_inc(*dve_done.mark("xn"))
                v.tensor_tensor(residual[:, :], mem.x[:, :], mem.row("l2a_bo"), ALU.add)
                dve.wait_ge(*pe_done.at("xnT"))
                v.tensor_copy(xnT[:, :], ps[0:C, 0, 0:T]).then_inc(*dve_done.mark("xnT"))
                dve.wait_ge(mem.loaded["l2a"], 16)
                dve.wait_ge(*pe_done.at("qkv"))
                v.tensor_scalar(heads.KT[:, :], ps[0:C, 0, T:2 * T], w("b_k"), None, ALU.add)
                step(v.tensor_scalar(heads.QT[:, :], ps[0:C, 0, 0:T], w("b_q"), SCALE, ALU.add, ALU.mult))
                heads.dve_Qbd(dve)
                v.tensor_tensor(heads.V[:, :], ps[0:T, 0, 128:256], mem.row("l2a_bv"), ALU.add)\
                    .then_inc(*dve_done.mark("V"))
                heads.dve(dve)
                dve.wait_ge(*pe_done.at("projected"))
                v.tensor_tensor(mem.x[:, :], residual[:, :], ps[0:T, 0, 0:C], ALU.add)\
                    .then_inc(*dve_done.mark("x"))



def stage_transformer_experts(mem):
    nc = mem.nc
    pe_done, act_done, dve_done, pool_done = mem.pe_done, mem.act_done, mem.dve_done, mem.pool_done
    step, ps = mem.dve_step, mem.psum
    ident = mem.w("consts", "ident")
    GROUPS = 4
    pe_done.stage("zT", "qkv", "turned", *SmallHeads.PE, "projected", "yT_in", "logits", "gates", "yT", "y")
    dve_done.stage("var", "z", "zT", "V", *SmallHeads.DVE, "mid_var", "mid", "midT", "scores", "gates", "yT",
                   "out_var", "x")
    act_done.stage("exps", "gate_exps")
    pool_done.stage("rstd", "mid_rstd", "out_rstd")
    weights = mem.packs["experts2"]

    def w(name):
        return mem.w("l2f", name)

    with ExitStack() as local:
        def sb(name, shape, dt=F32):
            return local.enter_context(nc.sbuf_tensor("l2f_" + name, shape, dt))

        heads = SmallHeads(mem, sb, None)
        experts = Experts(mem, sb, "l2f", E, HID2, ACT.Relu,
                          (weights[:, 0:E * HID2], weights[:, E * HID2:2 * E * HID2]))
        zT, midT = sb("zT", [C, T]), sb("midT", [C, T])
        qk, mid, out = sb("qk", [T, 2 * C]), sb("mid", [T, C]), sb("out", [T, C])
        residual = sb("residual", [T, C])
        scores, exps = sb("scores", [T, GROUPS + E]), sb("exps", [T, GROUPS + E])
        tops, totals = sb("tops", [T, 1 + GROUPS]), sb("totals", [T, 1 + GROUPS])
        padded, work, best = sb("padded", [T, 16]), sb("work", [T, 16]), sb("best", [T, 8])
        group_gate, pick = sb("group_gate", [T, GROUPS]), sb("pick", [T, GROUPS, 2])

        with nc.Block(no_gpsimd_drain=True) as block:

            @block.tensor
            def _(pe):
                pe.wait_ge(*dve_done.at("z"))
                nc.tensor.transpose(ps[0:C, 0, 0:T], mem.xn[:, :], ident[0:T, 0:T]).then_inc(*pe_done.mark("zT"))
                pe.wait_ge(mem.loaded["l2f"], 16)
                pe.wait_ge(*dve_done.at("zT"))
                nc.tensor.matmul(ps[0:T, 1, 0:3 * C], zT[:, :], w("w_in"), start=True, stop=True)\
                    .then_inc(*pe_done.mark("qkv"))
                pe.wait_ge(*dve_done.at("V"))
                nc.tensor.transpose(ps[0:C, 0, 0:T], qk[:, 0:C], ident[0:T, 0:T])
                nc.tensor.transpose(ps[0:C, 0, T:2 * T], qk[:, C:2 * C], ident[0:T, 0:T])\
                    .then_inc(*pe_done.mark("turned"))
                heads.pe(pe, "V")
                pe.wait_ge(*dve_done.at("OT"))
                nc.tensor.matmul(ps[0:T, 0, 0:C], heads.OT[:, :], w("w_out"), start=True, stop=True)\
                    .then_inc(*pe_done.mark("projected"))
                pe.wait_ge(*dve_done.at("mid"))
                nc.tensor.transpose(ps[0:C, 0, 0:T], mid[:, :], ident[0:T, 0:T]).then_inc(*pe_done.mark("yT_in"))
                pe.wait_ge(*dve_done.at("midT"))
                at, _, _ = column("l2f", "w_group")
                nc.tensor.matmul(ps[0:T, 0, 128:128 + GROUPS + E], midT[:, :],
                                 mem.packs["l2f"][:, at:at + GROUPS + E], start=True, stop=True)\
                    .then_inc(*pe_done.mark("logits"))
                pe.wait_ge(mem.loaded["experts2"], 16)
                experts.pe_hidden(pe, midT[:, :])
                experts.pe_gates(pe, 6)
                experts.pe_out(pe)

            @block.scalar
            def _(act):
                heads.act(act)
                act.wait_ge(*dve_done.at("scores"))
                nc.scalar.activation(exps[:, :], scores[:, :], ACT.Exp).then_inc(*act_done.mark("gate_exps"))
                experts.act_hidden(act)

            @block.gpsimd
            def _(pool):
                pool_rstd(mem, "var", "rstd")
                pool_rstd(mem, "mid_var", "mid_rstd")
                pool_rstd(mem, "out_var", "out_rstd")

            @block.vector
            def _(dve):
                v = nc.vector
                dve_moments(mem, mem.x[:, :], "var")
                dve_normalised(mem, mem.xn[:, :], mem.x[:, :], "rstd").then_inc(*dve_done.mark("z"))
                dve.wait_ge(*dve_done.at("z"))
                v.tensor_tensor(residual[:, :], mem.xn[:, :], mem.row("l2f_b_out"), ALU.add)
                v.memset(padded[:, GROUPS:16], -1.0)
                dve.wait_ge(*pe_done.at("zT"))
                v.tensor_copy(zT[:, :], ps[0:C, 0, 0:T]).then_inc(*dve_done.mark("zT"))
                dve.wait_ge(*pe_done.at("qkv"))
                bias = mem.row("l2f_b_in")
                v.tensor_tensor(qk[:, :], ps[0:T, 1, 0:2 * C], bias[:, 0:2 * C], ALU.add)
                v.tensor_tensor(heads.V[:, :], ps[0:T, 1, 2 * C:3 * C], bias[:, 2 * C:3 * C], ALU.add)\
                    .then_inc(*dve_done.mark("V"))
                dve.wait_ge(*pe_done.at("turned"))
                v.tensor_copy(heads.KT[:, :], ps[0:C, 0, T:2 * T])
                step(v.tensor_scalar(heads.QT[:, :], ps[0:C, 0, 0:T], SCALE, None, ALU.mult))
                heads.dve_Qbd(dve)
                heads.dve(dve)
                dve.wait_ge(*pe_done.at("projected"))
                step(v.tensor_tensor(mid[:, :], ps[0:T, 0, 0:C], residual[:, :], ALU.add))
                dve_moments(mem, mid[:, :], "mid_var")
                step(dve_normalised(mem, mid[:, :], mid[:, :], "mid_rstd"))
                step(v.tensor_tensor(mid[:, :], mid[:, :], mem.row("l2f_g1"), ALU.mult))
                v.tensor_tensor(mid[:, :], mid[:, :], mem.row("l2f_b1"), ALU.add).then_inc(*dve_done.mark("mid"))
                dve.wait_ge(*pe_done.at("yT_in"))
                v.tensor_copy(midT[:, :], ps[0:C, 0, 0:T]).then_inc(*dve_done.mark("midT"))
                dve.wait_ge(*pe_done.at("logits"))
                at, _, _ = column("rows", "l2f_b_group")
                step(v.tensor_tensor(scores[:, :], ps[0:T, 0, 128:128 + GROUPS + E],
                                     mem.rows[:, at:at + GROUPS + E], ALU.add))
                pairs = scores[:, GROUPS:GROUPS + E].rearrange("t (g e) -> t g e", e=2)
                v.tensor_reduce(tops[:, 0:1], scores[:, 0:GROUPS], AX_X, ALU.max)
                step(v.tensor_reduce(tops[:, 1:1 + GROUPS], pairs, AX_X, ALU.max))
                v.tensor_scalar(scores[:, 0:GROUPS], scores[:, 0:GROUPS], tops[:, 0:1], None, ALU.subtract)
                v.tensor_tensor(pairs, pairs, spread(tops[:, 1:1 + GROUPS], 2, [T, GROUPS, 2]), ALU.subtract)\
                    .then_inc(*dve_done.mark("scores"))
                dve.wait_ge(*act_done.at("gate_exps"))
                probs = exps[:, GROUPS:GROUPS + E].rearrange("t (g e) -> t g e", e=2)
                v.tensor_reduce(totals[:, 0:1], exps[:, 0:GROUPS], AX_X, ALU.add)
                step(v.tensor_reduce(totals[:, 1:1 + GROUPS], probs, AX_X, ALU.add))
                step(v.reciprocal(totals[:, :], totals[:, :]))
                v.tensor_scalar(padded[:, 0:GROUPS], exps[:, 0:GROUPS], totals[:, 0:1], None, ALU.mult)
                step(v.tensor_tensor(probs, probs, spread(totals[:, 1:1 + GROUPS], 2, [T, GROUPS, 2]), ALU.mult))
                dve_first_largest(mem, padded[:, :], best[:, :], work[:, :], group_gate[:, :], GROUPS, 1)
                step(v.tensor_tensor(group_gate[:, :], group_gate[:, :], padded[:, 0:GROUPS], ALU.mult))
                step(v.tensor_tensor(pick[:, :, 0], probs[:, :, 0], probs[:, :, 1], ALU.is_ge))
                step(v.tensor_scalar(pick[:, :, 1], pick[:, :, 0], -1.0, 1.0, ALU.mult, ALU.add))
                step(v.tensor_tensor(pick[:, :, :], pick[:, :, :], probs, ALU.mult))
                step(v.tensor_tensor(experts.gates[:, :].rearrange("t (g e) -> t g e", e=2), pick[:, :, :],
                                     spread(group_gate[:, :], 2, [T, GROUPS, 2]), ALU.mult))
                dve.wait_ge(mem.loaded["l2f"], 16)
                experts.dve_gates(dve)
                experts.dve_bias(dve)
                experts.dve_gate(dve, 6)
                experts.dve_yT(dve)
                dve.wait_ge(*pe_done.at("y"))
                step(v.tensor_tensor(out[:, :], mid[:, :], ps[0:T, 7, 128:128 + C], ALU.add))
                dve_moments(mem, out[:, :], "out_var")
                step(dve_normalised(mem, out[:, :], out[:, :], "out_rstd"))
                step(v.tensor_tensor(out[:, :], out[:, :], mem.row("l2f_g2"), ALU.mult))
                step(v.tensor_tensor(out[:, :], out[:, :], mem.row("l2f_b2"), ALU.add))
                v.tensor_tensor(mem.x[:, :], mem.x[:, :], out[:, :], ALU.add).then_inc(*dve_done.mark("x"))



def stage_past_attention(mem):
    nc = mem.nc
    pe_done, act_done, dve_done, pool_done = mem.pe_done, mem.act_done, mem.dve_done, mem.pool_done
    step, ps = mem.dve_step, mem.psum
    ident = mem.w("consts", "ident")
    pe_done.stage("zT", "qT", "scores", "probsT", "contextT", "out")
    dve_done.stage("var", "z", "zT", "qT", "less_max", "probs", "probsT", "contextT", "out", "x")
    act_done.stage("exps", "tanh")
    pool_done.stage("rstd")

    with ExitStack() as local:
        def sb(name, shape, dt=F32):
            return local.enter_context(nc.sbuf_tensor("l3a_" + name, shape, dt))

        zT, qT, contextT = sb("zT", [C, T]), sb("qT", [C, T]), sb("contextT", [C, T])
        S, P, PT = sb("S", [T, T]), sb("P", [T, T]), sb("PT", [T, T])
        top, total = sb("top", [T, 1]), sb("total", [T, 1])
        out = sb("out", [T, C])

        with nc.Block(no_gpsimd_drain=True) as block:

            @block.tensor
            def _(pe):
                pe.wait_ge(*dve_done.at("z"))
                nc.tensor.transpose(ps[0:C, 0, 0:T], mem.xn[:, :], ident[0:T, 0:T]).then_inc(*pe_done.mark("zT"))
                pe.wait_ge(mem.loaded["l3a"], 16)
                pe.wait_ge(*dve_done.at("zT"))
                nc.tensor.matmul(ps[0:C, 1, 0:T], mem.w("l3a", "w_dec"), zT[:, :], start=True, stop=True)\
                    .then_inc(*pe_done.mark("qT"))
                pe.wait_ge(*dve_done.at("qT"))
                nc.tensor.matmul(ps[0:T, 2, 0:T], qT[:, :], zT[:, :], start=True, stop=True)\
                    .then_inc(*pe_done.mark("scores"))
                pe.wait_ge(*dve_done.at("probs"))
                nc.tensor.transpose(ps[0:T, 3, 0:T], P[:, :], ident[0:T, 0:T]).then_inc(*pe_done.mark("probsT"))
                pe.wait_ge(*dve_done.at("probsT"))
                nc.tensor.matmul(ps[0:C, 4, 0:T], mem.xn[:, :], PT[:, :], start=True, stop=True)\
                    .then_inc(*pe_done.mark("contextT"))
                pe.wait_ge(*dve_done.at("contextT"))
                w_out = mem.w("l3a", "w_out")
                nc.tensor.matmul(ps[0:T, 5, 0:C], zT[:, :], w_out[:, 0:C], start=True, stop=False)
                nc.tensor.matmul(ps[0:T, 5, 0:C], contextT[:, :], w_out[:, C:2 * C], start=False, stop=True)\
                    .then_inc(*pe_done.mark("out"))

            @block.scalar
            def _(act):
                act.wait_ge(*dve_done.at("less_max"))
                nc.scalar.activation(P[:, :], S[:, :], ACT.Exp, accum_out=total[:, :])\
                    .then_inc(*act_done.mark("exps"))
                act.wait_ge(*dve_done.at("out"))
                nc.scalar.activation(out[:, :], out[:, :], ACT.Tanh).then_inc(*act_done.mark("tanh"))

            @block.gpsimd
            def _(pool):
                pool_rstd(mem, "var", "rstd")

            @block.vector
            def _(dve):
                v = nc.vector
                dve_moments(mem, mem.x[:, :], "var")
                dve_normalised(mem, mem.xn[:, :], mem.x[:, :], "rstd").then_inc(*dve_done.mark("z"))
                dve.wait_ge(*pe_done.at("zT"))
                v.tensor_copy(zT[:, :], ps[0:C, 0, 0:T]).then_inc(*dve_done.mark("zT"))
                dve.wait_ge(*pe_done.at("qT"))
                v.tensor_copy(qT[:, :], ps[0:C, 1, 0:T]).then_inc(*dve_done.mark("qT"))
                dve.wait_ge(*pe_done.at("scores"))
                step(v.tensor_tensor(S[:, :], ps[0:T, 2, 0:T], mem.w("consts", "strict"), ALU.add))
                step(v.tensor_reduce(top[:, :], S[:, :], AX_X, ALU.max))
                v.tensor_scalar(S[:, :], S[:, :], top[:, :], None, ALU.subtract)\
                    .then_inc(*dve_done.mark("less_max"))
                dve.wait_ge(*act_done.at("exps"))
                step(v.reciprocal(total[:, :], total[:, :]))
                v.tensor_scalar(P[:, :], P[:, :], total[:, :], None, ALU.mult).then_inc(*dve_done.mark("probs"))
                dve.wait_ge(*pe_done.at("probsT"))
                v.tensor_copy(PT[:, :], ps[0:T, 3, 0:T]).then_inc(*dve_done.mark("probsT"))
                dve.wait_ge(*pe_done.at("contextT"))
                v.tensor_copy(contextT[:, :], ps[0:C, 4, 0:T]).then_inc(*dve_done.mark("contextT"))
                dve.wait_ge(*pe_done.at("out"))
                v.tensor_tensor(out[:, :], ps[0:T, 5, 0:C], mem.row("l3a_bo"), ALU.add)\
                    .then_inc(*dve_done.mark("out"))
                dve.wait_ge(*act_done.at("tanh"))
                v.tensor_tensor(mem.x[:, :], mem.x[:, :], out[:, :], ALU.add).then_inc(*dve_done.mark("x"))



def stage_state_kernel(mem):
    nc = mem.nc
    dve_done, act_done = mem.dve_done, mem.act_done
    step = mem.dve_step
    dve_done.stage("angles", "kernel")
    act_done.stage("sines")
    mem.pe_done.stage()
    mem.pool_done.stage()
    N = NSTATE

    def w(name):
        return mem.w("l2x", name)

    with ExitStack() as local:
        def sb(name, shape, dt=F32):
            return local.enter_context(nc.sbuf_tensor("s4_" + name, shape, dt))

        def wide(name):
            return sb(name, [C, N])[:, :]

        dt, dt_m1 = sb("dt", [C, 1])[:, :], sb("dt_m1", [C, 1])[:, :]
        re, im, grow, grow_m1 = wide("re"), wide("im"), wide("grow"), wide("grow_m1")
        turns, angles, sines = wide("turns"), sb("angles", [C, 2, N]), sb("sines", [C, 2, N])
        cos, cos_m1, nr, ni = wide("cos"), wide("cos_m1"), wide("nr"), wide("ni")
        gr, gi, t1, t2, size = wide("gr"), wide("gi"), wide("t1"), wide("t2"), wide("size")
        pr, pi = sb("pr", [C, 2, N]), sb("pi", [C, 2, N])
        scratch = {n: (sb(f"n{n}", [C, n])[:, :], sb(f"r{n}", [C, n])[:, :], sb(f"s{n}", [C, n])[:, :],
                       sb(f"p{n}", [C, n], I32)[:, :]) for n in (1, N)}
        qr, qi = sb("qr", [C, T, N]), sb("qi", [C, T, N])
        prod1, prod2 = sb("prod1", [C, T // 2, N]), sb("prod2", [C, T // 2, N])
        kernel = sb("kernel", [C, T])

        with nc.Block(no_gpsimd_drain=True) as block:

            @block.scalar
            def _(act):
                act.wait_ge(*dve_done.at("angles"))
                nc.scalar.activation(sines[:, :, :], angles[:, :, :], ACT.Sin).then_inc(*act_done.mark("sines"))

            @block.vector
            def _(dve):
                v = nc.vector

                def mul(out, a, b):
                    step(v.tensor_tensor(out, a, b, ALU.mult))

                def add(out, a, b):
                    step(v.tensor_tensor(out, a, b, ALU.add))

                def sub(out, a, b):
                    step(v.tensor_tensor(out, a, b, ALU.subtract))

                def affine(out, a, scale, shift):
                    step(v.tensor_scalar(out, a, scale, shift, ALU.mult, ALU.add))

                def exponential(z, full, less_one, n):
                    whole, series, rest, power = scratch[n][0], scratch[n][2], scratch[n][1], scratch[n][3]
                    step(v.tensor_scalar(z, z, -87.0, 88.0, ALU.max, ALU.min))
                    affine(whole, z, LOG2E, ROUND)
                    step(v.tensor_scalar(whole, whole, ROUND, None, ALU.subtract))
                    step(v.scalar_tensor_tensor(out=rest, in0=whole, scalar=-LN2_HI, in1=z, op0=ALU.mult, op1=ALU.add))
                    step(v.scalar_tensor_tensor(out=rest, in0=whole, scalar=-LN2_LO, in1=rest, op0=ALU.mult, op1=ALU.add))
                    step(v.tensor_scalar(series, rest, 1.0 / 5040, None, ALU.mult))
                    for k in (720, 120, 24, 6, 2, 1):
                        step(v.scalar_tensor_tensor(out=series, in0=series, scalar=1.0 / k, in1=rest,
                                                    op0=ALU.add, op1=ALU.mult))
                    step(v.tensor_scalar(power, whole, 127.0, 8388608.0, ALU.add, ALU.mult))
                    two = power.bitcast(F32)
                    mul(series, series, two)
                    add(full, series, two)
                    step(v.scalar_tensor_tensor(out=less_one, in0=two, scalar=-1.0, in1=series,
                                                op0=ALU.add, op1=ALU.add))

                dve.wait_ge(mem.loaded["l2x"], 16)
                step(v.tensor_copy(t1[:, 0:1], w("log_dt")))
                exponential(t1[:, 0:1], dt, dt_m1, 1)
                step(v.tensor_scalar(re, w("A_re"), dt, None, ALU.mult))
                step(v.tensor_scalar(im, w("A_im"), dt, None, ALU.mult))
                affine(turns, im, 1.0 / (2 * np.pi), ROUND)
                step(v.tensor_scalar(turns, turns, ROUND, None, ALU.subtract))
                for part in (TWO_PI_HI, TWO_PI_MID, TWO_PI_LO):
                    step(v.scalar_tensor_tensor(out=im, in0=turns, scalar=-part, in1=im, op0=ALU.mult, op1=ALU.add))
                step(v.tensor_scalar(angles[:, 0, :], im, -3.1415925, 3.1415925, ALU.max, ALU.min))
                v.tensor_scalar(angles[:, 1, :], angles[:, 0, :], 0.5, None, ALU.mult)\
                    .then_inc(*dve_done.mark("angles"))
                exponential(re, grow, grow_m1, N)
                dve.wait_ge(*act_done.at("sines"))
                mul(t1, sines[:, 1, :], sines[:, 1, :])
                step(v.tensor_scalar(cos_m1, t1, -2.0, None, ALU.mult))
                step(v.tensor_scalar(cos, cos_m1, 1.0, None, ALU.add))
                mul(pr[:, 0, :], grow, cos)
                mul(pi[:, 0, :], grow, sines[:, 0, :])
                mul(nr, grow_m1, cos)
                add(nr, nr, cos_m1)
                ni = pi[:, 0, :]
                mul(t1, nr, w("A_re"))
                mul(t2, ni, w("A_im"))
                add(gr, t1, t2)
                mul(t1, ni, w("A_re"))
                mul(t2, nr, w("A_im"))
                sub(gi, t1, t2)
                mul(t1, w("A_re"), w("A_re"))
                mul(t2, w("A_im"), w("A_im"))
                add(size, t1, t2)
                step(v.reciprocal(size, size))
                mul(gr, gr, size)
                mul(gi, gi, size)
                mul(t1, gr, w("C_re"))
                mul(t2, gi, w("C_im"))
                sub(qr[:, 0, :], t1, t2)
                mul(t1, gi, w("C_re"))
                mul(t2, gr, w("C_im"))
                add(qi[:, 0, :], t1, t2)
                m = 1
                now = 0
                while m < T:
                    shape = [C, m, N]
                    r, i = spread(pr[:, now, :], 1, shape), spread(pi[:, now, :], 1, shape)
                    a, b = prod1[:, 0:m, :], prod2[:, 0:m, :]
                    mul(a, qr[:, 0:m, :], r)
                    mul(b, qi[:, 0:m, :], i)
                    sub(qr[:, m:2 * m, :], a, b)
                    if 2 * m < T:
                        mul(a, qr[:, 0:m, :], i)
                        mul(b, qi[:, 0:m, :], r)
                        add(qi[:, m:2 * m, :], a, b)
                        mul(t1, pr[:, now, :], pr[:, now, :])
                        mul(t2, pi[:, now, :], pi[:, now, :])
                        sub(pr[:, 1 - now, :], t1, t2)
                        mul(t1, pr[:, now, :], pi[:, now, :])
                        step(v.tensor_scalar(pi[:, 1 - now, :], t1, 2.0, None, ALU.mult))
                        now = 1 - now
                    m *= 2
                step(v.tensor_reduce(kernel[:, :], qr[:, :, :], AX_X, ALU.add))
                v.tensor_scalar(mem.kernel_reversed[:, :], kernel[:, ::-1], 2.0, None, ALU.mult)\
                    .then_inc(*dve_done.mark("kernel"))



def stage_topk_attention(mem):
    nc = mem.nc
    pe_done, act_done, dve_done, pool_done = mem.pe_done, mem.act_done, mem.dve_done, mem.pool_done
    step, ps = mem.dve_step, mem.psum
    ident = mem.w("consts", "ident")
    CHOSEN = -2.0e38
    R = 2
    TPB = CHUNK // T
    BLOCKS = -(-KT_TILES // TPB)
    HALF = C // R
    pe_done.stage("zT", "QT", "pooledT", "contextT", "film", "aT", "mixed",
                  "hT", "hidden", "out")
    dve_done.stage("var", "z", "zT", "mask", "Qbd", "max0", "kept0", "max1", "kept1", "picks", "pooled",
                   "contextT", "a_var", "a", "film_out", "x_mid_var", "h", "hT", "hidden",
                   "out_var", "x")
    act_done.stage("exp0", "exp1", "hidden")
    pool_done.stage("rstd", "a_rstd", "h_rstd", "out_rstd")
    keys_projected, keys_copied = mem.sem("l2x_keys_projected"), mem.sem("l2x_keys_copied")
    scores_ready, scores_copied = mem.sem("l2x_scores_ready"), mem.sem("l2x_scores_copied")
    turned, turned_copied = mem.sem("l2x_turned"), mem.sem("l2x_turned_copied")
    masks_loaded, tiles_loaded = mem.sem("l2x_masks_loaded"), mem.sem("l2x_tiles_loaded")

    def w(name):
        return mem.w("l2x", name)

    def chunk_keys(c):
        return c * CHUNK, min(KEYS, (c + 1) * CHUNK)

    with ExitStack() as local:
        def sb(name, shape, dt=F32):
            return local.enter_context(nc.sbuf_tensor("l2x_" + name, shape, dt))

        S = sb("S", [128, R, KEYS])
        left = mem.values[:, 0:KEYS]
        ctx_tiles = mem.keys_t[:, 0:KT_TILES * CTX]
        mask_bias = sb("mask_bias", [128, KEYS], BF16)
        mask8 = mem.values[:, 0:KEYS // 4].bitcast(U8)
        ones16 = sb("ones16", [128, 128], BF16)
        token8 = sb("token8", [C, T], U8)
        token_mask = sb("token_mask", [C, T])
        zT, QT, Qbd = sb("zT", [C, T]), sb("QT", [C, T]), sb("Qbd", [C, R, T])
        best = sb("best", [128, 4, 8])
        minus_max = sb("minus_max", [128, R])
        total, inverse = sb("total", [128, R]), sb("inverse", [128, R])
        pick = sb("pick", [128, R, T])
        turnedT = sb("turnedT", [128, KT_TILES, T])
        pooledT, contextT = sb("pooledT", [CTX, T]), sb("contextT", [C, T])
        a, aT = sb("a", [T, C]), sb("aT", [C, T])
        film = sb("film", [C, 4, T])
        padded = sb("padded", [C, 2 * T - 1])
        products = mem.values[:, 0:T * T].rearrange("p (t l) -> p t l", l=T)
        mixed = sb("mixed", [C, T])
        x_mid, h, hT = sb("x_mid", [T, C]), sb("h", [T, C]), sb("hT", [C, T])
        pre, hidden = sb("pre", [C, HID // C, T]), sb("hidden", [C, HID // C, T])
        out = sb("out", [T, C])

        with nc.Block(no_gpsimd_drain=True) as block:

            @block.sync
            def _(sp):
                sp.dma_start(mask8, mem.dram["context_mask"].to_broadcast([128, KEYS])).then_inc(masks_loaded, 16)
                sp.dma_start(token8[:, :], mem.dram["token_mask"].to_broadcast([C, T])).then_inc(masks_loaded, 16)
                sp.wait_ge(scores_ready, R * CHUNKS)
                sp.dma_start(ctx_tiles, mem.dram["ctx_tiles"]).then_inc(tiles_loaded, 16)
                sp.wait_ge(tiles_loaded, 16)

            @block.tensor
            def _(pe):
                pe.wait_ge(*dve_done.at("z"))
                pe.wait_ge(mem.loaded["l2x"], 16)
                nc.tensor.transpose(ps[0:C, 0, 0:T], mem.xn[:, :], ident[0:T, 0:T]).then_inc(*pe_done.mark("zT"))
                pe.wait_ge(*dve_done.at("zT"))
                nc.tensor.matmul(ps[0:C, 0, 128:192], w("Wq"), zT[:, :], start=True, stop=True)\
                    .then_inc(*pe_done.mark("QT"))
                for c in range(CHUNKS):
                    lo, hi = chunk_keys(c)
                    if c >= 3:
                        pe.wait_ge(keys_copied, c - 2)
                    nc.tensor.matmul(ps[:, 1 + c % 3, 0:hi - lo], w("Wk"), mem.ctx_t[0:CTX, lo:hi],
                                     start=True, stop=True).then_inc(keys_projected, 1)
                pe.wait_ge(*dve_done.at("Qbd"))
                pe.wait_ge(*dve_done.at("mask"))
                for r in range(R):
                    rows = slice(HALF * r, HALF * r + HALF)
                    for c in range(CHUNKS):
                        lo, hi = chunk_keys(c)
                        n = r * CHUNKS + c
                        if r == 0:
                            pe.wait_ge(keys_copied, c + 1)
                        if n >= 4:
                            pe.wait_ge(scores_copied, n - 3)
                        bank = ps[:, 4 + n % 4, 0:hi - lo]
                        nc.tensor.matmul(bank, Qbd[rows, :, :], mem.keys_t[rows, lo:hi], start=True, stop=False)
                        last = nc.tensor.matmul(bank, ones16[HALF * r:HALF * r + 1, :],
                                                mask_bias[HALF * r:HALF * r + 1, lo:hi], start=False, stop=True)
                        last.then_inc(scores_ready, 1)
                pe.wait_ge(*dve_done.at("picks"))
                for b in range(BLOCKS):
                    if b >= 3:
                        pe.wait_ge(turned_copied, b - 2)
                    for t in range(b * TPB, min(KT_TILES, (b + 1) * TPB)):
                        for r in range(R):
                            last = nc.tensor.matmul(ps[:, 1 + b % 3, (t % TPB) * T:(t % TPB + 1) * T],
                                                    S[:, r, t * 128:(t + 1) * 128], pick[:, r, :],
                                                    start=r == 0, stop=r == R - 1)
                    last.then_inc(turned, 1)
                pe.wait_ge(tiles_loaded, 16)
                for t in range(KT_TILES):
                    if t % TPB == 0:
                        pe.wait_ge(turned_copied, t // TPB + 1)
                    last = nc.tensor.matmul(ps[0:CTX, 7, 0:T], ctx_tiles[:, t * CTX:(t + 1) * CTX],
                                            turnedT[:, t, :], start=t == 0, stop=t == KT_TILES - 1)
                last.then_inc(*pe_done.mark("pooledT"))
                pe.wait_ge(*dve_done.at("pooled"))
                nc.tensor.matmul(ps[0:C, 0, 0:T], w("Wv"), pooledT[:, :], start=True, stop=True)\
                    .then_inc(*pe_done.mark("contextT"))
                pe.wait_ge(*dve_done.at("contextT"))
                for n in range(4):
                    half = slice((n % 2) * C, (n % 2 + 1) * C)
                    last = nc.tensor.matmul(ps[0:C, 4, n * T:(n + 1) * T],
                                            w(["W_film_in", "W_film_out"][n // 2])[:, half], contextT[:, :],
                                            start=True, stop=True)
                last.then_inc(*pe_done.mark("film"))
                pe.wait_ge(*dve_done.at("a"))
                nc.tensor.transpose(ps[0:C, 5, 0:T], a[:, :], ident[0:T, 0:T]).then_inc(*pe_done.mark("aT"))
                pe.wait_ge(*dve_done.at("film_out"))
                nc.tensor.transpose(ps[0:T, 6, 0:C], mixed[:, :], ident).then_inc(*pe_done.mark("mixed"))
                pe.wait_ge(*dve_done.at("h"))
                nc.tensor.transpose(ps[0:C, 0, 0:T], h[:, :], ident[0:T, 0:T]).then_inc(*pe_done.mark("hT"))
                pe.wait_ge(*dve_done.at("hT"))
                for n in range(HID // C):
                    last = nc.tensor.matmul(ps[0:C, 1, n * T:(n + 1) * T], w("W1")[:, n * C:(n + 1) * C],
                                            hT[:, :], start=True, stop=True)
                last.then_inc(*pe_done.mark("hidden"))
                pe.wait_ge(*act_done.at("hidden"))
                for n in range(HID // C):
                    last = nc.tensor.matmul(ps[0:T, 2, 0:C], hidden[:, n, :], w("W2")[:, n * C:(n + 1) * C],
                                            start=n == 0, stop=n == HID // C - 1)
                last.then_inc(*pe_done.mark("out"))

            @block.scalar
            def _(act):
                for c in range(CHUNKS):
                    lo, hi = chunk_keys(c)
                    act.wait_ge(keys_projected, c + 1)
                    nc.scalar.activation(mem.keys_t[:, lo:hi], ps[:, 1 + c % 3, 0:hi - lo], ACT.Identity)\
                        .then_inc(keys_copied, 1)
                for n in range(R * CHUNKS):
                    lo, hi = chunk_keys(n % CHUNKS)
                    act.wait_ge(scores_ready, n + 1)
                    nc.scalar.activation(S[:, n // CHUNKS, lo:hi], ps[:, 4 + n % 4, 0:hi - lo], ACT.Identity)\
                        .then_inc(scores_copied, 1)
                for r in range(R):
                    act.wait_ge(*dve_done.at(f"max{r}"))
                    nc.scalar.activation(S[:, r, :], S[:, r, :], ACT.Exp, bias=minus_max[:, r:r + 1])\
                        .then_inc(*act_done.mark(f"exp{r}"))
                act.wait_ge(*dve_done.at("hidden"))
                nc.scalar.activation(hidden[:, :, :], pre[:, :, :], ACT.Gelu).then_inc(*act_done.mark("hidden"))

            @block.gpsimd
            def _(pool):
                pool_rstd(mem, "var", "rstd")
                pool_rstd(mem, "a_var", "a_rstd")
                pool_rstd(mem, "x_mid_var", "h_rstd")
                pool_rstd(mem, "out_var", "out_rstd")

            @block.vector
            def _(dve):
                v = nc.vector
                dve_moments(mem, mem.x[:, :], "var")
                dve_normalised(mem, mem.xn[:, :], mem.x[:, :], "rstd").then_inc(*dve_done.mark("z"))
                v.memset(ones16[:, :], 1.0)
                v.memset(padded[:, :], 0.0)
                dve.wait_ge(*pe_done.at("zT"))
                v.tensor_copy(zT[:, :], ps[0:C, 0, 0:T]).then_inc(*dve_done.mark("zT"))
                dve.wait_ge(masks_loaded, 32)
                v.tensor_copy(token_mask[:, :], token8[:, :])
                v.tensor_scalar(mask_bias[:, :], mask8, 1.0, 1e30, ALU.subtract, ALU.mult)\
                    .then_inc(*dve_done.mark("mask"))
                dve.wait_ge(*pe_done.at("QT"))
                step(v.tensor_scalar(QT[:, :], ps[0:C, 0, 128:192], D2 ** -0.5, None, ALU.mult))
                v.tensor_tensor(Qbd[:, :, :], spread(QT[:, :], 1, [C, R, T]),
                                spread(mem.w("consts", "two_heads"), 2, [C, R, T]), ALU.mult)\
                    .then_inc(*dve_done.mark("Qbd"))
                dve.wait_ge(*dve_done.at("mask"))
                for r in range(R):
                    dve.wait_ge(scores_copied, (r + 1) * CHUNKS)
                    source = S[:, r, :]
                    for k in range(TOPK // 8):
                        step(v.max(best[:, k, :], source))
                        step(v.match_replace(left, best[:, k, :], source, LOWEST))
                        source = left
                        if k == 0:
                            v.tensor_scalar(minus_max[:, r:r + 1], best[:, 0, 0:1], -1.0, None, ALU.mult)\
                                .then_inc(*dve_done.mark(f"max{r}"))
                    dve.wait_ge(*act_done.at(f"exp{r}"))
                    v.scalar_tensor_tensor(out=S[:, r, :], in0=left, scalar=CHOSEN, in1=S[:, r, :],
                                           op0=ALU.is_le, op1=ALU.mult, accum_out=total[:, r:r + 1])\
                        .then_inc(*dve_done.mark(f"kept{r}"))
                    dve.wait_ge(*dve_done.at(f"kept{r}"))
                step(v.reciprocal(inverse[:, :], total[:, :]))
                for r in range(R):
                    ins = v.tensor_scalar(pick[:, r, :], mem.w("consts", "mean_heads"), inverse[:, r:r + 1],
                                          None, ALU.mult)
                ins.then_inc(*dve_done.mark("picks"))
                for b in range(BLOCKS):
                    lo, hi = b * TPB, min(KT_TILES, (b + 1) * TPB)
                    dve.wait_ge(turned, b + 1)
                    v.tensor_copy(turnedT[:, lo:hi, :],
                                  ps[:, 1 + b % 3, 0:(hi - lo) * T].rearrange("p (n t) -> p n t", t=T))\
                        .then_inc(turned_copied, 1)
                dve.wait_ge(*pe_done.at("pooledT"))
                v.tensor_copy(pooledT[:, :], ps[0:CTX, 7, 0:T]).then_inc(*dve_done.mark("pooled"))
                dve.wait_ge(*pe_done.at("contextT"))
                v.tensor_tensor(contextT[:, :], ps[0:C, 0, 0:T], token_mask[:, :], ALU.mult)\
                    .then_inc(*dve_done.mark("contextT"))
                dve_moments(mem, mem.xn[:, :], "a_var")
                dve_normalised(mem, a[:, :], mem.xn[:, :], "a_rstd").then_inc(*dve_done.mark("a"))
                gate, (at_in, _, _), (at_out, _, _) = w("mod_gate"), column("l2x", "b_film_in"), column("l2x", "b_film_out")
                dve.wait_ge(*pe_done.at("film"))
                for n in range(4):
                    at = (at_in, at_out)[n // 2] + n % 2
                    ins = v.tensor_scalar(film[:, n, :], ps[0:C, 4, n * T:(n + 1) * T],
                                          mem.packs["l2x"][:, at:at + 1], gate, ALU.add, ALU.mult)
                step(ins)
                dve.wait_ge(*pe_done.at("aT"))
                step(v.tensor_scalar(aT[:, :], ps[0:C, 5, 0:T], w("g_norm_in"), w("b_norm_in"), ALU.mult, ALU.add))
                step(v.scalar_tensor_tensor(out=aT[:, :], in0=film[:, 0, :], scalar=1.0, in1=aT[:, :],
                                            op0=ALU.add, op1=ALU.mult))
                recent = padded[:, T - 1:2 * T - 1]
                step(v.tensor_tensor(recent, aT[:, :], film[:, 1, :], ALU.add))
                window = padded[:, :]
                window = bass.AP(window.tensor, window.offset, [list(window.ap[0]), [1, T], [1, T]])
                step(v.tensor_tensor(products, window, spread(mem.kernel_reversed[:, :], 1, [C, T, T]),
                                     ALU.mult))
                step(v.tensor_reduce(mixed[:, :], products, AX_X, ALU.add))
                step(v.scalar_tensor_tensor(out=mixed[:, :], in0=recent, scalar=w("D_skip"), in1=mixed[:, :],
                                            op0=ALU.mult, op1=ALU.add))
                step(v.scalar_tensor_tensor(out=mixed[:, :], in0=film[:, 2, :], scalar=1.0, in1=mixed[:, :],
                                            op0=ALU.add, op1=ALU.mult))
                v.tensor_tensor(mixed[:, :], mixed[:, :], film[:, 3, :], ALU.add)\
                    .then_inc(*dve_done.mark("film_out"))
                dve.wait_ge(*pe_done.at("mixed"))
                step(v.tensor_tensor(x_mid[:, :], ps[0:T, 6, 0:C], mem.xn[:, :], ALU.add))
                dve_moments(mem, x_mid[:, :], "x_mid_var")
                dve_normalised(mem, h[:, :], x_mid[:, :], "h_rstd").then_inc(*dve_done.mark("h"))
                step(v.tensor_tensor(x_mid[:, :], x_mid[:, :], mem.row("l2x_b2"), ALU.add))
                dve.wait_ge(*pe_done.at("hT"))
                v.tensor_scalar(hT[:, :], ps[0:C, 0, 0:T], w("g_ffn"), w("b_ffn"), ALU.mult, ALU.add)\
                    .then_inc(*dve_done.mark("hT"))
                dve.wait_ge(*pe_done.at("hidden"))
                v.tensor_tensor(pre[:, :, :], ps[0:C, 1, 0:4 * T].rearrange("p (n t) -> p n t", t=T),
                                spread(w("b1"), 2, [C, 4, T]), ALU.add).then_inc(*dve_done.mark("hidden"))
                dve.wait_ge(*pe_done.at("out"))
                step(v.tensor_tensor(out[:, :], ps[0:T, 2, 0:C], x_mid[:, :], ALU.add))
                dve_moments(mem, out[:, :], "out_var")
                step(dve_normalised(mem, out[:, :], out[:, :], "out_rstd"))
                step(v.tensor_tensor(out[:, :], out[:, :], mem.row("l2x_g_out"), ALU.mult))
                step(v.tensor_tensor(out[:, :], out[:, :], mem.row("l2x_b_out"), ALU.add))
                v.tensor_tensor(mem.x[:, :], mem.x[:, :], out[:, :], ALU.add).then_inc(*dve_done.mark("x"))



def stage_store(mem):
    nc = mem.nc
    stored = mem.sem("stored")
    with nc.Block() as block:

        @block.sync
        def _(sp):
            sp.dma_start(mem.dram["out"], mem.x[:, :]).then_inc(stored, 16)
            sp.wait_ge(stored, 16)
            for pack in SMALL:
                sp.wait_ge(mem.loaded[pack], 16)


def build(nc, dram):
    with ExitStack() as ctx:
        mem = Memory(nc, ctx, dram)
        with nc.sbuf_tensor("experts0", [128, width("experts0")], F32) as mem.experts:
            stage_load(mem)
            for stage in FIRST:
                stage(mem)
        for stage in MIDDLE:
            if stage is stage_topk_attention:
                stage_state_kernel(mem)
            stage(mem)
        if SECOND_EXPERTS or LAST:
            with nc.sbuf_tensor("experts3", [128, width("experts3")], F32) as mem.experts:
                with nc.sbuf_tensor("experts2", [128, width("experts2")], F32) as mem.packs["experts2"]:
                    stage_load_late(mem)
                    for stage in SECOND_EXPERTS:
                        stage(mem)
                for stage in LAST:
                    stage(mem)
        stage_store(mem)


FIRST = [lambda m: stage_cross_attention(m, 0), stage_rwkv, lambda m: stage_topk_experts(m, 0)]
MIDDLE = [lambda m: stage_cross_attention(m, 1), stage_rope_attention, stage_quantised_ffn,
          stage_topk_attention]
SECOND_EXPERTS = [stage_local_attention, stage_transformer_experts]
LAST = [lambda m: stage_cross_attention(m, 3), stage_past_attention, lambda m: stage_topk_experts(m, 3)]



def shape_constants():
    p = np.arange(128)
    t = np.arange(T)
    key = np.arange(T)
    half = DH // 2
    inv_freq = (1.0 / 10000.0 ** (np.arange(half, dtype=np.float32) / half)).astype(np.float32)
    angle = t.astype(np.float32)[:, None] * inv_freq[None, :]
    cos, sin = np.cos(angle).astype(np.float32), np.sin(angle).astype(np.float32)
    query = p % T
    strict = (key[None, :] < t[:, None]) | ((t[:, None] == 0) & (key[None, :] == 0))

    def masked(keep):
        return np.where(keep, 0.0, -1e30).astype(np.float32)

    return {
        "ident": np.eye(128, dtype=np.float32),
        "four_heads": (p[:, None] // DH % HG == np.arange(HG)[None, :]).astype(np.float32),
        "two_heads": (p[:, None] // D2 % 2 == np.arange(2)[None, :]).astype(np.float32),
        "even_out": np.tile(p[None, :] % 2 == 0, (128, 1)).astype(np.float32),
        "odd_out": np.tile(p[None, :] % 2 == 1, (128, 1)).astype(np.float32),
        "causal": masked(key[None, :] <= query[:, None]),
        "band": masked(np.abs(key[None, :] - query[:, None]) <= 3),
        "strict": masked(strict),
        "cos": np.concatenate([cos, cos], axis=1),
        "sin": np.concatenate([-sin, sin], axis=1),
        "mean_heads": (np.float32(1.0 / H2) * (query[:, None] == t[None, :])).astype(np.float32),
    }


def layouts(a):
    def col(v):
        return v.reshape(-1, 1)

    def cols(v):
        return v.reshape(-1, C).T

    def fill(v):
        return np.broadcast_to(v.reshape(1, 1), (C, 1))

    def with_bias(w, b):
        return np.concatenate([w, b.reshape(1, -1)], axis=0)

    def rows_of(w):
        return w.reshape(-1, C, w.shape[-1]).transpose(1, 0, 2).reshape(C, -1)

    def whole_rows(w):
        n = -(-w.shape[0] // C)
        out = np.zeros((n * C, w.shape[1]), w.dtype)
        out[:w.shape[0]] = w
        return rows_of(out)

    def first(w):
        return w.transpose(1, 0, 2).reshape(C, -1)

    def second(w):
        return rows_of(w.reshape(-1, C))

    def get(prefix, **names):
        return {k: a[prefix + v] for k, v in names.items()}

    p0, p1, p2, p3 = "L0_attn_", "L1_ffn_", "L2_xattn_", "L3_ffn_"
    kv_w, kv_b = a["L3_xattn_Wkv"].reshape(H, 2, DH, CTX), a["L3_xattn_bkv"].reshape(H, 2, DH)
    shared = {n: np.concatenate([a[p3 + n], a[p3 + n + "_s"][None]], axis=0)
              for n in ["Wfc", "bfc", "Wproj", "bproj"]}
    packs = {
        "consts": shape_constants(),
        "l0x": {"Wq": a["L0_xattn_Wq"], "Wk": with_bias(a["L0_xattn_Wk"], a["L0_xattn_bk"]),
                "Wv": with_bias(a["L0_xattn_Wv"], a["L0_xattn_bv"]), "Wo": a["L0_xattn_Wo"]},
        "l0a": {"Wcv": rows_of(a[p0 + "Wcv"])}
        | {n: a[p0 + n] for n in ["Wk", "Wv", "Wr", "Wo", "Wck", "Wcr"]}
        | {n: col(a[p0 + n]) for n in ["ln0_g", "ln0_b", "ln1_g", "ln1_b", "time_decay", "time_first",
                                       "tm_k", "tm_v", "tm_r", "cm_k", "cm_r"]},
        "l0f": {"w_router": a["L0_ffn_w_router"], "b1": cols(a["L0_ffn_b1"]), "b2": a["L0_ffn_b2"]},
        "l1x": {"Wq": a["L1_xattn_Wq"].T, "Wk": with_bias(a["L1_xattn_Wk"].T, a["L1_xattn_bk"]),
                "Wv": with_bias(a["L1_xattn_Wv"].T, a["L1_xattn_bv"]), "Wo": a["L1_xattn_Wo"].T,
                "bq": col(a["L1_xattn_bq"])},
        "l1a": {"w_qkv": a["L1_attn_w_qkv"], "w_o": a["L1_attn_w_o"]},
        "l1f": {"w_gate": whole_rows(a[p1 + "w_gate"]), "w_up": whole_rows(a[p1 + "w_up"]),
                "w_down": a[p1 + "w_down"], "clip_x": fill(a[p1 + "clip_x"]),
                "clip_down": fill(a[p1 + "clip_down"])},
        "l2x": {n: a[p2 + n] for n in ["Wq", "Wk", "Wv", "W_film_in", "W_film_out", "W1", "A_re", "A_im",
                                       "C_re", "C_im"]}
        | {n: col(a[p2 + n]) for n in ["g_norm_in", "b_norm_in", "g_ffn", "b_ffn", "D_skip", "log_dt"]}
        | {n: cols(a[p2 + n]) for n in ["b_film_in", "b_film_out", "b1"]}
        | {"W2": rows_of(a[p2 + "W2"]), "mod_gate": fill(a[p2 + "mod_gate"])},
        "l2a": {n: a["L2_attn_" + n] for n in ["w_q", "w_k", "w_v", "w_o"]}
        | {n: col(a["L2_attn_" + n]) for n in ["b_q", "b_k"]},
        "l2f": {"w_in": a["L2_ffn_in_proj_w"].T, "w_out": a["L2_ffn_out_proj_w"].T,
                "w_group": a["L2_ffn_w_group"],
                "w_expert": a["L2_ffn_w_expert"].transpose(1, 0, 2).reshape(C, E),
                "b1": cols(a["L2_ffn_b1"]), "b2": a["L2_ffn_b2"]},
        "l3x": {"Wq": a["L3_xattn_Wq"].T, "Wo": a["L3_xattn_Wo"].T, "bq": col(a["L3_xattn_bq"]),
                "Wk": with_bias(kv_w[:, 0].reshape(C, CTX).T, kv_b[:, 0].reshape(C)),
                "Wv": with_bias(kv_w[:, 1].reshape(C, CTX).T, kv_b[:, 1].reshape(C))},
        "l3a": {"w_dec": a["L3_attn_w_dec_attn"], "w_out": rows_of(a["L3_attn_w_out"].T)},
        "l3f": {"w_router": a[p3 + "Wr"], "b1": cols(shared["bfc"]), "b2": shared["bproj"]},
        "experts0": {"w1": first(a["L0_ffn_w1"]), "w2": second(a["L0_ffn_w2"])},
        "experts2": {"w1": first(a["L2_ffn_w1"]), "w2": second(a["L2_ffn_w2"])},
        "experts3": {"w1": first(shared["Wfc"]), "w2": second(shared["Wproj"])},
        "rows": {n: v.reshape(1, -1) for n, v in {
            "l0x_bq": a["L0_xattn_bq"], "l0x_bo": a["L0_xattn_bo"], "l0x_gamma": a["L0_xattn_ln_gamma"],
            "l0x_beta": a["L0_xattn_ln_beta"], "l1x_bo": a["L1_xattn_bo"],
            "l2x_g_out": a[p2 + "g_norm_out"], "l2x_b_out": a[p2 + "b_norm_out"], "l2x_b2": a[p2 + "b2"],
            "l2a_bv": a["L2_attn_b_v"], "l2a_bo": a["L2_attn_b_o"], "l2f_b_in": a["L2_ffn_in_proj_b"],
            "l2f_b_out": a["L2_ffn_out_proj_b"], "l2f_g1": a["L2_ffn_ln1_g"], "l2f_b1": a["L2_ffn_ln1_b"],
            "l2f_g2": a["L2_ffn_ln2_g"], "l2f_b2": a["L2_ffn_ln2_b"], "l2f_b_group": a["L2_ffn_b_group"],
            "l2f_b_expert": a["L2_ffn_b_expert"], "l3x_bo": a["L3_xattn_bo"],
            "l3a_bo": a["L3_attn_b_out"]}.items()},
    }
    out = {}
    for pack, parts in packs.items():
        height = 1 if pack == "rows" else 128
        out[pack] = np.zeros((height, width(pack)), np.float32)
        for name, array in parts.items():
            at, rows, n = column(pack, name)
            assert array.shape == (rows, n), (pack, name, array.shape)
            out[pack][0:rows, at:at + n] = array
        assert len(parts) == len(PACKS[pack]), pack
    context = a["ctx_768"][0]
    out["ctx_t"] = np.concatenate([context.T, np.ones((1, KEYS), np.float32)], axis=0)
    out["ctx_tiles"] = context.reshape(KT_TILES, 128, CTX).transpose(1, 0, 2).reshape(128, KT_TILES * CTX)
    out["token_mask"] = a["mask_BxS_bf1"].view(np.uint8).reshape(1, T)
    out["context_mask"] = a["mask_BxS2_bf1"].view(np.uint8).reshape(1, KEYS)
    out["x"] = a["x"][0]
    return {k: np.ascontiguousarray(v) for k, v in out.items()}


def kernel(**inputs):
    import concourse.bacc as bacc
    from concourse.bass_utils import run_bass_kernel_spmd

    nc = bacc.Bacc("TRN2", target_bir_lowering=False, num_devices=1)
    arrays = layouts({k: np.asarray(v) for k, v in inputs.items()})
    dram = {name: nc.dram_tensor(f"in_{name}", array.shape, mybir.dt.from_np(array.dtype),
                                 kind="ExternalInput").ap() for name, array in arrays.items()}
    dram["out"] = nc.dram_tensor("out_x", (T, C), F32, kind="ExternalOutput").ap()
    build(nc, dram)
    result = run_bass_kernel_spmd(nc, [{f"in_{k}": v for k, v in arrays.items()}], core_ids=[0])
    return result.results[0]["out_x"].reshape(1, T, C)
```

```python
from contextlib import ExitStack

import concourse.bass as bass
from concourse import mybir
import numpy as np

F32 = mybir.dt.float32
BF16 = mybir.dt.bfloat16
F16 = mybir.dt.float16
I32 = mybir.dt.int32
U8 = mybir.dt.uint8
ACT = mybir.ActivationFunctionType
ALU = mybir.AluOpType
AX_X = mybir.AxisListType.X

T = 64
C = 128
H = 16
DH = C // H
G = 4
HG = H // G
KEYS = 6272
CTX = 96
KT_TILES = KEYS // 128
CHUNK = 512
CHUNKS = -(-KEYS // CHUNK)
SUPER = 896
SUPERS = KEYS // SUPER
TPS = SUPER // 128
HALF = SUPER // 2
E = 8
HID = 512
HID2 = 256
FFQ = 352
FFQ_CHUNKS = [(0, 128), (128, 128), (256, 96)]
H2, D2, TOPK = 4, 32, 32
NSTATE = 64
LN_EPS = 1e-5
SCALE = DH ** -0.5
LOWEST = -3.0e38
CTX_FIRST = 2
BIAS_ROW = 4096.0
EXPONENT_BITS, MAGNITUDE_BITS = 0x7F800000, 0x7FFFFFFF
ROUND = 12582912.0
LOG2E = 1.4426950408889634
LN2_HI, LN2_LO = 0.693145751953125, 1.4286068203094172e-06
TWO_PI_HI, TWO_PI_MID, TWO_PI_LO = 6.28125, 0.0019350051879882812, 3.0199157663e-07

PACKS = {
    "consts": [("ident", 128, 128), ("four_heads", 128, HG), ("two_heads", 128, 2),
               ("even_out", 128, 128), ("odd_out", 128, 128), ("causal", 128, T), ("band", 128, T),
               ("strict", T, T), ("cos", T, DH), ("sin", T, DH), ("mean_heads", 128, T)],
    "l0x": [("Wq", C, C), ("Wk", CTX + 1, C), ("Wv", CTX + 1, C), ("Wo", C, C)],
    "l0a": [("Wk", C, C), ("Wv", C, C), ("Wr", C, C), ("Wo", C, C), ("Wck", C, HID),
            ("Wcv", C, HID), ("Wcr", C, C), ("ln0_g", C, 1), ("ln0_b", C, 1), ("ln1_g", C, 1),
            ("ln1_b", C, 1), ("time_decay", C, 1), ("time_first", C, 1), ("tm_k", C, 1),
            ("tm_v", C, 1), ("tm_r", C, 1), ("cm_k", C, 1), ("cm_r", C, 1)],
    "l0f": [("w_router", C, E), ("b1", C, E * HID // C), ("b2", E, C)],
    "l1x": [("Wq", C, C), ("Wk", CTX + 1, C), ("Wv", CTX + 1, C), ("Wo", C, C), ("bq", C, 1)],
    "l1a": [("w_qkv", C, 192), ("w_o", C, C)],
    "l1f": [("w_gate", C, 3 * C), ("w_up", C, 3 * C), ("w_down", C, FFQ), ("clip_x", C, 1),
            ("clip_down", C, 1)],
    "l2x": [("Wq", C, C), ("Wk", CTX, C), ("Wv", CTX, C), ("W_film_in", C, 2 * C),
            ("W_film_out", C, 2 * C), ("W1", C, HID), ("W2", C, HID), ("b_film_in", C, 2),
            ("b_film_out", C, 2), ("g_norm_in", C, 1), ("b_norm_in", C, 1), ("g_ffn", C, 1),
            ("b_ffn", C, 1), ("b1", C, HID // C), ("D_skip", C, 1), ("log_dt", C, 1),
            ("mod_gate", C, 1), ("A_re", C, NSTATE), ("A_im", C, NSTATE), ("C_re", C, NSTATE),
            ("C_im", C, NSTATE)],
    "l2a": [("w_q", C, C), ("w_k", C, C), ("w_v", C, C), ("w_o", C, C), ("b_q", C, 1), ("b_k", C, 1)],
    "l2f": [("w_in", C, 3 * C), ("w_out", C, C), ("w_group", C, 4), ("w_expert", C, E),
            ("b1", C, E * HID2 // C), ("b2", E, C)],
    "l3x": [("Wq", C, C), ("Wk", CTX + 1, C), ("Wv", CTX + 1, C), ("Wo", C, C), ("bq", C, 1)],
    "l3a": [("w_dec", C, C), ("w_out", C, 2 * C)],
    "l3f": [("w_router", C, E), ("b1", C, (E + 1) * HID // C), ("b2", E + 1, C)],
    "experts0": [("w1", C, E * HID), ("w2", C, E * HID)],
    "experts2": [("w1", C, E * HID2), ("w2", C, E * HID2)],
    "experts3": [("w1", C, (E + 1) * HID), ("w2", C, (E + 1) * HID)],
    "rows": [(n, 1, w) for n, w in [
        ("l0x_bq", C), ("l0x_bo", C), ("l0x_gamma", C), ("l0x_beta", C), ("l1x_bo", C),
        ("l2x_g_out", C), ("l2x_b_out", C), ("l2x_b2", C), ("l2a_bv", C), ("l2a_bo", C),
        ("l2f_b_in", 3 * C), ("l2f_b_out", C), ("l2f_g1", C), ("l2f_b1", C), ("l2f_g2", C),
        ("l2f_b2", C), ("l2f_b_group", 4), ("l2f_b_expert", E), ("l3x_bo", C), ("l3a_bo", C)]],
}
SMALL = ["consts", "l0x", "l0a", "l0f", "l1x", "l1a", "l1f", "l2x", "l2a", "l2f", "l3x", "l3a", "l3f"]


def width(pack):
    return sum(cols for _, _, cols in PACKS[pack])


def column(pack, name):
    at = 0
    for n, rows, cols in PACKS[pack]:
        if n == name:
            return at, rows, cols
        at += cols
    raise KeyError(name)


class Events:

    def __init__(self, sem):
        self.sem, self.base, self.order, self.sent = sem, 0, [], 0

    def stage(self, *names):
        assert self.sent == len(self.order), self.order[self.sent:]
        self.base += len(self.order)
        self.order, self.sent = list(names), 0

    def mark(self, name):
        assert self.order[self.sent] == name, (self.order[self.sent], name)
        self.sent += 1
        return self.sem, 1

    def at(self, name):
        return self.sem, self.base + self.order.index(name) + 1


class Chain:

    def __init__(self, engine, sem):
        self.engine, self.sem, self.n = engine, sem, 0

    def __call__(self, ins):
        self.n += 1
        ins.then_inc(self.sem, 1)
        self.engine.wait_ge(self.sem, self.n)


def spread(ap, axis, shape):
    return ap.unsqueeze(axis).to_broadcast(shape)


class Memory:

    def __init__(self, nc, ctx, dram):
        self.nc, self.ctx, self.dram = nc, ctx, dram

        def sb(name, shape, dt=F32):
            return ctx.enter_context(nc.sbuf_tensor(name, shape, dt))

        self.sem = lambda name: ctx.enter_context(nc.semaphore(name))
        self.psum = ctx.enter_context(nc.psum_tensor("psum", [128, 8, 512], F32))
        self.x = sb("x", [T, C])
        self.wide = sb("wide", [128, 2 * KEYS])
        self.ctx_t = self.wide[0:CTX + 1, KEYS:2 * KEYS]
        self.keys_t = sb("keys_t", [128, KEYS])
        self.values = sb("values", [128, KT_TILES * C])
        self.experts = sb("experts", [128, width("experts3")])
        self.ctx_top = sb("ctx_top", [CTX + 1, SUPERS + 1])
        self.rows = sb("rows", [T, width("rows")])
        self.packs = {p: sb("w_" + p, [128, width(p)]) for p in SMALL}
        self.minus_half = sb("minus_half", [128, KT_TILES])
        self.ones = sb("ones", [128, 128])
        self.kernel_reversed = sb("kernel_reversed", [C, T])
        self.xn = sb("xn", [T, C])
        self.stats = sb("stats", [T, 6])
        self.moments = sb("moments", [T, 2])
        self.rstd = sb("rstd", [T, 2])
        self.loaded = {p: self.sem("loaded_" + p) for p in
                       SMALL + ["x", "ctx_first", "ctx_rest", "rows", "experts0", "experts2", "experts3"]}
        self.pe_done = Events(self.sem("pe_done"))
        self.act_done = Events(self.sem("act_done"))
        self.dve_done = Events(self.sem("dve_done"))
        self.pool_done = Events(self.sem("pool_done"))
        self.dve_step = Chain(nc.vector, self.sem("dve_order"))
        self.act_step = Chain(nc.scalar, self.sem("act_order"))
        self.pool_step = Chain(nc.gpsimd, self.sem("pool_order"))

    def w(self, pack, name):
        at, rows, cols = column(pack, name)
        return self.packs[pack][0:rows, at:at + cols]

    def row(self, name):
        at, _, cols = column("rows", name)
        return self.rows[:, at:at + cols]



def pool_power(mem, out, base, exponent, when, event):
    nc = mem.nc
    nc.gpsimd.wait_ge(*when)
    nc.gpsimd.tensor_tensor(out, base, exponent, ALU.pow).then_inc(*mem.pool_done.mark(event))


def dve_moments(mem, source, event, slot=0):
    nc, step = mem.nc, mem.dve_step
    step(nc.vector.bn_stats(mem.stats[:, :], source))
    step(nc.vector.bn_aggr(mem.moments[:, :], mem.stats[:, :]))
    nc.vector.tensor_scalar(mem.rstd[:, 0:1], mem.moments[:, 1:2], LN_EPS, None, ALU.add)\
        .then_inc(*mem.dve_done.mark(event))


def pool_rstd(mem, when, event):
    pool_power(mem, mem.rstd[:, 1:2], mem.rstd[:, 0:1], mem.minus_half[0:T, 0:1],
               mem.dve_done.at(when), event)


def dve_normalised(mem, out, source, when):
    mem.nc.vector.wait_ge(*mem.pool_done.at(when))
    return mem.nc.vector.tensor_scalar(out, source, mem.moments[:, 0:1], mem.rstd[:, 1:2],
                                       ALU.subtract, ALU.mult)



def load_context(mem, sp):
    for name, lo, hi in [("ctx_first", 0, CTX_FIRST * SUPER), ("ctx_rest", CTX_FIRST * SUPER, KEYS)]:
        sp.dma_start(mem.ctx_t[:, lo:hi], mem.dram["ctx_t"][:, lo:hi]).then_inc(mem.loaded[name], 16)


def stage_load(mem):
    nc, dram = mem.nc, mem.dram
    constants_set = mem.sem("constants_set")

    def load_pack(engine, pack, target):
        engine.dma_start(target[:, :], dram[pack]).then_inc(mem.loaded[pack], 16)

    with nc.Block(no_gpsimd_drain=True) as block:

        @block.sync
        def _(sp):
            sp.dma_start(mem.x[:, :], dram["x"]).then_inc(mem.loaded["x"], 16)
            load_pack(sp, "l0x", mem.packs["l0x"])
            load_pack(sp, "consts", mem.packs["consts"])
            load_context(mem, sp)
            sp.dma_start(mem.rows[:, :], dram["rows"].to_broadcast([T, width("rows")]))\
                .then_inc(mem.loaded["rows"], 16)
            for pack in ["l0a", "l0f"]:
                load_pack(sp, pack, mem.packs[pack])
            sp.dma_start(mem.experts[:, 0:width("experts0")], dram["experts0"])\
                .then_inc(mem.loaded["experts0"], 16)
            for pack in ["l1x", "l1a", "l1f", "l2x", "l2a", "l2f"]:
                load_pack(sp, pack, mem.packs[pack])
            for pack in ["l3x", "l3a", "l3f"]:
                load_pack(sp, pack, mem.packs[pack])

        @block.vector
        def _(dve):
            nc.vector.memset(mem.ones[:, :], 1.0).then_inc(constants_set, 1)
            nc.vector.memset(mem.minus_half[:, :], -0.5).then_inc(constants_set, 1)
            dve.wait_ge(constants_set, 2)



def stage_cross_attention(mem, level, context_load):
    nc = mem.nc
    pe_done, act_done, dve_done, pool_done = mem.pe_done, mem.act_done, mem.dve_done, mem.pool_done
    step = mem.dve_step
    pack = f"l{level}x"
    unit = level == 0
    ps = mem.psum
    ident = mem.w("consts", "ident")
    four_heads = mem.w("consts", "four_heads")
    O_BANK, DEN_BANK, Y_BANK = 6, 7, 0
    RING = 3
    PROBS = 4
    HALVES = 2 * SUPERS
    STACK = 96 if unit else 98
    BATCHES = [(0, 2), (2, 4), (4, 6), (6, 7)]
    PER_BATCH = 12 if unit else 13
    EARLY = [("K", 0), ("K", 1), ("V", 0), ("K", 2), ("V", 1)]
    LATER = [("K", 3)] + [p for u in range(2, SUPERS) for p in [("K", 2 * u), ("V", u), ("K", 2 * u + 1)]]

    act_done.stage()
    if unit:
        pe_done.stage("xnT", "Qp", "QT", "key_bound", "q_topT", "q_top_all", "den", "projected")
        dve_done.stage("keys_abs", "var", "xn", "xnT", "q_sum", "Qn", "ctx_top", "key_gain", "q_top", "q_top1",
                       "Q_stack", "key_sums", "key_scale", "OT", "out_var", "x")
        pool_done.stage("rstd", "q_rsqrt", "key_rsqrt", "out_rstd")
    else:
        pe_done.stage("xnT", "key_bound", "QT", "q_topT", "q_top_all", "max_cols", "den", "projected")
        dve_done.stage("keys_abs", "var", "xn", "xnT", "key_gain", "q_top", "q_top1", "Q_stack",
                       "max_parts", "max_cols", "OT", "x")
        pool_done.stage("rstd")

    def sem(name):
        return mem.sem(f"{pack}_{name}")

    keys_projected, high_ready, low_ready = sem("keys_projected"), sem("high_ready"), sem("low_ready")
    stacked = [sem(f"stacked{b}") for b in range(len(BATCHES))]
    values_projected, values_copied = sem("values_projected"), sem("values_copied")
    scores_ready, probs_ready = sem("scores_ready"), sem("probs_ready")
    pv_done, sum_done = sem("pv_done"), sem("sum_done")
    if unit:
        squares_ready, norms_ready = sem("squares_ready"), sem("norms_ready")
    else:
        max_scores, max_taken = sem("max_scores"), sem("max_taken")

    def stacked_with(u):
        return stacked[next(b for b, (lo, hi) in enumerate(BATCHES) if lo <= u < hi)], 16 * PER_BATCH

    stack = mem.wide[:, :].bitcast(F16).rearrange("p (u g k) -> p u g k", u=SUPERS, g=G)
    parts_of_keys = mem.keys_t[:, :].bitcast(F16).rearrange("p (u n k) -> p u n k", u=SUPERS, n=2)
    probs = mem.keys_t[:, 0:PROBS * H * T].rearrange("p (b n) -> p b n", b=PROBS)
    prob_sum = mem.keys_t[:, PROBS * H * T:(PROBS + 1) * H * T]

    with ExitStack() as local:
        def sb(name, shape, dt=F32):
            return local.enter_context(nc.sbuf_tensor(f"{pack}_{name}", shape, dt))

        keys_abs = sb("keys_abs", [CTX + 1, C])
        key_gain, query_gain = sb("key_gain", [C, 1]), sb("query_gain", [C, 1])
        exp_gain, gain = sb("exp_gain", [C, 1]), sb("gain", [C, 1])
        power, inverse = sb("power", [C, 1]), sb("inverse", [C, 1])
        q_top, q_top1 = sb("q_top", [C, 1]), sb("q_top1", [1, 1])
        xnT = sb("xnT", [C, T])
        QT = sb("QT", [C, T])
        Qbd = sb("Qbd", [C, HG, T])
        Q_high, Q_low = sb("Q_high", [C, HG * T], F16), sb("Q_low", [C, HG * T], F16)
        Q_stack = sb("Q_stack", [C, G, HG * T], F16)
        rden = sb("rden", [C, HG, T])
        weighted = sb("weighted", [C, HG, T])
        OT = sb("OT", [C, T])
        residual = sb("residual", [T, C])
        if unit:
            Qp, Qn, sq = sb("Qp", [T, C]), sb("Qn", [T, C]), sb("sq", [T, C])
            q_sum, q_rsqrt = sb("q_sum", [T, 1]), sb("q_rsqrt", [T, 1])
            squares = sb("squares", [128, 2, SUPER])
            key_sums, key_scale = sb("key_sums", [128, KT_TILES]), sb("key_scale", [128, KT_TILES])
            z, zn = sb("z", [T, C]), sb("zn", [T, C])
        else:
            maxima = sb("maxima", [128, 2, G, HALVES])
            row_max = sb("row_max", [128, G * 2])
            high16 = sb("high16", [128, G * 2], F16)
            parts = sb("parts", [128, 2, G * 2])
            diag = sb("diag", [128, 2, G * 2, 128], F16)
            picks = sb("picks", [128, 2, 128], F16)

        with nc.Block(no_gpsimd_drain=True) as block:

            @block.sync
            def _(sp):
                for b, (lo, hi) in enumerate(BATCHES):
                    sp.wait_ge(high_ready, 2 * hi)
                    sp.wait_ge(low_ready, 2 * hi)
                    under = max(0, 2 * hi - SUPERS)
                    sp.wait_ge(keys_projected, 2 * max(under, hi))
                    if under:
                        sp.wait_ge(values_projected, under)
                    for g in range(G):
                        for block_row, part in enumerate([0, 1, 0]):
                            sp.dma_start(stack[32 * block_row:32 * block_row + 32, lo:hi, g, :],
                                         parts_of_keys[32 * g:32 * g + 32, lo:hi, part, :]).then_inc(stacked[b], 16)
                    if not unit:
                        sp.dma_start(stack[96:98, lo:hi, :, :], mem.dram["bias_rows"][:, lo:hi, :, :])\
                            .then_inc(stacked[b], 16)

            @block.tensor
            def _(pe):
                def project(kind, n):
                    if kind == "K":
                        if n >= 3:
                            pe.wait_ge(low_ready, n - 2)
                        nc.tensor.matmul(ps[:, 1 + n % 3, 0:HALF], mem.w(pack, "Wk"),
                                         mem.ctx_t[:, n * HALF:(n + 1) * HALF], start=True, stop=True)\
                            .then_inc(keys_projected, 1)
                        return
                    if n >= 2:
                        pe.wait_ge(values_copied, n - 1)
                    for j in range(TPS):
                        key = n * SUPER + j * 128
                        last = nc.tensor.matmul(ps[:, 4 + 2 * (n % 2) + j // 4, (j % 4) * C:(j % 4 + 1) * C],
                                                mem.ctx_t[:, key:key + 128], mem.w(pack, "Wv"),
                                                start=True, stop=True)
                    last.then_inc(values_projected, 1)

                def sum_squares(u):
                    pe.wait_ge(squares_ready, 2 * u + 2)
                    for j in range(TPS):
                        t = u * TPS + j
                        last = nc.tensor.matmul(ps[:, 0, 384 + t:385 + t], squares[:, u % 2, j * 128:(j + 1) * 128],
                                                mem.ones[:, 0:1], start=True, stop=True)
                    last.then_inc(norms_ready, 1)

                pe.wait_ge(mem.loaded["ctx_first"], 16 * context_load)
                pe.wait_ge(mem.loaded[pack], 16)
                for kind, n in EARLY:
                    project(kind, n)
                pe.wait_ge(*dve_done.at("xn"))
                pe.wait_ge(mem.loaded["consts"], 16)
                nc.tensor.transpose(ps[0:C, 0, 0:T], mem.xn[:, :], ident[0:T, 0:T])\
                    .then_inc(*pe_done.mark("xnT"))
                pe.wait_ge(*dve_done.at("xnT"))

                def bound_keys():
                    pe.wait_ge(*dve_done.at("keys_abs"))
                    nc.tensor.matmul(ps[:, 0, 320:321], keys_abs[:, :], mem.ctx_top[:, SUPERS:SUPERS + 1],
                                     start=True, stop=True).then_inc(*pe_done.mark("key_bound"))

                if unit:
                    nc.tensor.matmul(ps[0:T, 0, 128:256], xnT[:, :], mem.w(pack, "Wq"), start=True,
                                     stop=True).then_inc(*pe_done.mark("Qp"))
                    pe.wait_ge(*dve_done.at("Qn"))
                    nc.tensor.transpose(ps[0:C, 0, 256:320], Qn[:, :], ident[0:T, 0:T])\
                        .then_inc(*pe_done.mark("QT"))
                    pe.wait_ge(*dve_done.at("ctx_top"))
                    bound_keys()
                else:
                    bound_keys()
                    nc.tensor.matmul(ps[0:C, 0, 256:320], mem.w(pack, "Wq"), xnT[:, :], start=True,
                                     stop=True).then_inc(*pe_done.mark("QT"))
                pe.wait_ge(*dve_done.at("q_top"))
                nc.tensor.transpose(ps[0:1, 0, 384:512], q_top[:, :], ident).then_inc(*pe_done.mark("q_topT"))
                pe.wait_ge(*dve_done.at("q_top1"))
                nc.tensor.matmul(ps[:, 0, 321:322], mem.ones[0:1, :], q_top1[:, :], start=True, stop=True)\
                    .then_inc(*pe_done.mark("q_top_all"))
                pe.wait_ge(mem.loaded["ctx_rest"], 16 * context_load)
                for kind, n in LATER:
                    project(kind, n)
                    if unit and kind == "V":
                        if n == 2:
                            pe.wait_ge(*dve_done.at("Q_stack"))
                        sum_squares(n - 2)
                if unit:
                    sum_squares(SUPERS - 2)
                    sum_squares(SUPERS - 1)
                pe.wait_ge(*dve_done.at("Q_stack"))
                pe.wait_ge(low_ready, HALVES)
                pe.wait_ge(values_copied, SUPERS)
                if unit:
                    pe.wait_ge(*dve_done.at("key_sums"))
                else:
                    for m in range(2 * HALVES):
                        n, s = m // 2, m % 2
                        u, keys = n // 2, slice((n % 2) * HALF, (n % 2 + 1) * HALF)
                        pe.wait_ge(*stacked_with(u))
                        if m >= 2:
                            pe.wait_ge(max_taken, m - 1)
                        for g in range(G):
                            last = nc.tensor.matmul(ps[:, (m % 2) * G + g, 0:HALF],
                                                    Q_stack[0:96, g, 128 * s:128 * s + 128],
                                                    stack[0:96, u, g, keys], start=True, stop=True)
                        last.then_inc(max_scores, 1)
                    pe.wait_ge(*dve_done.at("max_parts"))
                    for half in range(2):
                        for part in range(2):
                            last = nc.tensor.matmul(
                                ps[:, half, :], picks[:, part, :],
                                diag[:, part, 4 * half:4 * half + 4, :], start=part == 0, stop=part == 1)
                    last.then_inc(*pe_done.mark("max_cols"))
                    pe.wait_ge(*dve_done.at("max_cols"))

                def scores(t):
                    u, j, pair = t // TPS, t % TPS, 2 * (t % RING)
                    pe.wait_ge(*stacked_with(u))
                    if t >= RING:
                        pe.wait_ge(probs_ready, t - RING + 1)
                    for g in range(G):
                        last = nc.tensor.matmul(ps[:, pair + g // 2, (g % 2) * 256:(g % 2 + 1) * 256],
                                                stack[0:STACK, u, g, j * 128:(j + 1) * 128],
                                                Q_stack[0:STACK, g, :], start=True, stop=True)
                    last.then_inc(scores_ready, 1)

                def weigh(t):
                    pe.wait_ge(probs_ready, t + 1)
                    for g in range(G):
                        last = nc.tensor.matmul(
                            ps[32 * g:32 * g + 32, O_BANK, 0:256],
                            mem.values[:, t * C + 32 * g:t * C + 32 * g + 32],
                            probs[:, t % PROBS, 256 * g:256 * g + 256], start=t == 0, stop=t == KT_TILES - 1)
                    last.then_inc(pv_done, 1)

                scores(0)
                scores(1)
                for t in range(KT_TILES):
                    if t + 2 < KT_TILES:
                        scores(t + 2)
                    weigh(t)
                pe.wait_ge(sum_done, KT_TILES)
                for g in range(G):
                    last = nc.tensor.matmul(ps[32 * g:32 * g + 32, DEN_BANK, 0:256], mem.ones[:, 0:32],
                                            prob_sum[:, 256 * g:256 * g + 256], start=True, stop=True)
                last.then_inc(*pe_done.mark("den"))
                pe.wait_ge(*dve_done.at("OT"))
                nc.tensor.matmul(ps[0:T, Y_BANK, 0:C], OT[:, :], mem.w(pack, "Wo"), start=True,
                                 stop=True).then_inc(*pe_done.mark("projected"))

            @block.scalar
            def _(act):
                act.wait_ge(*dve_done.at("key_gain"))
                for n in range(HALVES):
                    u, half = n // 2, slice((n % 2) * HALF, (n % 2 + 1) * HALF)
                    act.wait_ge(keys_projected, n + 1)
                    bank = ps[:, 1 + n % 3, 0:HALF]
                    if unit:
                        if u >= 2:
                            act.wait_ge(norms_ready, u - 1)
                        nc.scalar.activation(squares[:, u % 2, half], bank, ACT.Square)\
                            .then_inc(squares_ready, 1)
                    nc.scalar.activation(parts_of_keys[:, u, 0, half], bank, ACT.Identity, scale=key_gain[:, :])\
                        .then_inc(high_ready, 1)
                for semaphore in stacked:
                    act.wait_ge(semaphore, 16 * PER_BATCH)
                if unit:
                    act.wait_ge(*dve_done.at("key_scale"))
                for t in range(KT_TILES):
                    pair = 2 * (t % RING)
                    act.wait_ge(scores_ready, t + 1)
                    if t >= PROBS:
                        act.wait_ge(pv_done, t - PROBS + 1)
                        act.wait_ge(sum_done, t - PROBS + 1)
                    nc.scalar.activation(
                        probs[:, t % PROBS, :].rearrange("p (b n) -> p b n", b=2), ps[:, pair:pair + 2, :],
                        ACT.Exp, scale=key_scale[:, t:t + 1] if unit else exp_gain[:, :]).then_inc(probs_ready, 1)

            @block.gpsimd
            def _(pool):
                pool_rstd(mem, "var", "rstd")
                if unit:
                    pool_power(mem, q_rsqrt[:, :], q_sum[:, :], mem.minus_half[0:T, 0:1],
                               dve_done.at("q_sum"), "q_rsqrt")
                    pool_power(mem, key_scale[:, :], key_sums[:, :], mem.minus_half[:, :],
                               dve_done.at("key_sums"), "key_rsqrt")
                    pool_rstd(mem, "out_var", "out_rstd")

            @block.vector
            def _(dve):
                v = nc.vector

                def power_of_two(source):
                    step(v.tensor_scalar(power[:, :], source, 1e-30, None, ALU.max))
                    bits = power[:, :].bitcast(I32)
                    step(v.tensor_scalar(bits, bits, EXPONENT_BITS, None, ALU.bitwise_and))
                    step(v.reciprocal(inverse[:, :], power[:, :]))

                def copy_out(kind, n):
                    if kind == "K":
                        u, half = n // 2, slice((n % 2) * HALF, (n % 2 + 1) * HALF)
                        dve.wait_ge(high_ready, n + 1)
                        v.scalar_tensor_tensor(out=parts_of_keys[:, u, 1, half], in0=ps[:, 1 + n % 3, 0:HALF],
                                               scalar=key_gain[:, :], in1=parts_of_keys[:, u, 0, half],
                                               op0=ALU.mult, op1=ALU.subtract).then_inc(low_ready, 1)
                        return
                    first = 4 + 2 * (n % 2)
                    dve.wait_ge(values_projected, n + 1)
                    v.tensor_copy(mem.values[:, n * SUPER:(n + 1) * SUPER],
                                  ps[:, first:first + 2, :].rearrange("p b n -> p (b n)")[:, 0:SUPER])\
                        .then_inc(values_copied, 1)

                dve.wait_ge(mem.loaded[pack], 16)
                v.tensor_scalar(keys_abs[:, :].bitcast(I32), mem.w(pack, "Wk").bitcast(I32), MAGNITUDE_BITS,
                                None, ALU.bitwise_and).then_inc(*dve_done.mark("keys_abs"))
                if unit:
                    dve.wait_ge(mem.loaded["x"], 16)
                dve_moments(mem, mem.x[:, :], "var")
                dve_normalised(mem, mem.xn[:, :], mem.x[:, :], "rstd").then_inc(*dve_done.mark("xn"))
                dve.wait_ge(*pe_done.at("xnT"))
                v.tensor_copy(xnT[:, :], ps[0:C, 0, 0:T]).then_inc(*dve_done.mark("xnT"))
                dve.wait_ge(mem.loaded["consts"], 16)
                dve.wait_ge(mem.loaded["rows"], 16)
                if unit:
                    dve.wait_ge(*pe_done.at("Qp"))
                    step(v.tensor_tensor(Qp[:, :], ps[0:T, 0, 128:256], mem.row("l0x_bq"), ALU.add))
                    step(v.tensor_tensor(sq[:, :], Qp[:, :], Qp[:, :], ALU.mult))
                    step(v.tensor_reduce(q_sum[:, :], sq[:, :], AX_X, ALU.add))
                    v.tensor_scalar(q_sum[:, :], q_sum[:, :], 1e-24, None, ALU.max)\
                        .then_inc(*dve_done.mark("q_sum"))
                    dve.wait_ge(*pool_done.at("q_rsqrt"))
                    v.tensor_scalar(Qn[:, :], Qp[:, :], q_rsqrt[:, :], None, ALU.mult)\
                        .then_inc(*dve_done.mark("Qn"))
                    dve.wait_ge(*pe_done.at("QT"))
                    step(v.tensor_scalar(QT[:, :], ps[0:C, 0, 256:320], SCALE, None, ALU.mult))
                    dve.wait_ge(mem.loaded["ctx_first"], 16)
                    for u in range(SUPERS):
                        if u == CTX_FIRST:
                            dve.wait_ge(mem.loaded["ctx_rest"], 16)
                        ins = v.tensor_reduce(mem.ctx_top[:, u:u + 1], mem.ctx_t[:, u * SUPER:(u + 1) * SUPER],
                                              AX_X, ALU.max, apply_absolute_value=True)
                    step(ins)
                    v.tensor_reduce(mem.ctx_top[:, SUPERS:SUPERS + 1], mem.ctx_top[:, 0:SUPERS], AX_X, ALU.max)\
                        .then_inc(*dve_done.mark("ctx_top"))
                else:
                    dve.wait_ge(*pe_done.at("QT"))
                    step(v.tensor_scalar(QT[:, :], ps[0:C, 0, 256:320], mem.w(pack, "bq"), SCALE,
                                         ALU.add, ALU.mult))
                dve.wait_ge(*pe_done.at("key_bound"))
                power_of_two(ps[:, 0, 320:321])
                v.tensor_scalar(key_gain[:, :], inverse[:, :], 2.0 ** 13, None, ALU.mult)\
                    .then_inc(*dve_done.mark("key_gain"))
                step(v.tensor_scalar(query_gain[:, :], power[:, :], 2.0 ** -13, None, ALU.mult))
                step(v.tensor_scalar(QT[:, :], QT[:, :], query_gain[:, :], None, ALU.mult))
                v.tensor_reduce(q_top[:, :], QT[:, :], AX_X, ALU.max, apply_absolute_value=True)\
                    .then_inc(*dve_done.mark("q_top"))
                dve.wait_ge(*pe_done.at("q_topT"))
                v.tensor_reduce(q_top1[:, :], ps[0:1, 0, 384:512], AX_X, ALU.max)\
                    .then_inc(*dve_done.mark("q_top1"))
                dve.wait_ge(*pe_done.at("q_top_all"))
                power_of_two(ps[:, 0, 321:322])
                step(v.tensor_scalar(gain[:, :], inverse[:, :], 2.0 ** 7, None, ALU.mult))
                step(v.tensor_scalar(exp_gain[:, :], power[:, :], 2.0 ** -7, None, ALU.mult))
                step(v.tensor_scalar(QT[:, :], QT[:, :], gain[:, :], None, ALU.mult))
                step(v.tensor_tensor(Qbd[:, :, :], spread(QT[:, :], 1, [C, HG, T]),
                                     spread(four_heads, 2, [C, HG, T]), ALU.mult))
                whole = Qbd[:, :, :].rearrange("p h t -> p (h t)")
                step(v.tensor_copy(Q_high[:, :], whole))
                step(v.tensor_tensor(Q_low[:, :], whole, Q_high[:, :], ALU.subtract))
                for g in range(G):
                    for block_row, part in enumerate([Q_high, Q_high, Q_low]):
                        ins = v.tensor_copy(Q_stack[32 * block_row:32 * block_row + 32, g, :],
                                            part[32 * g:32 * g + 32, :])
                ins.then_inc(*dve_done.mark("Q_stack"))
                for kind, n in EARLY + LATER:
                    copy_out(kind, n)
                if unit:
                    step(v.tensor_tensor(residual[:, :], Qp[:, :], mem.row("l0x_bo"), ALU.add))
                    dve.wait_ge(norms_ready, SUPERS)
                    v.tensor_scalar(key_sums[:, :], ps[:, 0, 384:384 + KT_TILES], 1e-24, None, ALU.max)\
                        .then_inc(*dve_done.mark("key_sums"))
                    dve.wait_ge(*pool_done.at("key_rsqrt"))
                    v.tensor_scalar(key_scale[:, :], key_scale[:, :], exp_gain[:, :], None, ALU.mult)\
                        .then_inc(*dve_done.mark("key_scale"))
                else:
                    step(v.tensor_tensor(residual[:, :], mem.x[:, :], mem.row(f"{pack}_bo"), ALU.add))
                    v.tensor_copy(picks[:, 0, :], mem.w("consts", "even_out"))
                    step(v.tensor_copy(picks[:, 1, :], mem.w("consts", "odd_out")))
                    for m in range(2 * HALVES):
                        dve.wait_ge(max_scores, m + 1)
                        v.tensor_reduce(
                            maxima[:, m % 2, :, m // 2], ps[:, (m % 2) * G:(m % 2) * G + G, 0:HALF],
                            AX_X, ALU.max).then_inc(max_taken, 1)
                    dve.wait_ge(max_taken, 2 * HALVES)
                    step(v.tensor_reduce(row_max[:, :].rearrange("p (g s) -> p s g", g=G),
                                         maxima[:, :, :, :], AX_X, ALU.max))
                    step(v.tensor_scalar(row_max[:, :], row_max[:, :], -1.0 / BIAS_ROW, None, ALU.mult))
                    step(v.tensor_copy(high16[:, :], row_max[:, :]))
                    step(v.tensor_copy(parts[:, 0, :], high16[:, :]))
                    step(v.tensor_tensor(parts[:, 1, :], row_max[:, :], parts[:, 0, :], ALU.subtract))
                    for part in range(2):
                        ins = v.tensor_tensor(diag[:, part, :, :], spread(ident, 1, [128, G * 2, 128]),
                                              spread(parts[:, part, :], 2, [128, G * 2, 128]), ALU.mult)
                    ins.then_inc(*dve_done.mark("max_parts"))
                    dve.wait_ge(*pe_done.at("max_cols"))
                    v.tensor_copy(Q_stack[96:98, :, :].rearrange("p g n -> p (g n)")
                                  .rearrange("p (b n) -> p b n", b=2), ps[96:98, 0:2, :])\
                        .then_inc(*dve_done.mark("max_cols"))
                for t in range(KT_TILES):
                    dve.wait_ge(probs_ready, t + 1)
                    if t == 0:
                        ins = v.tensor_copy(prob_sum, probs[:, 0, :])
                    else:
                        dve.wait_ge(sum_done, t)
                        ins = v.tensor_tensor(prob_sum, prob_sum, probs[:, t % PROBS, :], ALU.add)
                    ins.then_inc(sum_done, 1)
                dve.wait_ge(*pe_done.at("den"))
                step(v.reciprocal(rden[:, :, :], ps[:, DEN_BANK, 0:256].rearrange("p (h q) -> p h q", h=HG)))
                step(v.tensor_tensor(weighted[:, :, :],
                                     ps[:, O_BANK, 0:256].rearrange("p (h q) -> p h q", h=HG),
                                     rden[:, :, :], ALU.mult))
                step(v.tensor_tensor(weighted[:, :, :], weighted[:, :, :],
                                     spread(four_heads, 2, [C, HG, T]), ALU.mult))
                v.tensor_reduce(OT[:, :], weighted[:, :, :].rearrange("p h q -> p q h"), AX_X,
                                ALU.add).then_inc(*dve_done.mark("OT"))
                dve.wait_ge(*pe_done.at("projected"))
                if unit:
                    step(v.tensor_tensor(z[:, :], ps[0:T, Y_BANK, 0:C], residual[:, :], ALU.add))
                    dve_moments(mem, z[:, :], "out_var")
                    step(dve_normalised(mem, zn[:, :], z[:, :], "out_rstd"))
                    step(v.tensor_tensor(zn[:, :], zn[:, :], mem.row("l0x_gamma"), ALU.mult))
                    step(v.tensor_tensor(zn[:, :], zn[:, :], mem.row("l0x_beta"), ALU.add))
                    v.tensor_tensor(mem.x[:, :], mem.x[:, :], zn[:, :], ALU.add)\
                        .then_inc(*dve_done.mark("x"))
                else:
                    v.tensor_tensor(mem.x[:, :], ps[0:T, Y_BANK, 0:C], residual[:, :], ALU.add)\
                        .then_inc(*dve_done.mark("x"))



def stage_rwkv(mem):
    nc = mem.nc
    pe_done, act_done, dve_done, pool_done = mem.pe_done, mem.act_done, mem.dve_done, mem.pool_done
    step = mem.dve_step
    ps = mem.psum
    ident = mem.w("consts", "ident")
    pe_done.stage("aT", "kvr", "time_mixed", "cT", "kk", "kv")
    dve_done.stage("var", "z", "a_var", "a", "mixed", "scan_args", "rwkv", "c_var", "c", "c_mixed", "kk2", "x")
    act_done.stage("decay", "r_exp", "scan_exps", "rr_exp")
    pool_done.stage("rstd", "a_rstd", "c_rstd")

    def w(name):
        return mem.w("l0a", name)

    with ExitStack() as local:
        def sb(name, shape, dt=F32):
            return local.enter_context(nc.sbuf_tensor("l0a_" + name, shape, dt))

        a, c = sb("a", [T, C]), sb("c", [T, C])
        shifted_a, shifted_c = sb("shifted_a", [C, T + 1]), sb("shifted_c", [C, T + 1])
        delta = sb("delta", [C, T])
        mix = sb("mix", [C, 3, T])
        cmix = sb("cmix", [C, 2, T])
        kvr = sb("kvr", [C, 2, T])
        r_exp = sb("r_exp", [C, T])
        decay = sb("decay", [C, 1])
        decays = sb("decays", [C, T])
        top = sb("top", [C, T + 1])
        now = sb("now", [C, 2, T])
        args = sb("args", [C, 4, T])
        exps = sb("exps", [C, 4, T])
        sum_a, sum_b = sb("sum_a", [C, T + 1]), sb("sum_b", [C, T + 1])
        terms = sb("terms", [C, 4, T])
        rwkv = sb("rwkv", [C, T])
        x1 = sb("x1", [T, C])
        kk = sb("kk", [C, HID // C, T])
        kk2 = sb("kk2", [C, HID // C, T])
        rr = sb("rr", [T, C])
        gated = sb("gated", [T, C])

        with nc.Block(no_gpsimd_drain=True) as block:

            @block.sync
            def _(sp):
                load_context(mem, sp)

            @block.tensor
            def _(pe):
                pe.wait_ge(*dve_done.at("a"))
                nc.tensor.transpose(ps[0:C, 0, 0:T], a[:, :], ident[0:T, 0:T]).then_inc(*pe_done.mark("aT"))
                pe.wait_ge(mem.loaded["l0a"], 16)
                pe.wait_ge(*dve_done.at("mixed"))
                for n, name in enumerate(["Wk", "Wv", "Wr"]):
                    out = ps[0:C, 1, n * T:(n + 1) * T] if n < 2 else ps[0:C, 7, 0:T]
                    last = nc.tensor.matmul(out, w(name), mix[:, n, :], start=True, stop=True)
                last.then_inc(*pe_done.mark("kvr"))
                pe.wait_ge(*dve_done.at("rwkv"))
                nc.tensor.matmul(ps[0:T, 2, 0:C], rwkv[:, :], w("Wo"), start=True, stop=True)\
                    .then_inc(*pe_done.mark("time_mixed"))
                pe.wait_ge(*dve_done.at("c"))
                nc.tensor.transpose(ps[0:C, 3, 0:T], c[:, :], ident[0:T, 0:T]).then_inc(*pe_done.mark("cT"))
                pe.wait_ge(*dve_done.at("c_mixed"))
                for n in range(HID // C):
                    nc.tensor.matmul(ps[0:C, 4, n * T:(n + 1) * T], w("Wck")[:, n * C:(n + 1) * C],
                                     cmix[:, 0, :], start=True, stop=True)
                nc.tensor.matmul(ps[0:T, 5, 0:C], cmix[:, 1, :], w("Wcr"), start=True, stop=True)\
                    .then_inc(*pe_done.mark("kk"))
                pe.wait_ge(*dve_done.at("kk2"))
                for n in range(HID // C):
                    last = nc.tensor.matmul(ps[0:T, 6, 0:C], kk2[:, n, :], w("Wcv")[:, n * C:(n + 1) * C],
                                            start=n == 0, stop=n == HID // C - 1)
                last.then_inc(*pe_done.mark("kv"))

            @block.scalar
            def _(act):
                act.wait_ge(mem.loaded["l0a"], 16)
                nc.scalar.activation(decay[:, :], w("time_decay"), ACT.Exp).then_inc(*act_done.mark("decay"))
                act.wait_ge(*pe_done.at("kvr"))
                nc.scalar.activation(r_exp[:, :], ps[0:C, 7, 0:T], ACT.Exp, scale=-1.0)\
                    .then_inc(*act_done.mark("r_exp"))
                act.wait_ge(*dve_done.at("scan_args"))
                nc.scalar.activation(exps[:, :, :], args[:, :, :], ACT.Exp).then_inc(*act_done.mark("scan_exps"))
                act.wait_ge(*pe_done.at("kk"))
                nc.scalar.activation(rr[:, :], ps[0:T, 5, 0:C], ACT.Exp, scale=-1.0)\
                    .then_inc(*act_done.mark("rr_exp"))

            @block.gpsimd
            def _(pool):
                pool_rstd(mem, "var", "rstd")
                pool_rstd(mem, "a_var", "a_rstd")
                pool_rstd(mem, "c_var", "c_rstd")

            @block.vector
            def _(dve):
                v = nc.vector
                dve_moments(mem, mem.x[:, :], "var")
                dve_normalised(mem, mem.xn[:, :], mem.x[:, :], "rstd").then_inc(*dve_done.mark("z"))
                dve.wait_ge(*dve_done.at("z"))
                dve_moments(mem, mem.xn[:, :], "a_var")
                dve_normalised(mem, a[:, :], mem.xn[:, :], "a_rstd").then_inc(*dve_done.mark("a"))

                dve.wait_ge(mem.loaded["l0a"], 16)
                v.memset(shifted_a[:, 0:1], 0.0)
                v.memset(shifted_c[:, 0:1], 0.0)
                v.memset(sum_a[:, 0:1], 0.0)
                v.memset(sum_b[:, 0:1], 0.0)
                step(v.memset(top[:, 0:1], -1e38))

                dve.wait_ge(*pe_done.at("aT"))
                step(v.tensor_scalar(shifted_a[:, 1:T + 1], ps[0:C, 0, 0:T], w("ln0_g"), w("ln0_b"),
                                     ALU.mult, ALU.add))
                step(v.tensor_tensor(delta[:, :], shifted_a[:, 1:T + 1], shifted_a[:, 0:T], ALU.subtract))
                for n, name in enumerate(["tm_k", "tm_v", "tm_r"]):
                    ins = v.scalar_tensor_tensor(out=mix[:, n, :], in0=delta[:, :], scalar=w(name),
                                                 in1=shifted_a[:, 0:T], op0=ALU.mult, op1=ALU.add)
                ins.then_inc(*dve_done.mark("mixed"))
                dve.wait_ge(*act_done.at("decay"))
                step(v.tensor_scalar(decays[:, :], mem.ones[:, 0:T], decay[:, :], -1.0, ALU.mult, ALU.mult))
                dve.wait_ge(*pe_done.at("kvr"))
                step(v.tensor_copy(kvr[:, :, :], ps[0:C, 1, 0:2 * T].rearrange("p (n t) -> p n t", n=2)))
                k, val = kvr[:, 0, :], kvr[:, 1, :]
                step(v.tensor_tensor_scan(top[:, 1:T + 1], decays[:, :], k, -1e38, ALU.add, ALU.max))
                step(v.tensor_scalar(now[:, 0, :], k, w("time_first"), None, ALU.add))
                step(v.tensor_tensor(now[:, 1, :], top[:, 0:T], now[:, 0, :], ALU.max))
                v.tensor_tensor(args[:, 0, :], top[:, 0:T], now[:, 1, :], ALU.subtract)
                v.tensor_tensor(args[:, 1, :], now[:, 0, :], now[:, 1, :], ALU.subtract)
                v.tensor_tensor(args[:, 3, :], k, top[:, 1:T + 1], ALU.subtract)
                step(v.tensor_tensor(args[:, 2, :], top[:, 0:T], decays[:, :], ALU.add))
                v.tensor_tensor(args[:, 2, :], args[:, 2, :], top[:, 1:T + 1], ALU.subtract)\
                    .then_inc(*dve_done.mark("scan_args"))
                dve.wait_ge(*act_done.at("scan_exps"))
                v.tensor_tensor(terms[:, 0, :], exps[:, 3, :], val, ALU.mult)
                v.tensor_tensor(terms[:, 1, :], exps[:, 1, :], val, ALU.mult)
                step(v.tensor_tensor_scan(sum_b[:, 1:T + 1], exps[:, 2, :], exps[:, 3, :], 0.0, ALU.mult, ALU.add))
                step(v.tensor_tensor_scan(sum_a[:, 1:T + 1], exps[:, 2, :], terms[:, 0, :], 0.0, ALU.mult, ALU.add))
                v.tensor_tensor(terms[:, 2, :], exps[:, 0, :], sum_a[:, 0:T], ALU.mult)
                step(v.tensor_tensor(terms[:, 3, :], exps[:, 0, :], sum_b[:, 0:T], ALU.mult))
                v.tensor_tensor(terms[:, 2, :], terms[:, 2, :], terms[:, 1, :], ALU.add)
                step(v.tensor_tensor(terms[:, 3, :], terms[:, 3, :], exps[:, 1, :], ALU.add))
                dve.wait_ge(*act_done.at("r_exp"))
                step(v.scalar_tensor_tensor(out=terms[:, 3, :], in0=r_exp[:, :], scalar=1.0,
                                            in1=terms[:, 3, :], op0=ALU.add, op1=ALU.mult))
                step(v.reciprocal(terms[:, 3, :], terms[:, 3, :]))
                v.tensor_tensor(rwkv[:, :], terms[:, 2, :], terms[:, 3, :], ALU.mult)\
                    .then_inc(*dve_done.mark("rwkv"))
                dve.wait_ge(*pe_done.at("time_mixed"))
                step(v.tensor_tensor(x1[:, :], ps[0:T, 2, 0:C], mem.xn[:, :], ALU.add))
                dve_moments(mem, x1[:, :], "c_var")
                dve_normalised(mem, c[:, :], x1[:, :], "c_rstd").then_inc(*dve_done.mark("c"))
                step(v.tensor_tensor(x1[:, :], x1[:, :], mem.x[:, :], ALU.add))
                dve.wait_ge(*pe_done.at("cT"))
                step(v.tensor_scalar(shifted_c[:, 1:T + 1], ps[0:C, 3, 0:T], w("ln1_g"), w("ln1_b"),
                                     ALU.mult, ALU.add))
                step(v.tensor_tensor(delta[:, :], shifted_c[:, 1:T + 1], shifted_c[:, 0:T], ALU.subtract))
                for n, name in enumerate(["cm_k", "cm_r"]):
                    ins = v.scalar_tensor_tensor(out=cmix[:, n, :], in0=delta[:, :], scalar=w(name),
                                                 in1=shifted_c[:, 0:T], op0=ALU.mult, op1=ALU.add)
                ins.then_inc(*dve_done.mark("c_mixed"))
                dve.wait_ge(*pe_done.at("kk"))
                step(v.tensor_scalar(kk[:, :, :], ps[0:C, 4, 0:4 * T].rearrange("p (n t) -> p n t", n=4),
                                     0.0, None, ALU.max))
                v.tensor_tensor(kk2[:, :, :], kk[:, :, :], kk[:, :, :], ALU.mult)\
                    .then_inc(*dve_done.mark("kk2"))
                dve.wait_ge(*act_done.at("rr_exp"))
                step(v.tensor_scalar(rr[:, :], rr[:, :], 1.0, None, ALU.add))
                step(v.reciprocal(rr[:, :], rr[:, :]))
                dve.wait_ge(*pe_done.at("kv"))
                step(v.tensor_tensor(gated[:, :], ps[0:T, 6, 0:C], rr[:, :], ALU.mult))
                v.tensor_tensor(mem.x[:, :], x1[:, :], gated[:, :], ALU.add).then_inc(*dve_done.mark("x"))



class Experts:

    def __init__(self, mem, sb, name, experts, hidden, function, tensors):
        self.mem, self.name, self.n, self.chunks, self.function = mem, name, experts, hidden // C, function
        self.w1, self.w2 = tensors
        self.b1, self.b2 = mem.w(name, "b1"), mem.w(name, "b2")
        self.per_bank = CHUNK // (self.chunks * T)
        self.banks = -(-experts // self.per_bank)
        self.hidden_ready, self.biased, self.activated, self.gated = (
            mem.sem(f"{name}_{x}") for x in ["hidden_ready", "biased", "activated", "gated"])
        n = experts * self.chunks * T
        self.pre, self.act = mem.keys_t[:, 0:n], mem.keys_t[:, n:2 * n]
        self.spread_gates = sb("spread_gates", [T, experts, T])
        self.gates = sb("gates", [T, experts])
        self.gatesT = sb("gatesT", [experts, T])
        self.yT = sb("yT", [C, T])

    def of_bank(self, b):
        lo, hi = b * self.per_bank, min(self.n, (b + 1) * self.per_bank)
        return lo, hi, slice(lo * self.chunks * T, hi * self.chunks * T)

    def pe_hidden(self, pe, xT):
        nc, w = self.mem.nc, self.chunks * C
        for b in range(self.banks):
            lo, hi, _ = self.of_bank(b)
            for e in range(lo, hi):
                for c in range(self.chunks):
                    o = ((e - lo) * self.chunks + c) * T
                    last = nc.tensor.matmul(self.mem.psum[0:C, 1 + b, o:o + T],
                                            self.w1[:, e * w + c * C:e * w + (c + 1) * C], xT,
                                            start=True, stop=True)
            last.then_inc(self.hidden_ready, 1)

    def pe_gates(self, pe, first):
        mem, nc = self.mem, self.mem.nc
        pe.wait_ge(*mem.dve_done.at("gates"))
        nc.tensor.transpose(mem.psum[0:self.n, 0, 256:256 + T], self.gates[:, :],
                            mem.w("consts", "ident")[0:T, 0:T])
        nc.tensor.matmul(mem.psum[0:C, first, 0:8 * T], mem.ones[0:T, 0:C], self.spread_gates[:, 0:8, :],
                         start=True, stop=True).then_inc(*mem.pe_done.mark("gates"))

    def pe_out(self, pe):
        mem, nc, w = self.mem, self.mem.nc, self.chunks
        total = self.n * w
        for b in range(self.banks):
            lo, hi, _ = self.of_bank(b)
            if lo < E:
                pe.wait_ge(self.gated, b + 1)
            else:
                pe.wait_ge(self.activated, b + 1)
            for n in range(lo * w, hi * w):
                last = nc.tensor.matmul(mem.psum[0:C, 7, 0:T], self.w2[:, n * C:(n + 1) * C],
                                        self.act[:, n * T:(n + 1) * T], start=n == 0, stop=n == total - 1)
        last.then_inc(*mem.pe_done.mark("yT"))
        pe.wait_ge(*mem.dve_done.at("yT"))
        nc.tensor.matmul(mem.psum[0:T, 7, 128:128 + C], self.yT[:, :], mem.w("consts", "ident"),
                         start=True, stop=False)
        nc.tensor.matmul(mem.psum[0:T, 7, 128:128 + C], self.gatesT[:, :], self.b2,
                         start=False, stop=True).then_inc(*mem.pe_done.mark("y"))

    def act_hidden(self, act):
        for b in range(self.banks):
            _, _, cols = self.of_bank(b)
            act.wait_ge(self.biased, b + 1)
            self.mem.nc.scalar.activation(self.act[:, cols], self.pre[:, cols], self.function)\
                .then_inc(self.activated, 1)

    def dve_gates(self, dve):
        mem, v = self.mem, self.mem.nc.vector
        shape = [T, self.n, T]
        v.tensor_tensor(self.spread_gates[:, :, :], spread(mem.w("consts", "ident")[0:T, 0:T], 1, shape),
                        spread(self.gates[:, :], 2, shape), ALU.mult).then_inc(*mem.dve_done.mark("gates"))

    def dve_bias(self, dve):
        v, ch = self.mem.nc.vector, self.chunks
        for b in range(self.banks):
            lo, hi, cols = self.of_bank(b)
            n = (hi - lo) * ch
            dve.wait_ge(self.hidden_ready, b + 1)
            v.tensor_tensor(self.pre[:, cols].rearrange("p (n t) -> p n t", t=T),
                            self.mem.psum[0:C, 1 + b, 0:n * T].rearrange("p (n t) -> p n t", t=T),
                            spread(self.b1[:, lo * ch:hi * ch], 2, [C, n, T]), ALU.add)\
                .then_inc(self.biased, 1)

    def dve_gate(self, dve, gate_bank):
        mem, v, ch = self.mem, self.mem.nc.vector, self.chunks
        dve.wait_ge(*mem.pe_done.at("gates"))
        mem.dve_step(v.tensor_copy(self.gatesT[:, :], mem.psum[0:self.n, 0, 256:256 + T]))
        for b in range(self.banks):
            lo, hi, cols = self.of_bank(b)
            if lo >= E:
                continue
            dve.wait_ge(self.activated, b + 1)
            n = hi - lo
            act = self.act[:, cols].rearrange("p (e c t) -> p e c t", e=n, t=T)
            gate = mem.psum[0:C, gate_bank, lo * T:hi * T].rearrange("p (e t) -> p e t", t=T)
            v.tensor_tensor(act, act, spread(gate, 2, [C, n, ch, T]), ALU.mult).then_inc(self.gated, 1)

    def dve_yT(self, dve):
        mem = self.mem
        dve.wait_ge(*mem.pe_done.at("yT"))
        mem.nc.vector.tensor_copy(self.yT[:, :], mem.psum[0:C, 7, 0:T]).then_inc(*mem.dve_done.mark("yT"))


def dve_softmax(mem, sb_tiles, scores, out, event_scores, event_exp):
    v, step = mem.nc.vector, mem.dve_step
    top, total = sb_tiles
    step(v.tensor_reduce(top, scores, AX_X, ALU.max))
    v.tensor_scalar(scores, scores, top, None, ALU.subtract).then_inc(*mem.dve_done.mark(event_scores))
    mem.nc.vector.wait_ge(*mem.act_done.at(event_exp))
    step(v.tensor_reduce(total, out, AX_X, ALU.add))
    step(v.reciprocal(total, total))
    step(v.tensor_scalar(out, out, total, None, ALU.mult))


def dve_first_largest(mem, padded, best, work, mask, n, count):
    v, step = mem.nc.vector, mem.dve_step
    step(v.max(best, padded))
    step(v.memset(best[:, count:8], -1.0))
    step(v.match_replace(work, best, padded, -2.0))
    step(v.tensor_scalar(mask, work[:, 0:n], -2.0, None, ALU.is_equal))


def stage_topk_experts(mem, level):
    nc = mem.nc
    pe_done, act_done, dve_done, pool_done = mem.pe_done, mem.act_done, mem.dve_done, mem.pool_done
    step = mem.dve_step
    name = f"l{level}f"
    n_experts = E + (level == 3)
    ps = mem.psum
    pe_done.stage("xnT", "logits", "gates", "yT", "y")
    dve_done.stage("var", "xn", "xnT", "scores", "gates", "yT", "x")
    act_done.stage("exp")
    pool_done.stage("rstd")
    weights = mem.experts
    w1 = weights[:, 0:n_experts * HID]
    w2 = weights[:, n_experts * HID:2 * n_experts * HID]

    with ExitStack() as local:
        def sb(label, shape, dt=F32):
            return local.enter_context(nc.sbuf_tensor(f"{name}_{label}", shape, dt))

        experts = Experts(mem, sb, name, n_experts, HID, ACT.Gelu_apprx_tanh, (w1, w2))
        xnT = sb("xnT", [C, T])
        scores, top, total = sb("scores", [T, E]), sb("top", [T, 1]), sb("total", [T, 1])
        padded, work, best, mask = sb("padded", [T, 16]), sb("work", [T, 16]), sb("best", [T, 8]), sb("mask", [T, E])

        with nc.Block(no_gpsimd_drain=True) as block:

            @block.tensor
            def _(pe):
                pe.wait_ge(*dve_done.at("xn"))
                nc.tensor.transpose(ps[0:C, 0, 0:T], mem.xn[:, :], mem.w("consts", "ident")[0:T, 0:T])\
                    .then_inc(*pe_done.mark("xnT"))
                pe.wait_ge(mem.loaded[name], 16)
                pe.wait_ge(*dve_done.at("xnT"))
                nc.tensor.matmul(ps[0:T, 0, 128:128 + E], xnT[:, :], mem.w(name, "w_router"), start=True,
                                 stop=True).then_inc(*pe_done.mark("logits"))
                pe.wait_ge(mem.loaded[f"experts{level}"], 16)
                experts.pe_hidden(pe, xnT[:, :])
                experts.pe_gates(pe, 6)
                experts.pe_out(pe)

            @block.scalar
            def _(act):
                act.wait_ge(*dve_done.at("scores"))
                nc.scalar.activation(padded[:, 0:E], scores[:, :], ACT.Exp).then_inc(*act_done.mark("exp"))
                experts.act_hidden(act)

            @block.gpsimd
            def _(pool):
                pool_rstd(mem, "var", "rstd")

            @block.vector
            def _(dve):
                v = nc.vector
                dve_moments(mem, mem.x[:, :], "var")
                dve_normalised(mem, mem.xn[:, :], mem.x[:, :], "rstd").then_inc(*dve_done.mark("xn"))
                v.memset(padded[:, E:16], -1.0)
                dve.wait_ge(*pe_done.at("xnT"))
                v.tensor_copy(xnT[:, :], ps[0:C, 0, 0:T]).then_inc(*dve_done.mark("xnT"))
                dve.wait_ge(*pe_done.at("logits"))
                step(v.tensor_copy(scores[:, :], ps[0:T, 0, 128:128 + E]))
                dve_softmax(mem, (top[:, :], total[:, :]), scores[:, :], padded[:, 0:E], "scores", "exp")
                dve_first_largest(mem, padded[:, :], best[:, :], work[:, :], mask[:, :], E, 2)
                if level == 3:
                    step(v.memset(experts.gates[:, E:E + 1], 1.0))
                step(v.tensor_tensor(experts.gates[:, 0:E], padded[:, 0:E], mask[:, :], ALU.mult))
                if level == 3:
                    step(v.tensor_reduce(total[:, :], experts.gates[:, 0:E], AX_X, ALU.add))
                    step(v.reciprocal(total[:, :], total[:, :]))
                    step(v.tensor_scalar(experts.gates[:, 0:E], experts.gates[:, 0:E], total[:, :], None,
                                         ALU.mult))
                dve.wait_ge(mem.loaded[name], 16)
                experts.dve_gates(dve)
                experts.dve_bias(dve)
                experts.dve_gate(dve, 6)
                experts.dve_yT(dve)
                dve.wait_ge(*pe_done.at("y"))
                v.tensor_tensor(mem.x[:, :], mem.x[:, :], ps[0:T, 7, 128:128 + C], ALU.add)\
                    .then_inc(*dve_done.mark("x"))



class SmallHeads:
    PE = ["scores", "probsT", "heads"]
    DVE = ["Qbd", "less_max", "probs", "PT", "OT"]

    def __init__(self, mem, sb, mask):
        self.mem, self.mask = mem, mask
        self.QT, self.KT, self.V = sb("QT", [C, T]), sb("KT", [C, T]), sb("V", [T, C])
        self.Qbd = sb("Qbd", [C, HG, T])
        self.S = sb("S", [128, 2 * G, T])
        self.P = sb("P", [128, 2 * G, T])
        self.top, self.total = sb("top", [128, 2 * G]), sb("total", [128, 2 * G])
        self.PT = sb("PT", [T, H * T])
        self.weighted = sb("weighted", [C, HG, T])
        self.OT = sb("OT", [C, T])

    def pe(self, pe, v_event):
        nc, mem, ps = self.mem.nc, self.mem, self.mem.psum
        pe.wait_ge(*mem.dve_done.at("Qbd"))
        for s in range(2):
            for g in range(G):
                rows = slice(32 * g, 32 * g + 32)
                last = nc.tensor.matmul(ps[:, 1 + g, s * T:(s + 1) * T], self.Qbd[rows, 2 * s:2 * s + 2, :],
                                        self.KT[rows, :], start=True, stop=True)
        last.then_inc(*mem.pe_done.mark("scores"))
        pe.wait_ge(*mem.dve_done.at("probs"))
        for n in range(2 * G):
            last = nc.tensor.transpose(ps[0:T, 5 + n // G, (n % G) * 128:(n % G + 1) * 128],
                                       self.P[:, n, :], mem.w("consts", "ident"))
        last.then_inc(*mem.pe_done.mark("probsT"))
        pe.wait_ge(*mem.dve_done.at("PT"))
        pe.wait_ge(*mem.dve_done.at(v_event))
        for g in range(G):
            last = nc.tensor.matmul(ps[32 * g:32 * g + 32, 7, 0:HG * T], self.V[:, 32 * g:32 * g + 32],
                                    self.PT[:, 256 * g:256 * g + 256], start=True, stop=True)
        last.then_inc(*mem.pe_done.mark("heads"))

    def act(self, act):
        mem = self.mem
        act.wait_ge(*mem.dve_done.at("less_max"))
        mem.nc.scalar.activation(self.P[:, :, :], self.S[:, :, :], ACT.Exp).then_inc(*mem.act_done.mark("exps"))

    def dve_Qbd(self, dve):
        mem, shape = self.mem, [C, HG, T]
        mem.nc.vector.tensor_tensor(self.Qbd[:, :, :], spread(self.QT[:, :], 1, shape),
                                    spread(mem.w("consts", "four_heads"), 2, shape), ALU.mult)\
            .then_inc(*mem.dve_done.mark("Qbd"))

    def dve(self, dve):
        mem, v, step, ps = self.mem, self.mem.nc.vector, self.mem.dve_step, self.mem.psum
        shape = [128, 2 * G, T]
        dve.wait_ge(*mem.pe_done.at("scores"))
        scores = ps[:, 1:1 + G, 0:2 * T].rearrange("p g (s k) -> p g s k", s=2)
        if self.mask is None:
            step(v.tensor_copy(self.S[:, :, :].rearrange("p (g s) k -> p g s k", g=G), scores))
        else:
            mask = self.mask.unsqueeze(1).unsqueeze(1).to_broadcast([128, G, 2, T])
            step(v.tensor_tensor(self.S[:, :, :].rearrange("p (g s) k -> p g s k", g=G), scores, mask, ALU.add))
        step(v.tensor_reduce(self.top[:, :], self.S[:, :, :], AX_X, ALU.max))
        v.tensor_tensor(self.S[:, :, :], self.S[:, :, :], spread(self.top[:, :], 2, shape), ALU.subtract)\
            .then_inc(*mem.dve_done.mark("less_max"))
        dve.wait_ge(*mem.act_done.at("exps"))
        step(v.tensor_reduce(self.total[:, :], self.P[:, :, :], AX_X, ALU.add))
        step(v.reciprocal(self.total[:, :], self.total[:, :]))
        v.tensor_tensor(self.P[:, :, :], self.P[:, :, :], spread(self.total[:, :], 2, shape), ALU.mult)\
            .then_inc(*mem.dve_done.mark("probs"))
        dve.wait_ge(*mem.pe_done.at("probsT"))
        v.tensor_copy(self.PT[:, :].rearrange("p (b n) -> p b n", b=2), ps[0:T, 5:7, :])\
            .then_inc(*mem.dve_done.mark("PT"))
        dve.wait_ge(*mem.pe_done.at("heads"))
        step(v.tensor_tensor(self.weighted[:, :, :], ps[:, 7, 0:HG * T].rearrange("p (h q) -> p h q", h=HG),
                             spread(mem.w("consts", "four_heads"), 2, [C, HG, T]), ALU.mult))
        v.tensor_reduce(self.OT[:, :], self.weighted[:, :, :].rearrange("p h q -> p q h"), AX_X, ALU.add)\
            .then_inc(*mem.dve_done.mark("OT"))



def stage_rope_attention(mem):
    nc = mem.nc
    pe_done, act_done, dve_done, pool_done = mem.pe_done, mem.act_done, mem.dve_done, mem.pool_done
    step, ps = mem.dve_step, mem.psum
    ident = mem.w("consts", "ident")
    QK = H + G
    pe_done.stage("xnT", "qkv", "turned", *SmallHeads.PE, "projected")
    dve_done.stage("var", "xn", "xnT", "squares", "rotated", *SmallHeads.DVE, "x")
    act_done.stage("exps")
    pool_done.stage("rstd", "norms")

    with ExitStack() as local:
        def sb(name, shape, dt=F32):
            return local.enter_context(nc.sbuf_tensor("l1a_" + name, shape, dt))

        heads = SmallHeads(mem, sb, mem.w("consts", "causal"))
        xnT = sb("xnT", [C, T])
        qkv = sb("qkv", [T, (QK + G) * DH])
        squares, unit = sb("squares", [T, QK, DH]), sb("unit", [T, QK, DH])
        sums, norms, half = sb("sums", [T, QK]), sb("norms", [T, QK]), sb("half", [T, QK])
        straight, crossed = sb("straight", [T, QK, DH]), sb("crossed", [T, QK, DH])
        k_all = sb("k_all", [T, C])

        with nc.Block(no_gpsimd_drain=True) as block:

            @block.sync
            def _(sp):
                load_context(mem, sp)
                sp.dma_start(mem.experts[:, :], mem.dram["experts3"]).then_inc(mem.loaded["experts3"], 16)

            @block.tensor
            def _(pe):
                pe.wait_ge(*dve_done.at("xn"))
                nc.tensor.transpose(ps[0:C, 0, 0:T], mem.xn[:, :], ident[0:T, 0:T]).then_inc(*pe_done.mark("xnT"))
                pe.wait_ge(mem.loaded["l1a"], 16)
                pe.wait_ge(*dve_done.at("xnT"))
                nc.tensor.matmul(ps[0:T, 1, 0:192], xnT[:, :], mem.w("l1a", "w_qkv"), start=True, stop=True)\
                    .then_inc(*pe_done.mark("qkv"))
                pe.wait_ge(*dve_done.at("rotated"))
                nc.tensor.transpose(ps[0:C, 0, 0:T], straight[:, 0:H, :], ident[0:T, 0:T])
                nc.tensor.transpose(ps[0:C, 0, T:2 * T], k_all[:, :], ident[0:T, 0:T])\
                    .then_inc(*pe_done.mark("turned"))
                heads.pe(pe, "rotated")
                pe.wait_ge(*dve_done.at("OT"))
                nc.tensor.matmul(ps[0:T, 0, 0:C], heads.OT[:, :], mem.w("l1a", "w_o"), start=True, stop=True)\
                    .then_inc(*pe_done.mark("projected"))

            @block.scalar
            def _(act):
                heads.act(act)

            @block.gpsimd
            def _(pool):
                pool_rstd(mem, "var", "rstd")
                pool_power(mem, norms[:, :], sums[:, :], half[:, :], dve_done.at("squares"), "norms")

            @block.vector
            def _(dve):
                v = nc.vector
                dve_moments(mem, mem.x[:, :], "var")
                dve_normalised(mem, mem.xn[:, :], mem.x[:, :], "rstd").then_inc(*dve_done.mark("xn"))
                v.memset(half[:, :], 0.5)
                dve.wait_ge(*pe_done.at("xnT"))
                v.tensor_copy(xnT[:, :], ps[0:C, 0, 0:T]).then_inc(*dve_done.mark("xnT"))
                dve.wait_ge(*pe_done.at("qkv"))
                step(v.tensor_copy(qkv[:, :], ps[0:T, 1, 0:192]))
                qk = qkv[:, 0:QK * DH].rearrange("t (h d) -> t h d", d=DH)
                step(v.tensor_tensor(squares[:, :, :], qk, qk, ALU.mult))
                v.tensor_reduce(sums[:, :], squares[:, :, :], AX_X, ALU.add).then_inc(*dve_done.mark("squares"))
                dve.wait_ge(*pool_done.at("norms"))
                step(v.tensor_scalar(norms[:, :], norms[:, :], 1e-10, None, ALU.add))
                step(v.reciprocal(norms[:, :], norms[:, :]))
                step(v.tensor_tensor(unit[:, :, :], qk, spread(norms[:, :], 2, [T, QK, DH]), ALU.mult))
                f, h = DH, DH // 2
                sin = mem.w("consts", "sin")
                v.tensor_tensor(straight[:, :, :], unit[:, :, :],
                                spread(mem.w("consts", "cos"), 1, [T, QK, f]), ALU.mult)
                v.tensor_tensor(crossed[:, :, 0:h], unit[:, :, h:f], spread(sin[:, 0:h], 1, [T, QK, h]), ALU.mult)
                step(v.tensor_tensor(crossed[:, :, h:f], unit[:, :, 0:h], spread(sin[:, h:f], 1, [T, QK, h]), ALU.mult))
                step(v.tensor_tensor(straight[:, :, :], straight[:, :, :], crossed[:, :, :], ALU.add))
                v.tensor_copy(k_all[:, :].rearrange("t (g r d) -> t g r d", g=G, r=HG),
                              spread(straight[:, H:QK, :], 2, [T, G, HG, DH]))
                v.tensor_copy(heads.V[:, :].rearrange("t (g r d) -> t g r d", g=G, r=HG),
                              spread(qkv[:, QK * DH:192].rearrange("t (g d) -> t g d", g=G), 2, [T, G, HG, DH]))\
                    .then_inc(*dve_done.mark("rotated"))
                dve.wait_ge(*pe_done.at("turned"))
                v.tensor_copy(heads.KT[:, :], ps[0:C, 0, T:2 * T])
                step(v.tensor_scalar(heads.QT[:, :], ps[0:C, 0, 0:T], SCALE, None, ALU.mult))
                heads.dve_Qbd(dve)
                heads.dve(dve)
                dve.wait_ge(*pe_done.at("projected"))
                v.tensor_tensor(mem.x[:, :], mem.x[:, :], ps[0:T, 0, 0:C], ALU.add).then_inc(*dve_done.mark("x"))



def stage_quantised_ffn(mem):
    nc = mem.nc
    pe_done, act_done, dve_done, pool_done = mem.pe_done, mem.act_done, mem.dve_done, mem.pool_done
    step, ps = mem.dve_step, mem.psum
    ident = mem.w("consts", "ident")
    pe_done.stage("weightsT", "x_topT", "x_top", "xqT", "gate_up", "h_topT", "h_top", "hT", "out")
    dve_done.stage("var", "xn", "w_quantised", "wT", "x_top1", "x_top", "xq", "xqT",
                   "h", "h_top1", "h_top", "hq", "hT", "x")
    act_done.stage("clips", "silu")
    pool_done.stage("rstd")

    with ExitStack() as local:
        def sb(name, shape, dt=F32):
            return local.enter_context(nc.sbuf_tensor("l1f_" + name, shape, dt))

        gate_up = sb("gate_up", [128, 6, C])
        down = sb("down", [C, FFQ])
        tops, steps_, inverse = sb("tops", [128, 7]), sb("steps", [128, 7]), sb("inverse", [128, 7])
        gate_upT = sb("gate_upT", [C, 2, FFQ])
        downT = sb("downT", [128, 3, C])
        clips = sb("clips", [C, 2])
        top, top1 = sb("top", [T, 2]), sb("top1", [1, 2])
        a_step, a_inv = sb("a_step", [T, 2]), sb("a_inv", [T, 2])
        xq, xqT = sb("xq", [T, C]), sb("xqT", [C, T])
        silu, h = sb("silu", [T, FFQ]), sb("h", [T, FFQ])
        hT = sb("hT", [128, 3, T])

        with nc.Block(no_gpsimd_drain=True) as block:

            @block.tensor
            def _(pe):
                def spread_top(n):
                    name = "xh"[n]
                    pe.wait_ge(*dve_done.at(f"{name}_top1"))
                    nc.tensor.matmul(ps[0:T, 4, 128 + n:129 + n], mem.ones[0:1, 0:T], top1[0:1, n:n + 1],
                                     start=True, stop=True).then_inc(*pe_done.mark(f"{name}_top"))

                pe.wait_ge(*dve_done.at("w_quantised"))
                for m in range(2):
                    for n, (lo, rows) in enumerate(FFQ_CHUNKS):
                        nc.tensor.transpose(ps[0:C, 1 + m, lo:lo + rows], gate_up[0:rows, 3 * m + n, :],
                                            ident[0:rows, 0:rows])
                for n, (lo, rows) in enumerate(FFQ_CHUNKS):
                    last = nc.tensor.transpose(ps[0:rows, 3, n * C:(n + 1) * C], down[:, lo:lo + rows], ident)
                last.then_inc(*pe_done.mark("weightsT"))
                pe.wait_ge(*dve_done.at("xn"))
                nc.tensor.transpose(ps[0:1, 4, 0:T], top[:, 0:1], ident[0:T, 0:T])\
                    .then_inc(*pe_done.mark("x_topT"))
                spread_top(0)
                pe.wait_ge(*dve_done.at("xq"))
                nc.tensor.transpose(ps[0:C, 0, 0:T], xq[:, :], ident[0:T, 0:T]).then_inc(*pe_done.mark("xqT"))
                pe.wait_ge(*dve_done.at("xqT"))
                for m in range(2):
                    last = nc.tensor.matmul(ps[0:T, 5 + m, 0:FFQ], xqT[:, :], gate_upT[:, m, :], start=True,
                                            stop=True)
                last.then_inc(*pe_done.mark("gate_up"))
                pe.wait_ge(*dve_done.at("h"))
                nc.tensor.transpose(ps[0:1, 4, 0:T], top[:, 1:2], ident[0:T, 0:T])\
                    .then_inc(*pe_done.mark("h_topT"))
                spread_top(1)
                pe.wait_ge(*dve_done.at("hq"))
                for n, (lo, rows) in enumerate(FFQ_CHUNKS):
                    last = nc.tensor.transpose(ps[0:rows, 7, n * T:(n + 1) * T], h[:, lo:lo + rows],
                                               ident[0:T, 0:T])
                last.then_inc(*pe_done.mark("hT"))
                pe.wait_ge(*dve_done.at("hT"))
                for n, (lo, rows) in enumerate(FFQ_CHUNKS):
                    last = nc.tensor.matmul(ps[0:T, 0, 0:C], hT[0:rows, n, :], downT[0:rows, n, :],
                                            start=n == 0, stop=n == 2)
                last.then_inc(*pe_done.mark("out"))

            @block.scalar
            def _(act):
                act.wait_ge(mem.loaded["l1f"], 16)
                at, _, _ = column("l1f", "clip_x")
                nc.scalar.activation(clips[:, :], mem.packs["l1f"][:, at:at + 2], ACT.Exp, scale=-1.0)\
                    .then_inc(*act_done.mark("clips"))
                act.wait_ge(*pe_done.at("gate_up"))
                nc.scalar.activation(silu[:, :], ps[0:T, 5, 0:FFQ], ACT.Silu).then_inc(*act_done.mark("silu"))

            @block.gpsimd
            def _(pool):
                pool_rstd(mem, "var", "rstd")

            @block.vector
            def _(dve):
                v = nc.vector

                def rounded(out, scaled):
                    step(v.tensor_scalar(out, scaled, ROUND, ROUND, ALU.add, ALU.subtract))
                    step(v.tensor_scalar(out, out, 127.0, -128.0, ALU.min, ALU.max))

                def activation_step(n):
                    name = "xh"[n]
                    dve.wait_ge(*pe_done.at(f"{name}_topT"))
                    v.tensor_reduce(top1[0:1, n:n + 1], ps[0:1, 4, 0:T], AX_X, ALU.max)\
                        .then_inc(*dve_done.mark(f"{name}_top1"))
                    dve.wait_ge(*pe_done.at(f"{name}_top"))
                    step(v.tensor_scalar(a_step[:, n:n + 1], ps[0:T, 4, 128 + n:129 + n], clips[0:T, n:n + 1],
                                         1.0 / 127.0, ALU.mult, ALU.mult))
                    v.reciprocal(a_inv[:, n:n + 1], a_step[:, n:n + 1]).then_inc(*dve_done.mark(f"{name}_top"))
                    dve.wait_ge(*dve_done.at(f"{name}_top"))

                dve_moments(mem, mem.x[:, :], "var")
                step(dve_normalised(mem, mem.xn[:, :], mem.x[:, :], "rstd"))
                v.tensor_reduce(top[:, 0:1], mem.xn[:, :], AX_X, ALU.max, apply_absolute_value=True)\
                    .then_inc(*dve_done.mark("xn"))
                dve.wait_ge(mem.loaded["l1f"], 16)
                raw = mem.packs["l1f"][:, 0:6 * C].rearrange("p (n m) -> p n m", n=6)
                v.tensor_reduce(tops[:, 0:6], raw, AX_X, ALU.max, apply_absolute_value=True)
                step(v.tensor_reduce(tops[:, 6:7], mem.w("l1f", "w_down"), AX_X, ALU.max,
                                     apply_absolute_value=True))
                step(v.tensor_scalar(steps_[:, :], tops[:, :], 1e-30, 1.0 / 127.0, ALU.max, ALU.mult))
                step(v.reciprocal(inverse[:, :], steps_[:, :]))
                step(v.tensor_tensor(gate_up[:, :, :], raw, spread(inverse[:, 0:6], 2, [128, 6, C]), ALU.mult))
                rounded(gate_up[:, :, :], gate_up[:, :, :])
                step(v.tensor_tensor(gate_up[:, :, :], gate_up[:, :, :],
                                     spread(steps_[:, 0:6], 2, [128, 6, C]), ALU.mult))
                step(v.tensor_scalar(down[:, :], mem.w("l1f", "w_down"), inverse[:, 6:7], None, ALU.mult))
                rounded(down[:, :], down[:, :])
                v.tensor_scalar(down[:, :], down[:, :], steps_[:, 6:7], None, ALU.mult)\
                    .then_inc(*dve_done.mark("w_quantised"))
                dve.wait_ge(*pe_done.at("weightsT"))
                v.tensor_copy(gate_upT[:, :, :], ps[0:C, 1:3, 0:FFQ])
                v.tensor_copy(downT[:, 0:2, :], ps[:, 3, 0:2 * C].rearrange("p (n m) -> p n m", n=2))
                v.tensor_copy(downT[0:96, 2, :], ps[0:96, 3, 2 * C:3 * C]).then_inc(*dve_done.mark("wT"))
                dve.wait_ge(*act_done.at("clips"))
                step(v.tensor_scalar(clips[:, :], clips[:, :], 1.0, None, ALU.add))
                step(v.reciprocal(clips[:, :], clips[:, :]))
                activation_step(0)
                step(v.tensor_scalar(xq[:, :], mem.xn[:, :], a_inv[:, 0:1], None, ALU.mult))
                rounded(xq[:, :], xq[:, :])
                v.tensor_scalar(xq[:, :], xq[:, :], a_step[:, 0:1], None, ALU.mult)\
                    .then_inc(*dve_done.mark("xq"))
                dve.wait_ge(*pe_done.at("xqT"))
                v.tensor_copy(xqT[:, :], ps[0:C, 0, 0:T]).then_inc(*dve_done.mark("xqT"))
                dve.wait_ge(*act_done.at("silu"))
                step(v.tensor_tensor(h[:, :], silu[:, :], ps[0:T, 6, 0:FFQ], ALU.mult))
                v.tensor_reduce(top[:, 1:2], h[:, :], AX_X, ALU.max, apply_absolute_value=True)\
                    .then_inc(*dve_done.mark("h"))
                activation_step(1)
                step(v.tensor_scalar(h[:, :], h[:, :], a_inv[:, 1:2], None, ALU.mult))
                rounded(h[:, :], h[:, :])
                v.tensor_scalar(h[:, :], h[:, :], a_step[:, 1:2], None, ALU.mult).then_inc(*dve_done.mark("hq"))
                dve.wait_ge(*pe_done.at("hT"))
                v.tensor_copy(hT[:, 0:2, :], ps[:, 7, 0:2 * T].rearrange("p (n t) -> p n t", n=2))
                v.tensor_copy(hT[0:96, 2, :], ps[0:96, 7, 2 * T:3 * T]).then_inc(*dve_done.mark("hT"))
                dve.wait_ge(*pe_done.at("out"))
                v.tensor_tensor(mem.x[:, :], mem.x[:, :], ps[0:T, 0, 0:C], ALU.add).then_inc(*dve_done.mark("x"))



def stage_local_attention(mem):
    nc = mem.nc
    pe_done, act_done, dve_done, pool_done = mem.pe_done, mem.act_done, mem.dve_done, mem.pool_done
    step, ps = mem.dve_step, mem.psum
    ident = mem.w("consts", "ident")
    pe_done.stage("xnT", "qkv", *SmallHeads.PE, "projected")
    dve_done.stage("var", "xn", "xnT", *SmallHeads.DVE[:1], "V", *SmallHeads.DVE[1:], "x")
    act_done.stage("exps")
    pool_done.stage("rstd")

    def w(name):
        return mem.w("l2a", name)

    with ExitStack() as local:
        def sb(name, shape, dt=F32):
            return local.enter_context(nc.sbuf_tensor("l2a_" + name, shape, dt))

        heads = SmallHeads(mem, sb, mem.w("consts", "band"))
        xnT = sb("xnT", [C, T])
        residual = sb("residual", [T, C])

        with nc.Block(no_gpsimd_drain=True) as block:

            @block.sync
            def _(sp):
                load_context(mem, sp)
                sp.dma_start(mem.values[:, 0:width("experts2")], mem.dram["experts2"])\
                    .then_inc(mem.loaded["experts2"], 16)

            @block.tensor
            def _(pe):
                pe.wait_ge(*dve_done.at("xn"))
                nc.tensor.transpose(ps[0:C, 0, 0:T], mem.xn[:, :], ident[0:T, 0:T]).then_inc(*pe_done.mark("xnT"))
                pe.wait_ge(mem.loaded["l2a"], 16)
                pe.wait_ge(*dve_done.at("xnT"))
                nc.tensor.matmul(ps[0:C, 0, 0:T], w("w_q"), xnT[:, :], start=True, stop=True)
                nc.tensor.matmul(ps[0:C, 0, T:2 * T], w("w_k"), xnT[:, :], start=True, stop=True)
                nc.tensor.matmul(ps[0:T, 0, 128:256], xnT[:, :], w("w_v"), start=True, stop=True)\
                    .then_inc(*pe_done.mark("qkv"))
                heads.pe(pe, "V")
                pe.wait_ge(*dve_done.at("OT"))
                nc.tensor.matmul(ps[0:T, 0, 0:C], heads.OT[:, :], w("w_o"), start=True, stop=True)\
                    .then_inc(*pe_done.mark("projected"))

            @block.scalar
            def _(act):
                heads.act(act)

            @block.gpsimd
            def _(pool):
                pool_rstd(mem, "var", "rstd")

            @block.vector
            def _(dve):
                v = nc.vector
                dve_moments(mem, mem.x[:, :], "var")
                dve_normalised(mem, mem.xn[:, :], mem.x[:, :], "rstd").then_inc(*dve_done.mark("xn"))
                v.tensor_tensor(residual[:, :], mem.x[:, :], mem.row("l2a_bo"), ALU.add)
                dve.wait_ge(*pe_done.at("xnT"))
                v.tensor_copy(xnT[:, :], ps[0:C, 0, 0:T]).then_inc(*dve_done.mark("xnT"))
                dve.wait_ge(mem.loaded["l2a"], 16)
                dve.wait_ge(*pe_done.at("qkv"))
                v.tensor_scalar(heads.KT[:, :], ps[0:C, 0, T:2 * T], w("b_k"), None, ALU.add)
                step(v.tensor_scalar(heads.QT[:, :], ps[0:C, 0, 0:T], w("b_q"), SCALE, ALU.add, ALU.mult))
                heads.dve_Qbd(dve)
                v.tensor_tensor(heads.V[:, :], ps[0:T, 0, 128:256], mem.row("l2a_bv"), ALU.add)\
                    .then_inc(*dve_done.mark("V"))
                heads.dve(dve)
                dve.wait_ge(*pe_done.at("projected"))
                v.tensor_tensor(mem.x[:, :], residual[:, :], ps[0:T, 0, 0:C], ALU.add)\
                    .then_inc(*dve_done.mark("x"))



def stage_transformer_experts(mem):
    nc = mem.nc
    pe_done, act_done, dve_done, pool_done = mem.pe_done, mem.act_done, mem.dve_done, mem.pool_done
    step, ps = mem.dve_step, mem.psum
    ident = mem.w("consts", "ident")
    GROUPS = 4
    pe_done.stage("zT", "qkv", "turned", *SmallHeads.PE, "projected", "yT_in", "logits", "gates", "yT", "y")
    dve_done.stage("var", "z", "zT", "V", *SmallHeads.DVE, "mid_var", "mid", "midT", "scores", "gates", "yT",
                   "out_var", "x")
    act_done.stage("exps", "gate_exps")
    pool_done.stage("rstd", "mid_rstd", "out_rstd")
    weights = mem.values

    def w(name):
        return mem.w("l2f", name)

    with ExitStack() as local:
        def sb(name, shape, dt=F32):
            return local.enter_context(nc.sbuf_tensor("l2f_" + name, shape, dt))

        heads = SmallHeads(mem, sb, None)
        experts = Experts(mem, sb, "l2f", E, HID2, ACT.Relu,
                          (weights[:, 0:E * HID2], weights[:, E * HID2:2 * E * HID2]))
        zT, midT = sb("zT", [C, T]), sb("midT", [C, T])
        qk, mid, out = sb("qk", [T, 2 * C]), sb("mid", [T, C]), sb("out", [T, C])
        residual = sb("residual", [T, C])
        scores, exps = sb("scores", [T, GROUPS + E]), sb("exps", [T, GROUPS + E])
        tops, totals = sb("tops", [T, 1 + GROUPS]), sb("totals", [T, 1 + GROUPS])
        padded, work, best = sb("padded", [T, 16]), sb("work", [T, 16]), sb("best", [T, 8])
        group_gate, pick = sb("group_gate", [T, GROUPS]), sb("pick", [T, GROUPS, 2])

        with nc.Block(no_gpsimd_drain=True) as block:

            @block.tensor
            def _(pe):
                pe.wait_ge(*dve_done.at("z"))
                nc.tensor.transpose(ps[0:C, 0, 0:T], mem.xn[:, :], ident[0:T, 0:T]).then_inc(*pe_done.mark("zT"))
                pe.wait_ge(mem.loaded["l2f"], 16)
                pe.wait_ge(*dve_done.at("zT"))
                nc.tensor.matmul(ps[0:T, 1, 0:3 * C], zT[:, :], w("w_in"), start=True, stop=True)\
                    .then_inc(*pe_done.mark("qkv"))
                pe.wait_ge(*dve_done.at("V"))
                nc.tensor.transpose(ps[0:C, 0, 0:T], qk[:, 0:C], ident[0:T, 0:T])
                nc.tensor.transpose(ps[0:C, 0, T:2 * T], qk[:, C:2 * C], ident[0:T, 0:T])\
                    .then_inc(*pe_done.mark("turned"))
                heads.pe(pe, "V")
                pe.wait_ge(*dve_done.at("OT"))
                nc.tensor.matmul(ps[0:T, 0, 0:C], heads.OT[:, :], w("w_out"), start=True, stop=True)\
                    .then_inc(*pe_done.mark("projected"))
                pe.wait_ge(*dve_done.at("mid"))
                nc.tensor.transpose(ps[0:C, 0, 0:T], mid[:, :], ident[0:T, 0:T]).then_inc(*pe_done.mark("yT_in"))
                pe.wait_ge(*dve_done.at("midT"))
                at, _, _ = column("l2f", "w_group")
                nc.tensor.matmul(ps[0:T, 0, 128:128 + GROUPS + E], midT[:, :],
                                 mem.packs["l2f"][:, at:at + GROUPS + E], start=True, stop=True)\
                    .then_inc(*pe_done.mark("logits"))
                pe.wait_ge(mem.loaded["experts2"], 16)
                experts.pe_hidden(pe, midT[:, :])
                experts.pe_gates(pe, 6)
                experts.pe_out(pe)

            @block.scalar
            def _(act):
                heads.act(act)
                act.wait_ge(*dve_done.at("scores"))
                nc.scalar.activation(exps[:, :], scores[:, :], ACT.Exp).then_inc(*act_done.mark("gate_exps"))
                experts.act_hidden(act)

            @block.gpsimd
            def _(pool):
                pool_rstd(mem, "var", "rstd")
                pool_rstd(mem, "mid_var", "mid_rstd")
                pool_rstd(mem, "out_var", "out_rstd")

            @block.vector
            def _(dve):
                v = nc.vector
                dve_moments(mem, mem.x[:, :], "var")
                dve_normalised(mem, mem.xn[:, :], mem.x[:, :], "rstd").then_inc(*dve_done.mark("z"))
                dve.wait_ge(*dve_done.at("z"))
                v.tensor_tensor(residual[:, :], mem.xn[:, :], mem.row("l2f_b_out"), ALU.add)
                v.memset(padded[:, GROUPS:16], -1.0)
                dve.wait_ge(*pe_done.at("zT"))
                v.tensor_copy(zT[:, :], ps[0:C, 0, 0:T]).then_inc(*dve_done.mark("zT"))
                dve.wait_ge(*pe_done.at("qkv"))
                bias = mem.row("l2f_b_in")
                v.tensor_tensor(qk[:, :], ps[0:T, 1, 0:2 * C], bias[:, 0:2 * C], ALU.add)
                v.tensor_tensor(heads.V[:, :], ps[0:T, 1, 2 * C:3 * C], bias[:, 2 * C:3 * C], ALU.add)\
                    .then_inc(*dve_done.mark("V"))
                dve.wait_ge(*pe_done.at("turned"))
                v.tensor_copy(heads.KT[:, :], ps[0:C, 0, T:2 * T])
                step(v.tensor_scalar(heads.QT[:, :], ps[0:C, 0, 0:T], SCALE, None, ALU.mult))
                heads.dve_Qbd(dve)
                heads.dve(dve)
                dve.wait_ge(*pe_done.at("projected"))
                step(v.tensor_tensor(mid[:, :], ps[0:T, 0, 0:C], residual[:, :], ALU.add))
                dve_moments(mem, mid[:, :], "mid_var")
                step(dve_normalised(mem, mid[:, :], mid[:, :], "mid_rstd"))
                step(v.tensor_tensor(mid[:, :], mid[:, :], mem.row("l2f_g1"), ALU.mult))
                v.tensor_tensor(mid[:, :], mid[:, :], mem.row("l2f_b1"), ALU.add).then_inc(*dve_done.mark("mid"))
                dve.wait_ge(*pe_done.at("yT_in"))
                v.tensor_copy(midT[:, :], ps[0:C, 0, 0:T]).then_inc(*dve_done.mark("midT"))
                dve.wait_ge(*pe_done.at("logits"))
                at, _, _ = column("rows", "l2f_b_group")
                step(v.tensor_tensor(scores[:, :], ps[0:T, 0, 128:128 + GROUPS + E],
                                     mem.rows[:, at:at + GROUPS + E], ALU.add))
                pairs = scores[:, GROUPS:GROUPS + E].rearrange("t (g e) -> t g e", e=2)
                v.tensor_reduce(tops[:, 0:1], scores[:, 0:GROUPS], AX_X, ALU.max)
                step(v.tensor_reduce(tops[:, 1:1 + GROUPS], pairs, AX_X, ALU.max))
                v.tensor_scalar(scores[:, 0:GROUPS], scores[:, 0:GROUPS], tops[:, 0:1], None, ALU.subtract)
                v.tensor_tensor(pairs, pairs, spread(tops[:, 1:1 + GROUPS], 2, [T, GROUPS, 2]), ALU.subtract)\
                    .then_inc(*dve_done.mark("scores"))
                dve.wait_ge(*act_done.at("gate_exps"))
                probs = exps[:, GROUPS:GROUPS + E].rearrange("t (g e) -> t g e", e=2)
                v.tensor_reduce(totals[:, 0:1], exps[:, 0:GROUPS], AX_X, ALU.add)
                step(v.tensor_reduce(totals[:, 1:1 + GROUPS], probs, AX_X, ALU.add))
                step(v.reciprocal(totals[:, :], totals[:, :]))
                v.tensor_scalar(padded[:, 0:GROUPS], exps[:, 0:GROUPS], totals[:, 0:1], None, ALU.mult)
                step(v.tensor_tensor(probs, probs, spread(totals[:, 1:1 + GROUPS], 2, [T, GROUPS, 2]), ALU.mult))
                dve_first_largest(mem, padded[:, :], best[:, :], work[:, :], group_gate[:, :], GROUPS, 1)
                step(v.tensor_tensor(group_gate[:, :], group_gate[:, :], padded[:, 0:GROUPS], ALU.mult))
                step(v.tensor_tensor(pick[:, :, 0], probs[:, :, 0], probs[:, :, 1], ALU.is_ge))
                step(v.tensor_scalar(pick[:, :, 1], pick[:, :, 0], -1.0, 1.0, ALU.mult, ALU.add))
                step(v.tensor_tensor(pick[:, :, :], pick[:, :, :], probs, ALU.mult))
                step(v.tensor_tensor(experts.gates[:, :].rearrange("t (g e) -> t g e", e=2), pick[:, :, :],
                                     spread(group_gate[:, :], 2, [T, GROUPS, 2]), ALU.mult))
                dve.wait_ge(mem.loaded["l2f"], 16)
                experts.dve_gates(dve)
                experts.dve_bias(dve)
                experts.dve_gate(dve, 6)
                experts.dve_yT(dve)
                dve.wait_ge(*pe_done.at("y"))
                step(v.tensor_tensor(out[:, :], mid[:, :], ps[0:T, 7, 128:128 + C], ALU.add))
                dve_moments(mem, out[:, :], "out_var")
                step(dve_normalised(mem, out[:, :], out[:, :], "out_rstd"))
                step(v.tensor_tensor(out[:, :], out[:, :], mem.row("l2f_g2"), ALU.mult))
                step(v.tensor_tensor(out[:, :], out[:, :], mem.row("l2f_b2"), ALU.add))
                v.tensor_tensor(mem.x[:, :], mem.x[:, :], out[:, :], ALU.add).then_inc(*dve_done.mark("x"))



def stage_past_attention(mem):
    nc = mem.nc
    pe_done, act_done, dve_done, pool_done = mem.pe_done, mem.act_done, mem.dve_done, mem.pool_done
    step, ps = mem.dve_step, mem.psum
    ident = mem.w("consts", "ident")
    pe_done.stage("zT", "qT", "scores", "probsT", "contextT", "out")
    dve_done.stage("var", "z", "zT", "qT", "less_max", "probs", "probsT", "contextT", "out", "x")
    act_done.stage("exps", "tanh")
    pool_done.stage("rstd")

    with ExitStack() as local:
        def sb(name, shape, dt=F32):
            return local.enter_context(nc.sbuf_tensor("l3a_" + name, shape, dt))

        zT, qT, contextT = sb("zT", [C, T]), sb("qT", [C, T]), sb("contextT", [C, T])
        S, P, PT = sb("S", [T, T]), sb("P", [T, T]), sb("PT", [T, T])
        top, total = sb("top", [T, 1]), sb("total", [T, 1])
        out = sb("out", [T, C])

        with nc.Block(no_gpsimd_drain=True) as block:

            @block.tensor
            def _(pe):
                pe.wait_ge(*dve_done.at("z"))
                nc.tensor.transpose(ps[0:C, 0, 0:T], mem.xn[:, :], ident[0:T, 0:T]).then_inc(*pe_done.mark("zT"))
                pe.wait_ge(mem.loaded["l3a"], 16)
                pe.wait_ge(*dve_done.at("zT"))
                nc.tensor.matmul(ps[0:C, 1, 0:T], mem.w("l3a", "w_dec"), zT[:, :], start=True, stop=True)\
                    .then_inc(*pe_done.mark("qT"))
                pe.wait_ge(*dve_done.at("qT"))
                nc.tensor.matmul(ps[0:T, 2, 0:T], qT[:, :], zT[:, :], start=True, stop=True)\
                    .then_inc(*pe_done.mark("scores"))
                pe.wait_ge(*dve_done.at("probs"))
                nc.tensor.transpose(ps[0:T, 3, 0:T], P[:, :], ident[0:T, 0:T]).then_inc(*pe_done.mark("probsT"))
                pe.wait_ge(*dve_done.at("probsT"))
                nc.tensor.matmul(ps[0:C, 4, 0:T], mem.xn[:, :], PT[:, :], start=True, stop=True)\
                    .then_inc(*pe_done.mark("contextT"))
                pe.wait_ge(*dve_done.at("contextT"))
                w_out = mem.w("l3a", "w_out")
                nc.tensor.matmul(ps[0:T, 5, 0:C], zT[:, :], w_out[:, 0:C], start=True, stop=False)
                nc.tensor.matmul(ps[0:T, 5, 0:C], contextT[:, :], w_out[:, C:2 * C], start=False, stop=True)\
                    .then_inc(*pe_done.mark("out"))

            @block.scalar
            def _(act):
                act.wait_ge(*dve_done.at("less_max"))
                nc.scalar.activation(P[:, :], S[:, :], ACT.Exp, accum_out=total[:, :])\
                    .then_inc(*act_done.mark("exps"))
                act.wait_ge(*dve_done.at("out"))
                nc.scalar.activation(out[:, :], out[:, :], ACT.Tanh).then_inc(*act_done.mark("tanh"))

            @block.gpsimd
            def _(pool):
                pool_rstd(mem, "var", "rstd")

            @block.vector
            def _(dve):
                v = nc.vector
                dve_moments(mem, mem.x[:, :], "var")
                dve_normalised(mem, mem.xn[:, :], mem.x[:, :], "rstd").then_inc(*dve_done.mark("z"))
                dve.wait_ge(*pe_done.at("zT"))
                v.tensor_copy(zT[:, :], ps[0:C, 0, 0:T]).then_inc(*dve_done.mark("zT"))
                dve.wait_ge(*pe_done.at("qT"))
                v.tensor_copy(qT[:, :], ps[0:C, 1, 0:T]).then_inc(*dve_done.mark("qT"))
                dve.wait_ge(*pe_done.at("scores"))
                step(v.tensor_tensor(S[:, :], ps[0:T, 2, 0:T], mem.w("consts", "strict"), ALU.add))
                step(v.tensor_reduce(top[:, :], S[:, :], AX_X, ALU.max))
                v.tensor_scalar(S[:, :], S[:, :], top[:, :], None, ALU.subtract)\
                    .then_inc(*dve_done.mark("less_max"))
                dve.wait_ge(*act_done.at("exps"))
                step(v.reciprocal(total[:, :], total[:, :]))
                v.tensor_scalar(P[:, :], P[:, :], total[:, :], None, ALU.mult).then_inc(*dve_done.mark("probs"))
                dve.wait_ge(*pe_done.at("probsT"))
                v.tensor_copy(PT[:, :], ps[0:T, 3, 0:T]).then_inc(*dve_done.mark("probsT"))
                dve.wait_ge(*pe_done.at("contextT"))
                v.tensor_copy(contextT[:, :], ps[0:C, 4, 0:T]).then_inc(*dve_done.mark("contextT"))
                dve.wait_ge(*pe_done.at("out"))
                v.tensor_tensor(out[:, :], ps[0:T, 5, 0:C], mem.row("l3a_bo"), ALU.add)\
                    .then_inc(*dve_done.mark("out"))
                dve.wait_ge(*act_done.at("tanh"))
                v.tensor_tensor(mem.x[:, :], mem.x[:, :], out[:, :], ALU.add).then_inc(*dve_done.mark("x"))



def stage_state_kernel(mem):
    nc = mem.nc
    dve_done, act_done = mem.dve_done, mem.act_done
    step = mem.dve_step
    dve_done.stage("angles", "kernel")
    act_done.stage("sines")
    mem.pe_done.stage()
    mem.pool_done.stage()
    N = NSTATE

    def w(name):
        return mem.w("l2x", name)

    with ExitStack() as local:
        def sb(name, shape, dt=F32):
            return local.enter_context(nc.sbuf_tensor("s4_" + name, shape, dt))

        def wide(name):
            return sb(name, [C, N])[:, :]

        dt, dt_m1 = sb("dt", [C, 1])[:, :], sb("dt_m1", [C, 1])[:, :]
        re, im, grow, grow_m1 = wide("re"), wide("im"), wide("grow"), wide("grow_m1")
        turns, angles, sines = wide("turns"), sb("angles", [C, 2, N]), sb("sines", [C, 2, N])
        cos, cos_m1, nr, ni = wide("cos"), wide("cos_m1"), wide("nr"), wide("ni")
        gr, gi, t1, t2, size = wide("gr"), wide("gi"), wide("t1"), wide("t2"), wide("size")
        pr, pi = sb("pr", [C, 2, N]), sb("pi", [C, 2, N])
        scratch = {n: (sb(f"n{n}", [C, n])[:, :], sb(f"r{n}", [C, n])[:, :], sb(f"s{n}", [C, n])[:, :],
                       sb(f"p{n}", [C, n], I32)[:, :]) for n in (1, N)}
        def wide_in(memory, at, lags):
            return memory[:, at:at + lags * N].rearrange("p (l n) -> p l n", n=N)

        qr, qi = wide_in(mem.keys_t, 0, T), wide_in(mem.values, 0, T // 2)
        prod1, prod2 = wide_in(mem.keys_t, T * N, T // 2), wide_in(mem.values, T // 2 * N, T // 2)
        kernel = sb("kernel", [C, T])

        with nc.Block(no_gpsimd_drain=True) as block:

            @block.scalar
            def _(act):
                act.wait_ge(*dve_done.at("angles"))
                nc.scalar.activation(sines[:, :, :], angles[:, :, :], ACT.Sin).then_inc(*act_done.mark("sines"))

            @block.vector
            def _(dve):
                v = nc.vector

                def mul(out, a, b):
                    step(v.tensor_tensor(out, a, b, ALU.mult))

                def add(out, a, b):
                    step(v.tensor_tensor(out, a, b, ALU.add))

                def sub(out, a, b):
                    step(v.tensor_tensor(out, a, b, ALU.subtract))

                def affine(out, a, scale, shift):
                    step(v.tensor_scalar(out, a, scale, shift, ALU.mult, ALU.add))

                def exponential(z, full, less_one, n):
                    whole, series, rest, power = scratch[n][0], scratch[n][2], scratch[n][1], scratch[n][3]
                    step(v.tensor_scalar(z, z, -87.0, 88.0, ALU.max, ALU.min))
                    affine(whole, z, LOG2E, ROUND)
                    step(v.tensor_scalar(whole, whole, ROUND, None, ALU.subtract))
                    step(v.scalar_tensor_tensor(out=rest, in0=whole, scalar=-LN2_HI, in1=z, op0=ALU.mult, op1=ALU.add))
                    step(v.scalar_tensor_tensor(out=rest, in0=whole, scalar=-LN2_LO, in1=rest, op0=ALU.mult, op1=ALU.add))
                    step(v.tensor_scalar(series, rest, 1.0 / 5040, None, ALU.mult))
                    for k in (720, 120, 24, 6, 2, 1):
                        step(v.scalar_tensor_tensor(out=series, in0=series, scalar=1.0 / k, in1=rest,
                                                    op0=ALU.add, op1=ALU.mult))
                    step(v.tensor_scalar(power, whole, 127.0, 8388608.0, ALU.add, ALU.mult))
                    two = power.bitcast(F32)
                    mul(series, series, two)
                    add(full, series, two)
                    step(v.scalar_tensor_tensor(out=less_one, in0=two, scalar=-1.0, in1=series,
                                                op0=ALU.add, op1=ALU.add))

                dve.wait_ge(mem.loaded["l2x"], 16)
                step(v.tensor_copy(t1[:, 0:1], w("log_dt")))
                exponential(t1[:, 0:1], dt, dt_m1, 1)
                step(v.tensor_scalar(re, w("A_re"), dt, None, ALU.mult))
                step(v.tensor_scalar(im, w("A_im"), dt, None, ALU.mult))
                affine(turns, im, 1.0 / (2 * np.pi), ROUND)
                step(v.tensor_scalar(turns, turns, ROUND, None, ALU.subtract))
                for part in (TWO_PI_HI, TWO_PI_MID, TWO_PI_LO):
                    step(v.scalar_tensor_tensor(out=im, in0=turns, scalar=-part, in1=im, op0=ALU.mult, op1=ALU.add))
                step(v.tensor_scalar(angles[:, 0, :], im, -3.1415925, 3.1415925, ALU.max, ALU.min))
                v.tensor_scalar(angles[:, 1, :], angles[:, 0, :], 0.5, None, ALU.mult)\
                    .then_inc(*dve_done.mark("angles"))
                exponential(re, grow, grow_m1, N)
                dve.wait_ge(*act_done.at("sines"))
                mul(t1, sines[:, 1, :], sines[:, 1, :])
                step(v.tensor_scalar(cos_m1, t1, -2.0, None, ALU.mult))
                step(v.tensor_scalar(cos, cos_m1, 1.0, None, ALU.add))
                mul(pr[:, 0, :], grow, cos)
                mul(pi[:, 0, :], grow, sines[:, 0, :])
                mul(nr, grow_m1, cos)
                add(nr, nr, cos_m1)
                ni = pi[:, 0, :]
                mul(t1, nr, w("A_re"))
                mul(t2, ni, w("A_im"))
                add(gr, t1, t2)
                mul(t1, ni, w("A_re"))
                mul(t2, nr, w("A_im"))
                sub(gi, t1, t2)
                mul(t1, w("A_re"), w("A_re"))
                mul(t2, w("A_im"), w("A_im"))
                add(size, t1, t2)
                step(v.reciprocal(size, size))
                mul(gr, gr, size)
                mul(gi, gi, size)
                mul(t1, gr, w("C_re"))
                mul(t2, gi, w("C_im"))
                sub(qr[:, 0, :], t1, t2)
                mul(t1, gi, w("C_re"))
                mul(t2, gr, w("C_im"))
                add(qi[:, 0, :], t1, t2)
                m = 1
                now = 0
                while m < T:
                    shape = [C, m, N]
                    r, i = spread(pr[:, now, :], 1, shape), spread(pi[:, now, :], 1, shape)
                    a, b = prod1[:, 0:m, :], prod2[:, 0:m, :]
                    mul(a, qr[:, 0:m, :], r)
                    mul(b, qi[:, 0:m, :], i)
                    sub(qr[:, m:2 * m, :], a, b)
                    if 2 * m < T:
                        mul(a, qr[:, 0:m, :], i)
                        mul(b, qi[:, 0:m, :], r)
                        add(qi[:, m:2 * m, :], a, b)
                        mul(t1, pr[:, now, :], pr[:, now, :])
                        mul(t2, pi[:, now, :], pi[:, now, :])
                        sub(pr[:, 1 - now, :], t1, t2)
                        mul(t1, pr[:, now, :], pi[:, now, :])
                        step(v.tensor_scalar(pi[:, 1 - now, :], t1, 2.0, None, ALU.mult))
                        now = 1 - now
                    m *= 2
                step(v.tensor_reduce(kernel[:, :], qr, AX_X, ALU.add))
                v.tensor_scalar(mem.kernel_reversed[:, :], kernel[:, ::-1], 2.0, None, ALU.mult)\
                    .then_inc(*dve_done.mark("kernel"))



def stage_topk_attention(mem, context_load):
    nc = mem.nc
    pe_done, act_done, dve_done, pool_done = mem.pe_done, mem.act_done, mem.dve_done, mem.pool_done
    step, ps = mem.dve_step, mem.psum
    ident = mem.w("consts", "ident")
    CHOSEN = -2.0e38
    R = 2
    TPB = CHUNK // T
    BLOCKS = -(-KT_TILES // TPB)
    HALF = C // R
    pe_done.stage("zT", "QT", "pooledT", "contextT", "film", "aT", "mixed",
                  "hT", "hidden", "out")
    dve_done.stage("var", "z", "zT", "mask", "Qbd", "max0", "kept0", "max1", "kept1", "picks", "pooled",
                   "contextT", "a_var", "a", "film_out", "x_mid_var", "h", "hT", "hidden",
                   "out_var", "x")
    act_done.stage("exp0", "exp1", "hidden")
    pool_done.stage("rstd", "a_rstd", "h_rstd", "out_rstd")
    keys_projected, keys_copied = mem.sem("l2x_keys_projected"), mem.sem("l2x_keys_copied")
    scores_ready, scores_copied = mem.sem("l2x_scores_ready"), mem.sem("l2x_scores_copied")
    turned, turned_copied = mem.sem("l2x_turned"), mem.sem("l2x_turned_copied")
    masks_loaded, tiles_loaded = mem.sem("l2x_masks_loaded"), mem.sem("l2x_tiles_loaded")

    def w(name):
        return mem.w("l2x", name)

    def chunk_keys(c):
        return c * CHUNK, min(KEYS, (c + 1) * CHUNK)

    with ExitStack() as local:
        def sb(name, shape, dt=F32):
            return local.enter_context(nc.sbuf_tensor("l2x_" + name, shape, dt))

        S = mem.wide[:, :].rearrange("p (r k) -> p r k", r=R)
        left = mem.values[:, 0:KEYS]
        ctx_tiles = mem.keys_t[:, 0:KT_TILES * CTX]
        mask_bias = sb("mask_bias", [128, KEYS], BF16)
        mask8 = mem.values[:, 0:KEYS // 4].bitcast(U8)
        ones16 = sb("ones16", [128, 128], BF16)
        token8 = sb("token8", [C, T], U8)
        token_mask = sb("token_mask", [C, T])
        zT, QT, Qbd = sb("zT", [C, T]), sb("QT", [C, T]), sb("Qbd", [C, R, T])
        best = sb("best", [128, 4, 8])
        minus_max = sb("minus_max", [128, R])
        total, inverse = sb("total", [128, R]), sb("inverse", [128, R])
        pick = sb("pick", [128, R, T])
        turnedT = mem.values[:, 0:KT_TILES * T].rearrange("p (n t) -> p n t", t=T)
        pooledT, contextT = sb("pooledT", [CTX, T]), sb("contextT", [C, T])
        a, aT = sb("a", [T, C]), sb("aT", [C, T])
        film = sb("film", [C, 4, T])
        padded = sb("padded", [C, 2 * T - 1])
        products = mem.values[:, 0:T * T].rearrange("p (t l) -> p t l", l=T)
        mixed = sb("mixed", [C, T])
        x_mid, h, hT = sb("x_mid", [T, C]), sb("h", [T, C]), sb("hT", [C, T])
        pre, hidden = sb("pre", [C, HID // C, T]), sb("hidden", [C, HID // C, T])
        out = sb("out", [T, C])

        with nc.Block(no_gpsimd_drain=True) as block:

            @block.sync
            def _(sp):
                sp.dma_start(mask8, mem.dram["context_mask"].to_broadcast([128, KEYS])).then_inc(masks_loaded, 16)
                sp.dma_start(token8[:, :], mem.dram["token_mask"].to_broadcast([C, T])).then_inc(masks_loaded, 16)
                sp.wait_ge(scores_ready, R * CHUNKS)
                sp.dma_start(ctx_tiles, mem.dram["ctx_tiles"]).then_inc(tiles_loaded, 16)
                sp.wait_ge(tiles_loaded, 16)

            @block.tensor
            def _(pe):
                pe.wait_ge(*dve_done.at("z"))
                pe.wait_ge(mem.loaded["l2x"], 16)
                nc.tensor.transpose(ps[0:C, 0, 0:T], mem.xn[:, :], ident[0:T, 0:T]).then_inc(*pe_done.mark("zT"))
                pe.wait_ge(mem.loaded["ctx_first"], 16 * context_load)
                pe.wait_ge(mem.loaded["ctx_rest"], 16 * context_load)
                pe.wait_ge(*dve_done.at("zT"))
                nc.tensor.matmul(ps[0:C, 0, 128:192], w("Wq"), zT[:, :], start=True, stop=True)\
                    .then_inc(*pe_done.mark("QT"))
                for c in range(CHUNKS):
                    lo, hi = chunk_keys(c)
                    if c >= 3:
                        pe.wait_ge(keys_copied, c - 2)
                    nc.tensor.matmul(ps[:, 1 + c % 3, 0:hi - lo], w("Wk"), mem.ctx_t[0:CTX, lo:hi],
                                     start=True, stop=True).then_inc(keys_projected, 1)
                pe.wait_ge(*dve_done.at("Qbd"))
                pe.wait_ge(*dve_done.at("mask"))
                for r in range(R):
                    rows = slice(HALF * r, HALF * r + HALF)
                    for c in range(CHUNKS):
                        lo, hi = chunk_keys(c)
                        n = r * CHUNKS + c
                        if r == 0:
                            pe.wait_ge(keys_copied, c + 1)
                        if n >= 4:
                            pe.wait_ge(scores_copied, n - 3)
                        bank = ps[:, 4 + n % 4, 0:hi - lo]
                        nc.tensor.matmul(bank, Qbd[rows, :, :], mem.keys_t[rows, lo:hi], start=True, stop=False)
                        last = nc.tensor.matmul(bank, ones16[HALF * r:HALF * r + 1, :],
                                                mask_bias[HALF * r:HALF * r + 1, lo:hi], start=False, stop=True)
                        last.then_inc(scores_ready, 1)
                pe.wait_ge(*dve_done.at("picks"))
                for b in range(BLOCKS):
                    if b >= 3:
                        pe.wait_ge(turned_copied, b - 2)
                    for t in range(b * TPB, min(KT_TILES, (b + 1) * TPB)):
                        for r in range(R):
                            last = nc.tensor.matmul(ps[:, 1 + b % 3, (t % TPB) * T:(t % TPB + 1) * T],
                                                    S[:, r, t * 128:(t + 1) * 128], pick[:, r, :],
                                                    start=r == 0, stop=r == R - 1)
                    last.then_inc(turned, 1)
                pe.wait_ge(tiles_loaded, 16)
                for t in range(KT_TILES):
                    if t % TPB == 0:
                        pe.wait_ge(turned_copied, t // TPB + 1)
                    last = nc.tensor.matmul(ps[0:CTX, 7, 0:T], ctx_tiles[:, t * CTX:(t + 1) * CTX],
                                            turnedT[:, t, :], start=t == 0, stop=t == KT_TILES - 1)
                last.then_inc(*pe_done.mark("pooledT"))
                pe.wait_ge(*dve_done.at("pooled"))
                nc.tensor.matmul(ps[0:C, 0, 0:T], w("Wv"), pooledT[:, :], start=True, stop=True)\
                    .then_inc(*pe_done.mark("contextT"))
                pe.wait_ge(*dve_done.at("contextT"))
                for n in range(4):
                    half = slice((n % 2) * C, (n % 2 + 1) * C)
                    last = nc.tensor.matmul(ps[0:C, 4, n * T:(n + 1) * T],
                                            w(["W_film_in", "W_film_out"][n // 2])[:, half], contextT[:, :],
                                            start=True, stop=True)
                last.then_inc(*pe_done.mark("film"))
                pe.wait_ge(*dve_done.at("a"))
                nc.tensor.transpose(ps[0:C, 5, 0:T], a[:, :], ident[0:T, 0:T]).then_inc(*pe_done.mark("aT"))
                pe.wait_ge(*dve_done.at("film_out"))
                nc.tensor.transpose(ps[0:T, 6, 0:C], mixed[:, :], ident).then_inc(*pe_done.mark("mixed"))
                pe.wait_ge(*dve_done.at("h"))
                nc.tensor.transpose(ps[0:C, 0, 0:T], h[:, :], ident[0:T, 0:T]).then_inc(*pe_done.mark("hT"))
                pe.wait_ge(*dve_done.at("hT"))
                for n in range(HID // C):
                    last = nc.tensor.matmul(ps[0:C, 1, n * T:(n + 1) * T], w("W1")[:, n * C:(n + 1) * C],
                                            hT[:, :], start=True, stop=True)
                last.then_inc(*pe_done.mark("hidden"))
                pe.wait_ge(*act_done.at("hidden"))
                for n in range(HID // C):
                    last = nc.tensor.matmul(ps[0:T, 2, 0:C], hidden[:, n, :], w("W2")[:, n * C:(n + 1) * C],
                                            start=n == 0, stop=n == HID // C - 1)
                last.then_inc(*pe_done.mark("out"))

            @block.scalar
            def _(act):
                for c in range(CHUNKS):
                    lo, hi = chunk_keys(c)
                    act.wait_ge(keys_projected, c + 1)
                    nc.scalar.activation(mem.keys_t[:, lo:hi], ps[:, 1 + c % 3, 0:hi - lo], ACT.Identity)\
                        .then_inc(keys_copied, 1)
                for n in range(R * CHUNKS):
                    lo, hi = chunk_keys(n % CHUNKS)
                    act.wait_ge(scores_ready, n + 1)
                    nc.scalar.activation(S[:, n // CHUNKS, lo:hi], ps[:, 4 + n % 4, 0:hi - lo], ACT.Identity)\
                        .then_inc(scores_copied, 1)
                for r in range(R):
                    act.wait_ge(*dve_done.at(f"max{r}"))
                    nc.scalar.activation(S[:, r, :], S[:, r, :], ACT.Exp, bias=minus_max[:, r:r + 1])\
                        .then_inc(*act_done.mark(f"exp{r}"))
                act.wait_ge(*dve_done.at("hidden"))
                nc.scalar.activation(hidden[:, :, :], pre[:, :, :], ACT.Gelu).then_inc(*act_done.mark("hidden"))

            @block.gpsimd
            def _(pool):
                pool_rstd(mem, "var", "rstd")
                pool_rstd(mem, "a_var", "a_rstd")
                pool_rstd(mem, "x_mid_var", "h_rstd")
                pool_rstd(mem, "out_var", "out_rstd")

            @block.vector
            def _(dve):
                v = nc.vector
                dve_moments(mem, mem.x[:, :], "var")
                dve_normalised(mem, mem.xn[:, :], mem.x[:, :], "rstd").then_inc(*dve_done.mark("z"))
                v.memset(ones16[:, :], 1.0)
                v.memset(padded[:, :], 0.0)
                dve.wait_ge(*pe_done.at("zT"))
                v.tensor_copy(zT[:, :], ps[0:C, 0, 0:T]).then_inc(*dve_done.mark("zT"))
                dve.wait_ge(masks_loaded, 32)
                v.tensor_copy(token_mask[:, :], token8[:, :])
                v.tensor_scalar(mask_bias[:, :], mask8, 1.0, 1e30, ALU.subtract, ALU.mult)\
                    .then_inc(*dve_done.mark("mask"))
                dve.wait_ge(*pe_done.at("QT"))
                step(v.tensor_scalar(QT[:, :], ps[0:C, 0, 128:192], D2 ** -0.5, None, ALU.mult))
                v.tensor_tensor(Qbd[:, :, :], spread(QT[:, :], 1, [C, R, T]),
                                spread(mem.w("consts", "two_heads"), 2, [C, R, T]), ALU.mult)\
                    .then_inc(*dve_done.mark("Qbd"))
                dve.wait_ge(*dve_done.at("mask"))
                for r in range(R):
                    dve.wait_ge(scores_copied, (r + 1) * CHUNKS)
                    source = S[:, r, :]
                    for k in range(TOPK // 8):
                        step(v.max(best[:, k, :], source))
                        step(v.match_replace(left, best[:, k, :], source, LOWEST))
                        source = left
                        if k == 0:
                            v.tensor_scalar(minus_max[:, r:r + 1], best[:, 0, 0:1], -1.0, None, ALU.mult)\
                                .then_inc(*dve_done.mark(f"max{r}"))
                    dve.wait_ge(*act_done.at(f"exp{r}"))
                    v.scalar_tensor_tensor(out=S[:, r, :], in0=left, scalar=CHOSEN, in1=S[:, r, :],
                                           op0=ALU.is_le, op1=ALU.mult, accum_out=total[:, r:r + 1])\
                        .then_inc(*dve_done.mark(f"kept{r}"))
                    dve.wait_ge(*dve_done.at(f"kept{r}"))
                step(v.reciprocal(inverse[:, :], total[:, :]))
                for r in range(R):
                    ins = v.tensor_scalar(pick[:, r, :], mem.w("consts", "mean_heads"), inverse[:, r:r + 1],
                                          None, ALU.mult)
                ins.then_inc(*dve_done.mark("picks"))
                for b in range(BLOCKS):
                    lo, hi = b * TPB, min(KT_TILES, (b + 1) * TPB)
                    dve.wait_ge(turned, b + 1)
                    v.tensor_copy(turnedT[:, lo:hi, :],
                                  ps[:, 1 + b % 3, 0:(hi - lo) * T].rearrange("p (n t) -> p n t", t=T))\
                        .then_inc(turned_copied, 1)
                dve.wait_ge(*pe_done.at("pooledT"))
                v.tensor_copy(pooledT[:, :], ps[0:CTX, 7, 0:T]).then_inc(*dve_done.mark("pooled"))
                dve.wait_ge(*pe_done.at("contextT"))
                v.tensor_tensor(contextT[:, :], ps[0:C, 0, 0:T], token_mask[:, :], ALU.mult)\
                    .then_inc(*dve_done.mark("contextT"))
                dve_moments(mem, mem.xn[:, :], "a_var")
                dve_normalised(mem, a[:, :], mem.xn[:, :], "a_rstd").then_inc(*dve_done.mark("a"))
                gate, (at_in, _, _), (at_out, _, _) = w("mod_gate"), column("l2x", "b_film_in"), column("l2x", "b_film_out")
                dve.wait_ge(*pe_done.at("film"))
                for n in range(4):
                    at = (at_in, at_out)[n // 2] + n % 2
                    ins = v.tensor_scalar(film[:, n, :], ps[0:C, 4, n * T:(n + 1) * T],
                                          mem.packs["l2x"][:, at:at + 1], gate, ALU.add, ALU.mult)
                step(ins)
                dve.wait_ge(*pe_done.at("aT"))
                step(v.tensor_scalar(aT[:, :], ps[0:C, 5, 0:T], w("g_norm_in"), w("b_norm_in"), ALU.mult, ALU.add))
                step(v.scalar_tensor_tensor(out=aT[:, :], in0=film[:, 0, :], scalar=1.0, in1=aT[:, :],
                                            op0=ALU.add, op1=ALU.mult))
                recent = padded[:, T - 1:2 * T - 1]
                step(v.tensor_tensor(recent, aT[:, :], film[:, 1, :], ALU.add))
                window = padded[:, :]
                window = bass.AP(window.tensor, window.offset, [list(window.ap[0]), [1, T], [1, T]])
                step(v.tensor_tensor(products, window, spread(mem.kernel_reversed[:, :], 1, [C, T, T]),
                                     ALU.mult))
                step(v.tensor_reduce(mixed[:, :], products, AX_X, ALU.add))
                step(v.scalar_tensor_tensor(out=mixed[:, :], in0=recent, scalar=w("D_skip"), in1=mixed[:, :],
                                            op0=ALU.mult, op1=ALU.add))
                step(v.scalar_tensor_tensor(out=mixed[:, :], in0=film[:, 2, :], scalar=1.0, in1=mixed[:, :],
                                            op0=ALU.add, op1=ALU.mult))
                v.tensor_tensor(mixed[:, :], mixed[:, :], film[:, 3, :], ALU.add)\
                    .then_inc(*dve_done.mark("film_out"))
                dve.wait_ge(*pe_done.at("mixed"))
                step(v.tensor_tensor(x_mid[:, :], ps[0:T, 6, 0:C], mem.xn[:, :], ALU.add))
                dve_moments(mem, x_mid[:, :], "x_mid_var")
                dve_normalised(mem, h[:, :], x_mid[:, :], "h_rstd").then_inc(*dve_done.mark("h"))
                step(v.tensor_tensor(x_mid[:, :], x_mid[:, :], mem.row("l2x_b2"), ALU.add))
                dve.wait_ge(*pe_done.at("hT"))
                v.tensor_scalar(hT[:, :], ps[0:C, 0, 0:T], w("g_ffn"), w("b_ffn"), ALU.mult, ALU.add)\
                    .then_inc(*dve_done.mark("hT"))
                dve.wait_ge(*pe_done.at("hidden"))
                v.tensor_tensor(pre[:, :, :], ps[0:C, 1, 0:4 * T].rearrange("p (n t) -> p n t", t=T),
                                spread(w("b1"), 2, [C, 4, T]), ALU.add).then_inc(*dve_done.mark("hidden"))
                dve.wait_ge(*pe_done.at("out"))
                step(v.tensor_tensor(out[:, :], ps[0:T, 2, 0:C], x_mid[:, :], ALU.add))
                dve_moments(mem, out[:, :], "out_var")
                step(dve_normalised(mem, out[:, :], out[:, :], "out_rstd"))
                step(v.tensor_tensor(out[:, :], out[:, :], mem.row("l2x_g_out"), ALU.mult))
                step(v.tensor_tensor(out[:, :], out[:, :], mem.row("l2x_b_out"), ALU.add))
                v.tensor_tensor(mem.x[:, :], mem.x[:, :], out[:, :], ALU.add).then_inc(*dve_done.mark("x"))



def stage_store(mem):
    nc = mem.nc
    stored = mem.sem("stored")
    with nc.Block() as block:

        @block.sync
        def _(sp):
            sp.dma_start(mem.dram["out"], mem.x[:, :]).then_inc(stored, 16)
            sp.wait_ge(stored, 16)
            for pack in SMALL:
                sp.wait_ge(mem.loaded[pack], 16)


def build(nc, dram):
    with ExitStack() as ctx:
        mem = Memory(nc, ctx, dram)
        stage_load(mem)
        for stage in STAGES:
            stage(mem)
        stage_store(mem)


def first_cross_attention(mem):
    stage_cross_attention(mem, 0, context_load=1)


def second_cross_attention(mem):
    stage_cross_attention(mem, 1, context_load=2)


def third_cross_attention(mem):
    stage_state_kernel(mem)
    stage_topk_attention(mem, context_load=3)


def fourth_cross_attention(mem):
    stage_cross_attention(mem, 3, context_load=4)


STAGES = [first_cross_attention, stage_rwkv, lambda mem: stage_topk_experts(mem, 0),
          second_cross_attention, stage_rope_attention, stage_quantised_ffn,
          third_cross_attention, stage_local_attention, stage_transformer_experts,
          fourth_cross_attention, stage_past_attention, lambda mem: stage_topk_experts(mem, 3)]



def shape_constants():
    p = np.arange(128)
    t = np.arange(T)
    key = np.arange(T)
    half = DH // 2
    inv_freq = (1.0 / 10000.0 ** (np.arange(half, dtype=np.float32) / half)).astype(np.float32)
    angle = t.astype(np.float32)[:, None] * inv_freq[None, :]
    cos, sin = np.cos(angle).astype(np.float32), np.sin(angle).astype(np.float32)
    query = p % T
    strict = (key[None, :] < t[:, None]) | ((t[:, None] == 0) & (key[None, :] == 0))

    def masked(keep):
        return np.where(keep, 0.0, -1e30).astype(np.float32)

    return {
        "ident": np.eye(128, dtype=np.float32),
        "four_heads": (p[:, None] // DH % HG == np.arange(HG)[None, :]).astype(np.float32),
        "two_heads": (p[:, None] // D2 % 2 == np.arange(2)[None, :]).astype(np.float32),
        "even_out": np.tile(p[None, :] % 2 == 0, (128, 1)).astype(np.float32),
        "odd_out": np.tile(p[None, :] % 2 == 1, (128, 1)).astype(np.float32),
        "causal": masked(key[None, :] <= query[:, None]),
        "band": masked(np.abs(key[None, :] - query[:, None]) <= 3),
        "strict": masked(strict),
        "cos": np.concatenate([cos, cos], axis=1),
        "sin": np.concatenate([-sin, sin], axis=1),
        "mean_heads": (np.float32(1.0 / H2) * (query[:, None] == t[None, :])).astype(np.float32),
    }


def layouts(a):
    def col(v):
        return v.reshape(-1, 1)

    def cols(v):
        return v.reshape(-1, C).T

    def fill(v):
        return np.broadcast_to(v.reshape(1, 1), (C, 1))

    def with_bias(w, b):
        return np.concatenate([w, b.reshape(1, -1)], axis=0)

    def rows_of(w):
        return w.reshape(-1, C, w.shape[-1]).transpose(1, 0, 2).reshape(C, -1)

    def whole_rows(w):
        n = -(-w.shape[0] // C)
        out = np.zeros((n * C, w.shape[1]), w.dtype)
        out[:w.shape[0]] = w
        return rows_of(out)

    def first(w):
        return w.transpose(1, 0, 2).reshape(C, -1)

    def second(w):
        return rows_of(w.reshape(-1, C))

    def get(prefix, **names):
        return {k: a[prefix + v] for k, v in names.items()}

    p0, p1, p2, p3 = "L0_attn_", "L1_ffn_", "L2_xattn_", "L3_ffn_"
    kv_w, kv_b = a["L3_xattn_Wkv"].reshape(H, 2, DH, CTX), a["L3_xattn_bkv"].reshape(H, 2, DH)
    shared = {n: np.concatenate([a[p3 + n], a[p3 + n + "_s"][None]], axis=0)
              for n in ["Wfc", "bfc", "Wproj", "bproj"]}
    packs = {
        "consts": shape_constants(),
        "l0x": {"Wq": a["L0_xattn_Wq"], "Wk": with_bias(a["L0_xattn_Wk"], a["L0_xattn_bk"]),
                "Wv": with_bias(a["L0_xattn_Wv"], a["L0_xattn_bv"]), "Wo": a["L0_xattn_Wo"]},
        "l0a": {"Wcv": rows_of(a[p0 + "Wcv"])}
        | {n: a[p0 + n] for n in ["Wk", "Wv", "Wr", "Wo", "Wck", "Wcr"]}
        | {n: col(a[p0 + n]) for n in ["ln0_g", "ln0_b", "ln1_g", "ln1_b", "time_decay", "time_first",
                                       "tm_k", "tm_v", "tm_r", "cm_k", "cm_r"]},
        "l0f": {"w_router": a["L0_ffn_w_router"], "b1": cols(a["L0_ffn_b1"]), "b2": a["L0_ffn_b2"]},
        "l1x": {"Wq": a["L1_xattn_Wq"].T, "Wk": with_bias(a["L1_xattn_Wk"].T, a["L1_xattn_bk"]),
                "Wv": with_bias(a["L1_xattn_Wv"].T, a["L1_xattn_bv"]), "Wo": a["L1_xattn_Wo"].T,
                "bq": col(a["L1_xattn_bq"])},
        "l1a": {"w_qkv": a["L1_attn_w_qkv"], "w_o": a["L1_attn_w_o"]},
        "l1f": {"w_gate": whole_rows(a[p1 + "w_gate"]), "w_up": whole_rows(a[p1 + "w_up"]),
                "w_down": a[p1 + "w_down"], "clip_x": fill(a[p1 + "clip_x"]),
                "clip_down": fill(a[p1 + "clip_down"])},
        "l2x": {n: a[p2 + n] for n in ["Wq", "Wk", "Wv", "W_film_in", "W_film_out", "W1", "A_re", "A_im",
                                       "C_re", "C_im"]}
        | {n: col(a[p2 + n]) for n in ["g_norm_in", "b_norm_in", "g_ffn", "b_ffn", "D_skip", "log_dt"]}
        | {n: cols(a[p2 + n]) for n in ["b_film_in", "b_film_out", "b1"]}
        | {"W2": rows_of(a[p2 + "W2"]), "mod_gate": fill(a[p2 + "mod_gate"])},
        "l2a": {n: a["L2_attn_" + n] for n in ["w_q", "w_k", "w_v", "w_o"]}
        | {n: col(a["L2_attn_" + n]) for n in ["b_q", "b_k"]},
        "l2f": {"w_in": a["L2_ffn_in_proj_w"].T, "w_out": a["L2_ffn_out_proj_w"].T,
                "w_group": a["L2_ffn_w_group"],
                "w_expert": a["L2_ffn_w_expert"].transpose(1, 0, 2).reshape(C, E),
                "b1": cols(a["L2_ffn_b1"]), "b2": a["L2_ffn_b2"]},
        "l3x": {"Wq": a["L3_xattn_Wq"].T, "Wo": a["L3_xattn_Wo"].T, "bq": col(a["L3_xattn_bq"]),
                "Wk": with_bias(kv_w[:, 0].reshape(C, CTX).T, kv_b[:, 0].reshape(C)),
                "Wv": with_bias(kv_w[:, 1].reshape(C, CTX).T, kv_b[:, 1].reshape(C))},
        "l3a": {"w_dec": a["L3_attn_w_dec_attn"], "w_out": rows_of(a["L3_attn_w_out"].T)},
        "l3f": {"w_router": a[p3 + "Wr"], "b1": cols(shared["bfc"]), "b2": shared["bproj"]},
        "experts0": {"w1": first(a["L0_ffn_w1"]), "w2": second(a["L0_ffn_w2"])},
        "experts2": {"w1": first(a["L2_ffn_w1"]), "w2": second(a["L2_ffn_w2"])},
        "experts3": {"w1": first(shared["Wfc"]), "w2": second(shared["Wproj"])},
        "rows": {n: v.reshape(1, -1) for n, v in {
            "l0x_bq": a["L0_xattn_bq"], "l0x_bo": a["L0_xattn_bo"], "l0x_gamma": a["L0_xattn_ln_gamma"],
            "l0x_beta": a["L0_xattn_ln_beta"], "l1x_bo": a["L1_xattn_bo"],
            "l2x_g_out": a[p2 + "g_norm_out"], "l2x_b_out": a[p2 + "b_norm_out"], "l2x_b2": a[p2 + "b2"],
            "l2a_bv": a["L2_attn_b_v"], "l2a_bo": a["L2_attn_b_o"], "l2f_b_in": a["L2_ffn_in_proj_b"],
            "l2f_b_out": a["L2_ffn_out_proj_b"], "l2f_g1": a["L2_ffn_ln1_g"], "l2f_b1": a["L2_ffn_ln1_b"],
            "l2f_g2": a["L2_ffn_ln2_g"], "l2f_b2": a["L2_ffn_ln2_b"], "l2f_b_group": a["L2_ffn_b_group"],
            "l2f_b_expert": a["L2_ffn_b_expert"], "l3x_bo": a["L3_xattn_bo"],
            "l3a_bo": a["L3_attn_b_out"]}.items()},
    }
    out = {}
    for pack, parts in packs.items():
        height = 1 if pack == "rows" else 128
        out[pack] = np.zeros((height, width(pack)), np.float32)
        for name, array in parts.items():
            at, rows, n = column(pack, name)
            assert array.shape == (rows, n), (pack, name, array.shape)
            out[pack][0:rows, at:at + n] = array
        assert len(parts) == len(PACKS[pack]), pack
    context = a["ctx_768"][0]
    out["ctx_t"] = np.concatenate([context.T, np.ones((1, KEYS), np.float32)], axis=0)
    out["ctx_tiles"] = context.reshape(KT_TILES, 128, CTX).transpose(1, 0, 2).reshape(128, KT_TILES * CTX)
    out["bias_rows"] = np.full((2, SUPERS, G, SUPER), BIAS_ROW, np.float16)
    out["token_mask"] = a["mask_BxS_bf1"].view(np.uint8).reshape(1, T)
    out["context_mask"] = a["mask_BxS2_bf1"].view(np.uint8).reshape(1, KEYS)
    out["x"] = a["x"][0]
    return {k: np.ascontiguousarray(v) for k, v in out.items()}


def kernel(**inputs):
    import concourse.bacc as bacc
    from concourse.bass_utils import run_bass_kernel_spmd

    nc = bacc.Bacc("TRN2", target_bir_lowering=False, num_devices=1)
    arrays = layouts({k: np.asarray(v) for k, v in inputs.items()})
    dram = {name: nc.dram_tensor(f"in_{name}", array.shape, mybir.dt.from_np(array.dtype),
                                 kind="ExternalInput").ap() for name, array in arrays.items()}
    dram["out"] = nc.dram_tensor("out_x", (T, C), F32, kind="ExternalOutput").ap()
    build(nc, dram)
    result = run_bass_kernel_spmd(nc, [{f"in_{k}": v for k, v in arrays.items()}], core_ids=[0])
    return result.results[0]["out_x"].reshape(1, T, C)
```

```python
from contextlib import ExitStack
from itertools import islice

import concourse.bass as bass
from concourse import mybir
import numpy as np

F32 = mybir.dt.float32
BF16 = mybir.dt.bfloat16
F16 = mybir.dt.float16
I32 = mybir.dt.int32
U8 = mybir.dt.uint8
ACT = mybir.ActivationFunctionType
ALU = mybir.AluOpType
AX_X = mybir.AxisListType.X

T = 64
C = 128
H = 16
DH = C // H
G = 4
HG = H // G
KEYS = 6272
CTX = 96
KT_TILES = KEYS // 128
CHUNK = 512
CHUNKS = -(-KEYS // CHUNK)
SUPER = 896
SUPERS = KEYS // SUPER
TPS = SUPER // 128
HALF = SUPER // 2
E = 8
HID = 512
HID2 = 256
FFQ = 352
FFQ_CHUNKS = [(0, 128), (128, 128), (256, 96)]
H2, D2, TOPK = 4, 32, 32
NSTATE = 64
LN_EPS = 1e-5
SCALE = DH ** -0.5
LOWEST = -3.0e38
CTX_FIRST = 2
EARLY1 = [4, 2, 4, 2, 0]
EARLY3 = [2, 1, 1, 0, 4, 0, 2, 2, 2]
BIAS_ROW = 4096.0
EXPONENT_BITS, MAGNITUDE_BITS = 0x7F800000, 0x7FFFFFFF
ROUND = 12582912.0
LOG2E = 1.4426950408889634
LN2_HI, LN2_LO = 0.693145751953125, 1.4286068203094172e-06
TWO_PI_HI, TWO_PI_MID, TWO_PI_LO = 6.28125, 0.0019350051879882812, 3.0199157663e-07

PACKS = {
    "consts": [("ident", 128, 128), ("four_heads", 128, HG), ("large_heads", 128, H2),
               ("even_out", 128, 128), ("odd_out", 128, 128), ("causal", 128, T), ("band", 128, T),
               ("strict", T, T), ("cos", T, DH), ("sin", T, DH), ("mean_heads", 128, T), ("both_halves", 128, T)],
    "l0x": [("Wq", C, C), ("Wk", CTX + 1, C), ("Wv", CTX + 1, C), ("Wo", C, C)],
    "l0a": [("Wk", C, C), ("Wv", C, C), ("Wr", C, C), ("Wo", C, C), ("Wck", C, HID),
            ("Wcv", C, HID), ("Wcr", C, C), ("ln0_g", C, 1), ("ln0_b", C, 1), ("ln1_g", C, 1),
            ("ln1_b", C, 1), ("time_decay", C, 1), ("time_first", C, 1), ("tm_k", C, 1),
            ("tm_v", C, 1), ("tm_r", C, 1), ("cm_k", C, 1), ("cm_r", C, 1)],
    "l0f": [("w_router", C, E), ("b1", C, E * HID // C), ("b2", E, C)],
    "l1x": [("Wq", C, C), ("Wk", CTX + 1, C), ("Wv", CTX + 1, C), ("Wo", C, C), ("bq", C, 1)],
    "l1a": [("w_qkv", C, 192), ("w_o", C, C)],
    "l1f": [("w_gate", C, 3 * C), ("w_up", C, 3 * C), ("w_down", C, FFQ), ("clip_x", C, 1),
            ("clip_down", C, 1)],
    "l2x": [("Wq", C, C), ("WkT", C, CTX), ("Wv", CTX, C), ("W_film_in", C, 2 * C),
            ("W_film_out", C, 2 * C), ("W1", C, HID), ("W2", C, HID), ("b_film_in", C, 2),
            ("b_film_out", C, 2), ("g_norm_in", C, 1), ("b_norm_in", C, 1), ("g_ffn", C, 1),
            ("b_ffn", C, 1), ("b1", C, HID // C), ("D_skip", C, 1), ("log_dt", C, 1),
            ("mod_gate", C, 1), ("A_re", C, NSTATE), ("A_im", C, NSTATE), ("C_re", C, NSTATE),
            ("C_im", C, NSTATE)],
    "l2a": [("w_q", C, C), ("w_k", C, C), ("w_v", C, C), ("w_o", C, C), ("b_q", C, 1), ("b_k", C, 1)],
    "l2f": [("w_in", C, 3 * C), ("w_out", C, C), ("w_group", C, 4), ("w_expert", C, E),
            ("b1", C, E * HID2 // C), ("b2", E, C)],
    "l3x": [("Wq", C, C), ("Wk", CTX + 1, C), ("Wv", CTX + 1, C), ("Wo", C, C), ("bq", C, 1)],
    "l3a": [("w_dec", C, C), ("w_out", C, 2 * C)],
    "l3f": [("w_router", C, E), ("b1", C, (E + 1) * HID // C), ("b2", E + 1, C)],
    "experts0": [("w1", C, E * HID), ("w2", C, E * HID)],
    "experts2": [("w1", C, E * HID2), ("w2", C, E * HID2)],
    "experts3": [("w1", C, (E + 1) * HID), ("w2", C, (E + 1) * HID)],
    "rows": [(n, 1, w) for n, w in [
        ("l0x_bq", C), ("l0x_bo", C), ("l0x_gamma", C), ("l0x_beta", C), ("l1x_bo", C),
        ("l2x_g_out", C), ("l2x_b_out", C), ("l2x_b2", C), ("l2a_bv", C), ("l2a_bo", C),
        ("l2f_b_in", 3 * C), ("l2f_b_out", C), ("l2f_g1", C), ("l2f_b1", C), ("l2f_g2", C),
        ("l2f_b2", C), ("l2f_b_group", 4), ("l2f_b_expert", E), ("l3x_bo", C), ("l3a_bo", C)]],
}
SMALL = ["consts", "l0x", "l0a", "l0f", "l1x", "l1a", "l1f", "l2x", "l2a", "l2f", "l3x", "l3a", "l3f"]


def width(pack):
    return sum(cols for _, _, cols in PACKS[pack])


def column(pack, name):
    at = 0
    for n, rows, cols in PACKS[pack]:
        if n == name:
            return at, rows, cols
        at += cols
    raise KeyError(name)


class Events:

    def __init__(self, sem):
        self.sem, self.base, self.order, self.sent = sem, 0, [], 0

    def stage(self, *names):
        assert self.sent == len(self.order), self.order[self.sent:]
        self.base += len(self.order)
        self.order, self.sent = list(names), 0

    def mark(self, name):
        assert self.order[self.sent] == name, (self.order[self.sent], name)
        self.sent += 1
        return self.sem, 1

    def at(self, name):
        return self.sem, self.base + self.order.index(name) + 1


class Chain:

    def __init__(self, engine, sem):
        self.engine, self.sem, self.n = engine, sem, 0

    def __call__(self, ins):
        self.n += 1
        ins.then_inc(self.sem, 1)
        self.engine.wait_ge(self.sem, self.n)


def spread(ap, axis, shape):
    return ap.unsqueeze(axis).to_broadcast(shape)


class Memory:

    def __init__(self, nc, ctx, dram):
        self.nc, self.ctx, self.dram = nc, ctx, dram

        def sb(name, shape, dt=F32):
            return ctx.enter_context(nc.sbuf_tensor(name, shape, dt))

        self.sem = lambda name: ctx.enter_context(nc.semaphore(name))
        self.psum = ctx.enter_context(nc.psum_tensor("psum", [128, 8, 512], F32))
        self.x = sb("x", [T, C])
        self.wide = sb("wide", [128, 2 * KEYS])
        self.ctx_t = self.wide[0:CTX + 1, KEYS:2 * KEYS]
        self.keys_t = sb("keys_t", [128, KEYS])
        self.values = sb("values", [128, KT_TILES * C])
        self.experts = sb("experts", [128, width("experts3")])
        self.ctx_top = sb("ctx_top", [CTX + 1, SUPERS + 1])
        self.rows = sb("rows", [T, width("rows")])
        self.packs = {p: sb("w_" + p, [128, width(p)]) for p in SMALL}
        self.minus_half = sb("minus_half", [128, KT_TILES])
        self.ones = sb("ones", [128, 128])
        self.kernel_reversed = sb("kernel_reversed", [C, T])
        self.xn = sb("xn", [T, C])
        self.stats = sb("stats", [T, 6])
        self.moments = sb("moments", [T, 2])
        self.rstd = sb("rstd", [T, 2])
        self.loaded = {p: self.sem("loaded_" + p) for p in
                       SMALL + ["x", "ctx_first", "ctx_rest", "rows", "experts0", "experts2", "experts3"]}
        self.pe_done = Events(self.sem("pe_done"))
        self.act_done = Events(self.sem("act_done"))
        self.dve_done = Events(self.sem("dve_done"))
        self.pool_done = Events(self.sem("pool_done"))
        self.early_values = {}
        self.dve_step = Chain(nc.vector, self.sem("dve_order"))
        self.act_step = Chain(nc.scalar, self.sem("act_order"))
        self.pool_step = Chain(nc.gpsimd, self.sem("pool_order"))

    def w(self, pack, name):
        at, rows, cols = column(pack, name)
        return self.packs[pack][0:rows, at:at + cols]

    def row(self, name):
        at, _, cols = column("rows", name)
        return self.rows[:, at:at + cols]



def pool_power(mem, out, base, exponent, when, event):
    nc = mem.nc
    nc.gpsimd.wait_ge(*when)
    nc.gpsimd.tensor_tensor(out, base, exponent, ALU.pow).then_inc(*mem.pool_done.mark(event))


def dve_moments(mem, source, event, slot=0):
    nc, step = mem.nc, mem.dve_step
    step(nc.vector.bn_stats(mem.stats[:, :], source))
    step(nc.vector.bn_aggr(mem.moments[:, :], mem.stats[:, :]))
    nc.vector.tensor_scalar(mem.rstd[:, 0:1], mem.moments[:, 1:2], LN_EPS, None, ALU.add)\
        .then_inc(*mem.dve_done.mark(event))


def pool_rstd(mem, when, event):
    pool_power(mem, mem.rstd[:, 1:2], mem.rstd[:, 0:1], mem.minus_half[0:T, 0:1],
               mem.dve_done.at(when), event)


def dve_normalised(mem, out, source, when):
    mem.nc.vector.wait_ge(*mem.pool_done.at(when))
    return mem.nc.vector.tensor_scalar(out, source, mem.moments[:, 0:1], mem.rstd[:, 1:2],
                                       ALU.subtract, ALU.mult)



def load_context(mem, sp):
    for name, lo, hi in [("ctx_first", 0, CTX_FIRST * SUPER), ("ctx_rest", CTX_FIRST * SUPER, KEYS)]:
        sp.dma_start(mem.ctx_t[:, lo:hi], mem.dram["ctx_t"][:, lo:hi]).then_inc(mem.loaded[name], 16)


class EarlyValues:

    def __init__(self, mem, pack, context_load):
        self.mem, self.pack, self.context_load = mem, pack, context_load
        self.projected, self.copied = mem.sem(f"{pack}_early_projected"), mem.sem(f"{pack}_early_copied")
        self.units_projected = self.units_copied = 0

    def tiles(self, unit):
        first = unit // 2 * TPS + unit % 2 * 4
        tiles = range(first, first + (3 if unit % 2 else 4))
        return tiles, self.mem.psum[:, 5 + unit % 2, 0:len(tiles) * C]

    def pe(self, pe, count):
        for unit in range(self.units_projected, self.units_projected + count):
            tiles, bank = self.tiles(unit)
            if unit == 0:
                pe.wait_ge(self.mem.loaded[self.pack], 16)
                pe.wait_ge(self.mem.loaded["ctx_first"], 16 * self.context_load)
            if unit == 2 * CTX_FIRST:
                pe.wait_ge(self.mem.loaded["ctx_rest"], 16 * self.context_load)
            if unit >= 2:
                pe.wait_ge(self.copied, unit - 1)
            for i, t in enumerate(tiles):
                last = self.mem.nc.tensor.matmul(
                    bank[:, i * C:(i + 1) * C], self.mem.ctx_t[:, t * 128:(t + 1) * 128],
                    self.mem.w(self.pack, "Wv"), start=True, stop=True)
            last.then_inc(self.projected, 1)
        self.units_projected += count

    def act(self, act, count):
        for unit in range(self.units_copied, self.units_copied + count):
            tiles, bank = self.tiles(unit)
            act.wait_ge(self.projected, unit + 1)
            self.mem.nc.scalar.activation(self.mem.values[:, tiles[0] * C:(tiles[-1] + 1) * C], bank,
                                          ACT.Identity).then_inc(self.copied, 1)
        self.units_copied += count


def load_pack(mem, sp, pack):
    sp.dma_start(mem.packs[pack][:, :], mem.dram[pack]).then_inc(mem.loaded[pack], 16)


def load_later(mem, sp):
    for pack in ["l0a", "l0f"]:
        load_pack(mem, sp, pack)
    sp.dma_start(mem.experts[:, 0:width("experts0")], mem.dram["experts0"]).then_inc(mem.loaded["experts0"], 16)
    for pack in ["l1x", "l1a", "l1f", "l2x", "l2a", "l2f", "l3x", "l3a", "l3f"]:
        load_pack(mem, sp, pack)


def stage_load(mem):
    nc, dram = mem.nc, mem.dram
    constants_set = mem.sem("constants_set")

    with nc.Block(no_gpsimd_drain=True) as block:

        @block.sync
        def _(sp):
            sp.dma_start(mem.x[:, :], dram["x"]).then_inc(mem.loaded["x"], 16)
            load_pack(mem, sp, "l0x")
            load_pack(mem, sp, "consts")
            load_context(mem, sp)
            sp.dma_start(mem.rows[:, :], dram["rows"].to_broadcast([T, width("rows")]))\
                .then_inc(mem.loaded["rows"], 16)

        @block.vector
        def _(dve):
            nc.vector.memset(mem.ones[:, :], 1.0).then_inc(constants_set, 1)
            nc.vector.memset(mem.minus_half[:, :], -0.5).then_inc(constants_set, 1)
            dve.wait_ge(constants_set, 2)



def stage_cross_attention(mem, level, context_load):
    nc = mem.nc
    pe_done, act_done, dve_done, pool_done = mem.pe_done, mem.act_done, mem.dve_done, mem.pool_done
    step = mem.dve_step
    pack = f"l{level}x"
    unit = level == 0
    ps = mem.psum
    ident = mem.w("consts", "ident")
    four_heads = mem.w("consts", "four_heads")
    O_BANK, DEN_BANK, Y_BANK = 6, 7, 0
    RING = 3
    PROBS = 4
    POOL_TILES = range(2, KT_TILES, 3)
    HALVES = 2 * SUPERS
    COPIES = 3
    STACK = 96 if unit else 98
    BATCHES = [(0, 2), (2, 4), (4, 6), (6, 7)]
    PER_BATCH = 12 if unit else 13
    order = [("K", 0), ("K", 1), ("V", 0), ("K", 2), ("V", 1), ("K", 3)]
    order += [p for u in range(2, SUPERS) for p in [("V", u), ("K", 2 * u), ("K", 2 * u + 1)]]
    ready = mem.early_values[level].units_copied // 2 if level in mem.early_values else 0
    order = [(kind, n) for kind, n in order if kind == "K" or n >= ready]
    first = order.index(("K", 3))
    at_once, afterwards = order[:first], order[first:]

    act_done.stage()
    if unit:
        pe_done.stage("key_bound", "xnT", "Qp", "QT", "q_topT", "q_top_all", "den", "projected")
        dve_done.stage("keys_abs", "var", "xn", "ctx_top", "key_gain", "xnT", "q_sum", "Qn", "QT", "q_top",
                       "q_top1", "Q_stack", "key_scale", "OT", "out_var", "x")
        pool_done.stage("rstd", "q_rsqrt", "out_rstd")
    else:
        pe_done.stage("key_bound", "xnT", "QT", "q_topT", "q_top_all", "max_cols", "den", "projected")
        dve_done.stage("keys_abs", "var", "xn", "key_gain", "xnT", "QT", "q_top", "q_top1", "Q_stack",
                       "max_parts", "max_cols", "OT", "x")
        pool_done.stage("rstd")

    def sem(name):
        return mem.sem(f"{pack}_{name}")

    keys_projected, high_ready, low_ready = sem("keys_projected"), sem("high_ready"), sem("low_ready")
    stacked = [sem(f"stacked{b}") for b in range(len(BATCHES))]
    values_projected, values_copied = sem("values_projected"), sem("values_copied")
    scores_ready, probs_ready = sem("scores_ready"), sem("probs_ready")
    pv_done, sum_done, pool_sum_done = sem("pv_done"), sem("sum_done"), sem("pool_sum_done")
    if unit:
        squares_ready, norms_ready = sem("squares_ready"), sem("norms_ready")
        key_sum_tiles = [slice(0, (SUPERS - 2) * TPS), slice((SUPERS - 2) * TPS, KT_TILES)]
        key_sums_ready, key_rsqrt_ready = sem("key_sums_ready"), sem("key_rsqrt_ready")
    else:
        max_scores, max_taken = sem("max_scores"), sem("max_taken")
        max_copied, max_folded = sem("max_copied"), sem("max_folded")

    def stacked_with(u):
        return stacked[next(b for b, (lo, hi) in enumerate(BATCHES) if lo <= u < hi)], 16 * PER_BATCH

    def summed(t):
        before = len([p for p in POOL_TILES if p < t])
        return (pool_sum_done, before + 1) if t in POOL_TILES else (sum_done, t - before + 1)

    every_part = [(n, s) for n in range(HALVES) for s in range(2)]
    taken_parts = [(n, s) for n, s in every_part if s == 0 and n % 2 == 0]
    copied_parts = [part for part in every_part if part not in taken_parts]

    def part_read(n, s, p):
        if (n, s) in taken_parts:
            return max_taken, 2 * taken_parts.index((n, s)) + p + 1
        return max_copied, 2 * copied_parts.index((n, s)) + p + 1

    stack = mem.wide[:, :].bitcast(F16).rearrange("p (u g k) -> p u g k", u=SUPERS, g=G)
    parts_of_keys = mem.keys_t[:, :].bitcast(F16).rearrange("p (u n k) -> p u n k", u=SUPERS, n=2)
    probs = mem.keys_t[:, 0:PROBS * H * T].rearrange("p (b n) -> p b n", b=PROBS)
    prob_sum = mem.keys_t[:, PROBS * H * T:(PROBS + 1) * H * T]

    with ExitStack() as local:
        def sb(name, shape, dt=F32):
            return local.enter_context(nc.sbuf_tensor(f"{pack}_{name}", shape, dt))

        keys_abs = sb("keys_abs", [CTX + 1, C])
        key_gain, query_gain = sb("key_gain", [C, 1]), sb("query_gain", [C, 1])
        exp_gain, gain = sb("exp_gain", [C, 1]), sb("gain", [C, 1])
        power, inverse = sb("power", [C, 1]), sb("inverse", [C, 1])
        q_top, q_top1 = sb("q_top", [C, 1]), sb("q_top1", [1, 1])
        xnT = sb("xnT", [C, T])
        QT = sb("QT", [C, T])
        Qbd = sb("Qbd", [C, HG, T])
        Q_high, Q_low = sb("Q_high", [C, HG * T], F16), sb("Q_low", [C, HG * T], F16)
        Q_stack = sb("Q_stack", [C, G, HG * T], F16)
        OT = sb("OT", [C, T])
        residual = sb("residual", [T, C])
        if unit:
            Qp, Qn, sq = sb("Qp", [T, C]), sb("Qn", [T, C]), sb("sq", [T, C])
            q_sum, q_rsqrt = sb("q_sum", [T, 1]), sb("q_rsqrt", [T, 1])
            squares = sb("squares", [128, 2, SUPER])
            pool_sum = squares[:, :, :].rearrange("p u k -> p (u k)")[:, 0:H * T]
            key_sums, key_scale = sb("key_sums", [128, KT_TILES]), sb("key_scale", [128, KT_TILES])
            z, zn = sb("z", [T, C]), sb("zn", [T, C])
            rden, weighted = sb("rden", [C, HG, T]), sb("weighted", [C, HG, T])
        else:
            maxima = sb("maxima", [128, G, len(taken_parts)])
            taken_max = sb("taken_max", [128, G])
            rows16 = sb("rows16", [128, COPIES + 2, G, HALF], F16)
            copies, folded = rows16[:, 0:COPIES, :, :], rows16[:, COPIES:COPIES + 2, :, :]
            late = rows16[:, :, :, :].rearrange("p i g k -> p (i g k)").bitcast(F32)
            rden, weighted = [late[:, i * HG * T:(i + 1) * HG * T].rearrange("p (h t) -> p h t", h=HG)
                              for i in range(2)]
            pool_sum = late[:, 2 * HG * T:2 * HG * T + H * T]
            row_max = sb("row_max", [128, G * 2])
            high16 = sb("high16", [128, G * 2], F16)
            parts = sb("parts", [128, 2, G * 2])
            diag = rows16[:, :, :, :].rearrange("p i g k -> p (i g k)")[:, 0:4 * G * 128]\
                .rearrange("p (a c q) -> p a c q", a=2, c=G * 2)
            picks = sb("picks", [128, 2, 128], F16)

        with nc.Block(no_gpsimd_drain=True) as block:

            @block.sync
            def _(sp):
                if level == 3:
                    sp.dma_start(mem.experts[:, :], mem.dram["experts3"]).then_inc(mem.loaded["experts3"], 16)
                if level == 0:
                    load_later(mem, sp)
                for b, (lo, hi) in enumerate(BATCHES):
                    sp.wait_ge(high_ready, 2 * hi)
                    sp.wait_ge(low_ready, 2 * hi)
                    under = max(0, 2 * hi - SUPERS)
                    sp.wait_ge(keys_projected, 2 * max(under, hi))
                    if under > ready:
                        sp.wait_ge(values_projected, under - ready)
                    for g in range(G):
                        for block_row, part in enumerate([0, 1, 0]):
                            sp.dma_start(stack[32 * block_row:32 * block_row + 32, lo:hi, g, :],
                                         parts_of_keys[32 * g:32 * g + 32, lo:hi, part, :]).then_inc(stacked[b], 16)
                    if not unit:
                        sp.dma_start(stack[96:98, lo:hi, :, :], mem.dram["bias_rows"][:, lo:hi, :, :])\
                            .then_inc(stacked[b], 16)
                if level == 0:
                    sp.wait_ge(scores_ready, KT_TILES)
                    load_context(mem, sp)

            @block.tensor
            def _(pe):
                def project(kind, n):
                    if kind == "K":
                        if n >= 3:
                            pe.wait_ge(low_ready, n - 2)
                        nc.tensor.matmul(ps[:, 1 + n % 3, 0:HALF], mem.w(pack, "Wk"),
                                         mem.ctx_t[:, n * HALF:(n + 1) * HALF], start=True, stop=True)\
                            .then_inc(keys_projected, 1)
                        return
                    if n >= ready + 2:
                        pe.wait_ge(values_copied, n - ready - 1)
                    for j in range(TPS):
                        key = n * SUPER + j * 128
                        last = nc.tensor.matmul(ps[:, 4 + 2 * (n % 2) + j // 4, (j % 4) * C:(j % 4 + 1) * C],
                                                mem.ctx_t[:, key:key + 128], mem.w(pack, "Wv"),
                                                start=True, stop=True)
                    last.then_inc(values_projected, 1)

                def sum_squares(u):
                    pe.wait_ge(squares_ready, 2 * u + 2)
                    for j in range(TPS):
                        t = u * TPS + j
                        last = nc.tensor.matmul(ps[:, 0, 384 + t:385 + t], squares[:, u % 2, j * 128:(j + 1) * 128],
                                                mem.ones[:, 0:1], start=True, stop=True)
                    last.then_inc(norms_ready, 1)

                pe.wait_ge(mem.loaded["ctx_first"], 16 * context_load)
                pe.wait_ge(mem.loaded[pack], 16)
                later = iter(afterwards)

                def project_more(count):
                    for kind, n in islice(later, count):
                        project(kind, n)

                for kind, n in at_once:
                    project(kind, n)
                pe.wait_ge(*dve_done.at("keys_abs"))
                if unit:
                    pe.wait_ge(*dve_done.at("ctx_top"))
                nc.tensor.matmul(ps[:, 0, 320:321], keys_abs[:, :], mem.ctx_top[:, SUPERS:SUPERS + 1],
                                 start=True, stop=True).then_inc(*pe_done.mark("key_bound"))
                pe.wait_ge(*dve_done.at("key_gain"))
                pe.wait_ge(*dve_done.at("xn"))
                pe.wait_ge(mem.loaded["consts"], 16)
                nc.tensor.transpose(ps[0:C, 0, 0:T], mem.xn[:, :], ident[0:T, 0:T])\
                    .then_inc(*pe_done.mark("xnT"))
                pe.wait_ge(mem.loaded["ctx_rest"], 16 * context_load)
                project_more(1)
                pe.wait_ge(*dve_done.at("xnT"))
                if unit:
                    nc.tensor.matmul(ps[0:T, 0, 128:256], xnT[:, :], mem.w(pack, "Wq"), start=True,
                                     stop=True).then_inc(*pe_done.mark("Qp"))
                    project_more(1)
                    pe.wait_ge(*dve_done.at("Qn"))
                    nc.tensor.transpose(ps[0:C, 0, 256:320], Qn[:, :], ident[0:T, 0:T])\
                        .then_inc(*pe_done.mark("QT"))
                else:
                    nc.tensor.matmul(ps[0:C, 0, 256:320], mem.w(pack, "Wq"), xnT[:, :], start=True,
                                     stop=True).then_inc(*pe_done.mark("QT"))
                    project_more(1)
                pe.wait_ge(*dve_done.at("q_top"))
                if unit:
                    sum_squares(0)
                nc.tensor.transpose(ps[0:1, 0, 128:256], q_top[:, :], ident).then_inc(*pe_done.mark("q_topT"))
                project_more(2)
                pe.wait_ge(*dve_done.at("q_top1"))
                nc.tensor.matmul(ps[:, 0, 321:322], mem.ones[0:1, :], q_top1[:, :], start=True, stop=True)\
                    .then_inc(*pe_done.mark("q_top_all"))
                for kind, n in later:
                    project(kind, n)
                    if unit and kind == "V":
                        if n == 3:
                            pe.wait_ge(*dve_done.at("Q_stack"))
                        sum_squares(n - 2)
                if unit:
                    pe.wait_ge(key_sums_ready, 1)
                    sum_squares(SUPERS - 2)
                    sum_squares(SUPERS - 1)
                pe.wait_ge(*dve_done.at("Q_stack"))
                pe.wait_ge(low_ready, HALVES)
                if ready < SUPERS:
                    pe.wait_ge(values_copied, SUPERS - ready)
                if unit:
                    pe.wait_ge(key_sums_ready, 2)
                else:
                    for m in range(2 * HALVES):
                        n, s = m // 2, m % 2
                        u, keys = n // 2, slice((n % 2) * HALF, (n % 2 + 1) * HALF)
                        pe.wait_ge(*stacked_with(u))
                        for g in range(G):
                            if n >= 1 and g % 2 == 0:
                                pe.wait_ge(*part_read(n - 1, s, g // 2))
                            last = nc.tensor.matmul(ps[:, s * G + g, 0:HALF],
                                                    Q_stack[0:96, g, 128 * s:128 * s + 128],
                                                    stack[0:96, u, g, keys], start=True, stop=True)
                            if g % 2 == 1:
                                last.then_inc(max_scores, 1)
                    pe.wait_ge(*dve_done.at("max_parts"))
                    for half in range(2):
                        for part in range(2):
                            last = nc.tensor.matmul(
                                ps[:, half, :], picks[:, part, :],
                                diag[:, part, 4 * half:4 * half + 4, :], start=part == 0, stop=part == 1)
                    last.then_inc(*pe_done.mark("max_cols"))
                    pe.wait_ge(*dve_done.at("max_cols"))

                def scores(t):
                    u, j, pair = t // TPS, t % TPS, 2 * (t % RING)
                    pe.wait_ge(*stacked_with(u))
                    if t >= RING:
                        pe.wait_ge(probs_ready, t - RING + 1)
                    for g in range(G):
                        last = nc.tensor.matmul(ps[:, pair + g // 2, (g % 2) * 256:(g % 2 + 1) * 256],
                                                stack[0:STACK, u, g, j * 128:(j + 1) * 128],
                                                Q_stack[0:STACK, g, :], start=True, stop=True)
                    last.then_inc(scores_ready, 1)

                def weigh(t):
                    pe.wait_ge(probs_ready, t + 1)
                    for g in range(G):
                        last = nc.tensor.matmul(
                            ps[32 * g:32 * g + 32, O_BANK, 0:256],
                            mem.values[:, t * C + 32 * g:t * C + 32 * g + 32],
                            probs[:, t % PROBS, 256 * g:256 * g + 256], start=t == 0, stop=t == KT_TILES - 1)
                    last.then_inc(pv_done, 1)

                scores(0)
                scores(1)
                for t in range(KT_TILES):
                    if t + 2 < KT_TILES:
                        scores(t + 2)
                    weigh(t)
                pe.wait_ge(sum_done, KT_TILES - len(POOL_TILES))
                pe.wait_ge(pool_sum_done, len(POOL_TILES))
                for n, part in enumerate([pool_sum, prob_sum]):
                    for g in range(G):
                        last = nc.tensor.matmul(ps[32 * g:32 * g + 32, DEN_BANK, 0:256], mem.ones[:, 0:32],
                                                part[:, 256 * g:256 * g + 256], start=n == 0, stop=n == 1)
                last.then_inc(*pe_done.mark("den"))
                pe.wait_ge(*dve_done.at("OT"))
                nc.tensor.matmul(ps[0:T, Y_BANK, 0:C], OT[:, :], mem.w(pack, "Wo"), start=True,
                                 stop=True).then_inc(*pe_done.mark("projected"))

            @block.scalar
            def _(act):
                act.wait_ge(*dve_done.at("key_gain"))
                for n in range(HALVES):
                    u, half = n // 2, slice((n % 2) * HALF, (n % 2 + 1) * HALF)
                    act.wait_ge(keys_projected, n + 1)
                    bank = ps[:, 1 + n % 3, 0:HALF]
                    if unit:
                        if u >= 2:
                            act.wait_ge(norms_ready, u - 1)
                        nc.scalar.activation(squares[:, u % 2, half], bank, ACT.Square)\
                            .then_inc(squares_ready, 1)
                    nc.scalar.activation(parts_of_keys[:, u, 0, half], bank, ACT.Identity, scale=key_gain[:, :])\
                        .then_inc(high_ready, 1)
                if not unit:
                    for i, (n, s) in enumerate(copied_parts):
                        if i >= COPIES:
                            act.wait_ge(max_folded, i - COPIES + 1)
                        for p in range(2):
                            act.wait_ge(max_scores, 2 * (2 * n + s) + p + 1)
                            first = s * G + 2 * p
                            nc.scalar.activation(copies[:, i % COPIES, 2 * p:2 * p + 2, :],
                                                 ps[:, first:first + 2, 0:HALF], ACT.Identity,
                                                 scale=1.0 / BIAS_ROW).then_inc(max_copied, 1)
                for semaphore in stacked[:-1]:
                    act.wait_ge(semaphore, 16 * PER_BATCH)
                if unit:
                    act.wait_ge(*dve_done.at("key_scale"))
                for t in range(KT_TILES):
                    pair = 2 * (t % RING)
                    act.wait_ge(scores_ready, t + 1)
                    if t >= PROBS:
                        act.wait_ge(pv_done, t - PROBS + 1)
                        act.wait_ge(*summed(t - PROBS))
                    nc.scalar.activation(
                        probs[:, t % PROBS, :].rearrange("p (b n) -> p b n", b=2), ps[:, pair:pair + 2, :],
                        ACT.Exp, scale=key_scale[:, t:t + 1] if unit else exp_gain[:, :]).then_inc(probs_ready, 1)

            @block.gpsimd
            def _(pool):
                pool_rstd(mem, "var", "rstd")
                if unit:
                    pool_power(mem, q_rsqrt[:, :], q_sum[:, :], mem.minus_half[0:T, 0:1],
                               dve_done.at("q_sum"), "q_rsqrt")
                    for n, of_tiles in enumerate(key_sum_tiles):
                        pool.wait_ge(key_sums_ready, n + 1)
                        nc.gpsimd.tensor_tensor(key_scale[:, of_tiles], key_sums[:, of_tiles],
                                                mem.minus_half[:, of_tiles], ALU.pow).then_inc(key_rsqrt_ready, 1)
                if unit:
                    pool.wait_ge(norms_ready, SUPERS)
                else:
                    pool.wait_ge(*dve_done.at("max_cols"))
                for t in POOL_TILES:
                    pool.wait_ge(probs_ready, t + 1)
                    if t == POOL_TILES[0]:
                        ins = nc.gpsimd.tensor_copy(pool_sum, probs[:, t % PROBS, :])
                    else:
                        pool.wait_ge(*summed(t - 3))
                        ins = nc.gpsimd.tensor_tensor(pool_sum, pool_sum, probs[:, t % PROBS, :], ALU.add)
                    ins.then_inc(pool_sum_done, 1)
                if unit:
                    pool_rstd(mem, "out_var", "out_rstd")

            @block.vector
            def _(dve):
                v = nc.vector

                def power_of_two(source):
                    step(v.tensor_scalar(power[:, :], source, 1e-30, None, ALU.max))
                    bits = power[:, :].bitcast(I32)
                    step(v.tensor_scalar(bits, bits, EXPONENT_BITS, None, ALU.bitwise_and))
                    step(v.reciprocal(inverse[:, :], power[:, :]))

                def take_key_sums(n):
                    dve.wait_ge(norms_ready, [SUPERS - 2, SUPERS][n])
                    v.tensor_scalar(key_sums[:, key_sum_tiles[n]], ps[:, 0, 384:384 + KT_TILES][:, key_sum_tiles[n]],
                                    1e-24, None, ALU.max).then_inc(key_sums_ready, 1)

                def copy_out(kind, n):
                    if kind == "K":
                        u, half = n // 2, slice((n % 2) * HALF, (n % 2 + 1) * HALF)
                        dve.wait_ge(high_ready, n + 1)
                        v.scalar_tensor_tensor(out=parts_of_keys[:, u, 1, half], in0=ps[:, 1 + n % 3, 0:HALF],
                                               scalar=key_gain[:, :], in1=parts_of_keys[:, u, 0, half],
                                               op0=ALU.mult, op1=ALU.subtract).then_inc(low_ready, 1)
                        return
                    first = 4 + 2 * (n % 2)
                    dve.wait_ge(values_projected, n - ready + 1)
                    v.tensor_copy(mem.values[:, n * SUPER:(n + 1) * SUPER],
                                  ps[:, first:first + 2, :].rearrange("p b n -> p (b n)")[:, 0:SUPER])\
                        .then_inc(values_copied, 1)

                dve.wait_ge(mem.loaded[pack], 16)
                v.tensor_scalar(keys_abs[:, :].bitcast(I32), mem.w(pack, "Wk").bitcast(I32), MAGNITUDE_BITS,
                                None, ALU.bitwise_and).then_inc(*dve_done.mark("keys_abs"))
                if unit:
                    dve.wait_ge(mem.loaded["x"], 16)
                dve_moments(mem, mem.x[:, :], "var")
                dve_normalised(mem, mem.xn[:, :], mem.x[:, :], "rstd").then_inc(*dve_done.mark("xn"))
                if unit:
                    dve.wait_ge(mem.loaded["ctx_first"], 16)
                    for u in range(SUPERS):
                        if u == CTX_FIRST:
                            dve.wait_ge(mem.loaded["ctx_rest"], 16)
                        ins = v.tensor_reduce(mem.ctx_top[:, u:u + 1], mem.ctx_t[:, u * SUPER:(u + 1) * SUPER],
                                              AX_X, ALU.max, apply_absolute_value=True)
                    step(ins)
                    v.tensor_reduce(mem.ctx_top[:, SUPERS:SUPERS + 1], mem.ctx_top[:, 0:SUPERS], AX_X, ALU.max)\
                        .then_inc(*dve_done.mark("ctx_top"))
                dve.wait_ge(*pe_done.at("key_bound"))
                power_of_two(ps[:, 0, 320:321])
                step(v.tensor_scalar(query_gain[:, :], power[:, :], 2.0 ** -13, None, ALU.mult))
                v.tensor_scalar(key_gain[:, :], inverse[:, :], 2.0 ** 13, None, ALU.mult)\
                    .then_inc(*dve_done.mark("key_gain"))
                dve.wait_ge(*dve_done.at("key_gain"))
                later = iter(afterwards)

                def copy_more(count):
                    for kind, n in islice(later, count):
                        copy_out(kind, n)

                for kind, n in at_once:
                    copy_out(kind, n)
                dve.wait_ge(*pe_done.at("xnT"))
                v.tensor_copy(xnT[:, :], ps[0:C, 0, 0:T]).then_inc(*dve_done.mark("xnT"))
                dve.wait_ge(mem.loaded["consts"], 16)
                dve.wait_ge(mem.loaded["rows"], 16)
                copy_more(1)
                if unit:
                    dve.wait_ge(*pe_done.at("Qp"))
                    step(v.tensor_tensor(Qp[:, :], ps[0:T, 0, 128:256], mem.row("l0x_bq"), ALU.add))
                    step(v.tensor_tensor(sq[:, :], Qp[:, :], Qp[:, :], ALU.mult))
                    step(v.tensor_reduce(q_sum[:, :], sq[:, :], AX_X, ALU.add))
                    v.tensor_scalar(q_sum[:, :], q_sum[:, :], 1e-24, None, ALU.max)\
                        .then_inc(*dve_done.mark("q_sum"))
                    dve.wait_ge(*pool_done.at("q_rsqrt"))
                    v.tensor_scalar(Qn[:, :], Qp[:, :], q_rsqrt[:, :], None, ALU.mult)\
                        .then_inc(*dve_done.mark("Qn"))
                    copy_more(1)
                    dve.wait_ge(*pe_done.at("QT"))
                    v.tensor_scalar(QT[:, :], ps[0:C, 0, 256:320], SCALE, None, ALU.mult)\
                        .then_inc(*dve_done.mark("QT"))
                else:
                    dve.wait_ge(*pe_done.at("QT"))
                    v.tensor_scalar(QT[:, :], ps[0:C, 0, 256:320], mem.w(pack, "bq"), SCALE, ALU.add, ALU.mult)\
                        .then_inc(*dve_done.mark("QT"))
                dve.wait_ge(*dve_done.at("QT"))
                step(v.tensor_scalar(QT[:, :], QT[:, :], query_gain[:, :], None, ALU.mult))
                v.tensor_reduce(q_top[:, :], QT[:, :], AX_X, ALU.max, apply_absolute_value=True)\
                    .then_inc(*dve_done.mark("q_top"))
                if not unit:
                    copy_more(1)
                dve.wait_ge(*pe_done.at("q_topT"))
                v.tensor_reduce(q_top1[:, :], ps[0:1, 0, 128:256], AX_X, ALU.max)\
                    .then_inc(*dve_done.mark("q_top1"))
                copy_more(2)
                dve.wait_ge(*pe_done.at("q_top_all"))
                power_of_two(ps[:, 0, 321:322])
                step(v.tensor_scalar(gain[:, :], inverse[:, :], 2.0 ** 7, None, ALU.mult))
                step(v.tensor_scalar(exp_gain[:, :], power[:, :], 2.0 ** -7, None, ALU.mult))
                step(v.tensor_scalar(QT[:, :], QT[:, :], gain[:, :], None, ALU.mult))
                step(v.tensor_tensor(Qbd[:, :, :], spread(QT[:, :], 1, [C, HG, T]),
                                     spread(four_heads, 2, [C, HG, T]), ALU.mult))
                whole = Qbd[:, :, :].rearrange("p h t -> p (h t)")
                step(v.tensor_copy(Q_high[:, :], whole))
                step(v.tensor_tensor(Q_low[:, :], whole, Q_high[:, :], ALU.subtract))
                for g in range(G):
                    for block_row, part in enumerate([Q_high, Q_high, Q_low]):
                        ins = v.tensor_copy(Q_stack[32 * block_row:32 * block_row + 32, g, :],
                                            part[32 * g:32 * g + 32, :])
                ins.then_inc(*dve_done.mark("Q_stack"))
                for kind, n in later:
                    copy_out(kind, n)
                    if unit and (kind, n) == ("V", SUPERS - 1):
                        take_key_sums(0)
                if unit:
                    step(v.tensor_tensor(residual[:, :], Qp[:, :], mem.row("l0x_bo"), ALU.add))
                    take_key_sums(1)
                    dve.wait_ge(key_rsqrt_ready, 2)
                    v.tensor_scalar(key_scale[:, :], key_scale[:, :], exp_gain[:, :], None, ALU.mult)\
                        .then_inc(*dve_done.mark("key_scale"))
                else:
                    step(v.tensor_tensor(residual[:, :], mem.x[:, :], mem.row(f"{pack}_bo"), ALU.add))
                    v.tensor_copy(picks[:, 0, :], mem.w("consts", "even_out"))
                    step(v.tensor_copy(picks[:, 1, :], mem.w("consts", "odd_out")))

                    def fold(i):
                        s = copied_parts[i][1]
                        before = [j for j in range(i) if copied_parts[j][1] == s]
                        dve.wait_ge(max_copied, 2 * i + 2)
                        if not before:
                            ins = v.tensor_copy(folded[:, s, :, :], copies[:, i % COPIES, :, :])
                        else:
                            dve.wait_ge(max_folded, before[-1] + 1)
                            ins = v.tensor_tensor(folded[:, s, :, :], folded[:, s, :, :],
                                                  copies[:, i % COPIES, :, :], ALU.max)
                        ins.then_inc(max_folded, 1)

                    folds = iter(range(len(copied_parts)))
                    for k, (n, s) in enumerate(taken_parts):
                        for p in range(2):
                            dve.wait_ge(max_scores, 2 * (2 * n + s) + p + 1)
                            v.tensor_reduce(maxima[:, 2 * p:2 * p + 2, k], ps[:, 2 * p:2 * p + 2, 0:HALF],
                                            AX_X, ALU.max).then_inc(max_taken, 1)
                        for i in islice(folds, 2 if k == 0 else 3):
                            fold(i)
                    for i in folds:
                        fold(i)
                    dve.wait_ge(max_taken, 2 * len(taken_parts))
                    dve.wait_ge(max_folded, len(copied_parts))
                    pairs = row_max[:, :].rearrange("p (g s) -> p g s", g=G)
                    step(v.tensor_reduce(taken_max[:, :], maxima[:, :, :], AX_X, ALU.max))
                    for s in range(2):
                        step(v.tensor_reduce(pairs[:, :, s], folded[:, s, :, :], AX_X, ALU.max))
                    step(v.tensor_scalar(taken_max[:, :], taken_max[:, :], 1.0 / BIAS_ROW, None, ALU.mult))
                    step(v.tensor_tensor(pairs[:, :, 0], pairs[:, :, 0], taken_max[:, :], ALU.max))
                    step(v.tensor_scalar(row_max[:, :], row_max[:, :], -1.0, None, ALU.mult))
                    step(v.tensor_copy(high16[:, :], row_max[:, :]))
                    step(v.tensor_copy(parts[:, 0, :], high16[:, :]))
                    step(v.tensor_tensor(parts[:, 1, :], row_max[:, :], parts[:, 0, :], ALU.subtract))
                    for part in range(2):
                        ins = v.tensor_tensor(diag[:, part, :, :], spread(ident, 1, [128, G * 2, 128]),
                                              spread(parts[:, part, :], 2, [128, G * 2, 128]), ALU.mult)
                    ins.then_inc(*dve_done.mark("max_parts"))
                    dve.wait_ge(*pe_done.at("max_cols"))
                    v.tensor_copy(Q_stack[96:98, :, :].rearrange("p g n -> p (g n)")
                                  .rearrange("p (b n) -> p b n", b=2), ps[96:98, 0:2, :])\
                        .then_inc(*dve_done.mark("max_cols"))
                own = [t for t in range(KT_TILES) if t not in POOL_TILES]
                for n, t in enumerate(own):
                    dve.wait_ge(probs_ready, t + 1)
                    if n == 0:
                        ins = v.tensor_copy(prob_sum, probs[:, 0, :])
                    else:
                        dve.wait_ge(sum_done, n)
                        ins = v.tensor_tensor(prob_sum, prob_sum, probs[:, t % PROBS, :], ALU.add)
                    ins.then_inc(sum_done, 1)
                dve.wait_ge(*pe_done.at("den"))
                step(v.reciprocal(rden[:, :, :], ps[:, DEN_BANK, 0:256].rearrange("p (h q) -> p h q", h=HG)))
                step(v.tensor_tensor(weighted[:, :, :],
                                     ps[:, O_BANK, 0:256].rearrange("p (h q) -> p h q", h=HG),
                                     rden[:, :, :], ALU.mult))
                step(v.tensor_tensor(weighted[:, :, :], weighted[:, :, :],
                                     spread(four_heads, 2, [C, HG, T]), ALU.mult))
                v.tensor_reduce(OT[:, :], weighted[:, :, :].rearrange("p h q -> p q h"), AX_X,
                                ALU.add).then_inc(*dve_done.mark("OT"))
                dve.wait_ge(*pe_done.at("projected"))
                if unit:
                    step(v.tensor_tensor(z[:, :], ps[0:T, Y_BANK, 0:C], residual[:, :], ALU.add))
                    dve_moments(mem, z[:, :], "out_var")
                    step(dve_normalised(mem, zn[:, :], z[:, :], "out_rstd"))
                    step(v.tensor_tensor(zn[:, :], zn[:, :], mem.row("l0x_gamma"), ALU.mult))
                    step(v.tensor_tensor(zn[:, :], zn[:, :], mem.row("l0x_beta"), ALU.add))
                    v.tensor_tensor(mem.x[:, :], mem.x[:, :], zn[:, :], ALU.add)\
                        .then_inc(*dve_done.mark("x"))
                else:
                    v.tensor_tensor(mem.x[:, :], ps[0:T, Y_BANK, 0:C], residual[:, :], ALU.add)\
                        .then_inc(*dve_done.mark("x"))



def stage_rwkv(mem):
    nc = mem.nc
    pe_done, act_done, dve_done, pool_done = mem.pe_done, mem.act_done, mem.dve_done, mem.pool_done
    step = mem.dve_step
    ps = mem.psum
    ident = mem.w("consts", "ident")
    early = mem.early_values[1] = EarlyValues(mem, "l1x", context_load=2)
    pe_done.stage("aT", "kvr", "time_mixed", "cT", "kk", "kv")
    dve_done.stage("var", "z", "a_var", "a", "mixed", "scan_args", "rwkv", "c_var", "c", "c_mixed", "kk2", "x")
    act_done.stage("decay", "r_exp", "scan_exps", "rr_exp")
    pool_done.stage("rstd", "a_rstd", "c_rstd")

    def w(name):
        return mem.w("l0a", name)

    with ExitStack() as local:
        def sb(name, shape, dt=F32):
            return local.enter_context(nc.sbuf_tensor("l0a_" + name, shape, dt))

        a, c = sb("a", [T, C]), sb("c", [T, C])
        shifted_a, shifted_c = sb("shifted_a", [C, T + 1]), sb("shifted_c", [C, T + 1])
        delta = sb("delta", [C, T])
        mix = sb("mix", [C, 3, T])
        cmix = sb("cmix", [C, 2, T])
        kvr = sb("kvr", [C, 2, T])
        r_exp = sb("r_exp", [C, T])
        decay = sb("decay", [C, 1])
        decays = sb("decays", [C, T])
        top = sb("top", [C, T + 1])
        now = sb("now", [C, 2, T])
        args = sb("args", [C, 4, T])
        exps = sb("exps", [C, 4, T])
        sum_a, sum_b = sb("sum_a", [C, T + 1]), sb("sum_b", [C, T + 1])
        terms = sb("terms", [C, 4, T])
        rwkv = sb("rwkv", [C, T])
        x1 = sb("x1", [T, C])
        kk = sb("kk", [C, HID // C, T])
        kk2 = sb("kk2", [C, HID // C, T])
        rr = sb("rr", [T, C])
        gated = sb("gated", [T, C])

        with nc.Block(no_gpsimd_drain=True) as block:

            @block.tensor
            def _(pe):
                early.pe(pe, EARLY1[0])
                pe.wait_ge(*dve_done.at("a"))
                nc.tensor.transpose(ps[0:C, 0, 0:T], a[:, :], ident[0:T, 0:T]).then_inc(*pe_done.mark("aT"))
                pe.wait_ge(mem.loaded["l0a"], 16)
                pe.wait_ge(*dve_done.at("mixed"))
                for n, name in enumerate(["Wk", "Wv", "Wr"]):
                    out = ps[0:C, 1, n * T:(n + 1) * T] if n < 2 else ps[0:C, 7, 0:T]
                    last = nc.tensor.matmul(out, w(name), mix[:, n, :], start=True, stop=True)
                last.then_inc(*pe_done.mark("kvr"))
                early.pe(pe, EARLY1[1])
                pe.wait_ge(*dve_done.at("rwkv"))
                nc.tensor.matmul(ps[0:T, 2, 0:C], rwkv[:, :], w("Wo"), start=True, stop=True)\
                    .then_inc(*pe_done.mark("time_mixed"))
                early.pe(pe, EARLY1[2])
                pe.wait_ge(*dve_done.at("c"))
                nc.tensor.transpose(ps[0:C, 3, 0:T], c[:, :], ident[0:T, 0:T]).then_inc(*pe_done.mark("cT"))
                early.pe(pe, EARLY1[3])
                pe.wait_ge(*dve_done.at("c_mixed"))
                for n in range(HID // C):
                    nc.tensor.matmul(ps[0:C, 4, n * T:(n + 1) * T], w("Wck")[:, n * C:(n + 1) * C],
                                     cmix[:, 0, :], start=True, stop=True)
                nc.tensor.matmul(ps[0:T, 3, 0:C], cmix[:, 1, :], w("Wcr"), start=True, stop=True)\
                    .then_inc(*pe_done.mark("kk"))
                pe.wait_ge(*dve_done.at("kk2"))
                for n in range(HID // C):
                    last = nc.tensor.matmul(ps[0:T, 2, 0:C], kk2[:, n, :], w("Wcv")[:, n * C:(n + 1) * C],
                                            start=n == 0, stop=n == HID // C - 1)
                last.then_inc(*pe_done.mark("kv"))
                early.pe(pe, EARLY1[4])

            @block.scalar
            def _(act):
                act.wait_ge(mem.loaded["l0a"], 16)
                nc.scalar.activation(decay[:, :], w("time_decay"), ACT.Exp).then_inc(*act_done.mark("decay"))
                early.act(act, EARLY1[0])
                act.wait_ge(*pe_done.at("kvr"))
                nc.scalar.activation(r_exp[:, :], ps[0:C, 7, 0:T], ACT.Exp, scale=-1.0)\
                    .then_inc(*act_done.mark("r_exp"))
                act.wait_ge(*dve_done.at("scan_args"))
                nc.scalar.activation(exps[:, :, :], args[:, :, :], ACT.Exp).then_inc(*act_done.mark("scan_exps"))
                early.act(act, sum(EARLY1[1:4]))
                act.wait_ge(*pe_done.at("kk"))
                nc.scalar.activation(rr[:, :], ps[0:T, 3, 0:C], ACT.Exp, scale=-1.0)\
                    .then_inc(*act_done.mark("rr_exp"))
                early.act(act, EARLY1[4])

            @block.gpsimd
            def _(pool):
                pool_rstd(mem, "var", "rstd")
                pool_rstd(mem, "a_var", "a_rstd")
                pool_rstd(mem, "c_var", "c_rstd")

            @block.vector
            def _(dve):
                v = nc.vector
                dve_moments(mem, mem.x[:, :], "var")
                dve_normalised(mem, mem.xn[:, :], mem.x[:, :], "rstd").then_inc(*dve_done.mark("z"))
                dve.wait_ge(*dve_done.at("z"))
                dve_moments(mem, mem.xn[:, :], "a_var")
                dve_normalised(mem, a[:, :], mem.xn[:, :], "a_rstd").then_inc(*dve_done.mark("a"))

                dve.wait_ge(mem.loaded["l0a"], 16)
                v.memset(shifted_a[:, 0:1], 0.0)
                v.memset(shifted_c[:, 0:1], 0.0)
                v.memset(sum_a[:, 0:1], 0.0)
                v.memset(sum_b[:, 0:1], 0.0)
                step(v.memset(top[:, 0:1], -1e38))

                dve.wait_ge(*pe_done.at("aT"))
                step(v.tensor_scalar(shifted_a[:, 1:T + 1], ps[0:C, 0, 0:T], w("ln0_g"), w("ln0_b"),
                                     ALU.mult, ALU.add))
                step(v.tensor_tensor(delta[:, :], shifted_a[:, 1:T + 1], shifted_a[:, 0:T], ALU.subtract))
                for n, name in enumerate(["tm_k", "tm_v", "tm_r"]):
                    ins = v.scalar_tensor_tensor(out=mix[:, n, :], in0=delta[:, :], scalar=w(name),
                                                 in1=shifted_a[:, 0:T], op0=ALU.mult, op1=ALU.add)
                ins.then_inc(*dve_done.mark("mixed"))
                dve.wait_ge(*act_done.at("decay"))
                step(v.tensor_scalar(decays[:, :], mem.ones[:, 0:T], decay[:, :], -1.0, ALU.mult, ALU.mult))
                dve.wait_ge(*pe_done.at("kvr"))
                step(v.tensor_copy(kvr[:, :, :], ps[0:C, 1, 0:2 * T].rearrange("p (n t) -> p n t", n=2)))
                k, val = kvr[:, 0, :], kvr[:, 1, :]
                step(v.tensor_tensor_scan(top[:, 1:T + 1], decays[:, :], k, -1e38, ALU.add, ALU.max))
                step(v.tensor_scalar(now[:, 0, :], k, w("time_first"), None, ALU.add))
                step(v.tensor_tensor(now[:, 1, :], top[:, 0:T], now[:, 0, :], ALU.max))
                v.tensor_tensor(args[:, 0, :], top[:, 0:T], now[:, 1, :], ALU.subtract)
                v.tensor_tensor(args[:, 1, :], now[:, 0, :], now[:, 1, :], ALU.subtract)
                v.tensor_tensor(args[:, 3, :], k, top[:, 1:T + 1], ALU.subtract)
                step(v.tensor_tensor(args[:, 2, :], top[:, 0:T], decays[:, :], ALU.add))
                v.tensor_tensor(args[:, 2, :], args[:, 2, :], top[:, 1:T + 1], ALU.subtract)\
                    .then_inc(*dve_done.mark("scan_args"))
                dve.wait_ge(*act_done.at("scan_exps"))
                v.tensor_tensor(terms[:, 0, :], exps[:, 3, :], val, ALU.mult)
                v.tensor_tensor(terms[:, 1, :], exps[:, 1, :], val, ALU.mult)
                step(v.tensor_tensor_scan(sum_b[:, 1:T + 1], exps[:, 2, :], exps[:, 3, :], 0.0, ALU.mult, ALU.add))
                step(v.tensor_tensor_scan(sum_a[:, 1:T + 1], exps[:, 2, :], terms[:, 0, :], 0.0, ALU.mult, ALU.add))
                v.tensor_tensor(terms[:, 2, :], exps[:, 0, :], sum_a[:, 0:T], ALU.mult)
                step(v.tensor_tensor(terms[:, 3, :], exps[:, 0, :], sum_b[:, 0:T], ALU.mult))
                v.tensor_tensor(terms[:, 2, :], terms[:, 2, :], terms[:, 1, :], ALU.add)
                step(v.tensor_tensor(terms[:, 3, :], terms[:, 3, :], exps[:, 1, :], ALU.add))
                dve.wait_ge(*act_done.at("r_exp"))
                step(v.scalar_tensor_tensor(out=terms[:, 3, :], in0=r_exp[:, :], scalar=1.0,
                                            in1=terms[:, 3, :], op0=ALU.add, op1=ALU.mult))
                step(v.reciprocal(terms[:, 3, :], terms[:, 3, :]))
                v.tensor_tensor(rwkv[:, :], terms[:, 2, :], terms[:, 3, :], ALU.mult)\
                    .then_inc(*dve_done.mark("rwkv"))
                dve.wait_ge(*pe_done.at("time_mixed"))
                step(v.tensor_tensor(x1[:, :], ps[0:T, 2, 0:C], mem.xn[:, :], ALU.add))
                dve_moments(mem, x1[:, :], "c_var")
                dve_normalised(mem, c[:, :], x1[:, :], "c_rstd").then_inc(*dve_done.mark("c"))
                step(v.tensor_tensor(x1[:, :], x1[:, :], mem.x[:, :], ALU.add))
                dve.wait_ge(*pe_done.at("cT"))
                step(v.tensor_scalar(shifted_c[:, 1:T + 1], ps[0:C, 3, 0:T], w("ln1_g"), w("ln1_b"),
                                     ALU.mult, ALU.add))
                step(v.tensor_tensor(delta[:, :], shifted_c[:, 1:T + 1], shifted_c[:, 0:T], ALU.subtract))
                for n, name in enumerate(["cm_k", "cm_r"]):
                    ins = v.scalar_tensor_tensor(out=cmix[:, n, :], in0=delta[:, :], scalar=w(name),
                                                 in1=shifted_c[:, 0:T], op0=ALU.mult, op1=ALU.add)
                ins.then_inc(*dve_done.mark("c_mixed"))
                dve.wait_ge(*pe_done.at("kk"))
                step(v.tensor_scalar(kk[:, :, :], ps[0:C, 4, 0:4 * T].rearrange("p (n t) -> p n t", n=4),
                                     0.0, None, ALU.max))
                v.tensor_tensor(kk2[:, :, :], kk[:, :, :], kk[:, :, :], ALU.mult)\
                    .then_inc(*dve_done.mark("kk2"))
                dve.wait_ge(*act_done.at("rr_exp"))
                step(v.tensor_scalar(rr[:, :], rr[:, :], 1.0, None, ALU.add))
                step(v.reciprocal(rr[:, :], rr[:, :]))
                dve.wait_ge(*pe_done.at("kv"))
                step(v.tensor_tensor(gated[:, :], ps[0:T, 2, 0:C], rr[:, :], ALU.mult))
                v.tensor_tensor(mem.x[:, :], x1[:, :], gated[:, :], ALU.add).then_inc(*dve_done.mark("x"))



class Experts:

    def __init__(self, mem, sb, name, experts, hidden, function, tensors):
        self.mem, self.name, self.n, self.chunks, self.function = mem, name, experts, hidden // C, function
        self.w1, self.w2 = tensors
        self.b1, self.b2 = mem.w(name, "b1"), mem.w(name, "b2")
        self.per_bank = CHUNK // (self.chunks * T)
        self.banks = -(-experts // self.per_bank)
        self.hidden_ready, self.biased, self.activated, self.gated = (
            mem.sem(f"{name}_{x}") for x in ["hidden_ready", "biased", "activated", "gated"])
        n = experts * self.chunks * T
        self.pre, self.act = mem.keys_t[:, 0:n], mem.keys_t[:, n:2 * n]
        self.spread_gates = sb("spread_gates", [T, experts, T])
        self.gates = sb("gates", [T, experts])
        self.gatesT = sb("gatesT", [experts, T])
        self.y = sb("y", [2 * T, C])

    def of_bank(self, b):
        lo, hi = b * self.per_bank, min(self.n, (b + 1) * self.per_bank)
        return lo, hi, slice(lo * self.chunks * T, hi * self.chunks * T)

    def pe_hidden(self, pe, xT):
        nc, w = self.mem.nc, self.chunks * C
        for b in range(self.banks):
            lo, hi, _ = self.of_bank(b)
            for e in range(lo, hi):
                for c in range(self.chunks):
                    o = ((e - lo) * self.chunks + c) * T
                    last = nc.tensor.matmul(self.mem.psum[0:C, 1 + b, o:o + T],
                                            self.w1[:, e * w + c * C:e * w + (c + 1) * C], xT,
                                            start=True, stop=True)
            last.then_inc(self.hidden_ready, 1)

    def pe_gates(self, pe, first):
        mem, nc = self.mem, self.mem.nc
        pe.wait_ge(*mem.dve_done.at("gates"))
        nc.tensor.transpose(mem.psum[0:self.n, 0, 256:256 + T], self.gates[:, :],
                            mem.w("consts", "ident")[0:T, 0:T])
        nc.tensor.matmul(mem.psum[0:C, first, 0:8 * T], mem.ones[0:T, 0:C], self.spread_gates[:, 0:8, :],
                         start=True, stop=True).then_inc(*mem.pe_done.mark("gates"))

    def pe_out(self, pe):
        mem, nc, w = self.mem, self.mem.nc, self.chunks
        total = self.n * w
        for b in range(self.banks):
            lo, hi, _ = self.of_bank(b)
            if lo < E:
                pe.wait_ge(self.gated, b + 1)
            else:
                pe.wait_ge(self.activated, b + 1)
            for n in range(lo * w, hi * w):
                side = slice((n % 2) * T, (n % 2 + 1) * T)
                last = nc.tensor.matmul(mem.psum[side, 7, 0:C], self.act[:, n * T:(n + 1) * T],
                                        self.w2[:, n * C:(n + 1) * C], start=n < 2, stop=n >= total - 2)
        last.then_inc(*mem.pe_done.mark("halves"))
        pe.wait_ge(*mem.dve_done.at("halves"))
        nc.tensor.matmul(mem.psum[0:T, 7, 128:128 + C], mem.w("consts", "both_halves"), self.y[:, :],
                         start=True, stop=False)
        nc.tensor.matmul(mem.psum[0:T, 7, 128:128 + C], self.gatesT[:, :], self.b2,
                         start=False, stop=True).then_inc(*mem.pe_done.mark("y"))

    def act_hidden(self, act):
        for b in range(self.banks):
            _, _, cols = self.of_bank(b)
            act.wait_ge(self.biased, b + 1)
            self.mem.nc.scalar.activation(self.act[:, cols], self.pre[:, cols], self.function)\
                .then_inc(self.activated, 1)

    def dve_gates(self, dve):
        mem, v = self.mem, self.mem.nc.vector
        shape = [T, self.n, T]
        v.tensor_tensor(self.spread_gates[:, :, :], spread(mem.w("consts", "ident")[0:T, 0:T], 1, shape),
                        spread(self.gates[:, :], 2, shape), ALU.mult).then_inc(*mem.dve_done.mark("gates"))

    def dve_bias(self, dve):
        v, ch = self.mem.nc.vector, self.chunks
        for b in range(self.banks):
            lo, hi, cols = self.of_bank(b)
            n = (hi - lo) * ch
            dve.wait_ge(self.hidden_ready, b + 1)
            v.tensor_tensor(self.pre[:, cols].rearrange("p (n t) -> p n t", t=T),
                            self.mem.psum[0:C, 1 + b, 0:n * T].rearrange("p (n t) -> p n t", t=T),
                            spread(self.b1[:, lo * ch:hi * ch], 2, [C, n, T]), ALU.add)\
                .then_inc(self.biased, 1)

    def dve_gate(self, dve, gate_bank):
        mem, v, ch = self.mem, self.mem.nc.vector, self.chunks
        dve.wait_ge(*mem.pe_done.at("gates"))
        mem.dve_step(v.tensor_copy(self.gatesT[:, :], mem.psum[0:self.n, 0, 256:256 + T]))
        for b in range(self.banks):
            lo, hi, cols = self.of_bank(b)
            if lo >= E:
                continue
            dve.wait_ge(self.activated, b + 1)
            n = hi - lo
            act = self.act[:, cols].rearrange("p (e c t) -> p e c t", e=n, t=T)
            gate = mem.psum[0:C, gate_bank, lo * T:hi * T].rearrange("p (e t) -> p e t", t=T)
            v.tensor_tensor(act, act, spread(gate, 2, [C, n, ch, T]), ALU.mult).then_inc(self.gated, 1)

    def dve_halves(self, dve):
        mem = self.mem
        dve.wait_ge(*mem.pe_done.at("halves"))
        mem.nc.vector.tensor_copy(self.y[:, :], mem.psum[:, 7, 0:C]).then_inc(*mem.dve_done.mark("halves"))


def dve_softmax(mem, sb_tiles, scores, out, event_scores, event_exp):
    v, step = mem.nc.vector, mem.dve_step
    top, total = sb_tiles
    step(v.tensor_reduce(top, scores, AX_X, ALU.max))
    v.tensor_scalar(scores, scores, top, None, ALU.subtract).then_inc(*mem.dve_done.mark(event_scores))
    mem.nc.vector.wait_ge(*mem.act_done.at(event_exp))
    step(v.tensor_reduce(total, out, AX_X, ALU.add))
    step(v.reciprocal(total, total))
    step(v.tensor_scalar(out, out, total, None, ALU.mult))


def dve_first_largest(mem, padded, best, work, mask, n, count):
    v, step = mem.nc.vector, mem.dve_step
    step(v.max(best, padded))
    step(v.memset(best[:, count:8], -1.0))
    step(v.match_replace(work, best, padded, -2.0))
    step(v.tensor_scalar(mask, work[:, 0:n], -2.0, None, ALU.is_equal))


def stage_topk_experts(mem, level):
    nc = mem.nc
    pe_done, act_done, dve_done, pool_done = mem.pe_done, mem.act_done, mem.dve_done, mem.pool_done
    step = mem.dve_step
    name = f"l{level}f"
    n_experts = E + (level == 3)
    ps = mem.psum
    pe_done.stage("xnT", "logits", "gates", "halves", "y")
    dve_done.stage("var", "xn", "xnT", "scores", "gates", "halves", "x")
    act_done.stage("exp")
    pool_done.stage("rstd")
    weights = mem.experts
    w1 = weights[:, 0:n_experts * HID]
    w2 = weights[:, n_experts * HID:2 * n_experts * HID]

    with ExitStack() as local:
        def sb(label, shape, dt=F32):
            return local.enter_context(nc.sbuf_tensor(f"{name}_{label}", shape, dt))

        experts = Experts(mem, sb, name, n_experts, HID, ACT.Gelu_apprx_tanh, (w1, w2))
        xnT = sb("xnT", [C, T])
        scores, top, total = sb("scores", [T, E]), sb("top", [T, 1]), sb("total", [T, 1])
        padded, work, best, mask = sb("padded", [T, 16]), sb("work", [T, 16]), sb("best", [T, 8]), sb("mask", [T, E])

        with nc.Block(no_gpsimd_drain=True) as block:

            @block.tensor
            def _(pe):
                pe.wait_ge(*dve_done.at("xn"))
                nc.tensor.transpose(ps[0:C, 0, 0:T], mem.xn[:, :], mem.w("consts", "ident")[0:T, 0:T])\
                    .then_inc(*pe_done.mark("xnT"))
                pe.wait_ge(mem.loaded[name], 16)
                pe.wait_ge(*dve_done.at("xnT"))
                nc.tensor.matmul(ps[0:T, 0, 128:128 + E], xnT[:, :], mem.w(name, "w_router"), start=True,
                                 stop=True).then_inc(*pe_done.mark("logits"))
                pe.wait_ge(mem.loaded[f"experts{level}"], 16)
                experts.pe_hidden(pe, xnT[:, :])
                experts.pe_gates(pe, 6)
                experts.pe_out(pe)

            @block.scalar
            def _(act):
                act.wait_ge(*dve_done.at("scores"))
                nc.scalar.activation(padded[:, 0:E], scores[:, :], ACT.Exp).then_inc(*act_done.mark("exp"))
                experts.act_hidden(act)

            @block.gpsimd
            def _(pool):
                pool_rstd(mem, "var", "rstd")

            @block.vector
            def _(dve):
                v = nc.vector
                dve_moments(mem, mem.x[:, :], "var")
                dve_normalised(mem, mem.xn[:, :], mem.x[:, :], "rstd").then_inc(*dve_done.mark("xn"))
                v.memset(padded[:, E:16], -1.0)
                dve.wait_ge(*pe_done.at("xnT"))
                v.tensor_copy(xnT[:, :], ps[0:C, 0, 0:T]).then_inc(*dve_done.mark("xnT"))
                dve.wait_ge(*pe_done.at("logits"))
                step(v.tensor_copy(scores[:, :], ps[0:T, 0, 128:128 + E]))
                dve_softmax(mem, (top[:, :], total[:, :]), scores[:, :], padded[:, 0:E], "scores", "exp")
                dve_first_largest(mem, padded[:, :], best[:, :], work[:, :], mask[:, :], E, 2)
                if level == 3:
                    step(v.memset(experts.gates[:, E:E + 1], 1.0))
                step(v.tensor_tensor(experts.gates[:, 0:E], padded[:, 0:E], mask[:, :], ALU.mult))
                if level == 3:
                    step(v.tensor_reduce(total[:, :], experts.gates[:, 0:E], AX_X, ALU.add))
                    step(v.reciprocal(total[:, :], total[:, :]))
                    step(v.tensor_scalar(experts.gates[:, 0:E], experts.gates[:, 0:E], total[:, :], None,
                                         ALU.mult))
                dve.wait_ge(mem.loaded[name], 16)
                experts.dve_gates(dve)
                experts.dve_bias(dve)
                experts.dve_gate(dve, 6)
                experts.dve_halves(dve)
                dve.wait_ge(*pe_done.at("y"))
                v.tensor_tensor(mem.x[:, :], mem.x[:, :], ps[0:T, 7, 128:128 + C], ALU.add)\
                    .then_inc(*dve_done.mark("x"))



class SmallHeads:
    PE = ["scores", "probsT", "heads"]
    DVE = ["Qbd", "less_max", "probs", "PT", "OT"]

    def __init__(self, mem, sb, mask):
        self.mem, self.mask = mem, mask
        self.QT, self.KT, self.V = sb("QT", [C, T]), sb("KT", [C, T]), sb("V", [T, C])
        self.Qbd = sb("Qbd", [C, HG, T])
        self.S = sb("S", [128, 2 * G, T])
        self.P = sb("P", [128, 2 * G, T])
        self.top, self.total = sb("top", [128, 2 * G]), sb("total", [128, 2 * G])
        self.PT = sb("PT", [T, H * T])
        self.weighted = sb("weighted", [C, HG, T])
        self.OT = sb("OT", [C, T])

    def pe(self, pe, v_event, between=(lambda count: None), units=(0, 0, 0, 0)):
        nc, mem, ps = self.mem.nc, self.mem, self.mem.psum
        pe.wait_ge(*mem.dve_done.at("Qbd"))
        for s in range(2):
            for g in range(G):
                rows = slice(32 * g, 32 * g + 32)
                last = nc.tensor.matmul(ps[:, 1 + g, s * T:(s + 1) * T], self.Qbd[rows, 2 * s:2 * s + 2, :],
                                        self.KT[rows, :], start=True, stop=True)
        last.then_inc(*mem.pe_done.mark("scores"))
        between(units[0])
        pe.wait_ge(*mem.dve_done.at("probs"))
        for n in range(2 * G):
            last = nc.tensor.transpose(ps[0:T, 1 + n // G, (n % G) * 128:(n % G + 1) * 128],
                                       self.P[:, n, :], mem.w("consts", "ident"))
        last.then_inc(*mem.pe_done.mark("probsT"))
        between(units[1])
        pe.wait_ge(*mem.dve_done.at("PT"))
        pe.wait_ge(*mem.dve_done.at(v_event))
        for g in range(G):
            last = nc.tensor.matmul(ps[32 * g:32 * g + 32, 7, 0:HG * T], self.V[:, 32 * g:32 * g + 32],
                                    self.PT[:, 256 * g:256 * g + 256], start=True, stop=True)
        last.then_inc(*mem.pe_done.mark("heads"))
        between(units[2])

    def act(self, act):
        mem = self.mem
        act.wait_ge(*mem.dve_done.at("less_max"))
        mem.nc.scalar.activation(self.P[:, :, :], self.S[:, :, :], ACT.Exp).then_inc(*mem.act_done.mark("exps"))

    def dve_Qbd(self, dve):
        mem, shape = self.mem, [C, HG, T]
        mem.nc.vector.tensor_tensor(self.Qbd[:, :, :], spread(self.QT[:, :], 1, shape),
                                    spread(mem.w("consts", "four_heads"), 2, shape), ALU.mult)\
            .then_inc(*mem.dve_done.mark("Qbd"))

    def dve(self, dve):
        mem, v, step, ps = self.mem, self.mem.nc.vector, self.mem.dve_step, self.mem.psum
        shape = [128, 2 * G, T]
        dve.wait_ge(*mem.pe_done.at("scores"))
        scores = ps[:, 1:1 + G, 0:2 * T].rearrange("p g (s k) -> p g s k", s=2)
        if self.mask is None:
            step(v.tensor_copy(self.S[:, :, :].rearrange("p (g s) k -> p g s k", g=G), scores))
        else:
            mask = self.mask.unsqueeze(1).unsqueeze(1).to_broadcast([128, G, 2, T])
            step(v.tensor_tensor(self.S[:, :, :].rearrange("p (g s) k -> p g s k", g=G), scores, mask, ALU.add))
        step(v.tensor_reduce(self.top[:, :], self.S[:, :, :], AX_X, ALU.max))
        v.tensor_tensor(self.S[:, :, :], self.S[:, :, :], spread(self.top[:, :], 2, shape), ALU.subtract)\
            .then_inc(*mem.dve_done.mark("less_max"))
        dve.wait_ge(*mem.act_done.at("exps"))
        step(v.tensor_reduce(self.total[:, :], self.P[:, :, :], AX_X, ALU.add))
        step(v.reciprocal(self.total[:, :], self.total[:, :]))
        v.tensor_tensor(self.P[:, :, :], self.P[:, :, :], spread(self.total[:, :], 2, shape), ALU.mult)\
            .then_inc(*mem.dve_done.mark("probs"))
        dve.wait_ge(*mem.pe_done.at("probsT"))
        v.tensor_copy(self.PT[:, :].rearrange("p (b n) -> p b n", b=2), ps[0:T, 1:3, :])\
            .then_inc(*mem.dve_done.mark("PT"))
        dve.wait_ge(*mem.pe_done.at("heads"))
        step(v.tensor_tensor(self.weighted[:, :, :], ps[:, 7, 0:HG * T].rearrange("p (h q) -> p h q", h=HG),
                             spread(mem.w("consts", "four_heads"), 2, [C, HG, T]), ALU.mult))
        v.tensor_reduce(self.OT[:, :], self.weighted[:, :, :].rearrange("p h q -> p q h"), AX_X, ALU.add)\
            .then_inc(*mem.dve_done.mark("OT"))



def stage_rope_attention(mem):
    nc = mem.nc
    pe_done, act_done, dve_done, pool_done = mem.pe_done, mem.act_done, mem.dve_done, mem.pool_done
    step, ps = mem.dve_step, mem.psum
    ident = mem.w("consts", "ident")
    QK = H + G
    pe_done.stage("xnT", "qkv", "turned", *SmallHeads.PE, "projected")
    dve_done.stage("var", "xn", "xnT", "squares", "rotated", *SmallHeads.DVE, "x")
    act_done.stage("exps")
    pool_done.stage("rstd", "norms")

    with ExitStack() as local:
        def sb(name, shape, dt=F32):
            return local.enter_context(nc.sbuf_tensor("l1a_" + name, shape, dt))

        heads = SmallHeads(mem, sb, mem.w("consts", "causal"))
        xnT = sb("xnT", [C, T])
        qkv = sb("qkv", [T, (QK + G) * DH])
        squares, unit = sb("squares", [T, QK, DH]), sb("unit", [T, QK, DH])
        sums, norms, half = sb("sums", [T, QK]), sb("norms", [T, QK]), sb("half", [T, QK])
        straight, crossed = sb("straight", [T, QK, DH]), sb("crossed", [T, QK, DH])
        k_all = sb("k_all", [T, C])

        with nc.Block(no_gpsimd_drain=True) as block:

            @block.sync
            def _(sp):
                load_context(mem, sp)

            @block.tensor
            def _(pe):
                pe.wait_ge(*dve_done.at("xn"))
                nc.tensor.transpose(ps[0:C, 0, 0:T], mem.xn[:, :], ident[0:T, 0:T]).then_inc(*pe_done.mark("xnT"))
                pe.wait_ge(mem.loaded["l1a"], 16)
                pe.wait_ge(*dve_done.at("xnT"))
                nc.tensor.matmul(ps[0:T, 1, 0:192], xnT[:, :], mem.w("l1a", "w_qkv"), start=True, stop=True)\
                    .then_inc(*pe_done.mark("qkv"))
                pe.wait_ge(*dve_done.at("rotated"))
                nc.tensor.transpose(ps[0:C, 0, 0:T], straight[:, 0:H, :], ident[0:T, 0:T])
                nc.tensor.transpose(ps[0:C, 0, T:2 * T], k_all[:, :], ident[0:T, 0:T])\
                    .then_inc(*pe_done.mark("turned"))
                heads.pe(pe, "rotated")
                pe.wait_ge(*dve_done.at("OT"))
                nc.tensor.matmul(ps[0:T, 0, 0:C], heads.OT[:, :], mem.w("l1a", "w_o"), start=True, stop=True)\
                    .then_inc(*pe_done.mark("projected"))

            @block.scalar
            def _(act):
                heads.act(act)

            @block.gpsimd
            def _(pool):
                pool_rstd(mem, "var", "rstd")
                pool_power(mem, norms[:, :], sums[:, :], half[:, :], dve_done.at("squares"), "norms")

            @block.vector
            def _(dve):
                v = nc.vector
                dve_moments(mem, mem.x[:, :], "var")
                dve_normalised(mem, mem.xn[:, :], mem.x[:, :], "rstd").then_inc(*dve_done.mark("xn"))
                v.memset(half[:, :], 0.5)
                dve.wait_ge(*pe_done.at("xnT"))
                v.tensor_copy(xnT[:, :], ps[0:C, 0, 0:T]).then_inc(*dve_done.mark("xnT"))
                dve.wait_ge(*pe_done.at("qkv"))
                step(v.tensor_copy(qkv[:, :], ps[0:T, 1, 0:192]))
                qk = qkv[:, 0:QK * DH].rearrange("t (h d) -> t h d", d=DH)
                step(v.tensor_tensor(squares[:, :, :], qk, qk, ALU.mult))
                v.tensor_reduce(sums[:, :], squares[:, :, :], AX_X, ALU.add).then_inc(*dve_done.mark("squares"))
                dve.wait_ge(*pool_done.at("norms"))
                step(v.tensor_scalar(norms[:, :], norms[:, :], 1e-10, None, ALU.add))
                step(v.reciprocal(norms[:, :], norms[:, :]))
                step(v.tensor_tensor(unit[:, :, :], qk, spread(norms[:, :], 2, [T, QK, DH]), ALU.mult))
                f, h = DH, DH // 2
                sin = mem.w("consts", "sin")
                v.tensor_tensor(straight[:, :, :], unit[:, :, :],
                                spread(mem.w("consts", "cos"), 1, [T, QK, f]), ALU.mult)
                v.tensor_tensor(crossed[:, :, 0:h], unit[:, :, h:f], spread(sin[:, 0:h], 1, [T, QK, h]), ALU.mult)
                step(v.tensor_tensor(crossed[:, :, h:f], unit[:, :, 0:h], spread(sin[:, h:f], 1, [T, QK, h]), ALU.mult))
                step(v.tensor_tensor(straight[:, :, :], straight[:, :, :], crossed[:, :, :], ALU.add))
                v.tensor_copy(k_all[:, :].rearrange("t (g r d) -> t g r d", g=G, r=HG),
                              spread(straight[:, H:QK, :], 2, [T, G, HG, DH]))
                v.tensor_copy(heads.V[:, :].rearrange("t (g r d) -> t g r d", g=G, r=HG),
                              spread(qkv[:, QK * DH:192].rearrange("t (g d) -> t g d", g=G), 2, [T, G, HG, DH]))\
                    .then_inc(*dve_done.mark("rotated"))
                dve.wait_ge(*pe_done.at("turned"))
                v.tensor_copy(heads.KT[:, :], ps[0:C, 0, T:2 * T])
                step(v.tensor_scalar(heads.QT[:, :], ps[0:C, 0, 0:T], SCALE, None, ALU.mult))
                heads.dve_Qbd(dve)
                heads.dve(dve)
                dve.wait_ge(*pe_done.at("projected"))
                v.tensor_tensor(mem.x[:, :], mem.x[:, :], ps[0:T, 0, 0:C], ALU.add).then_inc(*dve_done.mark("x"))



def stage_quantised_ffn(mem):
    nc = mem.nc
    pe_done, act_done, dve_done, pool_done = mem.pe_done, mem.act_done, mem.dve_done, mem.pool_done
    step, ps = mem.dve_step, mem.psum
    ident = mem.w("consts", "ident")
    pe_done.stage("weightsT", "x_topT", "x_top", "xqT", "gate_up", "h_topT", "h_top", "hT", "out")
    dve_done.stage("var", "xn", "w_quantised", "wT", "x_top1", "x_top", "xq", "xqT",
                   "h", "h_top1", "h_top", "hq", "hT", "x")
    act_done.stage("clips", "silu")
    pool_done.stage("rstd")

    with ExitStack() as local:
        def sb(name, shape, dt=F32):
            return local.enter_context(nc.sbuf_tensor("l1f_" + name, shape, dt))

        gate_up = sb("gate_up", [128, 6, C])
        down = sb("down", [C, FFQ])
        tops, steps_, inverse = sb("tops", [128, 7]), sb("steps", [128, 7]), sb("inverse", [128, 7])
        gate_upT = sb("gate_upT", [C, 2, FFQ])
        downT = sb("downT", [128, 3, C])
        clips = sb("clips", [C, 2])
        top, top1 = sb("top", [T, 2]), sb("top1", [1, 2])
        a_step, a_inv = sb("a_step", [T, 2]), sb("a_inv", [T, 2])
        xq, xqT = sb("xq", [T, C]), sb("xqT", [C, T])
        silu, h = sb("silu", [T, FFQ]), sb("h", [T, FFQ])
        hT = sb("hT", [128, 3, T])

        with nc.Block(no_gpsimd_drain=True) as block:

            @block.tensor
            def _(pe):
                def spread_top(n):
                    name = "xh"[n]
                    pe.wait_ge(*dve_done.at(f"{name}_top1"))
                    nc.tensor.matmul(ps[0:T, 4, 128 + n:129 + n], mem.ones[0:1, 0:T], top1[0:1, n:n + 1],
                                     start=True, stop=True).then_inc(*pe_done.mark(f"{name}_top"))

                pe.wait_ge(*dve_done.at("w_quantised"))
                for m in range(2):
                    for n, (lo, rows) in enumerate(FFQ_CHUNKS):
                        nc.tensor.transpose(ps[0:C, 1 + m, lo:lo + rows], gate_up[0:rows, 3 * m + n, :],
                                            ident[0:rows, 0:rows])
                for n, (lo, rows) in enumerate(FFQ_CHUNKS):
                    last = nc.tensor.transpose(ps[0:rows, 3, n * C:(n + 1) * C], down[:, lo:lo + rows], ident)
                last.then_inc(*pe_done.mark("weightsT"))
                pe.wait_ge(*dve_done.at("xn"))
                nc.tensor.transpose(ps[0:1, 4, 0:T], top[:, 0:1], ident[0:T, 0:T])\
                    .then_inc(*pe_done.mark("x_topT"))
                spread_top(0)
                pe.wait_ge(*dve_done.at("xq"))
                nc.tensor.transpose(ps[0:C, 0, 0:T], xq[:, :], ident[0:T, 0:T]).then_inc(*pe_done.mark("xqT"))
                pe.wait_ge(*dve_done.at("xqT"))
                for m in range(2):
                    last = nc.tensor.matmul(ps[0:T, 5 + m, 0:FFQ], xqT[:, :], gate_upT[:, m, :], start=True,
                                            stop=True)
                last.then_inc(*pe_done.mark("gate_up"))
                pe.wait_ge(*dve_done.at("h"))
                nc.tensor.transpose(ps[0:1, 4, 0:T], top[:, 1:2], ident[0:T, 0:T])\
                    .then_inc(*pe_done.mark("h_topT"))
                spread_top(1)
                pe.wait_ge(*dve_done.at("hq"))
                for n, (lo, rows) in enumerate(FFQ_CHUNKS):
                    last = nc.tensor.transpose(ps[0:rows, 7, n * T:(n + 1) * T], h[:, lo:lo + rows],
                                               ident[0:T, 0:T])
                last.then_inc(*pe_done.mark("hT"))
                pe.wait_ge(*dve_done.at("hT"))
                for n, (lo, rows) in enumerate(FFQ_CHUNKS):
                    last = nc.tensor.matmul(ps[0:T, 0, 0:C], hT[0:rows, n, :], downT[0:rows, n, :],
                                            start=n == 0, stop=n == 2)
                last.then_inc(*pe_done.mark("out"))

            @block.scalar
            def _(act):
                act.wait_ge(mem.loaded["l1f"], 16)
                at, _, _ = column("l1f", "clip_x")
                nc.scalar.activation(clips[:, :], mem.packs["l1f"][:, at:at + 2], ACT.Exp, scale=-1.0)\
                    .then_inc(*act_done.mark("clips"))
                act.wait_ge(*pe_done.at("gate_up"))
                nc.scalar.activation(silu[:, :], ps[0:T, 5, 0:FFQ], ACT.Silu).then_inc(*act_done.mark("silu"))

            @block.gpsimd
            def _(pool):
                pool_rstd(mem, "var", "rstd")

            @block.vector
            def _(dve):
                v = nc.vector

                def rounded(out, scaled):
                    step(v.tensor_scalar(out, scaled, ROUND, ROUND, ALU.add, ALU.subtract))
                    step(v.tensor_scalar(out, out, 127.0, -128.0, ALU.min, ALU.max))

                def activation_step(n):
                    name = "xh"[n]
                    dve.wait_ge(*pe_done.at(f"{name}_topT"))
                    v.tensor_reduce(top1[0:1, n:n + 1], ps[0:1, 4, 0:T], AX_X, ALU.max)\
                        .then_inc(*dve_done.mark(f"{name}_top1"))
                    dve.wait_ge(*pe_done.at(f"{name}_top"))
                    step(v.tensor_scalar(a_step[:, n:n + 1], ps[0:T, 4, 128 + n:129 + n], clips[0:T, n:n + 1],
                                         1.0 / 127.0, ALU.mult, ALU.mult))
                    v.reciprocal(a_inv[:, n:n + 1], a_step[:, n:n + 1]).then_inc(*dve_done.mark(f"{name}_top"))
                    dve.wait_ge(*dve_done.at(f"{name}_top"))

                dve_moments(mem, mem.x[:, :], "var")
                step(dve_normalised(mem, mem.xn[:, :], mem.x[:, :], "rstd"))
                v.tensor_reduce(top[:, 0:1], mem.xn[:, :], AX_X, ALU.max, apply_absolute_value=True)\
                    .then_inc(*dve_done.mark("xn"))
                dve.wait_ge(mem.loaded["l1f"], 16)
                raw = mem.packs["l1f"][:, 0:6 * C].rearrange("p (n m) -> p n m", n=6)
                v.tensor_reduce(tops[:, 0:6], raw, AX_X, ALU.max, apply_absolute_value=True)
                step(v.tensor_reduce(tops[:, 6:7], mem.w("l1f", "w_down"), AX_X, ALU.max,
                                     apply_absolute_value=True))
                step(v.tensor_scalar(steps_[:, :], tops[:, :], 1e-30, 1.0 / 127.0, ALU.max, ALU.mult))
                step(v.reciprocal(inverse[:, :], steps_[:, :]))
                step(v.tensor_tensor(gate_up[:, :, :], raw, spread(inverse[:, 0:6], 2, [128, 6, C]), ALU.mult))
                rounded(gate_up[:, :, :], gate_up[:, :, :])
                step(v.tensor_tensor(gate_up[:, :, :], gate_up[:, :, :],
                                     spread(steps_[:, 0:6], 2, [128, 6, C]), ALU.mult))
                step(v.tensor_scalar(down[:, :], mem.w("l1f", "w_down"), inverse[:, 6:7], None, ALU.mult))
                rounded(down[:, :], down[:, :])
                v.tensor_scalar(down[:, :], down[:, :], steps_[:, 6:7], None, ALU.mult)\
                    .then_inc(*dve_done.mark("w_quantised"))
                dve.wait_ge(*pe_done.at("weightsT"))
                v.tensor_copy(gate_upT[:, :, :], ps[0:C, 1:3, 0:FFQ])
                v.tensor_copy(downT[:, 0:2, :], ps[:, 3, 0:2 * C].rearrange("p (n m) -> p n m", n=2))
                v.tensor_copy(downT[0:96, 2, :], ps[0:96, 3, 2 * C:3 * C]).then_inc(*dve_done.mark("wT"))
                dve.wait_ge(*act_done.at("clips"))
                step(v.tensor_scalar(clips[:, :], clips[:, :], 1.0, None, ALU.add))
                step(v.reciprocal(clips[:, :], clips[:, :]))
                activation_step(0)
                step(v.tensor_scalar(xq[:, :], mem.xn[:, :], a_inv[:, 0:1], None, ALU.mult))
                rounded(xq[:, :], xq[:, :])
                v.tensor_scalar(xq[:, :], xq[:, :], a_step[:, 0:1], None, ALU.mult)\
                    .then_inc(*dve_done.mark("xq"))
                dve.wait_ge(*pe_done.at("xqT"))
                v.tensor_copy(xqT[:, :], ps[0:C, 0, 0:T]).then_inc(*dve_done.mark("xqT"))
                dve.wait_ge(*act_done.at("silu"))
                step(v.tensor_tensor(h[:, :], silu[:, :], ps[0:T, 6, 0:FFQ], ALU.mult))
                v.tensor_reduce(top[:, 1:2], h[:, :], AX_X, ALU.max, apply_absolute_value=True)\
                    .then_inc(*dve_done.mark("h"))
                activation_step(1)
                step(v.tensor_scalar(h[:, :], h[:, :], a_inv[:, 1:2], None, ALU.mult))
                rounded(h[:, :], h[:, :])
                v.tensor_scalar(h[:, :], h[:, :], a_step[:, 1:2], None, ALU.mult).then_inc(*dve_done.mark("hq"))
                dve.wait_ge(*pe_done.at("hT"))
                v.tensor_copy(hT[:, 0:2, :], ps[:, 7, 0:2 * T].rearrange("p (n t) -> p n t", n=2))
                v.tensor_copy(hT[0:96, 2, :], ps[0:96, 7, 2 * T:3 * T]).then_inc(*dve_done.mark("hT"))
                dve.wait_ge(*pe_done.at("out"))
                v.tensor_tensor(mem.x[:, :], mem.x[:, :], ps[0:T, 0, 0:C], ALU.add).then_inc(*dve_done.mark("x"))



def stage_local_attention(mem):
    nc = mem.nc
    pe_done, act_done, dve_done, pool_done = mem.pe_done, mem.act_done, mem.dve_done, mem.pool_done
    step, ps = mem.dve_step, mem.psum
    ident = mem.w("consts", "ident")
    early = mem.early_values[3] = EarlyValues(mem, "l3x", context_load=4)
    pe_done.stage("xnT", "qkv", *SmallHeads.PE, "projected")
    dve_done.stage("var", "xn", "xnT", *SmallHeads.DVE[:1], "V", *SmallHeads.DVE[1:], "x")
    act_done.stage("exps")
    pool_done.stage("rstd")

    def w(name):
        return mem.w("l2a", name)

    with ExitStack() as local:
        def sb(name, shape, dt=F32):
            return local.enter_context(nc.sbuf_tensor("l2a_" + name, shape, dt))

        heads = SmallHeads(mem, sb, mem.w("consts", "band"))
        xnT = sb("xnT", [C, T])
        residual = sb("residual", [T, C])

        with nc.Block(no_gpsimd_drain=True) as block:

            @block.sync
            def _(sp):
                load_context(mem, sp)
                sp.dma_start(mem.experts[:, 0:width("experts2")], mem.dram["experts2"])\
                    .then_inc(mem.loaded["experts2"], 16)

            @block.tensor
            def _(pe):
                pe.wait_ge(*dve_done.at("xn"))
                nc.tensor.transpose(ps[0:C, 0, 0:T], mem.xn[:, :], ident[0:T, 0:T]).then_inc(*pe_done.mark("xnT"))
                pe.wait_ge(mem.loaded["l2a"], 16)
                pe.wait_ge(*dve_done.at("xnT"))
                nc.tensor.matmul(ps[0:C, 0, 0:T], w("w_q"), xnT[:, :], start=True, stop=True)
                nc.tensor.matmul(ps[0:C, 0, T:2 * T], w("w_k"), xnT[:, :], start=True, stop=True)
                nc.tensor.matmul(ps[0:T, 0, 128:256], xnT[:, :], w("w_v"), start=True, stop=True)\
                    .then_inc(*pe_done.mark("qkv"))
                heads.pe(pe, "V", lambda count: early.pe(pe, count), EARLY3[0:3])
                pe.wait_ge(*dve_done.at("OT"))
                nc.tensor.matmul(ps[0:T, 0, 0:C], heads.OT[:, :], w("w_o"), start=True, stop=True)\
                    .then_inc(*pe_done.mark("projected"))
                early.pe(pe, EARLY3[3])

            @block.scalar
            def _(act):
                heads.act(act)
                early.act(act, sum(EARLY3[0:4]))

            @block.gpsimd
            def _(pool):
                pool_rstd(mem, "var", "rstd")

            @block.vector
            def _(dve):
                v = nc.vector
                dve_moments(mem, mem.x[:, :], "var")
                dve_normalised(mem, mem.xn[:, :], mem.x[:, :], "rstd").then_inc(*dve_done.mark("xn"))
                v.tensor_tensor(residual[:, :], mem.x[:, :], mem.row("l2a_bo"), ALU.add)
                dve.wait_ge(*pe_done.at("xnT"))
                v.tensor_copy(xnT[:, :], ps[0:C, 0, 0:T]).then_inc(*dve_done.mark("xnT"))
                dve.wait_ge(mem.loaded["l2a"], 16)
                dve.wait_ge(*pe_done.at("qkv"))
                v.tensor_scalar(heads.KT[:, :], ps[0:C, 0, T:2 * T], w("b_k"), None, ALU.add)
                step(v.tensor_scalar(heads.QT[:, :], ps[0:C, 0, 0:T], w("b_q"), SCALE, ALU.add, ALU.mult))
                heads.dve_Qbd(dve)
                v.tensor_tensor(heads.V[:, :], ps[0:T, 0, 128:256], mem.row("l2a_bv"), ALU.add)\
                    .then_inc(*dve_done.mark("V"))
                heads.dve(dve)
                dve.wait_ge(*pe_done.at("projected"))
                v.tensor_tensor(mem.x[:, :], residual[:, :], ps[0:T, 0, 0:C], ALU.add)\
                    .then_inc(*dve_done.mark("x"))



def stage_transformer_experts(mem):
    nc = mem.nc
    pe_done, act_done, dve_done, pool_done = mem.pe_done, mem.act_done, mem.dve_done, mem.pool_done
    step, ps = mem.dve_step, mem.psum
    ident = mem.w("consts", "ident")
    GROUPS = 4
    early = mem.early_values[3]
    pe_done.stage("zT", "qkv", "turned", *SmallHeads.PE, "projected", "yT_in", "logits", "gates", "halves", "y")
    dve_done.stage("var", "z", "zT", "V", *SmallHeads.DVE, "mid_var", "mid", "midT", "scores", "gates", "halves",
                   "out_var", "x")
    act_done.stage("exps", "gate_exps")
    pool_done.stage("rstd", "mid_rstd", "out_rstd")
    weights = mem.experts

    def w(name):
        return mem.w("l2f", name)

    with ExitStack() as local:
        def sb(name, shape, dt=F32):
            return local.enter_context(nc.sbuf_tensor("l2f_" + name, shape, dt))

        heads = SmallHeads(mem, sb, None)
        experts = Experts(mem, sb, "l2f", E, HID2, ACT.Relu,
                          (weights[:, 0:E * HID2], weights[:, E * HID2:2 * E * HID2]))
        zT, midT = sb("zT", [C, T]), sb("midT", [C, T])
        qk, mid, out = sb("qk", [T, 2 * C]), sb("mid", [T, C]), sb("out", [T, C])
        residual = sb("residual", [T, C])
        scores, exps = sb("scores", [T, GROUPS + E]), sb("exps", [T, GROUPS + E])
        tops, totals = sb("tops", [T, 1 + GROUPS]), sb("totals", [T, 1 + GROUPS])
        padded, work, best = sb("padded", [T, 16]), sb("work", [T, 16]), sb("best", [T, 8])
        group_gate, pick = sb("group_gate", [T, GROUPS]), sb("pick", [T, GROUPS, 2])

        with nc.Block(no_gpsimd_drain=True) as block:

            @block.tensor
            def _(pe):
                pe.wait_ge(*dve_done.at("z"))
                nc.tensor.transpose(ps[0:C, 0, 0:T], mem.xn[:, :], ident[0:T, 0:T]).then_inc(*pe_done.mark("zT"))
                pe.wait_ge(mem.loaded["l2f"], 16)
                pe.wait_ge(*dve_done.at("zT"))
                nc.tensor.matmul(ps[0:T, 1, 0:3 * C], zT[:, :], w("w_in"), start=True, stop=True)\
                    .then_inc(*pe_done.mark("qkv"))
                pe.wait_ge(*dve_done.at("V"))
                nc.tensor.transpose(ps[0:C, 0, 0:T], qk[:, 0:C], ident[0:T, 0:T])
                nc.tensor.transpose(ps[0:C, 0, T:2 * T], qk[:, C:2 * C], ident[0:T, 0:T])\
                    .then_inc(*pe_done.mark("turned"))
                heads.pe(pe, "V", lambda count: early.pe(pe, count), EARLY3[4:7])
                pe.wait_ge(*dve_done.at("OT"))
                nc.tensor.matmul(ps[0:T, 0, 0:C], heads.OT[:, :], w("w_out"), start=True, stop=True)\
                    .then_inc(*pe_done.mark("projected"))
                early.pe(pe, EARLY3[7])
                pe.wait_ge(*dve_done.at("mid"))
                nc.tensor.transpose(ps[0:C, 0, 0:T], mid[:, :], ident[0:T, 0:T]).then_inc(*pe_done.mark("yT_in"))
                pe.wait_ge(*dve_done.at("midT"))
                at, _, _ = column("l2f", "w_group")
                nc.tensor.matmul(ps[0:T, 0, 128:128 + GROUPS + E], midT[:, :],
                                 mem.packs["l2f"][:, at:at + GROUPS + E], start=True, stop=True)\
                    .then_inc(*pe_done.mark("logits"))
                early.pe(pe, EARLY3[8])
                pe.wait_ge(mem.loaded["experts2"], 16)
                experts.pe_hidden(pe, midT[:, :])
                experts.pe_gates(pe, 3)
                experts.pe_out(pe)

            @block.scalar
            def _(act):
                heads.act(act)
                early.act(act, sum(EARLY3[4:8]))
                act.wait_ge(*dve_done.at("scores"))
                nc.scalar.activation(exps[:, :], scores[:, :], ACT.Exp).then_inc(*act_done.mark("gate_exps"))
                early.act(act, EARLY3[8])
                experts.act_hidden(act)

            @block.gpsimd
            def _(pool):
                pool_rstd(mem, "var", "rstd")
                pool_rstd(mem, "mid_var", "mid_rstd")
                pool_rstd(mem, "out_var", "out_rstd")

            @block.vector
            def _(dve):
                v = nc.vector
                dve_moments(mem, mem.x[:, :], "var")
                dve_normalised(mem, mem.xn[:, :], mem.x[:, :], "rstd").then_inc(*dve_done.mark("z"))
                dve.wait_ge(*dve_done.at("z"))
                v.tensor_tensor(residual[:, :], mem.xn[:, :], mem.row("l2f_b_out"), ALU.add)
                v.memset(padded[:, GROUPS:16], -1.0)
                dve.wait_ge(*pe_done.at("zT"))
                v.tensor_copy(zT[:, :], ps[0:C, 0, 0:T]).then_inc(*dve_done.mark("zT"))
                dve.wait_ge(*pe_done.at("qkv"))
                bias = mem.row("l2f_b_in")
                v.tensor_tensor(qk[:, :], ps[0:T, 1, 0:2 * C], bias[:, 0:2 * C], ALU.add)
                v.tensor_tensor(heads.V[:, :], ps[0:T, 1, 2 * C:3 * C], bias[:, 2 * C:3 * C], ALU.add)\
                    .then_inc(*dve_done.mark("V"))
                dve.wait_ge(*pe_done.at("turned"))
                v.tensor_copy(heads.KT[:, :], ps[0:C, 0, T:2 * T])
                step(v.tensor_scalar(heads.QT[:, :], ps[0:C, 0, 0:T], SCALE, None, ALU.mult))
                heads.dve_Qbd(dve)
                heads.dve(dve)
                dve.wait_ge(*pe_done.at("projected"))
                step(v.tensor_tensor(mid[:, :], ps[0:T, 0, 0:C], residual[:, :], ALU.add))
                dve_moments(mem, mid[:, :], "mid_var")
                step(dve_normalised(mem, mid[:, :], mid[:, :], "mid_rstd"))
                step(v.tensor_tensor(mid[:, :], mid[:, :], mem.row("l2f_g1"), ALU.mult))
                v.tensor_tensor(mid[:, :], mid[:, :], mem.row("l2f_b1"), ALU.add).then_inc(*dve_done.mark("mid"))
                dve.wait_ge(*pe_done.at("yT_in"))
                v.tensor_copy(midT[:, :], ps[0:C, 0, 0:T]).then_inc(*dve_done.mark("midT"))
                dve.wait_ge(*pe_done.at("logits"))
                at, _, _ = column("rows", "l2f_b_group")
                step(v.tensor_tensor(scores[:, :], ps[0:T, 0, 128:128 + GROUPS + E],
                                     mem.rows[:, at:at + GROUPS + E], ALU.add))
                pairs = scores[:, GROUPS:GROUPS + E].rearrange("t (g e) -> t g e", e=2)
                v.tensor_reduce(tops[:, 0:1], scores[:, 0:GROUPS], AX_X, ALU.max)
                step(v.tensor_reduce(tops[:, 1:1 + GROUPS], pairs, AX_X, ALU.max))
                v.tensor_scalar(scores[:, 0:GROUPS], scores[:, 0:GROUPS], tops[:, 0:1], None, ALU.subtract)
                v.tensor_tensor(pairs, pairs, spread(tops[:, 1:1 + GROUPS], 2, [T, GROUPS, 2]), ALU.subtract)\
                    .then_inc(*dve_done.mark("scores"))
                dve.wait_ge(*act_done.at("gate_exps"))
                probs = exps[:, GROUPS:GROUPS + E].rearrange("t (g e) -> t g e", e=2)
                v.tensor_reduce(totals[:, 0:1], exps[:, 0:GROUPS], AX_X, ALU.add)
                step(v.tensor_reduce(totals[:, 1:1 + GROUPS], probs, AX_X, ALU.add))
                step(v.reciprocal(totals[:, :], totals[:, :]))
                v.tensor_scalar(padded[:, 0:GROUPS], exps[:, 0:GROUPS], totals[:, 0:1], None, ALU.mult)
                step(v.tensor_tensor(probs, probs, spread(totals[:, 1:1 + GROUPS], 2, [T, GROUPS, 2]), ALU.mult))
                dve_first_largest(mem, padded[:, :], best[:, :], work[:, :], group_gate[:, :], GROUPS, 1)
                step(v.tensor_tensor(group_gate[:, :], group_gate[:, :], padded[:, 0:GROUPS], ALU.mult))
                step(v.tensor_tensor(pick[:, :, 0], probs[:, :, 0], probs[:, :, 1], ALU.is_ge))
                step(v.tensor_scalar(pick[:, :, 1], pick[:, :, 0], -1.0, 1.0, ALU.mult, ALU.add))
                step(v.tensor_tensor(pick[:, :, :], pick[:, :, :], probs, ALU.mult))
                step(v.tensor_tensor(experts.gates[:, :].rearrange("t (g e) -> t g e", e=2), pick[:, :, :],
                                     spread(group_gate[:, :], 2, [T, GROUPS, 2]), ALU.mult))
                dve.wait_ge(mem.loaded["l2f"], 16)
                experts.dve_gates(dve)
                experts.dve_bias(dve)
                experts.dve_gate(dve, 3)
                experts.dve_halves(dve)
                dve.wait_ge(*pe_done.at("y"))
                step(v.tensor_tensor(out[:, :], mid[:, :], ps[0:T, 7, 128:128 + C], ALU.add))
                dve_moments(mem, out[:, :], "out_var")
                step(dve_normalised(mem, out[:, :], out[:, :], "out_rstd"))
                step(v.tensor_tensor(out[:, :], out[:, :], mem.row("l2f_g2"), ALU.mult))
                step(v.tensor_tensor(out[:, :], out[:, :], mem.row("l2f_b2"), ALU.add))
                v.tensor_tensor(mem.x[:, :], mem.x[:, :], out[:, :], ALU.add).then_inc(*dve_done.mark("x"))



def stage_past_attention(mem):
    nc = mem.nc
    pe_done, act_done, dve_done, pool_done = mem.pe_done, mem.act_done, mem.dve_done, mem.pool_done
    step, ps = mem.dve_step, mem.psum
    ident = mem.w("consts", "ident")
    pe_done.stage("zT", "qT", "scores", "probsT", "contextT", "out")
    dve_done.stage("var", "z", "zT", "qT", "less_max", "probs", "probsT", "contextT", "out", "x")
    act_done.stage("exps", "tanh")
    pool_done.stage("rstd")

    with ExitStack() as local:
        def sb(name, shape, dt=F32):
            return local.enter_context(nc.sbuf_tensor("l3a_" + name, shape, dt))

        zT, qT, contextT = sb("zT", [C, T]), sb("qT", [C, T]), sb("contextT", [C, T])
        S, P, PT = sb("S", [T, T]), sb("P", [T, T]), sb("PT", [T, T])
        top, total = sb("top", [T, 1]), sb("total", [T, 1])
        out = sb("out", [T, C])

        with nc.Block(no_gpsimd_drain=True) as block:

            @block.tensor
            def _(pe):
                pe.wait_ge(*dve_done.at("z"))
                nc.tensor.transpose(ps[0:C, 0, 0:T], mem.xn[:, :], ident[0:T, 0:T]).then_inc(*pe_done.mark("zT"))
                pe.wait_ge(mem.loaded["l3a"], 16)
                pe.wait_ge(*dve_done.at("zT"))
                nc.tensor.matmul(ps[0:C, 1, 0:T], mem.w("l3a", "w_dec"), zT[:, :], start=True, stop=True)\
                    .then_inc(*pe_done.mark("qT"))
                pe.wait_ge(*dve_done.at("qT"))
                nc.tensor.matmul(ps[0:T, 2, 0:T], qT[:, :], zT[:, :], start=True, stop=True)\
                    .then_inc(*pe_done.mark("scores"))
                pe.wait_ge(*dve_done.at("probs"))
                nc.tensor.transpose(ps[0:T, 3, 0:T], P[:, :], ident[0:T, 0:T]).then_inc(*pe_done.mark("probsT"))
                pe.wait_ge(*dve_done.at("probsT"))
                nc.tensor.matmul(ps[0:C, 4, 0:T], mem.xn[:, :], PT[:, :], start=True, stop=True)\
                    .then_inc(*pe_done.mark("contextT"))
                pe.wait_ge(*dve_done.at("contextT"))
                w_out = mem.w("l3a", "w_out")
                nc.tensor.matmul(ps[0:T, 5, 0:C], zT[:, :], w_out[:, 0:C], start=True, stop=False)
                nc.tensor.matmul(ps[0:T, 5, 0:C], contextT[:, :], w_out[:, C:2 * C], start=False, stop=True)\
                    .then_inc(*pe_done.mark("out"))

            @block.scalar
            def _(act):
                act.wait_ge(*dve_done.at("less_max"))
                nc.scalar.activation(P[:, :], S[:, :], ACT.Exp, accum_out=total[:, :])\
                    .then_inc(*act_done.mark("exps"))
                act.wait_ge(*dve_done.at("out"))
                nc.scalar.activation(out[:, :], out[:, :], ACT.Tanh).then_inc(*act_done.mark("tanh"))

            @block.gpsimd
            def _(pool):
                pool_rstd(mem, "var", "rstd")

            @block.vector
            def _(dve):
                v = nc.vector
                dve_moments(mem, mem.x[:, :], "var")
                dve_normalised(mem, mem.xn[:, :], mem.x[:, :], "rstd").then_inc(*dve_done.mark("z"))
                dve.wait_ge(*pe_done.at("zT"))
                v.tensor_copy(zT[:, :], ps[0:C, 0, 0:T]).then_inc(*dve_done.mark("zT"))
                dve.wait_ge(*pe_done.at("qT"))
                v.tensor_copy(qT[:, :], ps[0:C, 1, 0:T]).then_inc(*dve_done.mark("qT"))
                dve.wait_ge(*pe_done.at("scores"))
                step(v.tensor_tensor(S[:, :], ps[0:T, 2, 0:T], mem.w("consts", "strict"), ALU.add))
                step(v.tensor_reduce(top[:, :], S[:, :], AX_X, ALU.max))
                v.tensor_scalar(S[:, :], S[:, :], top[:, :], None, ALU.subtract)\
                    .then_inc(*dve_done.mark("less_max"))
                dve.wait_ge(*act_done.at("exps"))
                step(v.reciprocal(total[:, :], total[:, :]))
                v.tensor_scalar(P[:, :], P[:, :], total[:, :], None, ALU.mult).then_inc(*dve_done.mark("probs"))
                dve.wait_ge(*pe_done.at("probsT"))
                v.tensor_copy(PT[:, :], ps[0:T, 3, 0:T]).then_inc(*dve_done.mark("probsT"))
                dve.wait_ge(*pe_done.at("contextT"))
                v.tensor_copy(contextT[:, :], ps[0:C, 4, 0:T]).then_inc(*dve_done.mark("contextT"))
                dve.wait_ge(*pe_done.at("out"))
                v.tensor_tensor(out[:, :], ps[0:T, 5, 0:C], mem.row("l3a_bo"), ALU.add)\
                    .then_inc(*dve_done.mark("out"))
                dve.wait_ge(*act_done.at("tanh"))
                v.tensor_tensor(mem.x[:, :], mem.x[:, :], out[:, :], ALU.add).then_inc(*dve_done.mark("x"))



class StateKernel:
    POOL = ["angles", "state_kernel"]
    ACT = ["sines"]
    LAGS = 16

    def __init__(self, mem, sb):
        N = NSTATE
        self.mem, self.sb = mem, sb
        self.wide = {n: sb("s4_" + n, [C, N])[:, :] for n in
                     ["re", "im", "grow", "grow_m1", "turns", "cos", "cos_m1", "nr", "gr", "gi", "t1", "t2", "size"]}
        self.dt, self.dt_m1 = sb("s4_dt", [C, 1])[:, :], sb("s4_dt_m1", [C, 1])[:, :]
        self.angles, self.sines = sb("s4_angles", [C, 2, N]), sb("s4_sines", [C, 2, N])
        self.pr, self.pi = sb("s4_pr", [C, 2, N]), sb("s4_pi", [C, 2, N])
        self.scratch = {n: (sb(f"s4_n{n}", [C, n])[:, :], sb(f"s4_r{n}", [C, n])[:, :], sb(f"s4_s{n}", [C, n])[:, :],
                            sb(f"s4_p{n}", [C, n], I32)[:, :]) for n in (1, N)}

        def lags(at, count):
            return mem.experts[:, at * N:(at + count) * N].rearrange("p (l n) -> p l n", n=N)

        self.qr, self.qi = lags(0, T), lags(T, T // 2)
        self.prod1, self.prod2 = lags(T + T // 2, self.LAGS), lags(T + T // 2 + self.LAGS, self.LAGS)

    def act(self, act):
        mem = self.mem
        act.wait_ge(*mem.pool_done.at("angles"))
        mem.nc.scalar.activation(self.sines[:, :, :], self.angles[:, :, :], ACT.Sin)\
            .then_inc(*mem.act_done.mark("sines"))

    def pool(self, pool):
        mem = self.mem
        p, step = mem.nc.gpsimd, mem.pool_step
        N = NSTATE
        (re, im, grow, grow_m1, turns, cos, cos_m1, nr, gr, gi, t1, t2, size) = self.wide.values()
        dt, dt_m1, angles, sines, pr, pi = self.dt, self.dt_m1, self.angles, self.sines, self.pr, self.pi
        qr, qi = self.qr, self.qi

        def w(name):
            return mem.w("l2x", name)

        def mul(out, a, b):
            step(p.tensor_tensor(out, a, b, ALU.mult))

        def add(out, a, b):
            step(p.tensor_tensor(out, a, b, ALU.add))

        def sub(out, a, b):
            step(p.tensor_tensor(out, a, b, ALU.subtract))

        def affine(out, a, scale, shift):
            step(p.tensor_scalar(out, a, scale, shift, ALU.mult, ALU.add))

        def exponential(z, full, less_one, n):
            whole, rest, series, power = self.scratch[n]
            step(p.tensor_scalar(z, z, -87.0, 88.0, ALU.max, ALU.min))
            affine(whole, z, LOG2E, ROUND)
            step(p.tensor_scalar(whole, whole, ROUND, None, ALU.subtract))
            step(p.tensor_scalar(series, whole, -LN2_HI, None, ALU.mult))
            add(rest, series, z)
            step(p.tensor_scalar(series, whole, -LN2_LO, None, ALU.mult))
            add(rest, series, rest)
            step(p.tensor_scalar(series, rest, 1.0 / 5040, None, ALU.mult))
            for k in (720, 120, 24, 6, 2, 1):
                step(p.tensor_scalar(series, series, 1.0 / k, None, ALU.add))
                mul(series, series, rest)
            step(p.tensor_scalar(power, whole, 127.0, 8388608.0, ALU.add, ALU.mult))
            two = power.bitcast(F32)
            mul(series, series, two)
            add(full, series, two)
            step(p.tensor_scalar(less_one, two, -1.0, None, ALU.add))
            add(less_one, less_one, series)

        pool.wait_ge(mem.loaded["l2x"], 16)
        step(p.tensor_copy(t1[:, 0:1], w("log_dt")))
        exponential(t1[:, 0:1], dt, dt_m1, 1)
        step(p.tensor_scalar(re, w("A_re"), dt, None, ALU.mult))
        step(p.tensor_scalar(im, w("A_im"), dt, None, ALU.mult))
        affine(turns, im, 1.0 / (2 * np.pi), ROUND)
        step(p.tensor_scalar(turns, turns, ROUND, None, ALU.subtract))
        for part in (TWO_PI_HI, TWO_PI_MID, TWO_PI_LO):
            step(p.tensor_scalar(t2, turns, -part, None, ALU.mult))
            add(im, im, t2)
        step(p.tensor_scalar(angles[:, 0, :], im, -3.1415925, 3.1415925, ALU.max, ALU.min))
        p.tensor_scalar(angles[:, 1, :], angles[:, 0, :], 0.5, None, ALU.mult)\
            .then_inc(*mem.pool_done.mark("angles"))
        exponential(re, grow, grow_m1, N)
        pool.wait_ge(*mem.act_done.at("sines"))
        mul(t1, sines[:, 1, :], sines[:, 1, :])
        step(p.tensor_scalar(cos_m1, t1, -2.0, None, ALU.mult))
        step(p.tensor_scalar(cos, cos_m1, 1.0, None, ALU.add))
        mul(pr[:, 0, :], grow, cos)
        mul(pi[:, 0, :], grow, sines[:, 0, :])
        mul(nr, grow_m1, cos)
        add(nr, nr, cos_m1)
        ni = pi[:, 0, :]
        mul(t1, nr, w("A_re"))
        mul(t2, ni, w("A_im"))
        add(gr, t1, t2)
        mul(t1, ni, w("A_re"))
        mul(t2, nr, w("A_im"))
        sub(gi, t1, t2)
        mul(t1, w("A_re"), w("A_re"))
        mul(t2, w("A_im"), w("A_im"))
        add(size, t1, t2)
        step(p.memset(t1, -1.0))
        step(p.tensor_tensor(size, size, t1, ALU.pow))
        mul(gr, gr, size)
        mul(gi, gi, size)
        mul(t1, gr, w("C_re"))
        mul(t2, gi, w("C_im"))
        sub(qr[:, 0, :], t1, t2)
        mul(t1, gi, w("C_re"))
        mul(t2, gr, w("C_im"))
        add(qi[:, 0, :], t1, t2)
        m = 1
        now = 0
        while m < T:
            for lo in range(0, m, self.LAGS):
                n = min(self.LAGS, m)
                terms, later = slice(lo, lo + n), slice(m + lo, m + lo + n)
                r, i = spread(pr[:, now, :], 1, [C, n, N]), spread(pi[:, now, :], 1, [C, n, N])
                a, b = self.prod1[:, 0:n, :], self.prod2[:, 0:n, :]
                mul(a, qr[:, terms, :], r)
                mul(b, qi[:, terms, :], i)
                sub(qr[:, later, :], a, b)
                if 2 * m < T:
                    mul(a, qr[:, terms, :], i)
                    mul(b, qi[:, terms, :], r)
                    add(qi[:, later, :], a, b)
            if 2 * m < T:
                mul(t1, pr[:, now, :], pr[:, now, :])
                mul(t2, pi[:, now, :], pi[:, now, :])
                sub(pr[:, 1 - now, :], t1, t2)
                mul(t1, pr[:, now, :], pi[:, now, :])
                step(p.tensor_scalar(pi[:, 1 - now, :], t1, 2.0, None, ALU.mult))
                now = 1 - now
            m *= 2
        n = N // 2
        while n:
            add(qr[:, :, 0:n], qr[:, :, 0:n], qr[:, :, n:2 * n])
            n //= 2
        p.tensor_scalar(mem.kernel_reversed[:, :], qr[:, ::-1, 0], 2.0, None, ALU.mult)\
            .then_inc(*mem.pool_done.mark("state_kernel"))



def stage_topk_attention(mem, context_load):
    nc = mem.nc
    pe_done, act_done, dve_done, pool_done = mem.pe_done, mem.act_done, mem.dve_done, mem.pool_done
    step, ps = mem.dve_step, mem.psum
    ident = mem.w("consts", "ident")
    CHOSEN = -2.0e38
    R = 2
    TPB = TPS
    BLOCKS = KT_TILES // TPB
    pe_done.stage("zT", "QT", "Q_ctx", "pooled", "pooledT", "contextT", "film", "aT", "mixed",
                  "hT", "hidden", "out")
    dve_done.stage("var", "z", "zT", "mask", "Qbd", "Q_ctx", "max0", "kept0", "picks0", "max1", "kept1",
                   "picks1", "pooled", "pooledT", "contextT", "a_var", "a", "film_out", "x_mid_var", "h", "hT",
                   "hidden", "out_var", "x")
    act_done.stage(*StateKernel.ACT, "exp0", "exp1", "hidden")
    pool_done.stage("rstd", *StateKernel.POOL, "a_rstd", "h_rstd", "out_rstd")
    scores_ready, scores_copied = mem.sem("l2x_scores_ready"), mem.sem("l2x_scores_copied")
    turned, turned_copied = mem.sem("l2x_turned"), mem.sem("l2x_turned_copied")
    masks_loaded, tiles_loaded = mem.sem("l2x_masks_loaded"), mem.sem("l2x_tiles_loaded")

    def w(name):
        return mem.w("l2x", name)

    def chunk_keys(c):
        return c * CHUNK, min(KEYS, (c + 1) * CHUNK)

    with ExitStack() as local:
        def sb(name, shape, dt=F32):
            return local.enter_context(nc.sbuf_tensor("l2x_" + name, shape, dt))

        S = mem.wide[:, :].rearrange("p (r k) -> p r k", r=R)
        left = mem.values[:, 0:KEYS]
        ctx_tiles = mem.keys_t[:, 0:KT_TILES * CTX]
        mask_row = mem.ctx_t[CTX:CTX + 1, :]
        mask8 = mem.values[CTX:CTX + 1, 0:KEYS // 4].bitcast(U8)
        zeros16 = sb("zeros16", [1, TPS * T], BF16)
        token8 = sb("token8", [C, T], U8)
        token_mask = sb("token_mask", [C, T])
        zT, QT, Qbd = sb("zT", [C, T]), sb("QT", [C, T]), sb("Qbd", [C, H2, T])
        Q_ctx = sb("Q_ctx", [CTX + 1, H2 * T])
        state_kernel = StateKernel(mem, sb)
        candidates = sb("candidates", [128, CHUNKS, 8])
        best = sb("best", [128, 4, 8])
        minus_max = sb("minus_max", [128, R])
        total, inverse = sb("total", [128, R]), sb("inverse", [128, R])
        pick = sb("pick", [128, R, T])
        turnedT = mem.values[:, 0:KT_TILES * T].rearrange("p (n t) -> p n t", t=T)
        pooled, pooledT, contextT = sb("pooled", [2 * T, CTX]), sb("pooledT", [CTX, T]), sb("contextT", [C, T])
        a, aT = sb("a", [T, C]), sb("aT", [C, T])
        film = sb("film", [C, 4, T])
        padded = sb("padded", [C, 2 * T - 1])
        products = mem.values[:, 0:T * T].rearrange("p (t l) -> p t l", l=T)
        mixed = sb("mixed", [C, T])
        x_mid, h, hT = sb("x_mid", [T, C]), sb("h", [T, C]), sb("hT", [C, T])
        pre, hidden = sb("pre", [C, HID // C, T]), sb("hidden", [C, HID // C, T])
        out = sb("out", [T, C])

        with nc.Block(no_gpsimd_drain=True) as block:

            @block.sync
            def _(sp):
                sp.dma_start(mask8, mem.dram["context_mask"]).then_inc(masks_loaded, 16)
                sp.dma_start(token8[:, :], mem.dram["token_mask"].to_broadcast([C, T])).then_inc(masks_loaded, 16)
                sp.dma_start(ctx_tiles, mem.dram["ctx_tiles"]).then_inc(tiles_loaded, 16)
                sp.wait_ge(tiles_loaded, 16)

            @block.tensor
            def _(pe):
                pe.wait_ge(*dve_done.at("z"))
                pe.wait_ge(mem.loaded["l2x"], 16)
                nc.tensor.transpose(ps[0:C, 0, 0:T], mem.xn[:, :], ident[0:T, 0:T]).then_inc(*pe_done.mark("zT"))
                pe.wait_ge(mem.loaded["ctx_first"], 16 * context_load)
                pe.wait_ge(mem.loaded["ctx_rest"], 16 * context_load)
                pe.wait_ge(*dve_done.at("zT"))
                nc.tensor.matmul(ps[0:C, 0, 128:192], w("Wq"), zT[:, :], start=True, stop=True)\
                    .then_inc(*pe_done.mark("QT"))
                pe.wait_ge(*dve_done.at("Qbd"))
                nc.tensor.matmul(ps[0:CTX, 0, 256:512], w("WkT"), Qbd[:, :, :], start=True, stop=True)\
                    .then_inc(*pe_done.mark("Q_ctx"))
                pe.wait_ge(*dve_done.at("Q_ctx"))
                pe.wait_ge(*dve_done.at("mask"))
                for r in range(R):
                    for c in range(CHUNKS):
                        lo, hi = chunk_keys(c)
                        n = r * CHUNKS + c
                        if n >= 4:
                            pe.wait_ge(scores_copied, n - 3)
                        bank = ps[:, 4 + n % 4, 0:hi - lo]
                        nc.tensor.matmul(bank, Q_ctx[:, 128 * r:128 * r + 128], mem.ctx_t[:, lo:hi],
                                         start=True, stop=True).then_inc(scores_ready, 1)
                pe.wait_ge(scores_copied, R * CHUNKS)
                for b in range(BLOCKS):
                    nc.tensor.matmul(ps[:, 1 + b, 0:TPB * T], zeros16[:, 0:128], zeros16[:, :], start=True, stop=False)
                for r in range(R):
                    pe.wait_ge(*dve_done.at(f"picks{r}"))
                    for t in range(KT_TILES):
                        at = t % TPB
                        last = nc.tensor.matmul(ps[:, 1 + t // TPB, at * T:(at + 1) * T],
                                                S[:, r, t * 128:(t + 1) * 128], pick[:, r, :],
                                                start=False,
                                                stop=r == R - 1 and at == TPB - 1)
                        if r == R - 1 and at == TPB - 1:
                            last.then_inc(turned, 1)
                pe.wait_ge(tiles_loaded, 16)
                for t in range(KT_TILES):
                    if t % TPB == 0:
                        pe.wait_ge(turned_copied, t // TPB + 1)
                    side = slice((t % 2) * T, (t % 2 + 1) * T)
                    last = nc.tensor.matmul(ps[side, 0, 0:CTX], turnedT[:, t, :],
                                            ctx_tiles[:, t * CTX:(t + 1) * CTX],
                                            start=t < 2, stop=t >= KT_TILES - 2)
                last.then_inc(*pe_done.mark("pooled"))
                pe.wait_ge(*dve_done.at("pooled"))
                nc.tensor.matmul(ps[0:CTX, 1, 0:T], pooled[:, :], mem.w("consts", "both_halves"), start=True,
                                 stop=True)\
                    .then_inc(*pe_done.mark("pooledT"))
                pe.wait_ge(*dve_done.at("pooledT"))
                nc.tensor.matmul(ps[0:C, 0, 0:T], w("Wv"), pooledT[:, :], start=True, stop=True)\
                    .then_inc(*pe_done.mark("contextT"))
                pe.wait_ge(*dve_done.at("contextT"))
                for n in range(4):
                    half = slice((n % 2) * C, (n % 2 + 1) * C)
                    last = nc.tensor.matmul(ps[0:C, 4, n * T:(n + 1) * T],
                                            w(["W_film_in", "W_film_out"][n // 2])[:, half], contextT[:, :],
                                            start=True, stop=True)
                last.then_inc(*pe_done.mark("film"))
                pe.wait_ge(*dve_done.at("a"))
                nc.tensor.transpose(ps[0:C, 5, 0:T], a[:, :], ident[0:T, 0:T]).then_inc(*pe_done.mark("aT"))
                pe.wait_ge(*dve_done.at("film_out"))
                nc.tensor.transpose(ps[0:T, 6, 0:C], mixed[:, :], ident).then_inc(*pe_done.mark("mixed"))
                pe.wait_ge(*dve_done.at("h"))
                nc.tensor.transpose(ps[0:C, 0, 0:T], h[:, :], ident[0:T, 0:T]).then_inc(*pe_done.mark("hT"))
                pe.wait_ge(*dve_done.at("hT"))
                for n in range(HID // C):
                    last = nc.tensor.matmul(ps[0:C, 1, n * T:(n + 1) * T], w("W1")[:, n * C:(n + 1) * C],
                                            hT[:, :], start=True, stop=True)
                last.then_inc(*pe_done.mark("hidden"))
                pe.wait_ge(*act_done.at("hidden"))
                for n in range(HID // C):
                    last = nc.tensor.matmul(ps[0:T, 2, 0:C], hidden[:, n, :], w("W2")[:, n * C:(n + 1) * C],
                                            start=n == 0, stop=n == HID // C - 1)
                last.then_inc(*pe_done.mark("out"))

            @block.scalar
            def _(act):
                state_kernel.act(act)
                for n in range(R * CHUNKS):
                    lo, hi = chunk_keys(n % CHUNKS)
                    act.wait_ge(scores_ready, n + 1)
                    nc.scalar.activation(S[:, n // CHUNKS, lo:hi], ps[:, 4 + n % 4, 0:hi - lo], ACT.Identity)\
                        .then_inc(scores_copied, 1)
                for r in range(R):
                    act.wait_ge(*dve_done.at(f"max{r}"))
                    nc.scalar.activation(S[:, r, :], S[:, r, :], ACT.Exp, bias=minus_max[:, r:r + 1])\
                        .then_inc(*act_done.mark(f"exp{r}"))
                act.wait_ge(*dve_done.at("hidden"))
                nc.scalar.activation(hidden[:, :, :], pre[:, :, :], ACT.Gelu).then_inc(*act_done.mark("hidden"))

            @block.gpsimd
            def _(pool):
                pool_rstd(mem, "var", "rstd")
                state_kernel.pool(pool)
                pool_rstd(mem, "a_var", "a_rstd")
                pool_rstd(mem, "x_mid_var", "h_rstd")
                pool_rstd(mem, "out_var", "out_rstd")

            @block.vector
            def _(dve):
                v = nc.vector
                dve_moments(mem, mem.x[:, :], "var")
                dve_normalised(mem, mem.xn[:, :], mem.x[:, :], "rstd").then_inc(*dve_done.mark("z"))
                v.memset(zeros16[:, :], 0.0)
                v.memset(padded[:, :], 0.0)
                dve.wait_ge(*pe_done.at("zT"))
                v.tensor_copy(zT[:, :], ps[0:C, 0, 0:T]).then_inc(*dve_done.mark("zT"))
                dve.wait_ge(masks_loaded, 32)
                v.tensor_copy(token_mask[:, :], token8[:, :])
                dve.wait_ge(mem.loaded["ctx_first"], 16 * context_load)
                dve.wait_ge(mem.loaded["ctx_rest"], 16 * context_load)
                v.tensor_scalar(mask_row, mask8, 1.0, 1e30, ALU.subtract, ALU.mult)\
                    .then_inc(*dve_done.mark("mask"))
                dve.wait_ge(*pe_done.at("QT"))
                step(v.tensor_scalar(QT[:, :], ps[0:C, 0, 128:192], D2 ** -0.5, None, ALU.mult))
                v.tensor_tensor(Qbd[:, :, :], spread(QT[:, :], 1, [C, H2, T]),
                                spread(mem.w("consts", "large_heads"), 2, [C, H2, T]), ALU.mult)\
                    .then_inc(*dve_done.mark("Qbd"))
                dve.wait_ge(*pe_done.at("Q_ctx"))
                v.memset(Q_ctx[CTX:CTX + 1, :], 1.0)
                v.tensor_copy(Q_ctx[0:CTX, :], ps[0:CTX, 0, 256:512]).then_inc(*dve_done.mark("Q_ctx"))
                dve.wait_ge(*dve_done.at("mask"))
                for c in range(CHUNKS):
                    lo, hi = chunk_keys(c)
                    dve.wait_ge(scores_copied, c + 1)
                    ins = v.max(candidates[:, c, :], S[:, 0, lo:hi])
                step(ins)
                for r in range(R):
                    dve.wait_ge(scores_copied, (r + 1) * CHUNKS)
                    source = S[:, r, :]
                    for k in range(TOPK // 8):
                        step(v.max(best[:, k, :], candidates[:, :, :] if k == r == 0 else source))
                        step(v.match_replace(left, best[:, k, :], source, LOWEST))
                        source = left
                        if k == 0:
                            v.tensor_scalar(minus_max[:, r:r + 1], best[:, 0, 0:1], -1.0, None, ALU.mult)\
                                .then_inc(*dve_done.mark(f"max{r}"))
                    dve.wait_ge(*act_done.at(f"exp{r}"))
                    v.scalar_tensor_tensor(out=S[:, r, :], in0=left, scalar=CHOSEN, in1=S[:, r, :],
                                           op0=ALU.is_le, op1=ALU.mult, accum_out=total[:, r:r + 1])\
                        .then_inc(*dve_done.mark(f"kept{r}"))
                    dve.wait_ge(*dve_done.at(f"kept{r}"))
                    step(v.reciprocal(inverse[:, r:r + 1], total[:, r:r + 1]))
                    v.tensor_scalar(pick[:, r, :], mem.w("consts", "mean_heads"), inverse[:, r:r + 1],
                                    None, ALU.mult).then_inc(*dve_done.mark(f"picks{r}"))
                for b in range(BLOCKS):
                    lo, hi = b * TPB, min(KT_TILES, (b + 1) * TPB)
                    dve.wait_ge(turned, b + 1)
                    v.tensor_copy(turnedT[:, lo:hi, :],
                                  ps[:, 1 + b, 0:(hi - lo) * T].rearrange("p (n t) -> p n t", t=T))\
                        .then_inc(turned_copied, 1)
                dve.wait_ge(*pe_done.at("pooled"))
                v.tensor_copy(pooled[:, :], ps[:, 0, 0:CTX]).then_inc(*dve_done.mark("pooled"))
                dve.wait_ge(*pe_done.at("pooledT"))
                v.tensor_copy(pooledT[:, :], ps[0:CTX, 1, 0:T]).then_inc(*dve_done.mark("pooledT"))
                dve.wait_ge(*pe_done.at("contextT"))
                v.tensor_tensor(contextT[:, :], ps[0:C, 0, 0:T], token_mask[:, :], ALU.mult)\
                    .then_inc(*dve_done.mark("contextT"))
                dve_moments(mem, mem.xn[:, :], "a_var")
                dve_normalised(mem, a[:, :], mem.xn[:, :], "a_rstd").then_inc(*dve_done.mark("a"))
                gate, (at_in, _, _), (at_out, _, _) = w("mod_gate"), column("l2x", "b_film_in"), column("l2x", "b_film_out")
                dve.wait_ge(*pe_done.at("film"))
                for n in range(4):
                    at = (at_in, at_out)[n // 2] + n % 2
                    ins = v.tensor_scalar(film[:, n, :], ps[0:C, 4, n * T:(n + 1) * T],
                                          mem.packs["l2x"][:, at:at + 1], gate, ALU.add, ALU.mult)
                step(ins)
                dve.wait_ge(*pe_done.at("aT"))
                step(v.tensor_scalar(aT[:, :], ps[0:C, 5, 0:T], w("g_norm_in"), w("b_norm_in"), ALU.mult, ALU.add))
                step(v.scalar_tensor_tensor(out=aT[:, :], in0=film[:, 0, :], scalar=1.0, in1=aT[:, :],
                                            op0=ALU.add, op1=ALU.mult))
                recent = padded[:, T - 1:2 * T - 1]
                step(v.tensor_tensor(recent, aT[:, :], film[:, 1, :], ALU.add))
                dve.wait_ge(*pool_done.at("state_kernel"))
                window = padded[:, :]
                window = bass.AP(window.tensor, window.offset, [list(window.ap[0]), [1, T], [1, T]])
                step(v.tensor_tensor(products, window, spread(mem.kernel_reversed[:, :], 1, [C, T, T]),
                                     ALU.mult))
                step(v.tensor_reduce(mixed[:, :], products, AX_X, ALU.add))
                step(v.scalar_tensor_tensor(out=mixed[:, :], in0=recent, scalar=w("D_skip"), in1=mixed[:, :],
                                            op0=ALU.mult, op1=ALU.add))
                step(v.scalar_tensor_tensor(out=mixed[:, :], in0=film[:, 2, :], scalar=1.0, in1=mixed[:, :],
                                            op0=ALU.add, op1=ALU.mult))
                v.tensor_tensor(mixed[:, :], mixed[:, :], film[:, 3, :], ALU.add)\
                    .then_inc(*dve_done.mark("film_out"))
                dve.wait_ge(*pe_done.at("mixed"))
                step(v.tensor_tensor(x_mid[:, :], ps[0:T, 6, 0:C], mem.xn[:, :], ALU.add))
                dve_moments(mem, x_mid[:, :], "x_mid_var")
                dve_normalised(mem, h[:, :], x_mid[:, :], "h_rstd").then_inc(*dve_done.mark("h"))
                step(v.tensor_tensor(x_mid[:, :], x_mid[:, :], mem.row("l2x_b2"), ALU.add))
                dve.wait_ge(*pe_done.at("hT"))
                v.tensor_scalar(hT[:, :], ps[0:C, 0, 0:T], w("g_ffn"), w("b_ffn"), ALU.mult, ALU.add)\
                    .then_inc(*dve_done.mark("hT"))
                dve.wait_ge(*pe_done.at("hidden"))
                v.tensor_tensor(pre[:, :, :], ps[0:C, 1, 0:4 * T].rearrange("p (n t) -> p n t", t=T),
                                spread(w("b1"), 2, [C, 4, T]), ALU.add).then_inc(*dve_done.mark("hidden"))
                dve.wait_ge(*pe_done.at("out"))
                step(v.tensor_tensor(out[:, :], ps[0:T, 2, 0:C], x_mid[:, :], ALU.add))
                dve_moments(mem, out[:, :], "out_var")
                step(dve_normalised(mem, out[:, :], out[:, :], "out_rstd"))
                step(v.tensor_tensor(out[:, :], out[:, :], mem.row("l2x_g_out"), ALU.mult))
                step(v.tensor_tensor(out[:, :], out[:, :], mem.row("l2x_b_out"), ALU.add))
                v.tensor_tensor(mem.x[:, :], mem.x[:, :], out[:, :], ALU.add).then_inc(*dve_done.mark("x"))



def stage_store(mem):
    nc = mem.nc
    stored = mem.sem("stored")
    with nc.Block() as block:

        @block.sync
        def _(sp):
            sp.dma_start(mem.dram["out"], mem.x[:, :]).then_inc(stored, 16)
            sp.wait_ge(stored, 16)
            for pack in SMALL:
                sp.wait_ge(mem.loaded[pack], 16)


def build(nc, dram):
    with ExitStack() as ctx:
        mem = Memory(nc, ctx, dram)
        stage_load(mem)
        for stage in STAGES:
            stage(mem)
        stage_store(mem)


def first_cross_attention(mem):
    stage_cross_attention(mem, 0, context_load=1)


def second_cross_attention(mem):
    stage_cross_attention(mem, 1, context_load=2)


def third_cross_attention(mem):
    stage_topk_attention(mem, context_load=3)


def fourth_cross_attention(mem):
    stage_cross_attention(mem, 3, context_load=4)


STAGES = [first_cross_attention, stage_rwkv, lambda mem: stage_topk_experts(mem, 0),
          second_cross_attention, stage_rope_attention, stage_quantised_ffn,
          third_cross_attention, stage_local_attention, stage_transformer_experts,
          fourth_cross_attention, stage_past_attention, lambda mem: stage_topk_experts(mem, 3)]



def shape_constants():
    p = np.arange(128)
    t = np.arange(T)
    key = np.arange(T)
    half = DH // 2
    inv_freq = (1.0 / 10000.0 ** (np.arange(half, dtype=np.float32) / half)).astype(np.float32)
    angle = t.astype(np.float32)[:, None] * inv_freq[None, :]
    cos, sin = np.cos(angle).astype(np.float32), np.sin(angle).astype(np.float32)
    query = p % T
    strict = (key[None, :] < t[:, None]) | ((t[:, None] == 0) & (key[None, :] == 0))

    def masked(keep):
        return np.where(keep, 0.0, -1e30).astype(np.float32)

    return {
        "ident": np.eye(128, dtype=np.float32),
        "four_heads": (p[:, None] // DH % HG == np.arange(HG)[None, :]).astype(np.float32),
        "large_heads": (p[:, None] // D2 == np.arange(H2)[None, :]).astype(np.float32),
        "even_out": np.tile(p[None, :] % 2 == 0, (128, 1)).astype(np.float32),
        "odd_out": np.tile(p[None, :] % 2 == 1, (128, 1)).astype(np.float32),
        "causal": masked(key[None, :] <= query[:, None]),
        "band": masked(np.abs(key[None, :] - query[:, None]) <= 3),
        "strict": masked(strict),
        "cos": np.concatenate([cos, cos], axis=1),
        "sin": np.concatenate([-sin, sin], axis=1),
        "both_halves": (query[:, None] == t[None, :]).astype(np.float32),
        "mean_heads": (np.float32(1.0 / H2) * (query[:, None] == t[None, :])).astype(np.float32),
    }


def layouts(a):
    def col(v):
        return v.reshape(-1, 1)

    def cols(v):
        return v.reshape(-1, C).T

    def fill(v):
        return np.broadcast_to(v.reshape(1, 1), (C, 1))

    def with_bias(w, b):
        return np.concatenate([w, b.reshape(1, -1)], axis=0)

    def rows_of(w):
        return w.reshape(-1, C, w.shape[-1]).transpose(1, 0, 2).reshape(C, -1)

    def whole_rows(w):
        n = -(-w.shape[0] // C)
        out = np.zeros((n * C, w.shape[1]), w.dtype)
        out[:w.shape[0]] = w
        return rows_of(out)

    def first(w):
        return w.transpose(1, 0, 2).reshape(C, -1)

    def second(w):
        return rows_of(w.reshape(-1, C))

    def get(prefix, **names):
        return {k: a[prefix + v] for k, v in names.items()}

    p0, p1, p2, p3 = "L0_attn_", "L1_ffn_", "L2_xattn_", "L3_ffn_"
    kv_w, kv_b = a["L3_xattn_Wkv"].reshape(H, 2, DH, CTX), a["L3_xattn_bkv"].reshape(H, 2, DH)
    shared = {n: np.concatenate([a[p3 + n], a[p3 + n + "_s"][None]], axis=0)
              for n in ["Wfc", "bfc", "Wproj", "bproj"]}
    packs = {
        "consts": shape_constants(),
        "l0x": {"Wq": a["L0_xattn_Wq"], "Wk": with_bias(a["L0_xattn_Wk"], a["L0_xattn_bk"]),
                "Wv": with_bias(a["L0_xattn_Wv"], a["L0_xattn_bv"]), "Wo": a["L0_xattn_Wo"]},
        "l0a": {"Wcv": rows_of(a[p0 + "Wcv"])}
        | {n: a[p0 + n] for n in ["Wk", "Wv", "Wr", "Wo", "Wck", "Wcr"]}
        | {n: col(a[p0 + n]) for n in ["ln0_g", "ln0_b", "ln1_g", "ln1_b", "time_decay", "time_first",
                                       "tm_k", "tm_v", "tm_r", "cm_k", "cm_r"]},
        "l0f": {"w_router": a["L0_ffn_w_router"], "b1": cols(a["L0_ffn_b1"]), "b2": a["L0_ffn_b2"]},
        "l1x": {"Wq": a["L1_xattn_Wq"].T, "Wk": with_bias(a["L1_xattn_Wk"].T, a["L1_xattn_bk"]),
                "Wv": with_bias(a["L1_xattn_Wv"].T, a["L1_xattn_bv"]), "Wo": a["L1_xattn_Wo"].T,
                "bq": col(a["L1_xattn_bq"])},
        "l1a": {"w_qkv": a["L1_attn_w_qkv"], "w_o": a["L1_attn_w_o"]},
        "l1f": {"w_gate": whole_rows(a[p1 + "w_gate"]), "w_up": whole_rows(a[p1 + "w_up"]),
                "w_down": a[p1 + "w_down"], "clip_x": fill(a[p1 + "clip_x"]),
                "clip_down": fill(a[p1 + "clip_down"])},
        "l2x": {n: a[p2 + n] for n in ["Wq", "Wv", "W_film_in", "W_film_out", "W1", "A_re", "A_im",
                                       "C_re", "C_im"]}
        | {n: col(a[p2 + n]) for n in ["g_norm_in", "b_norm_in", "g_ffn", "b_ffn", "D_skip", "log_dt"]}
        | {n: cols(a[p2 + n]) for n in ["b_film_in", "b_film_out", "b1"]}
        | {"WkT": a[p2 + "Wk"].T, "W2": rows_of(a[p2 + "W2"]), "mod_gate": fill(a[p2 + "mod_gate"])},
        "l2a": {n: a["L2_attn_" + n] for n in ["w_q", "w_k", "w_v", "w_o"]}
        | {n: col(a["L2_attn_" + n]) for n in ["b_q", "b_k"]},
        "l2f": {"w_in": a["L2_ffn_in_proj_w"].T, "w_out": a["L2_ffn_out_proj_w"].T,
                "w_group": a["L2_ffn_w_group"],
                "w_expert": a["L2_ffn_w_expert"].transpose(1, 0, 2).reshape(C, E),
                "b1": cols(a["L2_ffn_b1"]), "b2": a["L2_ffn_b2"]},
        "l3x": {"Wq": a["L3_xattn_Wq"].T, "Wo": a["L3_xattn_Wo"].T, "bq": col(a["L3_xattn_bq"]),
                "Wk": with_bias(kv_w[:, 0].reshape(C, CTX).T, kv_b[:, 0].reshape(C)),
                "Wv": with_bias(kv_w[:, 1].reshape(C, CTX).T, kv_b[:, 1].reshape(C))},
        "l3a": {"w_dec": a["L3_attn_w_dec_attn"], "w_out": rows_of(a["L3_attn_w_out"].T)},
        "l3f": {"w_router": a[p3 + "Wr"], "b1": cols(shared["bfc"]), "b2": shared["bproj"]},
        "experts0": {"w1": first(a["L0_ffn_w1"]), "w2": second(a["L0_ffn_w2"])},
        "experts2": {"w1": first(a["L2_ffn_w1"]), "w2": second(a["L2_ffn_w2"])},
        "experts3": {"w1": first(shared["Wfc"]), "w2": second(shared["Wproj"])},
        "rows": {n: v.reshape(1, -1) for n, v in {
            "l0x_bq": a["L0_xattn_bq"], "l0x_bo": a["L0_xattn_bo"], "l0x_gamma": a["L0_xattn_ln_gamma"],
            "l0x_beta": a["L0_xattn_ln_beta"], "l1x_bo": a["L1_xattn_bo"],
            "l2x_g_out": a[p2 + "g_norm_out"], "l2x_b_out": a[p2 + "b_norm_out"], "l2x_b2": a[p2 + "b2"],
            "l2a_bv": a["L2_attn_b_v"], "l2a_bo": a["L2_attn_b_o"], "l2f_b_in": a["L2_ffn_in_proj_b"],
            "l2f_b_out": a["L2_ffn_out_proj_b"], "l2f_g1": a["L2_ffn_ln1_g"], "l2f_b1": a["L2_ffn_ln1_b"],
            "l2f_g2": a["L2_ffn_ln2_g"], "l2f_b2": a["L2_ffn_ln2_b"], "l2f_b_group": a["L2_ffn_b_group"],
            "l2f_b_expert": a["L2_ffn_b_expert"], "l3x_bo": a["L3_xattn_bo"],
            "l3a_bo": a["L3_attn_b_out"]}.items()},
    }
    out = {}
    for pack, parts in packs.items():
        height = 1 if pack == "rows" else 128
        out[pack] = np.zeros((height, width(pack)), np.float32)
        for name, array in parts.items():
            at, rows, n = column(pack, name)
            assert array.shape == (rows, n), (pack, name, array.shape)
            out[pack][0:rows, at:at + n] = array
        assert len(parts) == len(PACKS[pack]), pack
    context = a["ctx_768"][0]
    out["ctx_t"] = np.concatenate([context.T, np.ones((1, KEYS), np.float32)], axis=0)
    out["ctx_tiles"] = context.reshape(KT_TILES, 128, CTX).transpose(1, 0, 2).reshape(128, KT_TILES * CTX)
    out["bias_rows"] = np.full((2, SUPERS, G, SUPER), BIAS_ROW, np.float16)
    out["token_mask"] = a["mask_BxS_bf1"].view(np.uint8).reshape(1, T)
    out["context_mask"] = a["mask_BxS2_bf1"].view(np.uint8).reshape(1, KEYS)
    out["x"] = a["x"][0]
    return {k: np.ascontiguousarray(v) for k, v in out.items()}


def kernel(**inputs):
    import concourse.bacc as bacc
    from concourse.bass_utils import run_bass_kernel_spmd

    nc = bacc.Bacc("TRN2", target_bir_lowering=False, num_devices=1)
    arrays = layouts({k: np.asarray(v) for k, v in inputs.items()})
    dram = {name: nc.dram_tensor(f"in_{name}", array.shape, mybir.dt.from_np(array.dtype),
                                 kind="ExternalInput").ap() for name, array in arrays.items()}
    dram["out"] = nc.dram_tensor("out_x", (T, C), F32, kind="ExternalOutput").ap()
    build(nc, dram)
    result = run_bass_kernel_spmd(nc, [{f"in_{k}": v for k, v in arrays.items()}], core_ids=[0])
    return result.results[0]["out_x"].reshape(1, T, C)
```
